# Optimizing a Trainium2 kernel written in Bass

```python
import numpy as np
import jax
import jax.numpy as jnp

def _softmax(x, axis=-1):
    return jax.nn.softmax(x, axis=axis)

def _gelu(x):
    return jax.nn.gelu(x, approximate=True)

def _silu(x):
    return jax.nn.silu(x)

def _sigmoid(x):
    return jax.nn.sigmoid(x)

def _layernorm(x, axis=-1, eps=1e-05):
    m = jnp.mean(x, axis=axis, keepdims=True)
    v = jnp.var(x, axis=axis, keepdims=True)
    return (x - m) / jnp.sqrt(v + eps)

def _scatter_add(tgt, idx, src, axis=0):
    return tgt.at[idx].add(src)

def _segment_sum(src, seg, n):
    return jax.ops.segment_sum(src, seg, n)
kernel_name = 'mk_gnn_ffn_d4_gnn_r32_0f6aa9'

def setup_inputs(seed: int=0):
    np.random.seed(seed)
    _w = jnp.asarray

    def _rec_inputs():
        import jax
        import jax.numpy as jnp
        _gk = jax.random.key(seed)
        x = -0.0002117 + 1 * jax.random.normal(jax.random.fold_in(_gk, 1), (3125, 256), jnp.float32)
        _s = jax.random.randint(jax.random.fold_in(_gk, 2), (25000,), 0, 3125, jnp.int32)
        _d = jax.random.randint(jax.random.fold_in(_gk, 3), (25000,), 0, 3125, jnp.int32)
        _loop = jnp.arange(3125, dtype=jnp.int32)
        src = jnp.concatenate([_s, _d, _loop])
        dst = jnp.concatenate([_d, _s, _loop])
        _o = jnp.argsort(dst, stable=True)
        src = src[_o]
        dst = dst[_o]
        edge_attr_64 = 0.000279952 + 1.00013 * jax.random.normal(jax.random.fold_in(_gk, 12), (53125, 64), jnp.float32)
        edge_type_8 = jax.random.randint(jax.random.fold_in(_gk, 14), (53125,), 0, 8, jnp.int32)
        return (x, src, dst, edge_attr_64, edge_type_8)
    x, src, dst, edge_attr_64, edge_type_8 = _rec_inputs()

    def _L0_gnn_setup():
        import jax, jax.numpy as jnp
        import numpy as np
        N = 3125
        E = 50000
        D = 256
        BN_EPS = 1e-05

        def _batchnorm(x, gamma, beta):
            mu = jnp.mean(x, axis=0)
            var = jnp.var(x, axis=0)
            return (x - mu) * jax.lax.rsqrt(var + BN_EPS) * gamma + beta

        def _gin_conv(x, src, dst, n, W1, b1, gamma, beta, W2, b2):
            agg = jax.ops.segment_sum(x[src], dst, num_segments=n)
            h = x + agg
            h = jax.nn.relu(_batchnorm(h @ W1 + b1, gamma, beta))
            return jax.nn.relu(h @ W2 + b2)
        key = jax.random.key(seed)
        ks = jax.random.split(key, 8)
        x = jax.random.normal(ks[0], (N, D), dtype=jnp.float32)
        edge_index = jax.random.randint(ks[1], (2, E), 0, N, dtype=jnp.int64)
        s = 0.02
        inp = {'x': x, 'edge_index': edge_index, 'g0': jnp.ones((D,), jnp.float32), 'b0': jnp.zeros((D,), jnp.float32), 'W1a': jax.random.normal(ks[2], (D, D), jnp.float32) * s, 'b1a': jnp.zeros((D,), jnp.float32), 'g1': jnp.ones((D,), jnp.float32), 'bt1': jnp.zeros((D,), jnp.float32), 'W1b': jax.random.normal(ks[3], (D, D), jnp.float32) * s, 'b1b': jnp.zeros((D,), jnp.float32), 'W2a': jax.random.normal(ks[4], (D, D), jnp.float32) * s, 'b2a': jnp.zeros((D,), jnp.float32), 'g2': jnp.ones((D,), jnp.float32), 'bt2': jnp.zeros((D,), jnp.float32), 'W2b': jax.random.normal(ks[5], (D, D), jnp.float32) * s, 'b2b': jnp.zeros((D,), jnp.float32)}
        return inp
    _L0_gnn_all = _L0_gnn_setup()
    _L0_gnn_in = {k: v for k, v in _L0_gnn_all.items() if k in ('g0', 'b0', 'W1a', 'b1a', 'g1', 'bt1', 'W1b', 'b1b', 'W2a', 'b2a', 'g2', 'bt2', 'W2b', 'b2b')}
    del _L0_gnn_all

    def _L0_ffn_setup():
        import jax, jax.numpy as jnp
        import numpy as np
        DIM = 256
        H = 8
        D = 64
        G = 64
        INNER = H * D
        SCALE = D ** (-0.5)
        key = jax.random.key(seed)
        ks = jax.random.split(key, 12)
        B, N = (4, 512)
        x = jax.random.normal(ks[0], (B, N, DIM), dtype=jnp.float32)
        s = lambda fan_in: 1.0 / np.sqrt(fan_in)
        W_fx = jax.random.normal(ks[1], (DIM, INNER), dtype=jnp.float32) * s(DIM)
        b_fx = jnp.zeros((INNER,), dtype=jnp.float32)
        W_x = jax.random.normal(ks[2], (DIM, INNER), dtype=jnp.float32) * s(DIM)
        b_x = jnp.zeros((INNER,), dtype=jnp.float32)
        A = jax.random.normal(ks[3], (G, D), dtype=jnp.float32)
        Q, _ = jnp.linalg.qr(A.T)
        W_slice = Q[:, :G].astype(jnp.float32)
        b_slice = jnp.zeros((G,), dtype=jnp.float32)
        W_q = jax.random.normal(ks[4], (D, D), dtype=jnp.float32) * s(D)
        W_k = jax.random.normal(ks[5], (D, D), dtype=jnp.float32) * s(D)
        W_v = jax.random.normal(ks[6], (D, D), dtype=jnp.float32) * s(D)
        W_out = jax.random.normal(ks[7], (INNER, DIM), dtype=jnp.float32) * s(INNER)
        b_out = jnp.zeros((DIM,), dtype=jnp.float32)
        temperature = jnp.ones((1, H, 1, 1), dtype=jnp.float32) * 0.5
        return {'x': x, 'W_fx': W_fx, 'b_fx': b_fx, 'W_x': W_x, 'b_x': b_x, 'W_slice': W_slice, 'b_slice': b_slice, 'W_q': W_q, 'W_k': W_k, 'W_v': W_v, 'W_out': W_out, 'b_out': b_out, 'temperature': temperature}
    _L0_ffn_all = _L0_ffn_setup()
    _L0_ffn_in = {k: v for k, v in _L0_ffn_all.items() if k in ('W_fx', 'b_fx', 'W_x', 'b_x', 'W_slice', 'b_slice', 'W_q', 'W_k', 'W_v', 'W_out', 'b_out', 'temperature')}
    del _L0_ffn_all

    def _L1_gnn_setup():
        import jax, jax.numpy as jnp
        import numpy as np
        N_NODES = 50000
        N_EDGES = 25000
        IN_CH = 256
        HEADS = 4
        HID = 64
        OUT_CH = 256
        NEG_SLOPE = 0.2
        key = jax.random.key(seed)
        ks = jax.random.split(key, 8)
        x = jax.random.normal(ks[0], (N_NODES, IN_CH), dtype=jnp.float32)
        edge_index = jax.random.randint(ks[1], (2, N_EDGES), 0, N_NODES, dtype=jnp.int64)
        W = jax.random.normal(ks[2], (IN_CH, HEADS * HID), dtype=jnp.float32) / np.sqrt(IN_CH)
        att_src = jax.random.normal(ks[3], (HEADS, HID), dtype=jnp.float32) / np.sqrt(HID)
        att_dst = jax.random.normal(ks[4], (HEADS, HID), dtype=jnp.float32) / np.sqrt(HID)
        bias = jnp.zeros((HEADS * HID,), dtype=jnp.float32)
        lin_w = jax.random.normal(ks[5], (HEADS * HID, OUT_CH), dtype=jnp.float32) / np.sqrt(HEADS * HID)
        lin_b = jnp.zeros((OUT_CH,), dtype=jnp.float32)
        return {'x': x, 'edge_index': edge_index, 'W': W, 'att_src': att_src, 'att_dst': att_dst, 'bias': bias, 'lin_w': lin_w, 'lin_b': lin_b}
    _L1_gnn_all = _L1_gnn_setup()
    _L1_gnn_in = {k: v for k, v in _L1_gnn_all.items() if k in ('W', 'att_src', 'att_dst', 'bias', 'lin_w', 'lin_b')}
    del _L1_gnn_all

    def _L1_ffn_setup():
        import jax, jax.numpy as jnp
        import numpy as np
        TOP_K = 2
        LN_EPS = 1e-05
        key = jax.random.key(seed)
        ks = jax.random.split(key, 8)
        B, S, D, E, H = (16, 1024, 256, 8, 1024)
        x = jax.random.normal(ks[0], (B, S, D), dtype=jnp.float32)
        Wr = jax.random.normal(ks[1], (D, E), dtype=jnp.float32) * 0.1
        br = jnp.zeros((E,), dtype=jnp.float32)
        ln_g = jnp.ones((E, D), dtype=jnp.float32)
        ln_b = jnp.zeros((E, D), dtype=jnp.float32)
        W1 = jax.random.normal(ks[2], (E, D, H), dtype=jnp.float32) * (1.0 / np.sqrt(D))
        b1 = jnp.zeros((E, H), dtype=jnp.float32)
        W2 = jax.random.normal(ks[3], (E, H, D), dtype=jnp.float32) * (1.0 / np.sqrt(H))
        b2 = jnp.zeros((E, D), dtype=jnp.float32)
        return {'x': x, 'Wr': Wr, 'br': br, 'ln_g': ln_g, 'ln_b': ln_b, 'W1': W1, 'b1': b1, 'W2': W2, 'b2': b2}
    _L1_ffn_all = _L1_ffn_setup()
    _L1_ffn_in = {k: v for k, v in _L1_ffn_all.items() if k in ('Wr', 'br', 'ln_g', 'ln_b', 'W1', 'b1', 'W2', 'b2')}
    del _L1_ffn_all

    def _L2_gnn_setup():
        import jax, jax.numpy as jnp
        import numpy as np
        N, E, H, ED = (625, 10000, 256, 64)
        key = jax.random.key(seed)
        ks = jax.random.split(key, 12)

        def init_w(k, shape, fan_in):
            return (jax.random.normal(k, shape, jnp.float32) / np.sqrt(fan_in)).astype(jnp.float32)
        h = jax.random.normal(ks[0], (N, H), jnp.float32)
        edge_indices = jax.random.randint(ks[1], (2, E), 0, N, jnp.int32)
        edge_attr = jax.random.normal(ks[2], (E, ED), jnp.float32)
        din = 2 * H + ED
        W1 = init_w(ks[3], (H, din), din)
        b1 = jnp.zeros((H,), jnp.float32)
        W2 = init_w(ks[4], (H, H), H)
        b2 = jnp.zeros((H,), jnp.float32)
        W_ih = init_w(ks[5], (3 * H, H), H)
        b_ih = jnp.zeros((3 * H,), jnp.float32)
        W_hh = init_w(ks[6], (3 * H, H), H)
        b_hh = jnp.zeros((3 * H,), jnp.float32)
        return {'h': h, 'edge_indices': edge_indices, 'edge_attr': edge_attr, 'W1': W1, 'b1': b1, 'W2': W2, 'b2': b2, 'W_ih': W_ih, 'b_ih': b_ih, 'W_hh': W_hh, 'b_hh': b_hh}
    _L2_gnn_all = _L2_gnn_setup()
    _L2_gnn_in = {k: v for k, v in _L2_gnn_all.items() if k in ('W1', 'b1', 'W2', 'b2', 'W_ih', 'b_ih', 'W_hh', 'b_hh')}
    del _L2_gnn_all

    def _L2_ffn_setup():
        import jax, jax.numpy as jnp
        import numpy as np
        B, K, D = (512, 16, 256)
        E = 32
        H = int(D * 0.25)
        key = jax.random.key(seed)
        ks = jax.random.split(key, 7)
        d_rs = D ** (-0.5)
        h_rs = H ** (-0.5)
        x = jax.random.normal(ks[0], (B, K, D), dtype=jnp.float32)
        router_w = jax.random.uniform(ks[1], (E, D), jnp.float32, -d_rs, d_rs)
        router_b = jax.random.uniform(ks[2], (E,), jnp.float32, -d_rs, d_rs)
        W1 = jax.random.uniform(ks[3], (E, D, H), jnp.float32, -h_rs, h_rs)
        b1 = jax.random.uniform(ks[4], (E, H), jnp.float32, -h_rs, h_rs)
        W2 = jax.random.uniform(ks[5], (E, H, D), jnp.float32, -d_rs, d_rs)
        b2 = jax.random.uniform(ks[6], (E, D), jnp.float32, -d_rs, d_rs)
        return {'x': x, 'router_w': router_w, 'router_b': router_b, 'W1': W1, 'b1': b1, 'W2': W2, 'b2': b2}
    _L2_ffn_all = _L2_ffn_setup()
    _L2_ffn_in = {k: v for k, v in _L2_ffn_all.items() if k in ('router_w', 'router_b', 'W1', 'b1', 'W2', 'b2')}
    del _L2_ffn_all

    def _L3_gnn_setup():
        import jax, jax.numpy as jnp
        import numpy as np
        N_NODES = 625
        N_EDGES = 10000
        IN_DIM = 256
        OUT_DIM = 256
        NUM_RELS = 8
        NUM_BASES = 4
        key = jax.random.key(seed)
        k = jax.random.split(key, 7)
        return {'h': jax.random.normal(k[0], (N_NODES, IN_DIM), dtype=jnp.float32), 'basis': jax.random.normal(k[1], (NUM_BASES, IN_DIM, OUT_DIM), dtype=jnp.float32) * (6.0 / (IN_DIM + OUT_DIM)) ** 0.5, 'w_comp': jax.random.normal(k[2], (NUM_RELS, NUM_BASES), dtype=jnp.float32), 'bias': jax.random.normal(k[3], (OUT_DIM,), dtype=jnp.float32) * 0.01, 'src': jax.random.randint(k[4], (N_EDGES,), 0, N_NODES, dtype=jnp.int32), 'dst': jax.random.randint(k[5], (N_EDGES,), 0, N_NODES, dtype=jnp.int32), 'etype': jax.random.randint(k[6], (N_EDGES,), 0, NUM_RELS, dtype=jnp.int32)}
    _L3_gnn_all = _L3_gnn_setup()
    _L3_gnn_in = {k: v for k, v in _L3_gnn_all.items() if k in ('basis', 'w_comp', 'bias')}
    del _L3_gnn_all

    def _L3_ffn_setup():
        import jax, jax.numpy as jnp
        import numpy as np
        E, D, H, TOP_K = (6, 256, 256, 2)
        ROUTER_H = D // 2
        key = jax.random.key(seed)
        ks = jax.random.split(key, 12)
        s = 1.0 / np.sqrt(D)
        sh = 1.0 / np.sqrt(H)
        sr = 1.0 / np.sqrt(ROUTER_H)
        return {'features': jax.random.normal(ks[0], (8, 128, D), dtype=jnp.float32), 'router_w1': jax.random.uniform(ks[1], (D, ROUTER_H), jnp.float32, -s, s), 'router_b1': jnp.zeros((ROUTER_H,), jnp.float32), 'router_w2': jax.random.uniform(ks[2], (ROUTER_H, E), jnp.float32, -sr, sr), 'router_b2': jnp.zeros((E,), jnp.float32), 'expert_w1': jax.random.uniform(ks[3], (E, D, H), jnp.float32, -s, s), 'expert_b1': jnp.zeros((E, H), jnp.float32), 'expert_w2': jax.random.uniform(ks[4], (E, H, H), jnp.float32, -sh, sh), 'expert_b2': jnp.zeros((E, H), jnp.float32), 'expert_w3': jax.random.uniform(ks[5], (E, H, D), jnp.float32, -sh, sh), 'expert_b3': jnp.zeros((E, D), jnp.float32)}
    _L3_ffn_all = _L3_ffn_setup()
    _L3_ffn_in = {k: v for k, v in _L3_ffn_all.items() if k in ('router_w1', 'router_b1', 'router_w2', 'router_b2', 'expert_w1', 'expert_b1', 'expert_w2', 'expert_b2', 'expert_w3', 'expert_b3')}
    del _L3_ffn_all
    return {'x': x, 'src': src, 'dst': dst, 'edge_attr_64': edge_attr_64, 'edge_type_8': edge_type_8, 'L0_gnn_g0': _L0_gnn_in['g0'], 'L0_gnn_b0': _L0_gnn_in['b0'], 'L0_gnn_W1a': _L0_gnn_in['W1a'], 'L0_gnn_b1a': _L0_gnn_in['b1a'], 'L0_gnn_g1': _L0_gnn_in['g1'], 'L0_gnn_bt1': _L0_gnn_in['bt1'], 'L0_gnn_W1b': _L0_gnn_in['W1b'], 'L0_gnn_b1b': _L0_gnn_in['b1b'], 'L0_gnn_W2a': _L0_gnn_in['W2a'], 'L0_gnn_b2a': _L0_gnn_in['b2a'], 'L0_gnn_g2': _L0_gnn_in['g2'], 'L0_gnn_bt2': _L0_gnn_in['bt2'], 'L0_gnn_W2b': _L0_gnn_in['W2b'], 'L0_gnn_b2b': _L0_gnn_in['b2b'], 'L0_ffn_W_fx': _L0_ffn_in['W_fx'], 'L0_ffn_b_fx': _L0_ffn_in['b_fx'], 'L0_ffn_W_x': _L0_ffn_in['W_x'], 'L0_ffn_b_x': _L0_ffn_in['b_x'], 'L0_ffn_W_slice': _L0_ffn_in['W_slice'], 'L0_ffn_b_slice': _L0_ffn_in['b_slice'], 'L0_ffn_W_q': _L0_ffn_in['W_q'], 'L0_ffn_W_k': _L0_ffn_in['W_k'], 'L0_ffn_W_v': _L0_ffn_in['W_v'], 'L0_ffn_W_out': _L0_ffn_in['W_out'], 'L0_ffn_b_out': _L0_ffn_in['b_out'], 'L0_ffn_temperature': _L0_ffn_in['temperature'], 'L1_gnn_W': _L1_gnn_in['W'], 'L1_gnn_att_src': _L1_gnn_in['att_src'], 'L1_gnn_att_dst': _L1_gnn_in['att_dst'], 'L1_gnn_bias': _L1_gnn_in['bias'], 'L1_gnn_lin_w': _L1_gnn_in['lin_w'], 'L1_gnn_lin_b': _L1_gnn_in['lin_b'], 'L1_ffn_Wr': _L1_ffn_in['Wr'], 'L1_ffn_br': _L1_ffn_in['br'], 'L1_ffn_ln_g': _L1_ffn_in['ln_g'], 'L1_ffn_ln_b': _L1_ffn_in['ln_b'], 'L1_ffn_W1': _L1_ffn_in['W1'], 'L1_ffn_b1': _L1_ffn_in['b1'], 'L1_ffn_W2': _L1_ffn_in['W2'], 'L1_ffn_b2': _L1_ffn_in['b2'], 'L2_gnn_W1': _L2_gnn_in['W1'], 'L2_gnn_b1': _L2_gnn_in['b1'], 'L2_gnn_W2': _L2_gnn_in['W2'], 'L2_gnn_b2': _L2_gnn_in['b2'], 'L2_gnn_W_ih': _L2_gnn_in['W_ih'], 'L2_gnn_b_ih': _L2_gnn_in['b_ih'], 'L2_gnn_W_hh': _L2_gnn_in['W_hh'], 'L2_gnn_b_hh': _L2_gnn_in['b_hh'], 'L2_ffn_router_w': _L2_ffn_in['router_w'], 'L2_ffn_router_b': _L2_ffn_in['router_b'], 'L2_ffn_W1': _L2_ffn_in['W1'], 'L2_ffn_b1': _L2_ffn_in['b1'], 'L2_ffn_W2': _L2_ffn_in['W2'], 'L2_ffn_b2': _L2_ffn_in['b2'], 'L3_gnn_basis': _L3_gnn_in['basis'], 'L3_gnn_w_comp': _L3_gnn_in['w_comp'], 'L3_gnn_bias': _L3_gnn_in['bias'], 'L3_ffn_router_w1': _L3_ffn_in['router_w1'], 'L3_ffn_router_b1': _L3_ffn_in['router_b1'], 'L3_ffn_router_w2': _L3_ffn_in['router_w2'], 'L3_ffn_router_b2': _L3_ffn_in['router_b2'], 'L3_ffn_expert_w1': _L3_ffn_in['expert_w1'], 'L3_ffn_expert_b1': _L3_ffn_in['expert_b1'], 'L3_ffn_expert_w2': _L3_ffn_in['expert_w2'], 'L3_ffn_expert_b2': _L3_ffn_in['expert_b2'], 'L3_ffn_expert_w3': _L3_ffn_in['expert_w3'], 'L3_ffn_expert_b3': _L3_ffn_in['expert_b3']}

def reference(x, src, dst, edge_attr_64, edge_type_8, L0_gnn_g0, L0_gnn_b0, L0_gnn_W1a, L0_gnn_b1a, L0_gnn_g1, L0_gnn_bt1, L0_gnn_W1b, L0_gnn_b1b, L0_gnn_W2a, L0_gnn_b2a, L0_gnn_g2, L0_gnn_bt2, L0_gnn_W2b, L0_gnn_b2b, L0_ffn_W_fx, L0_ffn_b_fx, L0_ffn_W_x, L0_ffn_b_x, L0_ffn_W_slice, L0_ffn_b_slice, L0_ffn_W_q, L0_ffn_W_k, L0_ffn_W_v, L0_ffn_W_out, L0_ffn_b_out, L0_ffn_temperature, L1_gnn_W, L1_gnn_att_src, L1_gnn_att_dst, L1_gnn_bias, L1_gnn_lin_w, L1_gnn_lin_b, L1_ffn_Wr, L1_ffn_br, L1_ffn_ln_g, L1_ffn_ln_b, L1_ffn_W1, L1_ffn_b1, L1_ffn_W2, L1_ffn_b2, L2_gnn_W1, L2_gnn_b1, L2_gnn_W2, L2_gnn_b2, L2_gnn_W_ih, L2_gnn_b_ih, L2_gnn_W_hh, L2_gnn_b_hh, L2_ffn_router_w, L2_ffn_router_b, L2_ffn_W1, L2_ffn_b1, L2_ffn_W2, L2_ffn_b2, L3_gnn_basis, L3_gnn_w_comp, L3_gnn_bias, L3_ffn_router_w1, L3_ffn_router_b1, L3_ffn_router_w2, L3_ffn_router_b2, L3_ffn_expert_w1, L3_ffn_expert_b1, L3_ffn_expert_w2, L3_ffn_expert_b2, L3_ffn_expert_w3, L3_ffn_expert_b3):
    import jax
    import jax.numpy as jnp

    def _L0_gnn_ref(x, edge_index, g0, b0, W1a, b1a, g1, bt1, W1b, b1b, W2a, b2a, g2, bt2, W2b, b2b):
        import jax, jax.numpy as jnp
        import numpy as np
        N = 3125
        E = 50000
        D = 256
        BN_EPS = 1e-05

        def _batchnorm(x, gamma, beta):
            mu = jnp.mean(x, axis=0)
            var = jnp.var(x, axis=0)
            return (x - mu) * jax.lax.rsqrt(var + BN_EPS) * gamma + beta

        def _gin_conv(x, src, dst, n, W1, b1, gamma, beta, W2, b2):
            agg = jax.ops.segment_sum(x[src], dst, num_segments=n)
            h = x + agg
            h = jax.nn.relu(_batchnorm(h @ W1 + b1, gamma, beta))
            return jax.nn.relu(h @ W2 + b2)
        n = x.shape[0]
        src, dst = (edge_index[0], edge_index[1])
        h = _batchnorm(x, g0, b0)
        h = _gin_conv(h, src, dst, n, W1a, b1a, g1, bt1, W1b, b1b)
        h = jax.nn.relu(h)
        h = _gin_conv(h, src, dst, n, W2a, b2a, g2, bt2, W2b, b2b)
        return jax.nn.relu(h)

    def _L0_ffn_ref(x, W_fx, b_fx, W_x, b_x, W_slice, b_slice, W_q, W_k, W_v, W_out, b_out, temperature):
        import jax, jax.numpy as jnp
        import numpy as np
        DIM = 256
        H = 8
        D = 64
        G = 64
        INNER = H * D
        SCALE = D ** (-0.5)
        B, N, _ = x.shape
        fx_mid = (x @ W_fx + b_fx).reshape(B, N, H, D).transpose(0, 2, 1, 3)
        x_mid = (x @ W_x + b_x).reshape(B, N, H, D).transpose(0, 2, 1, 3)
        temp = jnp.clip(temperature, 0.1, 5.0)
        slice_weights = jax.nn.softmax((x_mid @ W_slice + b_slice) / temp, axis=-1)
        slice_norm = slice_weights.sum(axis=2)
        slice_token = jnp.einsum('bhnc,bhng->bhgc', fx_mid, slice_weights)
        slice_token = slice_token / (slice_norm[..., None] + 1e-05)
        q = slice_token @ W_q
        k = slice_token @ W_k
        v = slice_token @ W_v
        attn = jax.nn.softmax(jnp.einsum('bhgc,bhkc->bhgk', q, k) * SCALE, axis=-1)
        out_slice = jnp.einsum('bhgk,bhkc->bhgc', attn, v)
        out_x = jnp.einsum('bhgc,bhng->bhnc', out_slice, slice_weights)
        out_x = out_x.transpose(0, 2, 1, 3).reshape(B, N, INNER)
        return out_x @ W_out + b_out

    def _L1_gnn_ref(x, edge_index, W, att_src, att_dst, bias, lin_w, lin_b):
        import jax, jax.numpy as jnp
        import numpy as np
        N_NODES = 50000
        N_EDGES = 25000
        IN_CH = 256
        HEADS = 4
        HID = 64
        OUT_CH = 256
        NEG_SLOPE = 0.2
        N = x.shape[0]
        H, C = att_src.shape
        loop = jnp.arange(N, dtype=edge_index.dtype)
        src = jnp.concatenate([edge_index[0], loop])
        dst = jnp.concatenate([edge_index[1], loop])
        h = (x @ W).reshape(N, H, C)
        a_s = jnp.einsum('nhc,hc->nh', h, att_src)
        a_d = jnp.einsum('nhc,hc->nh', h, att_dst)
        e = a_s[src] + a_d[dst]
        e = jnp.where(e > 0, e, NEG_SLOPE * e)
        m = jax.ops.segment_max(e, dst, num_segments=N)
        p = jnp.exp(e - m[dst])
        denom = jax.ops.segment_sum(p, dst, num_segments=N)
        alpha = p / (denom[dst] + 1e-16)
        msg = h[src] * alpha[:, :, None]
        agg = jax.ops.segment_sum(msg, dst, num_segments=N)
        out = agg.reshape(N, H * C) + bias
        out = out @ lin_w + lin_b
        return jnp.maximum(out, 0.0)

    def _L1_ffn_ref(x, Wr, br, ln_g, ln_b, W1, b1, W2, b2):
        import jax, jax.numpy as jnp
        import numpy as np
        TOP_K = 2
        LN_EPS = 1e-05
        B, S, D = x.shape
        N = B * S
        xt = x.reshape(N, D)
        logits = xt @ Wr + br
        probs = jax.nn.softmax(logits, axis=-1)
        top_p, top_idx = jax.lax.top_k(probs, TOP_K)
        weights = top_p / top_p.sum(axis=-1, keepdims=True)
        mu = xt.mean(axis=-1, keepdims=True)
        var = ((xt - mu) ** 2).mean(axis=-1, keepdims=True)
        xn = (xt - mu) * jax.lax.rsqrt(var + LN_EPS)
        xe = xn[None, :, :] * ln_g[:, None, :] + ln_b[:, None, :]
        h = jax.nn.gelu(jnp.einsum('end,edh->enh', xe, W1) + b1[:, None, :], approximate=False)
        y = jnp.einsum('enh,ehd->end', h, W2) + b2[:, None, :]
        y_tok = jnp.transpose(y, (1, 0, 2))
        sel = jnp.take_along_axis(y_tok, top_idx[:, :, None], axis=1)
        out = (weights[:, :, None] * sel).sum(axis=1)
        return out.reshape(B, S, D)

    def _L2_gnn_ref(h, edge_indices, edge_attr, W1, b1, W2, b2, W_ih, b_ih, W_hh, b_hh):
        import jax, jax.numpy as jnp
        import numpy as np
        N, E, H, ED = (625, 10000, 256, 64)
        row, col = (edge_indices[0], edge_indices[1])
        edge_in = jnp.concatenate([h[row], h[col], edge_attr], axis=-1)
        msg = jax.nn.relu(edge_in @ W1.T + b1) @ W2.T + b2
        agg = jax.ops.segment_sum(msg, row, num_segments=h.shape[0])
        gx = agg @ W_ih.T + b_ih
        gh = h @ W_hh.T + b_hh
        xr, xz, xn = jnp.split(gx, 3, axis=-1)
        hr, hz, hn = jnp.split(gh, 3, axis=-1)
        r = jax.nn.sigmoid(xr + hr)
        z = jax.nn.sigmoid(xz + hz)
        n = jnp.tanh(xn + r * hn)
        h_new = (1.0 - z) * n + z * h
        return h_new

    def _L2_ffn_ref(x, router_w, router_b, W1, b1, W2, b2):
        import jax, jax.numpy as jnp
        import numpy as np
        B, K, D = (512, 16, 256)
        E = 32
        H = int(D * 0.25)
        xf = x.reshape(-1, D)
        logits = xf @ router_w.T + router_b
        idx = jnp.argmax(logits, axis=-1)
        w1t = jnp.take(W1, idx, axis=0)
        h = jnp.einsum('nd,ndh->nh', xf, w1t) + jnp.take(b1, idx, axis=0)
        h = jax.nn.relu(h)
        w2t = jnp.take(W2, idx, axis=0)
        out = jnp.einsum('nh,nhd->nd', h, w2t) + jnp.take(b2, idx, axis=0)
        out = jax.nn.relu(out)
        return out.reshape(x.shape)

    def _L3_gnn_ref(h, basis, w_comp, bias, src, dst, etype):
        import jax, jax.numpy as jnp
        import numpy as np
        N_NODES = 625
        N_EDGES = 10000
        IN_DIM = 256
        OUT_DIM = 256
        NUM_RELS = 8
        NUM_BASES = 4
        in_dim, out_dim = (h.shape[1], basis.shape[2])
        num_rels = w_comp.shape[0]
        wr = basis.reshape(in_dim, NUM_BASES, out_dim)
        weight = jnp.einsum('rb,ibo->iro', w_comp, wr)
        weight = weight.reshape(num_rels, in_dim, out_dim)
        t = jnp.einsum('nd,rdo->rno', h, weight)
        msg = t[etype, src]
        agg = jax.ops.segment_sum(msg, dst, num_segments=h.shape[0])
        return jax.nn.relu(agg + bias)

    def _L3_ffn_ref(features, router_w1, router_b1, router_w2, router_b2, expert_w1, expert_b1, expert_w2, expert_b2, expert_w3, expert_b3):
        import jax, jax.numpy as jnp
        import numpy as np
        E, D, H, TOP_K = (6, 256, 256, 2)
        ROUTER_H = D // 2
        rh = jax.nn.relu(features @ router_w1 + router_b1)
        expert_logits = jax.nn.softmax(rh @ router_w2 + router_b2, axis=-1)
        top_w, top_i = jax.lax.top_k(expert_logits, TOP_K)
        routing_weights = jax.nn.softmax(top_w, axis=-1)
        h1 = jax.nn.relu(jnp.einsum('bsd,edh->bseh', features, expert_w1) + expert_b1)
        h2 = jax.nn.relu(jnp.einsum('bseh,ehf->bsef', h1, expert_w2) + expert_b2)
        expert_out = jnp.einsum('bsef,efo->bseo', h2, expert_w3) + expert_b3
        sel = jnp.take_along_axis(expert_out, top_i[:, :, :, None], axis=2)
        combined = jnp.sum(sel * routing_weights[..., None], axis=2)
        return combined
    edge_index = jnp.stack([src, dst])
    x = x + _L0_gnn_ref(_layernorm(x, axis=-1), edge_index, L0_gnn_g0, L0_gnn_b0, L0_gnn_W1a, L0_gnn_b1a, L0_gnn_g1, L0_gnn_bt1, L0_gnn_W1b, L0_gnn_b1b, L0_gnn_W2a, L0_gnn_b2a, L0_gnn_g2, L0_gnn_bt2, L0_gnn_W2b, L0_gnn_b2b)
    x = x + _L0_ffn_ref(_layernorm(x, axis=-1)[None], L0_ffn_W_fx, L0_ffn_b_fx, L0_ffn_W_x, L0_ffn_b_x, L0_ffn_W_slice, L0_ffn_b_slice, L0_ffn_W_q, L0_ffn_W_k, L0_ffn_W_v, L0_ffn_W_out, L0_ffn_b_out, L0_ffn_temperature)[0]
    x = x + _L1_gnn_ref(_layernorm(x, axis=-1), edge_index, L1_gnn_W, L1_gnn_att_src, L1_gnn_att_dst, L1_gnn_bias, L1_gnn_lin_w, L1_gnn_lin_b)
    x = x + _L1_ffn_ref(_layernorm(x, axis=-1)[None], L1_ffn_Wr, L1_ffn_br, L1_ffn_ln_g, L1_ffn_ln_b, L1_ffn_W1, L1_ffn_b1, L1_ffn_W2, L1_ffn_b2)[0]
    x = x + _L2_gnn_ref(_layernorm(x, axis=-1), edge_index, edge_attr_64, L2_gnn_W1, L2_gnn_b1, L2_gnn_W2, L2_gnn_b2, L2_gnn_W_ih, L2_gnn_b_ih, L2_gnn_W_hh, L2_gnn_b_hh)
    x = x + _L2_ffn_ref(_layernorm(x, axis=-1)[None], L2_ffn_router_w, L2_ffn_router_b, L2_ffn_W1, L2_ffn_b1, L2_ffn_W2, L2_ffn_b2)[0]
    x = x + _L3_gnn_ref(_layernorm(x, axis=-1), L3_gnn_basis, L3_gnn_w_comp, L3_gnn_bias, src, dst, edge_type_8)
    x = x + _L3_ffn_ref(_layernorm(x, axis=-1)[None], L3_ffn_router_w1, L3_ffn_router_b1, L3_ffn_router_w2, L3_ffn_router_b2, L3_ffn_expert_w1, L3_ffn_expert_b1, L3_ffn_expert_w2, L3_ffn_expert_b2, L3_ffn_expert_w3, L3_ffn_expert_b3)[0]
    return x

_drawn_inputs = setup_inputs


def setup_inputs(seed=0):
    import zlib

    import numpy as np

    out = dict(_drawn_inputs(seed))
    spreads = {'L0_gnn_g0': (1.0, 0.2),
     'L0_gnn_b0': (0.0, 0.1),
     'L0_gnn_b1a': (0.0, 2.0),
     'L0_gnn_g1': (1.0, 0.2),
     'L0_gnn_bt1': (0.0, 0.1),
     'L0_gnn_b1b': (0.0, 0.1),
     'L0_gnn_b2a': (0.0, 2.0),
     'L0_gnn_g2': (1.0, 0.2),
     'L0_gnn_bt2': (0.0, 0.1),
     'L0_gnn_b2b': (0.0, 0.1),
     'L0_ffn_b_fx': (0.0, 0.1),
     'L0_ffn_b_x': (0.0, 0.372),
     'L0_ffn_b_slice': (0.0, 0.525),
     'L0_ffn_b_out': (0.0, 0.1),
     'L0_ffn_temperature': (0.5, 0.6),
     'L1_gnn_bias': (0.0, 0.1),
     'L1_gnn_lin_b': (0.0, 0.1),
     'L1_ffn_br': (0.0, 0.1),
     'L1_ffn_ln_g': (1.0, 0.2),
     'L1_ffn_ln_b': (0.0, 0.1),
     'L1_ffn_b1': (0.0, 0.1),
     'L1_ffn_b2': (0.0, 0.1),
     'L2_gnn_b1': (0.0, 0.1),
     'L2_gnn_b2': (0.0, 0.1),
     'L2_gnn_b_ih': (0.0, 0.535),
     'L2_gnn_b_hh': (0.0, 0.619),
     'L3_ffn_router_b1': (0.0, 0.8),
     'L3_ffn_router_b2': (0.0, 0.8),
     'L3_ffn_expert_b1': (0.0, 0.8),
     'L3_ffn_expert_b2': (0.0, 0.8),
     'L3_ffn_expert_b3': (0.0, 2.0)}
    factors = {'L0_ffn_W_slice': 3.17,
     'L0_ffn_W_q': 7.857,
     'L0_ffn_W_k': 8.0,
     'L2_ffn_b1': 8.0,
     'L2_ffn_b2': 4.635,
     'L3_gnn_bias': 8.0,
     'L3_ffn_router_w1': 8.0,
     'L3_ffn_router_w2': 7.57,
     'L3_ffn_expert_w1': 8.0,
     'L3_ffn_expert_w2': 8.0,
     'L3_ffn_expert_w3': 8.0}
    for name, (base, spread) in spreads.items():
        noise = np.random.default_rng([zlib.crc32(name.encode()), seed]).standard_normal(out[name].shape)
        drawn = base * np.exp(spread * noise) if base else spread * noise
        out[name] = jnp.asarray(drawn.astype(out[name].dtype))
    for name, factor in factors.items():
        out[name] = (out[name] * factor).astype(out[name].dtype)
    return out
```

```python
from contextlib import ExitStack

import numpy as np
import concourse.bass as bass
from concourse import mybir

ALU = mybir.AluOpType
ACT = mybir.ActivationFunctionType
F32 = mybir.dt.float32
BF16 = mybir.dt.bfloat16
I32 = mybir.dt.int32
U32 = mybir.dt.uint32
AX = mybir.AxisListType.X

P = 128
D = 256
KD = D // P
N = 3125
NT = -(-N // P)
NP = NT * P
E = 53125
ET = -(-E // P)
EA = 64
G = 8
WT = -(-(ET + NT) // G) * G
WP = WT + 1
U = 5
SG = 8
AW = 264
CH = 400
CB, CH2 = 640, 320
TB = CB // P
assert TB == U
BLANK = next(k for k in range(WP // 8, 0, -1) if WP % k == 0)
EPS = 1e-5
BIG = 1e30
assert NT % U == 0 and WT % G == 0 and ET % SG == 0 and NP % (2 * CH) == 0


class Chain:

    def __init__(self, eng, sem):
        self.eng, self.sem, self.base, self.k = eng, sem, 0, 0

    def at(self, base):
        self.base, self.k = base, 0

    def step(self, ins):
        ins.then_inc(self.sem, 1)
        self.k += 1
        self.eng.wait_ge(self.sem, self.base + self.k)


class Stage:

    number = 0

    def __init__(self, nc):
        self.nc, self.ctx, self.handles = nc, ExitStack(), []
        Stage.number += 1

    def __enter__(self):
        return self

    def sem(self, name):
        self.handles.append(self.nc.alloc_semaphore(f"{name}_{Stage.number}"))
        return self.handles[-1]

    def sems(self, name, n):
        return [self.sem(f"{name}{i}") for i in range(n)]

    def block(self):
        return self.ctx.enter_context(self.nc.Block())

    def __exit__(self, *a):
        self.ctx.close()
        self.nc.clear_and_free_semaphores(self.handles)
        self.nc.all_engine_barrier()
        return False


def view(buf, off, *shape):
    n = 1
    for s in shape:
        n *= s
    v = buf[:, off:off + n]
    if len(shape) == 2:
        v = v.rearrange("p (a b) -> p a b", b=shape[1])
    if len(shape) == 3:
        v = v.rearrange("p (a b c) -> p a b c", b=shape[1], c=shape[2])
    return v


def tile_at(buf, t, a=0, b=D):
    return buf[:, bass.ds(t, 1), a:b].rearrange("p o d -> p (o d)")


def bcast(col, shape):
    return col.unsqueeze(len(col.shape)).to_broadcast(shape)


def setup_memory(nc, ctx):
    class M:
        pass

    m = M()

    def sb(name, shape, dt=F32):
        return ctx.enter_context(nc.sbuf_tensor(name, shape, dt))

    m.X = sb("residual", [P, NT, D])
    m.XN = sb("normed", [P, NT, D])
    m.XT = sb("normed_T", [P, KD, NP])
    m.AGG = sb("sums", [P, NT, AW])
    m.BB = sb("wide", [P, 2 * NT * D])
    m.WS = sb("work", [P, 7168])
    m.PS = ctx.enter_context(nc.psum_tensor("ps", [P, 8, 512], F32))
    m.ident = sb("ident", [P, P])
    m.identb = sb("identb", [P, P], BF16)
    m.iota = sb("iota", [P, P])
    m.before = sb("before", [P, P])
    m.after = sb("after", [P, P])
    m.ones = sb("ones", [P, P])
    m.zerob = sb("zerob", [P, 160], BF16)
    m.real = sb("real", [P, NT])
    m.wiota = sb("wiota", [1, WP])
    m.coef = sb("coef", [P, KD, 2])
    m.gate = sb("gate", [P, NT, 8])
    m.lo1 = sb("lo1", [P, WP])
    m.src1 = sb("src1", [P, WP], I32)
    m.rel1 = sb("rel1", [P, WP], I32)
    m.tn1 = sb("tn1", [1, WP], I32)
    m.tn2 = sb("tn2", [1, WP], I32)
    m.B2 = m.BB[:, 0:NT * D]
    m.B3 = m.BB[:, NT * D:2 * NT * D]
    m.AF = m.AGG[:].rearrange("p t d -> p (t d)")
    m.rec1 = nc.dram_tensor("rec1", (P * WP, 4), F32).ap()
    m.rec2 = nc.dram_tensor("rec2", (P * WP, EA + 4), F32).ap()
    m.table = nc.dram_tensor("table", (NP, D), F32).ap()
    m.table_gat = nc.dram_tensor("table_gat", (NP, D + 4), F32).ap()
    m.table_max = nc.dram_tensor("table_max", (NP, 4), F32).ap()
    m.table_rel = nc.dram_tensor("table_rel", (8 * NP, D), F32).ap()
    return m


def constants(nc, m, x):
    with Stage(nc) as st:
        pool_step, filled, loaded = st.sem("pool_step"), st.sem("filled"), st.sem("loaded")
        block = st.block()

        @block.sync
        def _(sp):
            sp.dma_start(m.X[:], x.rearrange("(t p) d -> p t d", p=P)).then_inc(loaded, 16)
            sp.wait_ge(loaded, 16)

        @block.gpsimd
        def _(pool):
            c = Chain(pool, pool_step)
            g = nc.gpsimd
            c.step(g.memset(m.ones[:], 1.0))
            c.step(g.iota(m.iota[:], [[1, P]], base=0, channel_multiplier=0,
                          allow_small_or_imprecise_dtypes=True))
            c.step(g.iota(m.wiota[:], [[1, WP]], base=0, channel_multiplier=0,
                          allow_small_or_imprecise_dtypes=True))
            for out, op, sign in ((m.ident, ALU.is_equal, 1), (m.before, ALU.is_gt, 1), (m.after, ALU.is_gt, -1)):
                c.step(g.affine_select(out=out[:], in_=m.ones[:], compare_op=op, fill=0.0, base=0,
                                       pattern=[[-sign, P]], channel_multiplier=sign))
            c.step(g.affine_select(out=m.real[:], in_=m.ones[:, 0:NT], compare_op=ALU.is_ge, fill=0.0,
                                   base=N - 1, pattern=[[-P, NT]], channel_multiplier=-1))

        @block.vector
        def _(dve):
            dve.wait_ge(pool_step, 4)
            nc.vector.tensor_copy(m.identb[:], m.ident[:]).then_inc(filled, 1)
            nc.vector.memset(m.zerob[:], 0.0).then_inc(filled, 1)


def sort_edges(nc, m, keys, keys_row, etype, attr, other, by_source):
    W = EA + 4 if by_source else 4
    rec = m.rec2 if by_source else m.rec1
    tn = m.tn2 if by_source else m.tn1
    GROUPS = ET // SG
    ROUNDS = GROUPS // 2
    assert GROUPS % 2 == 0
    o = 0

    def take(n, *shape):
        nonlocal o
        v = view(m.BB, o, *(shape or (n,)))
        o += n
        return v

    keyi = take(ET).bitcast(I32)
    lo_i = take(ET).bitcast(I32)
    hi_i = take(ET).bitcast(I32)
    key = take(ET)
    lo = take(ET)
    hi = take(ET)
    trash = take(ET)
    othf = take(ET)
    ty_i = take(ET).bitcast(I32)
    pay = take(ET * 4, ET, 4)
    back = take(WP * 4, WP, 4)
    counts = take(32)
    base = take(32)
    first = take(NT)
    tiles_i = take(NT).bitcast(I32)
    tiles = take(NT)
    tnf = take(WP)
    blank = view(m.AF, 0, BLANK * W) if by_source else view(m.AF, 0, WP * 4)
    blank3 = blank.rearrange("p (a b) -> p a b", b=W)
    rank = take(2 * SG, 2, SG)
    slot, slot_f, hi_f = take(SG), take(SG), take(SG)
    slot_i, hi_s = take(SG).bitcast(I32), take(SG).bitcast(I32)
    idxr = take(2 * SG, 2, SG).bitcast(I32)
    prod = take(SG * NT, SG, NT)
    snap = take(2 * SG * NT, 2, SG, NT)
    rowk = view(m.WS, 0, 2, SG * P).bitcast(I32)
    eqs = view(m.WS, 2 * SG * P, SG, P)
    payr = view(m.WS, 3 * SG * P, 2 * SG, EA + 4)
    fl = m.XN[:].rearrange("p t d -> p (t d)")
    ol = fl[:, 0:SG * P].bitcast(BF16).rearrange("p (u s e) -> p u s e", u=2, s=SG)
    oh = fl[:, 1024:1024 + SG * NT].bitcast(BF16).rearrange("p (u s e) -> p u s e", u=2, s=SG)
    olt = view(fl, 2048, 2, SG, P)

    def one_hots(v, g, u):
        v.tensor_tensor(ol[:, u], m.iota[:].unsqueeze(1).to_broadcast([P, SG, P]),
                        bcast(lo[:, bass.ds(g * SG, SG)], [P, SG, P]), ALU.is_equal)
        return v.tensor_tensor(oh[:, u], m.iota[:, 0:NT].unsqueeze(1).to_broadcast([P, SG, NT]),
                               bcast(hi[:, bass.ds(g * SG, SG)], [P, SG, NT]), ALU.is_equal)

    with Stage(nc) as st:
        loaded, blanked, stored = st.sem("loaded"), st.sem("blanked"), st.sem("stored")
        dstep, hot, used, counted = st.sem("dstep"), st.sem("hot"), st.sem("used"), st.sem("counted")
        tstep, sums, prefix = st.sem("tstep"), st.sem("sums"), st.sem("prefix")
        block = st.block()

        @block.sync
        def _(sp):
            sp.dma_start(keyi, keys).then_inc(loaded, 16)
            sp.dma_start(othf.bitcast(I32), other).then_inc(loaded, 16)
            if not by_source:
                sp.dma_start(ty_i, etype).then_inc(loaded, 16)
            sp.wait_ge(blanked, 2)
            r = rec.rearrange("(p w) c -> p (w c)", p=P)
            n = blank3.shape[1] * W
            for k in range(WP * W // n):
                sp.dma_start(r[:, k * n:(k + 1) * n], blank).then_inc(stored, 16)
            sp.wait_ge(stored, 16 * (WP * W // n))

        @block.gpsimd
        def _(pool):
            nc.gpsimd.memset(payr[:, :, EA:EA + 4], 0.0)
            nc.gpsimd.memset(blank, 0.0).then_inc(blanked, 1)
            pool.wait_ge(blanked, 1)
            col = EA + 1 if by_source else 1
            nc.gpsimd.memset(blank3[:, :, col:col + 1], -1.0).then_inc(blanked, 1)

        @block.vector
        def _(dve):
            v = nc.vector
            c = Chain(dve, dstep)
            dve.wait_ge(loaded, 32 if by_source else 48)
            c.step(v.tensor_scalar(hi_i, keyi, 7, None, ALU.arith_shift_right))
            c.step(v.tensor_scalar(lo_i, keyi, 127, None, ALU.bitwise_and))
            c.step(v.tensor_copy(key, keyi))
            c.step(v.tensor_copy(lo, lo_i))
            c.step(v.tensor_copy(hi, hi_i))
            c.step(v.tensor_scalar(trash, key, 0.0, float(WT * P), ALU.is_lt, ALU.mult))
            c.step(v.tensor_copy(othf, othf.bitcast(I32)))
            if not by_source:
                c.step(v.tensor_copy(pay[:, :, 0], othf))
                c.step(v.tensor_copy(pay[:, :, 1], lo))
                c.step(v.tensor_copy(pay[:, :, 3], ty_i))
                c.step(v.scalar_tensor_tensor(pay[:, :, 2], pay[:, :, 3], float(NP), othf, ALU.mult, ALU.add))
            with dve.Fori(0, ROUNDS) as i:
                for u in range(2):
                    dve.wait_ge(used, i * 2 + u + 1)
                    one_hots(v, i * 2 + u, u).then_inc(hot, 1)
            dve.wait_ge(counted, 1)
            v.tensor_copy(counts[:, 0:NT], m.PS[:, 0, 0:NT]).then_inc(sums, 1)
            dve.wait_ge(prefix, 1)
            c2 = Chain(dve, tstep)
            c2.step(v.tensor_scalar(tiles, m.PS[:, 1, 0:NT], float(P - 1), None, ALU.add))
            c2.step(v.tensor_copy(tiles_i, tiles))
            c2.step(v.tensor_scalar(tiles_i, tiles_i, 7, None, ALU.arith_shift_right))
            c2.step(v.tensor_copy(tiles, tiles_i))
            c2.step(v.tensor_tensor_scan(first, m.ones[:, 0:NT], tiles, 0.0, ALU.mult, ALU.add))
            c2.step(v.tensor_tensor(first, first, tiles, ALU.subtract))
            c2.step(v.scalar_tensor_tensor(base[:, 0:NT], first, float(P), m.PS[:, 2, 0:NT],
                                           ALU.mult, ALU.add))
            c2.step(v.tensor_scalar(tnf[0:1, :], m.wiota[:], first[0:1, 1:2], None, ALU.is_ge))
            for j in range(2, NT):
                c2.step(v.scalar_tensor_tensor(tnf[0:1, :], m.wiota[:], first[0:1, j:j + 1], tnf[0:1, :],
                                               ALU.is_ge, ALU.add))
            c2.step(v.tensor_copy(tn[:], tnf[0:1, :]))

        @block.tensor
        def _(pe):
            pe.sem_inc(used, 2)
            nc.tensor.matmul(m.PS[:, 0, 0:NT], m.zerob[:, 0:P], m.zerob[:, 0:NT], start=True, stop=False,
                             skip_group_check=True)
            with pe.Fori(0, ROUNDS) as i:
                for u in range(2):
                    pe.wait_ge(hot, i * 2 + u + 1)
                    for s in range(SG):
                        mm = nc.tensor.matmul(m.PS[:, 0, 0:NT], ol[:, u, s], oh[:, u, s], start=False, stop=False,
                                              skip_group_check=True)
                    mm.then_inc(used, 1)
            nc.tensor.matmul(m.PS[:, 0, 0:NT], m.zerob[:, 0:P], m.zerob[:, 0:NT], start=False, stop=True,
                             skip_group_check=True).then_inc(counted, 1)
            pe.wait_ge(sums, 1)
            nc.tensor.matmul(m.PS[:, 1, 0:NT], m.ones[:], counts[:, 0:NT], start=True, stop=True)
            nc.tensor.matmul(m.PS[:, 2, 0:NT], m.after[:], counts[:, 0:NT], start=True,
                             stop=True).then_inc(prefix, 1)

    with Stage(nc) as st:
        names = ("rows_used", "hot", "turned", "olt_ready", "prefixed", "snapped", "picked", "taken", "dstep",
                 "ready", "drained", "issue", "carried")
        (rows_used, hot, turned, olt_ready, prefixed, snapped, picked, taken, dstep, ready, drained, issue,
         carried) = (st.sem(s) for s in names)
        rows, arrived, sent = st.sems("rows", 2), st.sems("arrived", 2), st.sems("sent", 2 * SG)
        block = st.block()

        @block.sync
        def _(sp):
            kr = keys_row.rearrange("(i e) -> i e", e=SG * P)
            at = attr.rearrange("(t p) c -> p t c", p=P) if by_source else None

            def keys_in(g, u):
                sp.wait_ge(rows_used, g + 1)
                sp.dma_start(rowk[:, u, :], kr[bass.ds(g, 1), :].to_broadcast([P, SG * P])).then_inc(rows[u], 16)

            def attributes_in(g, u):
                if by_source:
                    sp.dma_start(payr[:, u * SG:(u + 1) * SG, 0:EA], at[:, bass.ds(g * SG, SG), :]
                                 ).then_inc(arrived[u], 16)

            sp.sem_inc(drained, 2)
            for g in range(2):
                keys_in(g, g)
                attributes_in(g, g)
            with sp.Fori(1, ROUNDS) as i:
                for u in range(2):
                    keys_in(i * 2 + u, u)
                    for s in range(SG):
                        sp.wait_ge(sent[u * SG + s], i * 16)
                    sp.sem_inc(drained, 1)
                    attributes_in(i * 2 + u, u)
            for s in range(2 * SG):
                sp.wait_ge(sent[s], ROUNDS * 16)

        @block.vector
        def _(dve):
            v = nc.vector
            c = Chain(dve, dstep)
            STEPS = 11
            dve.sem_inc(rows_used, 2)

            def front(g, u):
                one_hots(v, g, u).then_inc(hot, 1)

            def counts_so_far(g, u):
                dve.wait_ge(prefixed, g + 1)
                dve.wait_ge(carried, g + 2)
                v.tensor_tensor(snap[:, u], m.PS[:, u, 0:SG * NT].rearrange("p (s e) -> p s e", s=SG),
                                base[:, 0:NT].unsqueeze(1).to_broadcast([P, SG, NT]), ALU.add).then_inc(snapped, 1)
                dve.wait_ge(snapped, g + 1)
                v.tensor_tensor(base[:, 0:NT], base[:, 0:NT], m.PS[:, u, SG * NT:(SG + 1) * NT], ALU.add
                                ).then_inc(carried, 1)

            def ranks(i, g, u):
                dve.wait_ge(rows[u], i * 16 + 16)
                for s in range(SG):
                    ins = v.scalar_tensor_tensor(eqs[:, s], rowk[:, u, s * P:(s + 1) * P], key[:, bass.ds(g * SG + s, 1)],
                                                 m.before[:], ALU.is_equal, ALU.mult, accum_out=rank[:, u, s:s + 1])
                c.at(g * STEPS)
                c.step(ins)
                dve.sem_inc(rows_used, 1)

            def place(g, u):
                group = bass.ds(g * SG, SG)
                dve.wait_ge(picked, g + 3)
                c.step(v.tensor_tensor(prod, m.PS[:, 4 + u, 0:SG * NT].rearrange("p (s e) -> p s e", s=SG), oh[:, u],
                                       ALU.mult))
                dve.sem_inc(taken, 1)
                c.step(v.reduce_sum(slot, prod, AX))
                c.step(v.tensor_tensor(slot, slot, rank[:, u], ALU.add))
                c.step(v.tensor_tensor(slot, slot, trash[:, group], ALU.add))
                c.step(v.tensor_copy(slot_i, slot))
                c.step(v.tensor_scalar(hi_s, slot_i, 7, None, ALU.arith_shift_right))
                c.step(v.tensor_copy(hi_f, hi_s))
                c.step(v.scalar_tensor_tensor(slot_f, hi_f, -float(P), slot, ALU.mult, ALU.add))
                c.step(v.scalar_tensor_tensor(slot_f, slot_f, float(WP), hi_f, ALU.mult, ALU.add))
                dve.wait_ge(drained, g + 1)
                if by_source:
                    v.tensor_copy(payr[:, u * SG:(u + 1) * SG, EA], othf[:, group])
                    v.tensor_copy(payr[:, u * SG:(u + 1) * SG, EA + 1], lo[:, group])
                else:
                    v.tensor_copy(payr[:, u * SG:(u + 1) * SG, 0:4], pay[:, group, :])
                c.step(v.tensor_copy(idxr[:, u, :], slot_f))
                assert c.k == STEPS
                dve.sem_inc(ready, 1)

            def two_groups(i, last=False):
                for u in range(2):
                    g = i * 2 + u
                    more = not (last and u == 1)
                    if more:
                        front(g + 1, 1 - u)
                    ranks(i, g, u)
                    if more:
                        counts_so_far(g + 1, 1 - u)
                    place(g, u)

            dve.sem_inc(carried, 2)
            dve.sem_inc(taken, 2)
            front(0, 0)
            counts_so_far(0, 0)
            with dve.Fori(0, ROUNDS - 1) as i:
                two_groups(i)
            two_groups(ROUNDS - 1, last=True)

        @block.scalar
        def _(act):
            with act.Fori(0, ROUNDS) as i:
                for u in range(2):
                    g = i * 2 + u
                    act.wait_ge(turned, g + 1)
                    act.wait_ge(picked, g + 1)
                    nc.scalar.copy(olt[:, u].rearrange("p s e -> p (s e)"), m.PS[:, 2 + u, :].bitcast(BF16)
                                   ).then_inc(olt_ready, 1)

        @block.tensor
        def _(pe):
            te = nc.tensor
            pe.sem_inc(picked, 2)

            def counts_before(g, u):
                pe.wait_ge(hot, g + 1)
                pe.wait_ge(carried, g + 1)
                te.matmul(m.PS[:, u, 0:(SG + 1) * NT], m.zerob[:, 0:P],
                          m.zerob[:, 0:NT].unsqueeze(1).to_broadcast([P, SG + 1, NT]), start=True, stop=False,
                          skip_group_check=True)
                for s in range(SG):
                    mm = te.matmul(m.PS[:, u, (s + 1) * NT:(SG + 1) * NT], ol[:, u, s],
                                   oh[:, u, s].unsqueeze(1).to_broadcast([P, SG - s, NT]), start=False,
                                   stop=(s == SG - 1), skip_group_check=True)
                mm.then_inc(prefixed, 1)
                for s in range(SG):
                    mm = te.transpose(m.PS[:, 2 + u, s * P // 2:(s + 1) * P // 2].bitcast(BF16), ol[:, u, s],
                                      m.identb[:])
                mm.then_inc(turned, 1)

            def read_counts(g, u):
                pe.wait_ge(olt_ready, g + 1)
                pe.wait_ge(snapped, g + 1)
                pe.wait_ge(taken, g + 1)
                for s in range(SG):
                    mm = te.matmul(m.PS[:, 4 + u, s * NT:(s + 1) * NT], olt[:, u, s], snap[:, u, s], start=True,
                                   stop=True)
                mm.then_inc(picked, 1)

            counts_before(0, 0)
            with pe.Fori(0, ROUNDS - 1) as i:
                for u in range(2):
                    counts_before(i * 2 + u + 1, 1 - u)
                    read_counts(i * 2 + u, u)
            counts_before(GROUPS - 1, 1)
            read_counts(GROUPS - 2, 0)
            read_counts(GROUPS - 1, 1)

        @block.gpsimd
        def _(pool):
            with pool.Fori(0, ROUNDS) as i:
                for u in range(2):
                    pool.wait_ge(ready, i * 2 + u + 1)
                    if by_source:
                        pool.wait_ge(arrived[u], i * 16 + 16)
                    pool.sem_inc(issue, 1)
                    for s in range(SG):
                        nc.gpsimd.indirect_dma_start(rec, bass.IndirectOffsetOnAxis(ap=idxr[:, u, s:s + 1], axis=0),
                                                     payr[:, u * SG + s, 0:W], None).then_inc(sent[u * SG + s], 16)

    if by_source:
        return
    with Stage(nc) as st:
        loaded, split = st.sem("loaded"), st.sem("split")
        block = st.block()

        @block.sync
        def _(sp):
            sp.dma_start(back, rec.rearrange("(p w) c -> p w c", p=P)).then_inc(loaded, 16)

        @block.vector
        def _(dve):
            dve.wait_ge(loaded, 16)
            nc.vector.tensor_copy(m.src1[:], back[:, :, 0])
            nc.vector.tensor_copy(m.lo1[:], back[:, :, 1])
            nc.vector.tensor_copy(m.rel1[:], back[:, :, 2])


def layernorm(nc, m, src, dst):
    with Stage(nc) as st:
        dstep, centred, squared, vared, rooted = (st.sem(s) for s in ("dstep", "centred", "squared", "vared", "rooted"))
        mean, var, rstd = (view(m.WS, k * 32, 32)[:, 0:NT] for k in range(3))
        sq = view(m.BB, 0, NT, D)
        block = st.block()

        @block.vector
        def _(dve):
            v, c = nc.vector, Chain(dve, dstep)
            c.step(v.reduce_sum(mean, src[:], AX))
            c.step(v.tensor_scalar(mean, mean, 1.0 / D, None, ALU.mult))
            v.tensor_tensor(dst[:], src[:], bcast(mean, [P, NT, D]), ALU.subtract).then_inc(centred, 1)
            dve.wait_ge(squared, 1)
            c.step(v.reduce_sum(var, sq, AX))
            v.tensor_scalar(var, var, 1.0 / D, EPS, ALU.mult, ALU.add).then_inc(vared, 1)
            dve.wait_ge(rooted, 1)
            c.step(v.reciprocal(rstd, rstd))
            dve.wait_ge(centred, 1)
            c.step(v.tensor_tensor(dst[:], dst[:], bcast(rstd, [P, NT, D]), ALU.mult))

        @block.scalar
        def _(act):
            act.wait_ge(centred, 1)
            nc.scalar.activation(sq, dst[:], ACT.Square).then_inc(squared, 1)
            act.wait_ge(vared, 1)
            nc.scalar.activation(rstd, var, ACT.Sqrt).then_inc(rooted, 1)


def turn(nc, m, src, dst, affine=None):
    with Stage(nc) as st:
        staged, turned, ps_used = (st.sem(s) for s in ("staged", "turned", "ps_used"))
        ring = view(m.WS, 0, U, D)
        block = st.block()

        @block.scalar
        def _(act):
            with act.Fori(0, NT // U) as i:
                for s in range(U):
                    t = i * U + s
                    act.wait_ge(turned, t + 1)
                    nc.scalar.copy(ring[:, s, :], tile_at(src, t)).then_inc(staged, 1)

        @block.tensor
        def _(pe):
            pe.sem_inc(turned, U)
            with pe.Fori(0, NT // U) as i:
                for s in range(U):
                    t = i * U + s
                    pe.wait_ge(staged, t + 1)
                    pe.wait_ge(ps_used, t + 1)
                    for k in range(KD):
                        mm = nc.tensor.transpose(m.PS[:, s, k * P:(k + 1) * P], ring[:, s, k * P:(k + 1) * P],
                                                 m.ident[:])
                    mm.then_inc(turned, 1)

        @block.vector
        def _(dve):
            dve.sem_inc(ps_used, U)
            with dve.Fori(0, NT // U) as i:
                for s in range(U):
                    t = i * U + s
                    dve.wait_ge(turned, t + 1 + U)
                    nc.vector.tensor_copy(dst[:, :, bass.ds(t * P, P)],
                                          m.PS[:, s, 0:D].rearrange("p (k n) -> p k n", k=KD)).then_inc(ps_used, 1)


def aggregate(nc, m, table, index):
    with Stage(nc) as st:
        indexed, index_used, hot, hot_used = (st.sem(s) for s in ("indexed", "index_used", "hot", "hot_used"))
        gathered, summed, added, issue = st.sems("gathered", G), st.sem("summed"), st.sem("added"), st.sem("issue")
        rows = view(m.WS, 0, G, D)
        S = view(m.WS, G * D, G, P)
        idx = view(m.WS, G * D + G * P, G).bitcast(I32)
        block = st.block()

        @block.scalar
        def _(act):
            with act.Fori(0, WT // G) as i:
                for s in range(G):
                    w = i * G + s
                    act.wait_ge(summed, w + 1)
                    nc.scalar.copy(idx[:, s:s + 1], index[:, bass.ds(w, 1)]).then_inc(indexed, 1)

        @block.gpsimd
        def _(pool):
            with pool.Fori(0, WT // G) as i:
                for s in range(G):
                    pool.wait_ge(indexed, i * G + s + 1)
                    pool.sem_inc(issue, 1)
                    nc.gpsimd.indirect_dma_start(rows[:, s, :], None, table,
                                                 bass.IndirectOffsetOnAxis(ap=idx[:, s:s + 1], axis=0)
                                                 ).then_inc(gathered[s], 16)

        @block.tensor
        def _(pe):
            pe.sem_inc(summed, G)
            with pe.Fori(0, WT // G) as i:
                for s in range(G):
                    w = i * G + s
                    pe.wait_ge(hot, w + 1)
                    pe.wait_ge(added, w + 1)
                    pe.wait_ge(gathered[s], i * 16 + 16)
                    nc.tensor.matmul(m.PS[:, s, 0:D], S[:, s, :], rows[:, s, :], start=True,
                                     stop=True).then_inc(summed, 1)

        @block.vector
        def _(dve):
            v = nc.vector
            dve.sem_inc(added, G)
            with dve.Fori(0, WT // G) as i:
                for s in range(G):
                    w = i * G + s
                    dve.wait_ge(summed, w + 1)
                    v.tensor_scalar(S[:, s, :], m.iota[:], m.lo1[:, bass.ds(w, 1)], None,
                                    ALU.is_equal).then_inc(hot, 1)
                for s in range(G):
                    w = i * G + s
                    dve.wait_ge(summed, w + 1 + G)
                    dve.wait_ge(added, w + G)
                    tn = dve.value_load(m.tn1[0:1, bass.ds(w, 1)], min_val=0, max_val=NT - 1)
                    at = tile_at(m.AGG, tn)
                    v.tensor_tensor(at, at, m.PS[:, s, 0:D], ALU.add).then_inc(added, 1)


def store_table(nc, m, src, table, sums=None):
    with Stage(nc) as st:
        stored = st.sem("stored")
        block = st.block()

        @block.sync
        def _(sp):
            sp.dma_start(table.rearrange("(t p) d -> p t d", p=P), src[:]).then_inc(stored, 16)
            sp.wait_ge(stored, 16)

        @block.vector
        def _(dve):
            if sums is None:
                nc.vector.tensor_copy(m.AGG[:, :, 0:D], src[:])
            else:
                nc.vector.memset(m.AGG[:], sums)


def free2(eng, sem, s, t):
    eng.wait_ge(sem, t + 2 if s == 0 else t + 1)


def linear_nodes(nc, m, srcT, weight, bias, width, finish):
    with Stage(nc) as st:
        loaded, staged, made, taken, fstep = (st.sem(s) for s in ("loaded", "staged", "made", "taken", "fstep"))
        ring = view(m.WS, 0, U, KD, P)
        w = view(m.WS, U * D, KD, width)
        b = m.WS[0:1, U * D + KD * width:U * D + KD * width + width]
        block = st.block()

        @block.sync
        def _(sp):
            sp.dma_start(w, weight.rearrange("(k p) n -> p k n", p=P)).then_inc(loaded, 16)
            if bias is not None:
                sp.dma_start(b, bias.unsqueeze(0)).then_inc(loaded, 16)

        @block.scalar
        def _(act):
            with act.Fori(0, NT // U) as i:
                for s in range(U):
                    t = i * U + s
                    act.wait_ge(made, t + 1)
                    nc.scalar.copy(ring[:, s, :, :], srcT[:, :, bass.ds(t * P, P)]).then_inc(staged, 1)

        @block.tensor
        def _(pe):
            pe.sem_inc(made, U)
            pe.wait_ge(loaded, 32 if bias is not None else 16)
            with pe.Fori(0, NT // U) as i:
                for s in range(U):
                    t = i * U + s
                    pe.wait_ge(staged, t + 1)
                    pe.wait_ge(taken, t + 1)
                    for k in range(KD):
                        mm = nc.tensor.matmul(m.PS[:, s, 0:width], ring[:, s, k, :], w[:, k, :], start=(k == 0),
                                              stop=(bias is None and k == KD - 1))
                    if bias is not None:
                        mm = nc.tensor.matmul(m.PS[:, s, 0:width], m.ones[0:1, :], b, start=False, stop=True)
                    mm.then_inc(made, 1)

        @block.vector
        def _(dve):
            dve.sem_inc(taken, U)
            c = Chain(dve, fstep)
            with dve.Fori(0, NT // U) as i:
                for s in range(U):
                    t = i * U + s
                    dve.wait_ge(made, t + 1 + U)
                    c.at(t * finish.steps)
                    finish(dve, c, t, m.PS[:, s, 0:width]).then_inc(taken, 1)


class Finish:

    def __init__(self, fn, steps=0):
        self.fn, self.steps = fn, steps

    def __call__(self, *a):
        return self.fn(*a)



def batch_stats(nc, m, zT, gamma, beta):
    with Stage(nc) as st:
        loaded, dstep, vared, rooted = (st.sem(s) for s in ("loaded", "dstep", "vared", "rooted"))
        cuts = [(a, min(a + 512, N)) for a in range(0, N, 512)]
        stats = view(m.WS, 0, KD, 6 * len(cuts))
        mv = view(m.WS, 200, KD, 2)
        gb = view(m.WS, 210, 2, KD)
        std = view(m.WS, 220, KD)
        block = st.block()

        @block.sync
        def _(sp):
            sp.dma_start(gb[:, 0, :], gamma).then_inc(loaded, 16)
            sp.dma_start(gb[:, 1, :], beta).then_inc(loaded, 16)

        @block.vector
        def _(dve):
            v, c = nc.vector, Chain(dve, dstep)
            for k in range(KD):
                for j, (a, b) in enumerate(cuts):
                    ins = v.bn_stats(stats[:, k, 6 * j:6 * j + 6], zT[:, k, a:b])
            c.step(ins)
            for k in range(KD):
                ins = v.bn_aggr(mv[:, k, :], stats[:, k, :])
            c.step(ins)
            v.tensor_scalar(std, mv[:, :, 1], EPS, None, ALU.add).then_inc(vared, 1)
            dve.wait_ge(rooted, 1)
            c.step(v.reciprocal(std, std))
            dve.wait_ge(loaded, 32)
            c.step(v.tensor_tensor(m.coef[:, :, 0], std, gb[:, 0, :], ALU.mult))
            c.step(v.tensor_tensor(std, mv[:, :, 0], m.coef[:, :, 0], ALU.mult))
            c.step(v.tensor_tensor(m.coef[:, :, 1], gb[:, 1, :], std, ALU.subtract))

        @block.scalar
        def _(act):
            act.wait_ge(vared, 1)
            nc.scalar.activation(std, std, ACT.Sqrt).then_inc(rooted, 1)


def normalise_nodes(nc, m, zT, dst):
    with Stage(nc) as st:
        scaled, turned, taken = (st.sem(s) for s in ("scaled", "turned", "taken"))
        ring = view(m.WS, 0, U, KD, P)
        block = st.block()

        @block.scalar
        def _(act):
            with act.Fori(0, NT // U) as i:
                for s in range(U):
                    t = i * U + s
                    act.wait_ge(turned, t + 1)
                    for k in range(KD):
                        ins = nc.scalar.activation(ring[:, s, k, :], zT[:, k, bass.ds(t * P, P)], ACT.Identity,
                                                   bias=m.coef[:, k, 1:2], scale=m.coef[:, k, 0:1])
                    ins.then_inc(scaled, 1)

        @block.tensor
        def _(pe):
            pe.sem_inc(turned, U)
            with pe.Fori(0, NT // U) as i:
                for s in range(U):
                    t = i * U + s
                    pe.wait_ge(scaled, t + 1)
                    pe.wait_ge(taken, t + 1)
                    for k in range(KD):
                        mm = nc.tensor.transpose(m.PS[:, s, k * P:(k + 1) * P], ring[:, s, k, :], m.ident[:])
                    mm.then_inc(turned, 1)

        @block.vector
        def _(dve):
            dve.sem_inc(taken, U)
            with dve.Fori(0, NT // U) as i:
                for s in range(U):
                    t = i * U + s
                    dve.wait_ge(turned, t + 1 + U)
                    nc.vector.tensor_copy(tile_at(dst, t), m.PS[:, s, 0:D]).then_inc(taken, 1)


def linear_features(nc, m, srcT, weight, bias, dstT):
    with Stage(nc) as st:
        loaded, made, taken = (st.sem(s) for s in ("loaded", "made", "taken"))
        w = view(m.WS, 0, KD, D)
        b = view(m.WS, KD * D, KD)
        block = st.block()

        @block.sync
        def _(sp):
            sp.dma_start(w, weight.rearrange("(k p) n -> p k n", p=P)).then_inc(loaded, 16)
            sp.dma_start(b, bias).then_inc(loaded, 16)

        @block.tensor
        def _(pe):
            pe.wait_ge(loaded, 32)
            with pe.Fori(0, NP // CH // 2) as i:
                for u in range(2):
                    for j in range(KD):
                        n = (i * 2 + u) * KD + j
                        pe.wait_ge(taken, n + 1)
                        for k in range(KD):
                            mm = nc.tensor.matmul(m.PS[:, u * KD + j, 0:CH], w[:, k, j * P:(j + 1) * P],
                                                  srcT[:, k, bass.ds((i * 2 + u) * CH, CH)], start=(k == 0),
                                                  stop=(k == KD - 1))
                        mm.then_inc(made, 1)

        @block.scalar
        def _(act):
            act.sem_inc(taken, 2 * KD)
            act.wait_ge(loaded, 32)
            with act.Fori(0, NP // CH // 2) as i:
                for u in range(2):
                    for j in range(KD):
                        n = (i * 2 + u) * KD + j
                        act.wait_ge(made, n + 1)
                        nc.scalar.activation(dstT[:, j, bass.ds((i * 2 + u) * CH, CH)], m.PS[:, u * KD + j, 0:CH],
                                             ACT.Identity, bias=b[:, j:j + 1]).then_inc(taken, 1)


def gin_output(nc, m, zT, weight, bias, into_residual):
    with Stage(nc) as st:
        loaded, scaled, made, taken = (st.sem(s) for s in ("loaded", "scaled", "made", "taken"))
        ring = view(m.WS, 0, U, KD, P)
        w = view(m.WS, U * D, KD, D)
        b = m.WS[0:1, U * D + KD * D:U * D + KD * D + D]
        block = st.block()

        @block.sync
        def _(sp):
            sp.dma_start(w, weight.rearrange("(k p) n -> p k n", p=P)).then_inc(loaded, 16)
            sp.dma_start(b, bias.unsqueeze(0)).then_inc(loaded, 16)

        @block.scalar
        def _(act):
            with act.Fori(0, NT // U) as i:
                for s in range(U):
                    t = i * U + s
                    act.wait_ge(made, t + 1)
                    for k in range(KD):
                        ins = nc.scalar.activation(ring[:, s, k, :], zT[:, k, bass.ds(t * P, P)], ACT.Relu,
                                                   bias=m.coef[:, k, 1:2], scale=m.coef[:, k, 0:1])
                    ins.then_inc(scaled, 1)

        @block.tensor
        def _(pe):
            pe.sem_inc(made, U)
            pe.wait_ge(loaded, 32)
            with pe.Fori(0, NT // U) as i:
                for s in range(U):
                    t = i * U + s
                    pe.wait_ge(scaled, t + 1)
                    pe.wait_ge(taken, t + 1)
                    for k in range(KD):
                        nc.tensor.matmul(m.PS[:, s, 0:D], ring[:, s, k, :], w[:, k, :], start=(k == 0), stop=False)
                    nc.tensor.matmul(m.PS[:, s, 0:D], m.ones[0:1, :], b, start=False, stop=True).then_inc(made, 1)

        @block.vector
        def _(dve):
            dve.sem_inc(taken, U)
            with dve.Fori(0, NT // U) as i:
                for s in range(U):
                    t = i * U + s
                    dve.wait_ge(made, t + 1 + U)
                    if into_residual:
                        at = tile_at(m.X, t)
                        ins = nc.vector.scalar_tensor_tensor(at, m.PS[:, s, 0:D], 0.0, at, ALU.max, ALU.add)
                    else:
                        ins = nc.vector.tensor_scalar(tile_at(m.XN, t), m.PS[:, s, 0:D], 0.0, None, ALU.max)
                    ins.then_inc(taken, 1)


def gin(nc, m, a):
    zT = view(m.BB, 0, KD, NP)
    layernorm(nc, m, m.X, m.XN)
    turn(nc, m, m.XN, m.XT)
    batch_stats(nc, m, m.XT, a["L0_gnn_g0"], a["L0_gnn_b0"])
    normalise_nodes(nc, m, m.XT, m.XN)
    for conv, last in (("1", False), ("2", True)):
        store_table(nc, m, m.XN, m.table)
        aggregate(nc, m, m.table, m.src1)
        turn(nc, m, m.AGG, m.XT)
        linear_features(nc, m, m.XT, a[f"L0_gnn_W{conv}a"], a[f"L0_gnn_b{conv}a"], zT)
        batch_stats(nc, m, zT, a[f"L0_gnn_g{conv}"], a[f"L0_gnn_bt{conv}"])
        gin_output(nc, m, zT, a[f"L0_gnn_W{conv}b"], a[f"L0_gnn_b{conv}b"], last)


def slice_attention(nc, m, a):
    H, C, QG = 8, 64, 64
    PR = H // 2
    HW = H * QG
    layernorm(nc, m, m.X, m.XN)
    turn(nc, m, m.XN, m.XT)
    weights = view(m.BB, 0, NT, HW)
    o = 0

    def take(*shape):
        nonlocal o
        v = view(m.AF, o, *shape)
        n = 1
        for k in shape:
            n *= k
        o += n
        return v

    w_fx, w_xs = take(KD, HW), take(KD, HW)
    w_xT, w_out, w_mix = take(PR, D), take(PR, D), take(PR, D)
    w_sl = take(P)
    b_fx, b_xs = take(HW), take(HW)
    xn = m.XN[:].rearrange("p t d -> p (t d)")
    w_q, w_k, w_v = (xn[:, k * P:(k + 1) * P] for k in range(3))
    b_x = xn[:, 384:384 + PR]
    temp = xn[:, 400:408]
    b_sl = xn[:, 416:480]
    b_out = xn[:, 512:768]
    tok, tokT, qT, kT, vv, att, attT, oT = (view(xn, 1024 + 512 * k, PR, P) for k in range(8))
    small = view(xn, 5200, 8, 8)

    with Stage(nc) as st:
        zeroed, loaded, dstep, folded = (st.sem(s) for s in ("zeroed", "loaded", "dstep", "folded"))
        block = st.block()
        LOADS = 8 + 5

        @block.gpsimd
        def _(pool):
            for w in (w_sl, w_q, w_k, w_v):
                nc.gpsimd.memset(w, 0.0).then_inc(zeroed, 1)

        @block.sync
        def _(sp):
            sp.wait_ge(zeroed, 4)
            for w, name in ((w_sl, "W_slice"), (w_q, "W_q"), (w_k, "W_k"), (w_v, "W_v")):
                for h in range(2):
                    sp.dma_start(w[h * C:(h + 1) * C, h * C:(h + 1) * C], a["L0_ffn_" + name]).then_inc(loaded, 16)
            sp.dma_start(w_xT, a["L0_ffn_W_x"].rearrange("(r p) d -> p r d", p=P)).then_inc(loaded, 16)
            sp.dma_start(b_x, a["L0_ffn_b_x"]).then_inc(loaded, 16)
            sp.dma_start(temp, a["L0_ffn_temperature"].rearrange("a h b c -> a (h b c)").to_broadcast([P, H])
                         ).then_inc(loaded, 16)
            sp.dma_start(b_sl[0:1, :], a["L0_ffn_b_slice"].unsqueeze(0)).then_inc(loaded, 16)
            sp.dma_start(w_fx, a["L0_ffn_W_fx"].rearrange("(k p) n -> p k n", p=P)).then_inc(loaded, 16)

        @block.tensor
        def _(pe):
            pe.wait_ge(loaded, 16 * LOADS)
            for r in range(PR):
                for k in range(KD):
                    nc.tensor.matmul(m.PS[:, k, r * P:(r + 1) * P], w_xT[:, r, k * P:(k + 1) * P], w_sl,
                                     start=True, stop=True)
                mm = nc.tensor.matmul(m.PS[0:1, KD, r * P:(r + 1) * P], b_x[:, r:r + 1], w_sl,
                                      start=True, stop=True)
            mm.then_inc(folded, 1)

        @block.vector
        def _(dve):
            v, c = nc.vector, Chain(dve, dstep)
            dve.wait_ge(loaded, 16 * LOADS)
            c.step(v.tensor_scalar(temp, temp, 0.1, 5.0, ALU.max, ALU.min))
            c.step(v.reciprocal(temp, temp))
            dve.wait_ge(folded, 1)
            for k in range(KD):
                v.tensor_tensor(w_xs[:, k, :].rearrange("p (h g) -> p h g", h=H),
                                m.PS[:, k, :].rearrange("p (h g) -> p h g", h=H), bcast(temp, [P, H, QG]), ALU.mult)
            row = b_xs[0:1, :].rearrange("p (h g) -> p h g", h=H)
            c.step(v.tensor_tensor(row, m.PS[0:1, KD, :].rearrange("p (h g) -> p h g", h=H),
                                   b_sl[0:1, :].unsqueeze(1).to_broadcast([1, H, QG]), ALU.add))
            c.step(v.tensor_tensor(row, row, bcast(temp[0:1, :], [1, H, QG]), ALU.mult))

    FW = C * 2 + 1
    with Stage(nc) as st:
        names = ("loaded", "staged", "scored", "read", "centred", "expd", "weighted", "fxed", "fxcopied", "summed",
                 "kept", "dstep", "oned", "outed")
        (loaded, staged, scored, read, centred, expd, weighted, fxed, fxcopied, summed, kept, dstep, oned,
         outed) = (st.sem(s) for s in names)
        ring = view(m.WS, 0, U, KD, P)
        sw = view(m.WS, U * D, U, HW)
        fx = m.WS[:, U * D + U * HW:U * D + U * HW + U * PR * FW].rearrange("p (u r f) -> p u r f", u=U, r=PR)
        mx = view(xn, 5200, 8)
        den = view(xn, 5216, 8)
        block = st.block()

        @block.sync
        def _(sp):
            sp.dma_start(b_fx[0:1, :], a["L0_ffn_b_fx"].unsqueeze(0)).then_inc(loaded, 16)
            sp.dma_start(w_out, a["L0_ffn_W_out"].rearrange("(r p) d -> p r d", p=P)).then_inc(loaded, 16)
            sp.dma_start(b_out[0:1, :], a["L0_ffn_b_out"].unsqueeze(0)).then_inc(loaded, 16)
            sp.wait_ge(loaded, 48)

        @block.gpsimd
        def _(pool):
            for s in range(U):
                ins = nc.gpsimd.memset(fx[:, s, :, FW - 1], 1.0)
            ins.then_inc(oned, 1)

        @block.scalar
        def _(act):
            act.sem_inc(fxcopied, 2)
            with act.Fori(0, NT // U) as i:
                for s in range(U):
                    t = i * U + s
                    act.wait_ge(summed, t + 1)
                    nc.scalar.copy(ring[:, s, :, :], m.XT[:, :, bass.ds(t * P, P)]).then_inc(staged, 1)
                    act.wait_ge(centred, t + 1)
                    nc.scalar.activation(sw[:, s, :], sw[:, s, :], ACT.Exp).then_inc(expd, 1)
                    act.wait_ge(fxed, t + 1)
                    nc.scalar.copy(fx[:, s, :, 0:FW - 1], m.PS[:, 2 + s % 2, :].rearrange("p (r f) -> p r f", r=PR)
                                   ).then_inc(fxcopied, 1)
                    act.wait_ge(weighted, t + 1)
                    nc.scalar.copy(weights[:, bass.ds(t, 1), :].rearrange("p o d -> p (o d)"), sw[:, s, :]
                                   ).then_inc(kept, 1)

        @block.tensor
        def _(pe):
            pe.sem_inc(summed, U)
            pe.wait_ge(loaded, 48)
            pe.wait_ge(oned, 1)
            for r in range(PR):
                nc.tensor.matmul(m.PS[:, 4 + r, 0:FW], m.zerob[:, 0:P], m.zerob[:, 0:FW], start=True, stop=False,
                                 skip_group_check=True)

            def tokens(i, s):
                t = i * U + s
                pe.wait_ge(weighted, t + 1)
                pe.wait_ge(fxcopied, t + 3)
                for r in range(PR):
                    mm = nc.tensor.matmul(m.PS[:, 4 + r, 0:FW], sw[:, s, r * P:(r + 1) * P], fx[:, s, r, :],
                                          start=False, stop=False, skip_group_check=True)
                mm.then_inc(summed, 1)

            with pe.Fori(0, NT // U) as i:
                for s in range(U):
                    t = i * U + s
                    pe.wait_ge(staged, t + 1)
                    free2(pe, read, s, t)
                    for k in range(KD):
                        nc.tensor.matmul(m.PS[:, s % 2, :], ring[:, s, k, :], w_xs[:, k, :], start=(k == 0),
                                         stop=False)
                    nc.tensor.matmul(m.PS[:, s % 2, :], m.ones[0:1, :], b_xs[0:1, :], start=False,
                                     stop=True).then_inc(scored, 1)
                    free2(pe, fxcopied, s, t)
                    for k in range(KD):
                        nc.tensor.matmul(m.PS[:, 2 + s % 2, :], ring[:, s, k, :], w_fx[:, k, :], start=(k == 0),
                                         stop=False)
                    nc.tensor.matmul(m.PS[:, 2 + s % 2, :], m.ones[0:1, :], b_fx[0:1, :], start=False,
                                     stop=True).then_inc(fxed, 1)
                    tokens(i, s)

            for r in range(PR):
                mm = nc.tensor.matmul(m.PS[:, 4 + r, 0:FW], m.zerob[:, 0:P], m.zerob[:, 0:FW], start=False,
                                      stop=True, skip_group_check=True)
            mm.then_inc(outed, 1)

        @block.vector
        def _(dve):
            v, c = nc.vector, Chain(dve, dstep)
            dve.sem_inc(read, 2)
            dve.sem_inc(kept, U)
            with dve.Fori(0, NT // U) as i:
                for s in range(U):
                    t = i * U + s
                    c.at(t * 5)
                    dve.wait_ge(scored, t + 1)
                    ps = m.PS[:, s % 2, :].rearrange("p (h g) -> p h g", h=H)
                    at = sw[:, s, :].rearrange("p (h g) -> p h g", h=H)
                    c.step(v.reduce_max(mx, ps, AX))
                    dve.wait_ge(summed, t + 1)
                    dve.wait_ge(kept, t + 1)
                    c.step(v.tensor_tensor(at, ps, bcast(mx, [P, H, QG]), ALU.subtract))
                    dve.sem_inc(read, 1)
                    dve.sem_inc(centred, 1)
                    dve.wait_ge(expd, t + 1)
                    c.step(v.reduce_sum(den, at, AX))
                    c.step(v.reciprocal(den, den))
                    c.step(v.tensor_scalar(den, den, m.real[:, bass.ds(t, 1)], None, ALU.mult))
                    v.tensor_tensor(at, at, bcast(den, [P, H, QG]), ALU.mult).then_inc(weighted, 1)
            dve.wait_ge(outed, 1)

    with Stage(nc) as st:
        dstep, zeroed, made, expd, copied = (st.sem(s) for s in ("dstep", "zeroed", "made", "expd", "copied"))
        rn = small[:, 0, 0:PR]
        mx = small[:, 1, 0:PR]
        den = small[:, 2, 0:PR]
        SCALE = C ** -0.5
        halves = [slice(h * C, (h + 1) * C) for h in range(2)]
        bank = [m.PS[:, b, :].rearrange("p (r f) -> p r f", r=PR) for b in range(8)]
        block = st.block()

        @block.gpsimd
        def _(pool):
            nc.gpsimd.memset(tok, 0.0).then_inc(zeroed, 1)
            nc.gpsimd.memset(att, 0.0).then_inc(zeroed, 1)

        @block.vector
        def _(dve):
            v, c = nc.vector, Chain(dve, dstep)
            dve.wait_ge(zeroed, 2)
            c.step(v.tensor_scalar(rn, m.PS[:, 4:8, FW - 1], 1e-5, None, ALU.add))
            c.step(v.reciprocal(rn, rn))
            for h in halves:
                ins = v.tensor_tensor(tok[h, :, h], m.PS[h, 4:8, h], bcast(rn[h, :], [C, PR, C]), ALU.mult)
            ins.then_inc(copied, 1)
            n = 0

            def copy(outs):
                nonlocal n
                n += 1
                dve.wait_ge(made, n)
                for dst, b in outs:
                    ins = v.tensor_copy(dst, bank[b])
                ins.then_inc(copied, 1)

            copy([(tokT, 0)])
            copy([(qT, 1), (kT, 2), (vv, 3)])
            n += 1
            dve.wait_ge(made, n)
            for h in halves:
                c.step(v.reduce_max(mx[h, :], bank[0][h, :, h], AX))
                c.step(v.tensor_tensor(att[h, :, h], bank[0][h, :, h], bcast(mx[h, :], [C, PR, C]), ALU.subtract))
            dve.sem_inc(copied, 1)
            dve.wait_ge(expd, 2)
            for h in halves:
                c.step(v.reduce_sum(den[h, :], att[h, :, h], AX))
                c.step(v.reciprocal(den[h, :], den[h, :]))
                c.step(v.tensor_tensor(att[h, :, h], att[h, :, h], bcast(den[h, :], [C, PR, C]), ALU.mult))
            dve.sem_inc(copied, 1)
            copy([(attT, 4)])
            copy([(oT, 5)])
            n += 1
            dve.wait_ge(made, n)
            for r in range(PR):
                ins = v.tensor_copy(w_mix[:, r, :], m.PS[:, 6 + r // 2, (r % 2) * D:(r % 2 + 1) * D])

        @block.scalar
        def _(act):
            act.wait_ge(copied, 4)
            for h in halves:
                nc.scalar.activation(att[h, :, h], att[h, :, h], ACT.Exp, scale=SCALE).then_inc(expd, 1)

        @block.tensor
        def _(pe):
            te = nc.tensor
            pe.wait_ge(copied, 1)
            for r in range(PR):
                mm = te.transpose(bank[0][:, r, :], tok[:, r, :], m.ident[:])
            mm.then_inc(made, 1)
            pe.wait_ge(copied, 2)
            te.matmul(bank[1], w_q, tokT, start=True, stop=True)
            te.matmul(bank[2], w_k, tokT, start=True, stop=True)
            for r in range(PR):
                mm = te.matmul(bank[3][:, r, :], tokT[:, r, :], w_v, start=True, stop=True)
            mm.then_inc(made, 1)
            pe.wait_ge(copied, 3)
            for r in range(PR):
                mm = te.matmul(bank[0][:, r, :], qT[:, r, :], kT[:, r, :], start=True, stop=True)
            mm.then_inc(made, 1)
            pe.wait_ge(copied, 5)
            for r in range(PR):
                mm = te.transpose(bank[4][:, r, :], att[:, r, :], m.ident[:])
            mm.then_inc(made, 1)
            pe.wait_ge(copied, 6)
            for r in range(PR):
                mm = te.matmul(bank[5][:, r, :], vv[:, r, :], attT[:, r, :], start=True, stop=True)
            mm.then_inc(made, 1)
            pe.wait_ge(copied, 7)
            for r in range(PR):
                mm = te.matmul(m.PS[:, 6 + r // 2, (r % 2) * D:(r % 2 + 1) * D], oT[:, r, :], w_out[:, r, :],
                               start=True, stop=True)
            mm.then_inc(made, 1)

    with Stage(nc) as st:
        staged, turned, copied, made, taken = (st.sem(s) for s in ("staged", "turned", "copied", "made", "taken"))
        ring = view(m.WS, 0, U, HW)
        ringT = view(m.WS, U * HW, U, HW)
        block = st.block()

        @block.scalar
        def _(act):
            with act.Fori(0, NT // U) as i:
                for s in range(U):
                    t = i * U + s
                    act.wait_ge(turned, t + 1)
                    nc.scalar.copy(ring[:, s, :], weights[:, bass.ds(t, 1), :].rearrange("p o d -> p (o d)")
                                   ).then_inc(staged, 1)

        @block.tensor
        def _(pe):
            pe.sem_inc(turned, U)
            with pe.Fori(0, NT // U) as i:
                for s in range(U + 1):
                    t = i * U + s
                    if s < U:
                        pe.wait_ge(staged, t + 1)
                        free2(pe, copied, s, t)
                        for r in range(PR):
                            mm = nc.tensor.transpose(m.PS[:, s % 2, r * P:(r + 1) * P], ring[:, s, r * P:(r + 1) * P],
                                                     m.ident[:])
                        mm.then_inc(turned, 1)
                    if s > 0:
                        q = s - 1
                        pe.wait_ge(copied, t + 2)
                        free2(pe, taken, q, t - 1)
                        for r in range(PR):
                            nc.tensor.matmul(m.PS[:, 2 + q % 2, 0:D], ringT[:, q, r * P:(r + 1) * P], w_mix[:, r, :],
                                             start=(r == 0), stop=False)
                        nc.tensor.matmul(m.PS[:, 2 + q % 2, 0:D], m.ones[0:1, :], b_out[0:1, :], start=False,
                                         stop=True).then_inc(made, 1)

        @block.vector
        def _(dve):
            dve.sem_inc(copied, 2)
            dve.sem_inc(taken, 2)
            dve.sem_inc(made, U)
            with dve.Fori(0, NT // U) as i:
                for s in range(U + 1):
                    t = i * U + s
                    if s < U:
                        dve.wait_ge(turned, t + 1 + U)
                        dve.wait_ge(made, t + 1)
                        nc.vector.tensor_copy(ringT[:, s, :], m.PS[:, s % 2, :]).then_inc(copied, 1)
                    if s > 0:
                        q = s - 1
                        dve.wait_ge(made, t + U)
                        at = tile_at(m.X, t - 1)
                        nc.vector.tensor_tensor(at, at, m.PS[:, 2 + q % 2, 0:D], ALU.add).then_inc(taken, 1)



def graph_attention(nc, m, a):
    H, C = 4, 64
    RW = D + H
    layernorm(nc, m, m.X, m.XN)
    turn(nc, m, m.XN, m.XT)
    node = m.BB[:, 0:NT * 8].rearrange("p (t c) -> p t c", c=8)
    src_score = m.BB[:, 256:256 + NT * H].rearrange("p (t c) -> p t c", c=H)
    best = m.BB[:, 384:384 + NT * H].rearrange("p (t c) -> p t c", c=H)
    high = m.BB[:, 512:]

    with Stage(nc) as st:
        (loaded, staged, made, copied, rowed, dstep, tabled) = (
            st.sem(s) for s in ("loaded", "staged", "made", "copied", "rowed", "dstep", "tabled"))
        stored = st.sems("stored", U)
        ring = view(m.WS, 0, U, KD, P)
        row = view(m.WS, U * D, U, RW)
        w = view(m.WS, U * D + U * RW, KD, D)
        o = U * D + U * RW + KD * D
        att = [m.WS[:, o + k * D:o + (k + 1) * D] for k in range(2)]
        tmp = m.WS[:, o + 2 * D:o + 3 * D]
        block = st.block()

        @block.sync
        def _(sp):
            sp.dma_start(w, a["L1_gnn_W"].rearrange("(k p) n -> p k n", p=P)).then_inc(loaded, 16)
            for k, name in enumerate(("L1_gnn_att_src", "L1_gnn_att_dst")):
                sp.dma_start(att[k], a[name].rearrange("h c -> (h c)").unsqueeze(0).to_broadcast([P, D])
                             ).then_inc(loaded, 16)
            to = m.table_gat.rearrange("(t p) c -> p t c", p=P)
            with sp.Fori(0, NT // U) as i:
                for s in range(U):
                    t = i * U + s
                    sp.wait_ge(rowed, t + 1)
                    sp.dma_start(to[:, bass.ds(t, 1), :].rearrange("p o c -> p (o c)"), row[:, s, :]
                                 ).then_inc(stored[s], 16)
            for s in range(U):
                sp.wait_ge(stored[s], 16 * (NT // U + 1))
            sp.dma_start(m.table_max.rearrange("(t p) c -> p t c", p=P), src_score).then_inc(tabled, 16)
            sp.wait_ge(tabled, 16)

        @block.scalar
        def _(act):
            act.sem_inc(copied, U)
            for s in range(U):
                act.sem_inc(stored[s], 16)
            with act.Fori(0, NT // U) as i:
                for s in range(U):
                    t = i * U + s
                    act.wait_ge(made, t + 1)
                    nc.scalar.copy(ring[:, s, :, :], m.XT[:, :, bass.ds(t * P, P)]).then_inc(staged, 1)
                    act.wait_ge(made, t + 1 + U)
                    act.wait_ge(stored[s], i * 16 + 16)
                    nc.scalar.copy(row[:, s, 0:D], m.PS[:, s, 0:D]).then_inc(copied, 1)

        @block.tensor
        def _(pe):
            pe.sem_inc(made, U)
            pe.wait_ge(loaded, 48)

            with pe.Fori(0, NT // U) as i:
                for s in range(U):
                    t = i * U + s
                    pe.wait_ge(staged, t + 1)
                    pe.wait_ge(copied, t + 1)
                    for k in range(KD):
                        mm = nc.tensor.matmul(m.PS[:, s, 0:D], ring[:, s, k, :], w[:, k, :], start=(k == 0),
                                              stop=(k == KD - 1))
                    mm.then_inc(made, 1)

        @block.vector
        def _(dve):
            v, c = nc.vector, Chain(dve, dstep)
            dve.wait_ge(loaded, 48)
            with dve.Fori(0, NT // U) as i:
                for s in range(U):
                    t = i * U + s
                    c.at(t * 4)
                    dve.wait_ge(copied, t + 1 + U)
                    ps = row[:, s, 0:D]
                    heads = tmp.rearrange("p (h c) -> p h c", h=H)
                    c.step(v.tensor_tensor(tmp, ps, att[0], ALU.mult))
                    c.step(v.reduce_sum(row[:, s, D:RW], heads, AX))
                    c.step(v.tensor_tensor(tmp, ps, att[1], ALU.mult))
                    c.step(v.reduce_sum(tile_at(node, t, 0, H), heads, AX))
                    v.tensor_copy(tile_at(src_score, t, 0, H), row[:, s, D:RW]).then_inc(rowed, 1)

    with Stage(nc) as st:
        names = ("indexed", "hot", "masked", "made", "reduced", "dstep", "issue", "initial")
        indexed, hot, masked, made, reduced, dstep, issue, initial = (st.sem(s) for s in names)
        gathered = st.sems("gathered", G)
        S = view(m.WS, 0, G, P)
        rows = view(m.WS, G * P, G, H)
        idx = view(m.WS, G * P + G * H, G).bitcast(I32)
        top = view(m.WS, G * P + 6 * G, G, H)
        off = view(m.WS, 2048, G * P // 2).bitcast(BF16).rearrange("p (u e) -> p u e", u=G)
        minus = m.WS[:, 3000:3001]
        diag = view(high, 0, G, H * P)
        MASK = float(2.0 ** 100)
        block = st.block()

        @block.scalar
        def _(act):
            act.wait_ge(initial, 2)
            with act.Fori(0, WT // G) as i:
                for s in range(G):
                    w = i * G + s
                    act.wait_ge(made, w + 1)
                    nc.scalar.copy(idx[:, s:s + 1], m.src1[:, bass.ds(w, 1)]).then_inc(indexed, 1)
                for s in range(G):
                    w = i * G + s
                    act.wait_ge(hot, w + 1)
                    nc.scalar.activation(off[:, s, :], S[:, s, :], ACT.Identity, bias=minus, scale=MASK
                                         ).then_inc(masked, 1)

        @block.gpsimd
        def _(pool):
            nc.gpsimd.memset(minus, -MASK).then_inc(initial, 1)
            nc.gpsimd.tensor_copy(best, src_score).then_inc(initial, 1)
            with pool.Fori(0, WT // G) as i:
                for s in range(G):
                    pool.wait_ge(indexed, i * G + s + 1)
                    pool.sem_inc(issue, 1)
                    nc.gpsimd.indirect_dma_start(rows[:, s, :], None, m.table_max,
                                                 bass.IndirectOffsetOnAxis(ap=idx[:, s:s + 1], axis=0)
                                                 ).then_inc(gathered[s], 16)

        @block.tensor
        def _(pe):
            pe.sem_inc(made, G)
            with pe.Fori(0, WT // G) as i:
                for s in range(G):
                    w = i * G + s
                    pe.wait_ge(masked, w + 1)
                    pe.wait_ge(reduced, w + 1)
                    nc.tensor.matmul(m.PS[:, s, :], off[:, s, :],
                                     m.identb[:].unsqueeze(1).to_broadcast([P, H, P]), start=True, stop=False)
                    nc.tensor.matmul(m.PS[:, s, :], S[:, s, :], diag[:, s, :], start=False,
                                     stop=True).then_inc(made, 1)

        @block.vector
        def _(dve):
            v, c = nc.vector, Chain(dve, dstep)
            dve.sem_inc(reduced, G)
            dve.wait_ge(initial, 2)
            with dve.Fori(0, WT // G) as i:
                for s in range(G):
                    w = i * G + s
                    dve.wait_ge(made, w + 1)
                    dve.wait_ge(gathered[s], i * 16 + 16)
                    v.tensor_tensor(diag[:, s, :].rearrange("p (h e) -> p h e", h=H),
                                    m.ident[:].unsqueeze(1).to_broadcast([P, H, P]), bcast(rows[:, s, :], [P, H, P]),
                                    ALU.mult)
                    v.tensor_scalar(S[:, s, :], m.iota[:], m.lo1[:, bass.ds(w, 1)], None,
                                    ALU.is_equal).then_inc(hot, 1)
                for s in range(G):
                    w = i * G + s
                    c.at(w)
                    dve.wait_ge(made, w + 1 + G)
                    c.step(v.reduce_max(top[:, s, :], m.PS[:, s, :].rearrange("p (h e) -> p h e", h=H), AX))
                    tn = dve.value_load(m.tn1[0:1, bass.ds(w, 1)], min_val=0, max_val=NT - 1)
                    at = tile_at(best, tn, 0, H)
                    dve.wait_ge(reduced, w + G)
                    v.tensor_tensor(at, at, top[:, s, :], ALU.max).then_inc(reduced, 1)

    with Stage(nc) as st:
        names = ("dstep", "ready", "indexed", "hot", "turned", "tcopied", "scored", "expd", "summed", "added",
                 "issue", "dstep2", "weighted", "taken", "diffed", "selfed")
        (dstep, ready, indexed, hot, turned, tcopied, scored, expd, summed, added, issue, dstep2, weighted,
         taken, diffed, selfed) = (st.sem(s) for s in names)
        gathered = st.sems("gathered", G)
        S = view(m.WS, 0, G, P)
        ST = view(m.WS, G * P, G, P)
        rows = view(m.WS, 2 * G * P, G, RW)
        o = 2 * G * P + G * RW
        idx = view(m.WS, o, G).bitcast(I32)
        e = view(m.WS, o + 8, G, H)
        lk = view(m.WS, o + 8 + 32, G, H)
        p = view(m.WS, o + 8 + 64, G, H)
        own = view(high, 0, NT, H)
        block = st.block()

        @block.sync
        def _(sp):
            sp.dma_start(m.AGG[:, :, 0:RW], m.table_gat.rearrange("(t p) c -> p t c", p=P)).then_inc(selfed, 16)

        @block.scalar
        def _(act):
            act.sem_inc(tcopied, 2)
            act.wait_ge(diffed, 1)
            nc.scalar.activation(own, own, ACT.Exp).then_inc(expd, 1)
            with act.Fori(0, WT // G) as i:
                for s in range(G):
                    w = i * G + s
                    act.wait_ge(summed, w + 1)
                    nc.scalar.copy(idx[:, s:s + 1], m.src1[:, bass.ds(w, 1)]).then_inc(indexed, 1)
                for s in range(G):
                    w = i * G + s
                    act.wait_ge(turned, w + 1)
                    nc.scalar.copy(ST[:, s, :], m.PS[:, s % 2, 0:P]).then_inc(tcopied, 1)
                act.wait_ge(diffed, i + 2)
                nc.scalar.activation(p, e, ACT.Exp).then_inc(expd, 1)

        @block.gpsimd
        def _(pool):
            with pool.Fori(0, WT // G) as i:
                for s in range(G):
                    pool.wait_ge(indexed, i * G + s + 1)
                    pool.sem_inc(issue, 1)
                    nc.gpsimd.indirect_dma_start(rows[:, s, :], None, m.table_gat,
                                                 bass.IndirectOffsetOnAxis(ap=idx[:, s:s + 1], axis=0)
                                                 ).then_inc(gathered[s], 16)

        @block.tensor
        def _(pe):
            pe.sem_inc(summed, G)
            pe.wait_ge(ready, 1)
            with pe.Fori(0, WT // G) as i:
                for s in range(G):
                    w = i * G + s
                    pe.wait_ge(hot, w + 1)
                    pe.wait_ge(tcopied, w + 1)
                    nc.tensor.transpose(m.PS[:, s % 2, 0:P], S[:, s, :], m.ident[:]).then_inc(turned, 1)
                pe.wait_ge(taken, i + 1)
                for s in range(G):
                    w = i * G + s
                    pe.wait_ge(tcopied, w + 3)
                    tn = pe.value_load(m.tn1[0:1, bass.ds(w, 1)], min_val=0, max_val=NT - 1)
                    mm = nc.tensor.matmul(m.PS[:, 2, s * 8:(s + 1) * 8], ST[:, s, :], tile_at(node, tn, 0, 8),
                                          start=True, stop=True)
                mm.then_inc(scored, 1)
                pe.wait_ge(weighted, i + 1)
                for s in range(G):
                    w = i * G + s
                    pe.wait_ge(added, w + 1)
                    nc.tensor.matmul(m.PS[:, 4 + s % 4, 0:RW], S[:, s, :], rows[:, s, :], start=True,
                                     stop=True).then_inc(summed, 1)

        @block.vector
        def _(dve):
            v, c = nc.vector, Chain(dve, dstep)
            dve.sem_inc(added, 4)
            dve.sem_inc(taken, 1)
            c.step(v.tensor_tensor(best, best, node[:, :, 0:H], ALU.add))
            c.step(v.scalar_tensor_tensor(node[:, :, H:2 * H], best, 0.2, best, ALU.mult, ALU.max))
            dve.wait_ge(selfed, 16)
            c.step(v.tensor_tensor(best, m.AGG[:, :, D:RW], node[:, :, 0:H], ALU.add))
            c.step(v.scalar_tensor_tensor(own, best, 0.2, best, ALU.mult, ALU.max))
            c.step(v.tensor_tensor(own, own, node[:, :, H:2 * H], ALU.subtract))
            v.tensor_scalar(own, own, 0.0, None, ALU.min).then_inc(diffed, 1)
            dve.wait_ge(expd, 1)
            at = m.AGG[:, :, 0:D].rearrange("p t (h c) -> p t h c", h=H)
            c.step(v.tensor_tensor(at, at, own.unsqueeze(3).to_broadcast([P, NT, H, C]), ALU.mult))
            c.step(v.tensor_copy(m.AGG[:, :, D:RW], own))
            dve.sem_inc(ready, 1)
            c2 = Chain(dve, dstep2)
            with dve.Fori(0, WT // G) as i:
                c2.at(i * 3)
                for s in range(G):
                    w = i * G + s
                    dve.wait_ge(summed, w + 1)
                    v.tensor_scalar(S[:, s, :], m.iota[:], m.lo1[:, bass.ds(w, 1)], None,
                                    ALU.is_equal).then_inc(hot, 1)
                for s in range(G):
                    dve.wait_ge(gathered[s], i * 16 + 16)
                dve.wait_ge(scored, i + 1)
                sc = m.PS[:, 2, 0:G * 8].rearrange("p (u c) -> p u c", u=G)
                c2.step(v.tensor_tensor(e, rows[:, :, D:RW], sc[:, :, 0:H], ALU.add))
                c2.step(v.scalar_tensor_tensor(lk, e, 0.2, e, ALU.mult, ALU.max))
                c2.step(v.tensor_tensor(e, lk, sc[:, :, H:2 * H], ALU.subtract))
                dve.sem_inc(taken, 1)
                v.tensor_scalar(e, e, 0.0, None, ALU.min).then_inc(diffed, 1)
                dve.wait_ge(expd, i + 2)
                f = rows[:, :, 0:D].rearrange("p u (h c) -> p u h c", h=H)
                v.tensor_tensor(f, f, p.unsqueeze(3).to_broadcast([P, G, H, C]), ALU.mult)
                v.tensor_copy(rows[:, :, D:RW], p).then_inc(weighted, 1)
                for s in range(G):
                    w = i * G + s
                    dve.wait_ge(summed, w + 1 + G)
                    dve.wait_ge(added, w + 4)
                    tn = dve.value_load(m.tn1[0:1, bass.ds(w, 1)], min_val=0, max_val=NT - 1)
                    at = tile_at(m.AGG, tn, 0, RW)
                    v.tensor_tensor(at, at, m.PS[:, 4 + s % 4, 0:RW], ALU.add).then_inc(added, 1)

    with Stage(nc) as st:
        loaded, dstep = st.sem("loaded"), st.sem("dstep")
        bias = m.WS[:, 0:D]
        rd = view(m.WS, D, NT, H)
        block = st.block()

        @block.sync
        def _(sp):
            sp.dma_start(bias, a["L1_gnn_bias"].unsqueeze(0).to_broadcast([P, D])).then_inc(loaded, 16)

        @block.vector
        def _(dve):
            v, c = nc.vector, Chain(dve, dstep)
            c.step(v.tensor_scalar(rd, m.AGG[:, :, D:RW], 1e-16, None, ALU.add))
            c.step(v.reciprocal(rd, rd))
            heads = [x.rearrange("p t (h c) -> p t h c", h=H) for x in (m.XN[:], m.AGG[:, :, 0:D])]
            c.step(v.tensor_tensor(heads[0], heads[1], rd.unsqueeze(3).to_broadcast([P, NT, H, C]), ALU.mult))
            dve.wait_ge(loaded, 16)
            c.step(v.tensor_tensor(m.XN[:], m.XN[:], bias.unsqueeze(1).to_broadcast([P, NT, D]), ALU.add))

    turn(nc, m, m.XN, m.XT)

    def finish(dve, c, t, ps):
        at = tile_at(m.X, t)
        return nc.vector.scalar_tensor_tensor(at, ps, 0.0, at, ALU.max, ALU.add)

    linear_nodes(nc, m, m.XT, a["L1_gnn_lin_w"], a["L1_gnn_lin_b"], D, Finish(finish))


def expert_pair(nc, m, a):
    NE, HD = 8, 1024
    KH = HD // P
    layernorm(nc, m, m.X, m.XN)
    gates(nc, m, a["L1_ffn_Wr"], a["L1_ffn_br"], NE, False)
    layernorm(nc, m, m.XN, m.XN)
    turn(nc, m, m.XN, m.XT)
    with Stage(nc) as st:
        names = ("shifted", "made_b", "w1_used", "w2_used", "scaled", "made", "active", "done", "taken", "smalls", "passed")
        shifted, made_b, w1_used, w2_used, scaled, made, active, done, taken, smalls, passed = (st.sem(s) for s in names)
        came1, came2 = st.sems("came1", 2), st.sems("came2", 2)
        hid = view(m.BB, 0, KH, CB)
        o = KH * CB
        w1 = [view(m.BB, o + q * KD * HD, KD, HD) for q in range(2)]
        o += 2 * KD * HD
        w2 = [view(m.BB, o, KH, D), view(m.AF, 0, KH, D)]
        ln_g = view(m.WS, 0, NE, KD)
        ln_b = view(m.WS, 16, NE, KD)
        b1 = view(m.WS, 32, NE, KH)
        b1s = view(m.WS, 96, 2, KH)
        b2 = m.WS[0:1, 128:128 + NE * D]
        block = st.block()

        @block.sync
        def _(sp):
            sp.dma_start(ln_g, a["L1_ffn_ln_g"].rearrange("p (e k) -> p e k", k=KD)).then_inc(smalls, 16)
            sp.dma_start(ln_b, a["L1_ffn_ln_b"].rearrange("p (e k) -> p e k", k=KD)).then_inc(smalls, 16)
            sp.dma_start(b1, a["L1_ffn_b1"].rearrange("p (e k) -> p e k", k=KH)).then_inc(smalls, 16)
            sp.dma_start(b2, a["L1_ffn_b2"].rearrange("e d -> (e d)").unsqueeze(0)).then_inc(smalls, 16)
            w1d = a["L1_ffn_W1"].rearrange("e (k p) h -> e p k h", p=P)
            w2d = a["L1_ffn_W2"].rearrange("e (k p) d -> e p k d", p=P)
            with sp.Fori(0, NE // 2) as i:
                for q in range(2):
                    ex = i * 2 + q
                    sp.wait_ge(w1_used, ex + 1)
                    sp.dma_start(w1[q], w1d[bass.ds(ex, 1), :, :, :].rearrange("o p k h -> (o p) k h")
                                 ).then_inc(came1[q], 16)
                    sp.dma_start(w2[q], w2d[bass.ds(ex, 1), :, :, :].rearrange("o p k d -> (o p) k d")
                                 ).then_inc(came2[q], 16)

        @block.tensor
        def _(pe):
            pe.sem_inc(w1_used, 2)
            pe.wait_ge(smalls, 64)
            te = nc.tensor
            with pe.Fori(0, NE // 2) as i:
                for q in range(2):
                    ex = i * 2 + q
                    pe.wait_ge(came1[q], i * 16 + 16)
                    pe.wait_ge(taken, ex * NT + U)
                    for j in range(KH):
                        for k in range(KD):
                            mm = te.matmul(m.PS[:, 3, j:j + 1], w1[q][:, k, j * P:(j + 1) * P],
                                           ln_b[:, bass.ds(ex, 1), k:k + 1].rearrange("p o k -> p (o k)"),
                                           start=(k == 0), stop=(k == KD - 1))
                    mm.then_inc(made_b, 1)
                    pe.wait_ge(scaled, ex + 1)
                    pe.wait_ge(came2[q], i * 16 + 16)
                    pe.sem_inc(passed, 1)
                    with pe.Fori(0, NT // TB) as b:
                        base = (ex * (NT // TB) + b) * KH * 2
                        for j in range(KH):
                            for h in range(2):
                                n = base + j * 2 + h
                                pe.wait_ge(active, n + 1)
                                for k in range(KD):
                                    mm = te.matmul(m.PS[:, h, 0:CH2], w1[q][:, k, j * P:(j + 1) * P],
                                                   m.XT[:, k, bass.ds(b * CB + h * CH2, CH2)], start=(k == 0),
                                                   stop=(k == KD - 1))
                                mm.then_inc(made, 1)
                        pe.wait_ge(active, base + KH * 2 + 2)
                        for s in range(TB):
                            t = ex * NT + b * TB + s
                            pe.wait_ge(taken, t + 1)
                            for j in range(KH):
                                te.matmul(m.PS[:, 3 + s, 0:D], hid[:, j, s * P:(s + 1) * P], w2[q][:, j, :],
                                          start=(j == 0), stop=False)
                            te.matmul(m.PS[:, 3 + s, 0:D], m.ones[0:1, :],
                                      b2[:, bass.ds(ex * D, D)], start=False, stop=True).then_inc(done, 1)
                    pe.wait_ge(done, (ex + 1) * NT)
                    pe.sem_inc(w1_used, 1)

        @block.scalar
        def _(act):
            act.sem_inc(active, 2)
            with act.Fori(0, NE // 2) as i:
                for q in range(2):
                    ex = i * 2 + q
                    act.wait_ge(shifted, ex + 1)
                    act.sem_inc(passed, 1)
                    with act.Fori(0, NT // TB) as b:
                        base = (ex * (NT // TB) + b) * KH * 2
                        for j in range(KH):
                            for h in range(2):
                                n = base + j * 2 + h
                                act.wait_ge(made, n + 1)
                                nc.scalar.activation(hid[:, j, h * CH2:(h + 1) * CH2], m.PS[:, h, 0:CH2], ACT.Gelu,
                                                     bias=b1s[:, q, j:j + 1]).then_inc(active, 1)

        @block.vector
        def _(dve):
            v = nc.vector
            dve.sem_inc(taken, U)
            dve.wait_ge(smalls, 64)
            with dve.Fori(0, NE // 2) as i:
                for q in range(2):
                    ex = i * 2 + q
                    dve.wait_ge(made_b, ex + 1)
                    v.tensor_tensor(b1s[:, q, :], m.PS[:, 3, 0:KH],
                                    b1[:, bass.ds(ex, 1), :].rearrange("p o k -> p (o k)"), ALU.add
                                    ).then_inc(shifted, 1)
                    for k in range(KD):
                        ins = v.tensor_scalar(w1[q][:, k, :], w1[q][:, k, :],
                                              ln_g[:, bass.ds(ex, 1), k:k + 1].rearrange("p o k -> p (o k)"), None,
                                              ALU.mult)
                    ins.then_inc(scaled, 1)
                    with dve.Fori(0, NT // TB) as b:
                        for s in range(TB):
                            t = b * TB + s
                            n = ex * NT + t
                            dve.wait_ge(done, n + 1)
                            dve.wait_ge(taken, n + U)
                            at = tile_at(m.X, t)
                            g = m.gate[:, bass.ds(t, 1), bass.ds(ex, 1)].rearrange("p o k -> p (o k)")
                            v.scalar_tensor_tensor(at, m.PS[:, 3 + s, 0:D], g, at, ALU.mult,
                                                   ALU.add).then_inc(taken, 1)


def gates(nc, m, weight, bias, ne, softmax_first, hidden=None):
    if hidden is None:
        turn(nc, m, m.XN, m.XT)
    srcT = m.XT if hidden is None else hidden
    KX = 1 if hidden is not None else KD
    with Stage(nc) as st:
        names = ("loaded", "staged", "made", "taken", "dstep", "differed", "expd", "passed")
        loaded, staged, made, taken, dstep, differed, expd, passed = (st.sem(s) for s in names)
        ring = view(m.WS, 0, U, KX, P)
        w = view(m.WS, U * D, KX, ne)
        b = m.WS[0:1, U * D + 64:U * D + 64 + ne]
        lg = m.WS[:, 2000:2008]
        top = m.WS[:, 2008:2016]
        which = m.WS[:, 2016:2024].bitcast(U32)
        whichf = m.WS[:, 2024:2032]
        ex = m.WS[:, 2032:2040]
        sh = m.WS[:, 2040:2048]
        eq = m.WS[:, 2048:2056]
        eq2 = m.WS[:, 2064:2072]
        prob = m.WS[:, 2072:2080]
        total = m.WS[:, 2056:2057]
        block = st.block()

        @block.sync
        def _(sp):
            sp.dma_start(w, weight.rearrange("(k p) n -> p k n", p=P)).then_inc(loaded, 16)
            sp.dma_start(b, bias.unsqueeze(0)).then_inc(loaded, 16)

        @block.scalar
        def _(act):
            with act.Fori(0, NT // U) as i:
                for s in range(U):
                    t = i * U + s
                    act.wait_ge(made, t + 1)
                    nc.scalar.copy(ring[:, s, :, :], srcT[:, 0:KX, bass.ds(t * P, P)]).then_inc(staged, 1)
                for s in range(U):
                    t = i * U + s
                    if softmax_first:
                        act.wait_ge(differed, t * 2 + 1)
                        nc.scalar.activation(ex, sh, ACT.Exp).then_inc(expd, 1)
                        act.wait_ge(differed, t * 2 + 2)
                        nc.scalar.activation(ex[:, 0:2], sh[:, 0:2], ACT.Exp).then_inc(expd, 1)
                    else:
                        act.wait_ge(differed, t + 1)
                        nc.scalar.activation(ex[:, 0:2], sh[:, 0:2], ACT.Exp).then_inc(expd, 1)

        @block.tensor
        def _(pe):
            pe.sem_inc(made, U)
            pe.wait_ge(loaded, 32)
            with pe.Fori(0, NT // U) as i:
                for s in range(U):
                    t = i * U + s
                    pe.wait_ge(staged, t + 1)
                    pe.wait_ge(taken, t + 1)
                    for k in range(KX):
                        nc.tensor.matmul(m.PS[:, s, 0:ne], ring[:, s, k, :], w[:, k, :], start=(k == 0), stop=False)
                    nc.tensor.matmul(m.PS[:, s, 0:ne], m.ones[0:1, :], b, start=False, stop=True).then_inc(made, 1)

        @block.vector
        def _(dve):
            v, c = nc.vector, Chain(dve, dstep)
            dve.sem_inc(taken, U)
            c.step(v.memset(lg, -BIG))

            def tile(t, s):
                dve.wait_ge(made, t + 1 + U)
                c.step(v.tensor_copy(lg[:, 0:ne], m.PS[:, s, 0:ne]))
                dve.sem_inc(taken, 1)
                c.step(v.max(top, lg))
                if softmax_first:
                    v.tensor_scalar(sh, lg, top[:, 0:1], None, ALU.subtract).then_inc(differed, 1)
                    dve.wait_ge(expd, t * 2 + 1)
                    c.step(v.reduce_sum(total, ex, AX))
                    c.step(v.reciprocal(total, total))
                    c.step(v.tensor_scalar(prob[:, 0:ne], ex[:, 0:ne], total, None, ALU.mult))
                    dve.sem_inc(passed, 1)
                    c.step(v.max(top, prob))
                dve.sem_inc(passed, 1)
                c.step(v.max_index(which, top, prob if softmax_first else lg))
                c.step(v.tensor_copy(whichf, which))
                v.tensor_scalar(sh[:, 0:2], top[:, 0:2], top[:, 0:1], None, ALU.subtract).then_inc(differed, 1)
                dve.wait_ge(expd, t * 2 + 2 if softmax_first else t + 1)
                c.step(v.reduce_sum(total, ex[:, 0:2], AX))
                c.step(v.reciprocal(total, total))
                c.step(v.tensor_scalar(eq, m.iota[:, 0:8], whichf[:, 0:1], ex[:, 0:1], ALU.is_equal, ALU.mult))
                c.step(v.tensor_scalar(eq2, m.iota[:, 0:8], whichf[:, 1:2], ex[:, 1:2], ALU.is_equal, ALU.mult))
                c.step(v.tensor_tensor(eq, eq, eq2, ALU.add))
                v.tensor_scalar(tile_at(m.gate, t, 0, 8), eq, total, None, ALU.mult)

            c.step(v.memset(prob, -1.0))
            steps = 13 if softmax_first else 9
            with dve.Fori(0, NT // U) as i:
                for s in range(U):
                    c.at((i * U + s) * steps + 2)
                    tile(i * U + s, s)
                    assert c.k == steps



def edge_update(nc, m, a):
    layernorm(nc, m, m.X, m.XN)
    turn(nc, m, m.XN, m.XT)
    w1 = a["L2_gnn_W1"]
    by_dst = view(m.BB, 0, NT, D)
    by_src = view(m.BB, NT * D, NT, D)

    def keep(dst):
        return Finish(lambda dve, c, t, ps: nc.vector.tensor_copy(tile_at(dst, t), ps))

    linear_nodes(nc, m, m.XT, w1[D:2 * D, :], None, D, keep(by_dst))
    store_table(nc, m, by_dst, m.table, sums=0.0)
    linear_nodes(nc, m, m.XT, w1[0:D, :], a["L2_gnn_b1"], D, keep(by_src))

    CW = D + 1
    with Stage(nc) as st:
        names = ("loaded", "oned", "indexed", "hot", "turned", "tcopied", "made", "mixed", "active", "summed",
                 "added", "issue")
        loaded, oned, indexed, hot, turned, tcopied, made, mixed, active, summed, added, issue = (
            st.sem(s) for s in names)
        gathered, came = st.sems("gathered", G), st.sems("came", G)
        S = view(m.WS, 0, G, P)
        ST = view(m.WS, G * P, G, P)
        rows = view(m.WS, 2 * G * P, G, CW)
        o = 2 * G * P + G * CW
        idx = view(m.WS, o, G).bitcast(I32)
        rec = view(m.WS, o + 8, G, EA + 4)
        attT = view(m.WS, o + 8 + G * (EA + 4), G, P)
        wa = m.BB[0:EA, 0:D]
        block = st.block()

        @block.sync
        def _(sp):
            sp.dma_start(wa, w1[2 * D:2 * D + EA, :]).then_inc(loaded, 16)
            r = m.rec2.rearrange("(p w) c -> p w c", p=P)
            with sp.Fori(0, WT // G) as i:
                for s in range(G):
                    w = i * G + s
                    sp.wait_ge(summed, w + 1)
                    sp.dma_start(rec[:, s, :], r[:, bass.ds(w, 1), :].rearrange("p o c -> p (o c)")
                                 ).then_inc(came[s], 16)

        @block.scalar
        def _(act):
            act.sem_inc(tcopied, 2)
            with act.Fori(0, WT // G) as i:
                for s in range(G):
                    w = i * G + s
                    act.wait_ge(came[s], i * 16 + 16)
                    nc.scalar.copy(idx[:, s:s + 1], rec[:, s, EA:EA + 1]).then_inc(indexed, 1)
                for s in range(G):
                    w = i * G + s
                    act.wait_ge(turned, w + 1)
                    nc.scalar.copy(ST[:, s, :], m.PS[:, s % 2, 0:P])
                    nc.scalar.copy(attT[0:EA, s, :], m.PS[0:EA, s % 2, P:2 * P]).then_inc(tcopied, 1)
                for s in range(G):
                    w = i * G + s
                    act.wait_ge(mixed, w + 3)
                    nc.scalar.activation(rows[:, s, 0:D], rows[:, s, 0:D], ACT.Relu).then_inc(active, 1)

        @block.gpsimd
        def _(pool):
            nc.gpsimd.memset(rows[:, :, D:CW], 1.0).then_inc(oned, 1)
            with pool.Fori(0, WT // G) as i:
                for s in range(G):
                    pool.wait_ge(indexed, i * G + s + 1)
                    pool.sem_inc(issue, 1)
                    nc.gpsimd.indirect_dma_start(rows[:, s, 0:D], None, m.table,
                                                 bass.IndirectOffsetOnAxis(ap=idx[:, s:s + 1], axis=0)
                                                 ).then_inc(gathered[s], 16)

        @block.tensor
        def _(pe):
            pe.sem_inc(summed, G)
            pe.wait_ge(loaded, 16)
            pe.wait_ge(oned, 1)
            te = nc.tensor
            with pe.Fori(0, WT // G) as i:
                for s in range(G):
                    w = i * G + s
                    pe.wait_ge(hot, w + 1)
                    pe.wait_ge(tcopied, w + 1)
                    te.transpose(m.PS[:, s % 2, 0:P], S[:, s, :], m.ident[:])
                    te.transpose(m.PS[0:EA, s % 2, P:2 * P], rec[:, s, 0:EA], m.ident[:]).then_inc(turned, 1)
                for s in range(G):
                    w = i * G + s
                    pe.wait_ge(tcopied, w + 3)
                    pe.wait_ge(mixed, w + 1)
                    tn = pe.value_load(m.tn2[0:1, bass.ds(w, 1)], min_val=0, max_val=NT - 1)
                    te.matmul(m.PS[:, 2 + s % 2, 0:D], ST[:, s, :], tile_at(by_src, tn), start=True, stop=False)
                    te.matmul(m.PS[:, 2 + s % 2, 0:D], attT[0:EA, s, :], wa, start=False,
                              stop=True).then_inc(made, 1)
                for s in range(G):
                    w = i * G + s
                    pe.wait_ge(active, w + 1)
                    pe.wait_ge(added, w + 1)
                    te.matmul(m.PS[:, 4 + s % 4, 0:CW], S[:, s, :], rows[:, s, :], start=True,
                              stop=True).then_inc(summed, 1)

        @block.vector
        def _(dve):
            v = nc.vector
            dve.sem_inc(added, 4)
            dve.sem_inc(mixed, 2)
            with dve.Fori(0, WT // G) as i:
                for s in range(G):
                    w = i * G + s
                    dve.wait_ge(came[s], i * 16 + 16)
                    v.tensor_scalar(S[:, s, :], m.iota[:], rec[:, s, EA + 1:EA + 2], None,
                                    ALU.is_equal).then_inc(hot, 1)
                for s in range(G):
                    w = i * G + s
                    dve.wait_ge(gathered[s], i * 16 + 16)
                    dve.wait_ge(made, w + 1)
                    v.tensor_tensor(rows[:, s, 0:D], rows[:, s, 0:D], m.PS[:, 2 + s % 2, 0:D],
                                    ALU.add).then_inc(mixed, 1)
                for s in range(G):
                    w = i * G + s
                    dve.wait_ge(summed, w + 1 + G)
                    dve.wait_ge(added, w + 4)
                    tn = dve.value_load(m.tn2[0:1, bass.ds(w, 1)], min_val=0, max_val=NT - 1)
                    at = tile_at(m.AGG, tn, 0, CW)
                    v.tensor_tensor(at, at, m.PS[:, 4 + s % 4, 0:CW], ALU.add).then_inc(added, 1)

    sumsT = view(m.BB, 0, KD, NP)
    b2 = view(m.BB, 12800 - D, D)
    turn(nc, m, m.AGG, sumsT)
    with Stage(nc) as st:
        loaded = st.sem("loaded")
        block = st.block()

        @block.sync
        def _(sp):
            sp.dma_start(b2, a["L2_gnn_b2"].unsqueeze(0).to_broadcast([P, D])).then_inc(loaded, 16)
            sp.wait_ge(loaded, 16)

    def message(dve, c, t, ps):
        count = tile_at(m.AGG, t, D, D + 1)
        return nc.vector.scalar_tensor_tensor(tile_at(m.AGG, t), b2, count, ps, ALU.mult, ALU.add)

    linear_nodes(nc, m, sumsT, a["L2_gnn_W2"], None, D, Finish(message))
    turn(nc, m, m.AGG, sumsT)

    with Stage(nc) as st:
        names = ("loaded", "dstep", "rowed", "staged", "made", "gated", "sread", "tanhed", "inner", "used")
        loaded, dstep, rowed, staged, made, gated, sread, tanhed, inner, used = (st.sem(s) for s in names)
        D3 = 3 * D
        wi = view(m.BB, KD * NP, KD, D3)
        wh = view(m.BB, KD * NP + KD * D3, KD, D3)
        o = KD * NP + 2 * KD * D3
        bi, bh = (m.BB[0:1, o + k * D3:o + (k + 1) * D3] for k in range(2))
        ring = view(m.WS, 0, U, 2 * KD, P)
        rz = view(m.WS, U * 512, U, 512)
        cand = view(m.AF, 0, U, D)
        gap = view(m.AF, U * D, U, D)
        block = st.block()

        @block.sync
        def _(sp):
            sp.dma_start(wi, a["L2_gnn_W_ih"].rearrange("(k p) n -> p k n", p=P)).then_inc(loaded, 16)
            sp.dma_start(wh, a["L2_gnn_W_hh"].rearrange("(k p) n -> p k n", p=P)).then_inc(loaded, 16)
            sp.dma_start(bi, a["L2_gnn_b_ih"].unsqueeze(0)).then_inc(loaded, 16)
            sp.dma_start(bh, a["L2_gnn_b_hh"].unsqueeze(0)).then_inc(loaded, 16)

        @block.scalar
        def _(act):
            with act.Fori(0, NT // U) as i:
                for s in range(U):
                    t = i * U + s
                    act.wait_ge(made, t + 1)
                    nc.scalar.copy(ring[:, s, 0:KD, :], sumsT[:, :, bass.ds(t * P, P)])
                    nc.scalar.copy(ring[:, s, KD:2 * KD, :], m.XT[:, :, bass.ds(t * P, P)]).then_inc(staged, 1)
                    act.wait_ge(made, t + 1 + U)
                    nc.scalar.activation(rz[:, s, :], m.PS[:, s % 2, :], ACT.Sigmoid).then_inc(gated, 1)
                    act.wait_ge(inner, t + 1)
                    nc.scalar.activation(cand[:, s, :], cand[:, s, :], ACT.Tanh).then_inc(tanhed, 1)

        @block.tensor
        def _(pe):
            te = nc.tensor
            pe.sem_inc(made, U)
            pe.wait_ge(loaded, 64)
            one = m.ones[0:1, :]
            with pe.Fori(0, NT // U) as i:
                for s in range(U):
                    t = i * U + s
                    pe.wait_ge(staged, t + 1)
                    free2(pe, used, s, t)
                    b0, b1 = m.PS[:, s % 2, :], m.PS[:, 2 + s % 2, :]
                    for k in range(KD):
                        te.matmul(b0, ring[:, s, k, :], wi[:, k, 0:2 * D], start=(k == 0), stop=False)
                        te.matmul(b0, ring[:, s, KD + k, :], wh[:, k, 0:2 * D], start=False, stop=False)
                    te.matmul(b0, one, bi[:, 0:2 * D], start=False, stop=False)
                    te.matmul(b0, one, bh[:, 0:2 * D], start=False, stop=True)
                    for half, (w, b, q) in enumerate(((wi, bi, 0), (wh, bh, KD))):
                        at = b1[:, half * D:(half + 1) * D]
                        for k in range(KD):
                            te.matmul(at, ring[:, s, q + k, :], w[:, k, 2 * D:D3], start=(k == 0), stop=False)
                        mm = te.matmul(at, one, b[:, 2 * D:D3], start=False, stop=True)
                    mm.then_inc(made, 1)

        @block.vector
        def _(dve):
            v, c = nc.vector, Chain(dve, dstep)
            dve.sem_inc(used, 2)
            with dve.Fori(0, NT // U) as i:
                for s in range(U):
                    t = i * U + s
                    c.at(t * 5)
                    dve.wait_ge(gated, t + 1)
                    b1 = m.PS[:, 2 + s % 2, :]
                    c.step(v.tensor_tensor(cand[:, s, :], rz[:, s, 0:D], b1[:, D:2 * D], ALU.mult))
                    c.step(v.tensor_tensor(cand[:, s, :], cand[:, s, :], b1[:, 0:D], ALU.add))
                    dve.sem_inc(used, 1)
                    dve.sem_inc(inner, 1)
                    dve.wait_ge(tanhed, t + 1)
                    c.step(v.tensor_tensor(gap[:, s, :], tile_at(m.XN, t), cand[:, s, :], ALU.subtract))
                    c.step(v.tensor_tensor(gap[:, s, :], gap[:, s, :], rz[:, s, D:2 * D], ALU.mult))
                    c.step(v.tensor_tensor(gap[:, s, :], gap[:, s, :], cand[:, s, :], ALU.add))
                    at = tile_at(m.X, t)
                    v.tensor_tensor(at, at, gap[:, s, :], ALU.add)


def one_expert(nc, m, a):
    NE, HD = 32, 64
    KH = NE * HD // P
    layernorm(nc, m, m.X, m.XN)
    turn(nc, m, m.XN, m.XT)
    w1 = view(m.AF, 0, KD, NE * HD)
    pick = m.AF[0:NE, KD * NE * HD:KD * NE * HD + KH * P]
    w2 = m.XN[:].rearrange("p t d -> p (t d)")[:, 0:KH * D].rearrange("p (k d) -> p k d", d=D)
    chosen = m.WS[0:NE, 0:NP]
    others = m.WS[0:NE, NP:2 * NP]
    b2 = m.WS[0:NE, 2 * NP:2 * NP + D]
    b1 = view(m.WS, 2 * NP + D, KH)
    high = view(m.BB, 0, 3000)

    with Stage(nc) as st:
        names = ("loaded", "staged", "made", "dstep", "passed", "turned", "taken", "read", "hot", "picked")
        loaded, staged, made, dstep, passed, turned, taken, read, hot, picked = (st.sem(s) for s in names)
        ring = view(high, 0, U, KD, P)
        wr = view(high, U * D, KD, NE)
        br = high[0:1, U * D + 64:U * D + 96]
        lg = high[:, 1400:1400 + NE]
        top = high[:, 1440:1448]
        which = high[:, 1448:1456].bitcast(U32)
        whichf = high[:, 1456:1464]
        hots = view(high, 1500, U, NE)
        block = st.block()

        @block.sync
        def _(sp):
            sp.dma_start(wr, a["L2_ffn_router_w"].rearrange("(k p) n -> p k n", p=P)).then_inc(loaded, 16)
            sp.dma_start(br, a["L2_ffn_router_b"].unsqueeze(0)).then_inc(loaded, 16)

        @block.gpsimd
        def _(pool):
            g = nc.gpsimd
            pv = pick.rearrange("p (k j) -> p k j", k=KH)
            g.memset(pick, BIG).then_inc(picked, 1)
            pool.wait_ge(picked, 1)
            g.affine_select(out=pv, in_=pv, compare_op=ALU.is_ge, fill=0.0, base=0, pattern=[[P, KH], [1, P]],
                            channel_multiplier=-HD).then_inc(picked, 1)
            pool.wait_ge(picked, 2)
            g.affine_select(out=pv, in_=pv, compare_op=ALU.is_ge, fill=0.0, base=HD - 1,
                            pattern=[[-P, KH], [-1, P]], channel_multiplier=HD).then_inc(picked, 1)

        @block.scalar
        def _(act):
            with act.Fori(0, NT // U) as i:
                for s in range(U):
                    t = i * U + s
                    act.wait_ge(made, t + 1)
                    nc.scalar.copy(ring[:, s, :, :], m.XT[:, :, bass.ds(t * P, P)]).then_inc(staged, 1)

        @block.tensor
        def _(pe):
            pe.sem_inc(made, U)
            pe.sem_inc(turned, U)
            pe.wait_ge(loaded, 32)
            with pe.Fori(0, NT // U) as i:
                for s in range(U):
                    t = i * U + s
                    pe.wait_ge(staged, t + 1)
                    pe.wait_ge(read, t + 1)
                    for k in range(KD):
                        nc.tensor.matmul(m.PS[:, s, 0:NE], ring[:, s, k, :], wr[:, k, :], start=(k == 0), stop=False)
                    nc.tensor.matmul(m.PS[:, s, 0:NE], m.ones[0:1, :], br, start=False, stop=True).then_inc(made, 1)
                for s in range(U):
                    t = i * U + s
                    pe.wait_ge(hot, t + 1)
                    free2(pe, taken, s, t)
                    nc.tensor.transpose(m.PS[0:NE, 5 + s % 2, 0:P], hots[:, s, :], m.ident[:]).then_inc(turned, 1)

        @block.vector
        def _(dve):
            v, c = nc.vector, Chain(dve, dstep)
            dve.sem_inc(read, U)
            dve.sem_inc(taken, 2)
            with dve.Fori(0, NT // U) as i:
                for s in range(U):
                    t = i * U + s
                    c.at(t * 4)
                    dve.wait_ge(made, t + 1 + U)
                    c.step(v.tensor_copy(lg, m.PS[:, s, 0:NE]))
                    dve.sem_inc(read, 1)
                    c.step(v.max(top, lg))
                    dve.sem_inc(passed, 1)
                    c.step(v.max_index(which, top, lg))
                    c.step(v.tensor_copy(whichf, which))
                    dve.wait_ge(turned, t + 1)
                    v.tensor_scalar(hots[:, s, :], m.iota[:, 0:NE], whichf[:, 0:1], None,
                                    ALU.is_equal).then_inc(hot, 1)
                for s in range(U):
                    t = i * U + s
                    dve.wait_ge(turned, t + 1 + U)
                    v.tensor_copy(chosen[:, bass.ds(t * P, P)], m.PS[0:NE, 5 + s % 2, 0:P])
                    v.tensor_scalar(others[:, bass.ds(t * P, P)], m.PS[0:NE, 5 + s % 2, 0:P], 1.0, None,
                                    ALU.subtract).then_inc(taken, 1)

    with Stage(nc) as st:
        loaded, made, active, done, taken, cstaged = (
            st.sem(s) for s in ("loaded", "made", "active", "done", "taken", "cstaged"))
        hid = view(m.BB, 0, KH, CB)
        cring = m.BB[0:NE, KH * CB:KH * CB + U * P].rearrange("p (u n) -> p u n", u=U)
        block = st.block()

        @block.sync
        def _(sp):
            for k in range(KD):
                sp.dma_start(w1[:, k, :].rearrange("p (e h) -> p e h", e=NE),
                             a["L2_ffn_W1"].rearrange("e (k p) h -> k p e h", p=P)[k]).then_inc(loaded, 16)
            sp.dma_start(w2, a["L2_ffn_W2"].rearrange("e h d -> (e h) d").rearrange("(k p) d -> p k d", p=P)
                         ).then_inc(loaded, 16)
            sp.dma_start(b1, a["L2_ffn_b1"]).then_inc(loaded, 16)
            sp.dma_start(b2, a["L2_ffn_b2"]).then_inc(loaded, 16)

        @block.tensor
        def _(pe):
            te = nc.tensor
            pe.wait_ge(loaded, 80)
            with pe.Fori(0, NT // TB) as b:
                for j in range(KH):
                    for h in range(2):
                        pe.wait_ge(active, (b * KH + j) * 2 + h + 1)
                        cols = bass.ds(b * CB + h * CH2, CH2)
                        for k in range(KD):
                            te.matmul(m.PS[:, h, 0:CH2], w1[:, k, j * P:(j + 1) * P], m.XT[:, k, cols],
                                      start=(k == 0), stop=False)
                        te.matmul(m.PS[:, h, 0:CH2], pick[:, j * P:(j + 1) * P], others[:, cols], start=False,
                                  stop=True).then_inc(made, 1)
                pe.wait_ge(active, (b + 1) * KH * 2 + 2)
                pe.wait_ge(cstaged, b + 1)
                for s in range(TB):
                    pe.wait_ge(taken, b * TB + s + 1)
                    for j in range(KH):
                        te.matmul(m.PS[:, 3 + s, 0:D], hid[:, j, s * P:(s + 1) * P], w2[:, j, :], start=(j == 0),
                                  stop=False)
                    te.matmul(m.PS[:, 3 + s, 0:D], cring[:, s, :], b2, start=False, stop=True).then_inc(done, 1)

        @block.scalar
        def _(act):
            act.sem_inc(active, 2)
            act.wait_ge(loaded, 80)
            with act.Fori(0, NT // TB) as b:
                for j in range(KH):
                    for h in range(2):
                        act.wait_ge(made, (b * KH + j) * 2 + h + 1)
                        nc.scalar.activation(hid[:, j, h * CH2:(h + 1) * CH2], m.PS[:, h, 0:CH2], ACT.Relu,
                                             bias=b1[:, j:j + 1]).then_inc(active, 1)

        @block.vector
        def _(dve):
            v = nc.vector
            dve.sem_inc(taken, U)
            with dve.Fori(0, NT // TB) as b:
                v.tensor_copy(cring.rearrange("p u n -> p (u n)"), chosen[:, bass.ds(b * CB, CB)]).then_inc(cstaged, 1)
                for s in range(TB):
                    t = b * TB + s
                    dve.wait_ge(done, t + 1)
                    at = tile_at(m.X, t)
                    v.scalar_tensor_tensor(at, m.PS[:, 3 + s, 0:D], 0.0, at, ALU.max, ALU.add).then_inc(taken, 1)



def relations(nc, m, a):
    NR, NB = 8, 4
    layernorm(nc, m, m.X, m.XN)
    turn(nc, m, m.XN, m.XT)
    IL = 16
    w = m.BB[:, 0:KD * NR * D].rearrange("p (k r d) -> p k r d", k=KD, r=NR)
    mixer = m.AF[0:IL * NB, 0:P]
    comp = m.AF[0:IL * NB, P:P + NR]
    basis = m.AF[0:IL * NB, 256:256 + NR * KD * D].rearrange("p (q d) -> p q d", d=D)

    with Stage(nc) as st:
        loaded, masked, mixed, made, taken = (st.sem(s) for s in ("loaded", "masked", "mixed", "made", "taken"))
        block = st.block()

        @block.sync
        def _(sp):
            for i in range(IL):
                sp.dma_start(comp[i * NB:(i + 1) * NB, :], a["L3_gnn_w_comp"]).then_inc(loaded, 16)
            sp.dma_start(basis, a["L3_gnn_basis"].rearrange("b i d -> (b i) d").rearrange("(q p) d -> p q d", p=IL * NB)
                         ).then_inc(loaded, 16)

        @block.gpsimd
        def _(pool):
            g = nc.gpsimd
            mv = mixer.rearrange("p (i r) -> p i r", r=NR)
            g.memset(mixer, 1.0).then_inc(masked, 1)
            pool.wait_ge(masked, 1)
            g.affine_select(out=mv, in_=mv, compare_op=ALU.is_ge, fill=0.0, base=0, pattern=[[-NB, IL], [0, NR]],
                            channel_multiplier=1).then_inc(masked, 1)
            pool.wait_ge(masked, 2)
            g.affine_select(out=mv, in_=mv, compare_op=ALU.is_ge, fill=0.0, base=NB - 1,
                            pattern=[[NB, IL], [0, NR]], channel_multiplier=-1).then_inc(masked, 1)

        @block.vector
        def _(dve):
            dve.wait_ge(masked, 3)
            dve.wait_ge(loaded, 16 * (IL + 1))
            mv = mixer.rearrange("p (i r) -> p i r", r=NR)
            nc.vector.tensor_tensor(mv, mv, comp.unsqueeze(1).to_broadcast([IL * NB, IL, NR]), ALU.mult
                                    ).then_inc(mixed, 1)
            for q in range(NR * KD):
                dve.wait_ge(made, q + 1)
                nc.vector.tensor_copy(w[:, q % KD, q // KD, :], m.PS[:, q % 4, 0:D]).then_inc(taken, 1)

        @block.tensor
        def _(pe):
            pe.wait_ge(mixed, 1)
            for q in range(NR * KD):
                if q >= 4:
                    pe.wait_ge(taken, q - 3)
                nc.tensor.matmul(m.PS[:, q % 4, 0:D], mixer, basis[:, q, :], start=True, stop=True).then_inc(made, 1)

    with Stage(nc) as st:
        staged, made, taken_a, taken_v = (st.sem(s) for s in ("staged", "made", "taken_a", "taken_v"))
        stored = st.sems("stored", U)
        ring = view(m.WS, 0, U, KD, P)
        RO = NR * D
        outs = [view(m.BB, KD * RO + s * RO, RO) if s < 4 else view(m.AF, 0, RO) for s in range(U)]
        block = st.block()
        QB = RO // 512

        @block.sync
        def _(sp):
            to = m.table_rel.rearrange("(r t p) d -> p t r d", p=P, t=NT)
            with sp.Fori(0, NT // U) as i:
                for s in range(U):
                    t = i * U + s
                    sp.wait_ge(taken_a, 2 * t + 4)
                    sp.wait_ge(taken_v, 2 * t + 4)
                    sp.dma_start(to[:, bass.ds(t, 1), :, :].rearrange("p o r d -> p (o r) d"),
                                 outs[s].rearrange("p (r d) -> p r d", r=NR)).then_inc(stored[s], 16)
            for s in range(U):
                sp.wait_ge(stored[s], 16 * (NT // U + 1))

        @block.tensor
        def _(pe):
            pe.sem_inc(made, 2 * U)
            with pe.Fori(0, NT // U) as i:
                for s in range(U):
                    t = i * U + s
                    pe.wait_ge(staged, t + 1)
                    for half, sem in ((0, taken_a), (1, taken_v)):
                        pe.wait_ge(sem, 2 * t + 2)
                        for q in range(QB // 2 * half, QB // 2 * (half + 1)):
                            for k in range(KD):
                                mm = nc.tensor.matmul(m.PS[:, q, :], ring[:, s, k, :],
                                                      w[:, k, 2 * q:2 * q + 2, :].rearrange("p r d -> p (r d)"),
                                                      start=(k == 0), stop=(k == KD - 1))
                        mm.then_inc(made, 1)

        @block.scalar
        def _(act):
            act.sem_inc(taken_a, 2)
            for s in range(U):
                act.sem_inc(stored[s], 16)
            with act.Fori(0, NT // U) as i:
                for s in range(U):
                    t = i * U + s
                    act.wait_ge(made, 2 * t + 2)
                    nc.scalar.copy(ring[:, s, :, :], m.XT[:, :, bass.ds(t * P, P)]).then_inc(staged, 1)
                    act.wait_ge(made, 2 * t + 1 + 2 * U)
                    act.wait_ge(stored[s], i * 16 + 16)
                    for q in range(2):
                        nc.scalar.copy(outs[s][:, q * 512:(q + 1) * 512], m.PS[:, q, :]).then_inc(taken_a, 1)

        @block.vector
        def _(dve):
            dve.sem_inc(taken_v, 2)
            with dve.Fori(0, NT // U) as i:
                for s in range(U):
                    t = i * U + s
                    dve.wait_ge(made, 2 * t + 2 + 2 * U)
                    dve.wait_ge(stored[s], i * 16 + 16)
                    for q in range(2, 4):
                        nc.vector.tensor_copy(outs[s][:, q * 512:(q + 1) * 512], m.PS[:, q, :]).then_inc(taken_v, 1)

    with Stage(nc) as st:
        block = st.block()

        @block.vector
        def _(dve):
            nc.vector.memset(m.AGG[:], 0.0)

    aggregate(nc, m, m.table_rel, m.rel1)
    with Stage(nc) as st:
        loaded, dstep = st.sem("loaded"), st.sem("dstep")
        bias = m.WS[:, 0:D]
        block = st.block()

        @block.sync
        def _(sp):
            sp.dma_start(bias, a["L3_gnn_bias"].unsqueeze(0).to_broadcast([P, D])).then_inc(loaded, 16)

        @block.vector
        def _(dve):
            c = Chain(dve, dstep)
            dve.wait_ge(loaded, 16)
            c.step(nc.vector.tensor_tensor(m.XN[:], m.AGG[:, :, 0:D], bias.unsqueeze(1).to_broadcast([P, NT, D]),
                                           ALU.add))
            c.step(nc.vector.scalar_tensor_tensor(m.X[:], m.XN[:], 0.0, m.X[:], ALU.max, ALU.add))


def deep_experts(nc, m, a):
    NE, HR = 6, 128
    layernorm(nc, m, m.X, m.XN)
    turn(nc, m, m.XN, m.XT)
    routed = view(m.BB, 0, 1, NP)
    with Stage(nc) as st:
        loaded, made, taken = (st.sem(s) for s in ("loaded", "made", "taken"))
        w = view(m.WS, 0, KD, HR)
        b = view(m.WS, KD * HR, 1)
        block = st.block()

        @block.sync
        def _(sp):
            sp.dma_start(w, a["L3_ffn_router_w1"].rearrange("(k p) n -> p k n", p=P)).then_inc(loaded, 16)
            sp.dma_start(b, a["L3_ffn_router_b1"]).then_inc(loaded, 16)

        @block.tensor
        def _(pe):
            pe.wait_ge(loaded, 32)
            with pe.Fori(0, NP // CH // 2) as i:
                for u in range(2):
                    n = i * 2 + u
                    pe.wait_ge(taken, n + 1)
                    for k in range(KD):
                        mm = nc.tensor.matmul(m.PS[:, u, 0:CH], w[:, k, :], m.XT[:, k, bass.ds(n * CH, CH)],
                                              start=(k == 0), stop=(k == KD - 1))
                    mm.then_inc(made, 1)

        @block.scalar
        def _(act):
            act.sem_inc(taken, 2)
            act.wait_ge(loaded, 32)
            with act.Fori(0, NP // CH // 2) as i:
                for u in range(2):
                    n = i * 2 + u
                    act.wait_ge(made, n + 1)
                    nc.scalar.activation(routed[:, 0, bass.ds(n * CH, CH)], m.PS[:, u, 0:CH], ACT.Relu, bias=b
                                         ).then_inc(taken, 1)

    gates(nc, m, a["L3_ffn_router_w2"], a["L3_ffn_router_b2"], NE, True, hidden=routed)

    with Stage(nc) as st:
        loaded, made, active, done, taken = (st.sem(s) for s in ("loaded", "made", "active", "done", "taken"))
        w = [view(m.BB, q * NE * KD * D, NE * KD, D) for q in range(3)]
        h1 = view(m.AF, 0, KD, CB)
        h2 = view(m.AF, KD * CB, KD, CB)
        b1, b2 = view(m.AF, 3000, NE, KD), view(m.AF, 3020, NE, KD)
        b3 = m.AF[0:1, 3100:3100 + NE * D]
        block = st.block()
        LAYER = KD * 2

        @block.sync
        def _(sp):
            for q in range(3):
                sp.dma_start(w[q], a[f"L3_ffn_expert_w{q + 1}"].rearrange("e (k p) n -> p (e k) n", p=P)
                             ).then_inc(loaded, 16)
            sp.dma_start(b1, a["L3_ffn_expert_b1"].rearrange("p (e k) -> p e k", k=KD)).then_inc(loaded, 16)
            sp.dma_start(b2, a["L3_ffn_expert_b2"].rearrange("p (e k) -> p e k", k=KD)).then_inc(loaded, 16)
            sp.dma_start(b3, a["L3_ffn_expert_b3"].rearrange("e d -> (e d)").unsqueeze(0)).then_inc(loaded, 16)

        @block.tensor
        def _(pe):
            te = nc.tensor
            pe.wait_ge(loaded, 96)
            with pe.Fori(0, NT // TB) as b:
                for e in range(NE):
                    for layer in range(2):
                        base = ((b * NE + e) * 2 + layer) * LAYER
                        for j in range(KD):
                            for h in range(2):
                                pe.wait_ge(active, base + j * 2 + h + 1)
                                if layer == 1 and j == 0 and h == 0:
                                    pe.wait_ge(active, base + 2)
                                for k in range(KD):
                                    src = (m.XT[:, k, bass.ds(b * CB + h * CH2, CH2)] if layer == 0
                                           else h1[:, k, h * CH2:(h + 1) * CH2])
                                    mm = te.matmul(m.PS[:, h, 0:CH2], w[layer][:, e * KD + k, j * P:(j + 1) * P], src,
                                                   start=(k == 0), stop=(k == KD - 1))
                                mm.then_inc(made, 1)
                    pe.wait_ge(active, ((b * NE + e) * 2 + 2) * LAYER + 2)
                    for s in range(TB):
                        pe.wait_ge(taken, (b * NE + e) * TB + s + 1)
                        for k in range(KD):
                            te.matmul(m.PS[:, 3 + s, 0:D], h2[:, k, s * P:(s + 1) * P], w[2][:, e * KD + k, :],
                                      start=(k == 0), stop=False)
                        te.matmul(m.PS[:, 3 + s, 0:D], m.ones[0:1, :], b3[:, e * D:(e + 1) * D], start=False,
                                  stop=True).then_inc(done, 1)

        @block.scalar
        def _(act):
            act.sem_inc(active, 2)
            act.wait_ge(loaded, 96)
            with act.Fori(0, NT // TB) as b:
                for e in range(NE):
                    for layer, (dst, bias) in enumerate(((h1, b1), (h2, b2))):
                        base = ((b * NE + e) * 2 + layer) * LAYER
                        for j in range(KD):
                            for h in range(2):
                                act.wait_ge(made, base + j * 2 + h + 1)
                                nc.scalar.activation(dst[:, j, h * CH2:(h + 1) * CH2], m.PS[:, h, 0:CH2], ACT.Relu,
                                                     bias=bias[:, e, j:j + 1]).then_inc(active, 1)

        @block.vector
        def _(dve):
            dve.sem_inc(taken, U)
            with dve.Fori(0, NT // TB) as b:
                for e in range(NE):
                    for s in range(TB):
                        t = b * TB + s
                        n = (b * NE + e) * TB + s
                        dve.wait_ge(done, n + 1)
                        dve.wait_ge(taken, n + U)
                        at = tile_at(m.X, t)
                        g = tile_at(m.gate, t, e, e + 1)
                        nc.vector.scalar_tensor_tensor(at, m.PS[:, 3 + s, 0:D], g, at, ALU.mult, ALU.add
                                                       ).then_inc(taken, 1)


def build(nc, a, out):
    with ExitStack() as ctx:
        m = setup_memory(nc, ctx)
        constants(nc, m, a["x"])
        sort_edges(nc, m, a["dst_cols"], a["dst"], a["edge_type_8_cols"], None, a["src_cols"], False)
        gin(nc, m, a)
        slice_attention(nc, m, a)
        graph_attention(nc, m, a)
        expert_pair(nc, m, a)
        sort_edges(nc, m, a["src_cols"], a["src"], None, a["edge_attr_64"], a["dst_cols"], True)
        edge_update(nc, m, a)
        one_expert(nc, m, a)
        relations(nc, m, a)
        deep_experts(nc, m, a)
        with Stage(nc) as st:
            stored = st.sem("stored")
            block = st.block()

            @block.sync
            def _(sp):
                sp.dma_start(out.rearrange("(t p) d -> p t d", p=P), m.X[:]).then_inc(stored, 16)
                sp.wait_ge(stored, 16)


EDGE_ROWS = ET * P
TURNED = ("L0_ffn_W_x", "L2_gnn_W1", "L2_gnn_W2", "L2_gnn_W_ih", "L2_gnn_W_hh", "L2_ffn_router_w", "L3_gnn_w_comp")
COLUMNS = ("L0_gnn_g0", "L0_gnn_b0", "L0_gnn_b1a", "L0_gnn_g1", "L0_gnn_bt1", "L0_gnn_b2a", "L0_gnn_g2",
           "L0_gnn_bt2", "L0_ffn_b_x", "L1_ffn_ln_g", "L1_ffn_ln_b", "L1_ffn_b1", "L2_ffn_b1", "L3_ffn_router_b1",
           "L3_ffn_expert_b1", "L3_ffn_expert_b2")


def kernel(**inputs):
    import concourse.bacc as bacc
    from concourse.bass_utils import run_bass_kernel_spmd

    def pad(a, rows, fill=0):
        return np.concatenate([a, np.full((rows - a.shape[0],) + a.shape[1:], fill, a.dtype)])

    arrays = {}
    for name, a in inputs.items():
        a = np.asarray(a)
        if name == "x":
            a = pad(a, NP)
        elif name in ("src", "dst", "edge_type_8"):
            a = pad(a, EDGE_ROWS, 0 if name == "edge_type_8" else -1)
            arrays[name + "_cols"] = np.ascontiguousarray(a.reshape(ET, P).T)
        elif name == "edge_attr_64":
            a = pad(a, EDGE_ROWS)
        elif name in TURNED:
            a = a.T
        elif name in COLUMNS:
            a = a.reshape(-1, P).T
        arrays[name] = np.ascontiguousarray(a)
    nc = bacc.Bacc("TRN2", target_bir_lowering=False, num_devices=1)
    arrays = {f"in_{k}": a for k, a in arrays.items()}
    ins = {k[3:]: nc.dram_tensor(k, a.shape, mybir.dt.from_np(a.dtype), kind="ExternalInput").ap()
           for k, a in arrays.items()}
    out = nc.dram_tensor("out", (NP, D), F32, kind="ExternalOutput").ap()
    build(nc, ins, out)
    r = run_bass_kernel_spmd(nc, [arrays], core_ids=[0])
    return r.results[0]["out"][:N]
```

```python
from contextlib import ExitStack

import numpy as np
import concourse.bass as bass
from concourse import mybir

ALU = mybir.AluOpType
ACT = mybir.ActivationFunctionType
F32 = mybir.dt.float32
BF16 = mybir.dt.bfloat16
I32 = mybir.dt.int32
U32 = mybir.dt.uint32
AX = mybir.AxisListType.X

P = 128
D = 256
KD = D // P
N = 3125
NT = -(-N // P)
NP = NT * P
E = 53125
ET = -(-E // P)
EA = 64
G = 8
Q = 4
WT = -(-(ET + NT) // (8 * Q)) * 8 * Q
WP = WT + 1
U = 5
SG = 8
AW = 264
CH = 400
CB, CH2 = 640, 320
TB = CB // P
assert TB == U
GROUPS = WT // G
ROUNDS = GROUPS // 2
QUADS = WT // Q
BLANK = next(k for k in range(WP // 8, 0, -1) if WP % k == 0)
EPS = 1e-5
BIG = 1e30
assert NT % U == 0 and GROUPS % 2 == 0 and G % 2 == 0 and ET % SG == 0 and NP % (2 * CH) == 0


class Chain:

    def __init__(self, eng, sem):
        self.eng, self.sem, self.base, self.k = eng, sem, 0, 0

    def at(self, base):
        self.base, self.k = base, 0

    def step(self, ins):
        ins.then_inc(self.sem, 1)
        self.k += 1
        self.eng.wait_ge(self.sem, self.base + self.k)


class Stage:

    number = 0

    def __init__(self, nc):
        self.nc, self.ctx, self.handles = nc, ExitStack(), []
        Stage.number += 1

    def __enter__(self):
        return self

    def sem(self, name):
        self.handles.append(self.nc.alloc_semaphore(f"{name}_{Stage.number}"))
        return self.handles[-1]

    def sems(self, name, n):
        return [self.sem(f"{name}{i}") for i in range(n)]

    def block(self):
        return self.ctx.enter_context(self.nc.Block())

    def __exit__(self, *a):
        self.ctx.close()
        self.nc.clear_and_free_semaphores(self.handles)
        self.nc.all_engine_barrier()
        return False


def view(buf, off, *shape):
    n = 1
    for s in shape:
        n *= s
    v = buf[:, off:off + n]
    if len(shape) == 2:
        v = v.rearrange("p (a b) -> p a b", b=shape[1])
    if len(shape) == 3:
        v = v.rearrange("p (a b c) -> p a b c", b=shape[1], c=shape[2])
    return v


def tile_at(buf, t, a=0, b=D):
    return buf[:, bass.ds(t, 1), a:b].rearrange("p o d -> p (o d)")


def bcast(col, shape):
    return col.unsqueeze(len(col.shape)).to_broadcast(shape)


def one_hot_rows(v, m, S, rows):
    n = S.shape[1]
    return v.tensor_tensor(S, m.iota[:].unsqueeze(1).to_broadcast([P, n, P]), bcast(rows, [P, n, P]), ALU.is_equal)


def pipeline(eng, ring, *steps):
    def turn_of(q):
        for ahead, step in steps:
            if 0 <= q + ahead < QUADS:
                step(q + ahead, (q + ahead) % ring, (q + ahead) // ring)

    for q in range(-max(ahead for ahead, _ in steps), 0):
        turn_of(q)
    with eng.Fori(0, QUADS // ring - 1) as i:
        for u in range(ring):
            for ahead, step in steps:
                step(i * ring + (u + ahead), (u + ahead) % ring, i + (u + ahead) // ring)
    for q in range(QUADS - ring, QUADS):
        turn_of(q)


def node_tiles(nc, eng, tn, g, n=G):
    return nc.values_load_multi_w_load_instructions(tn[0:1, bass.ds(g * n, n)], engines=[eng.engine], min_val=0,
                                                    max_val=NT - 1)[1]


def setup_memory(nc, ctx):
    class M:
        pass

    m = M()

    def sb(name, shape, dt=F32):
        return ctx.enter_context(nc.sbuf_tensor(name, shape, dt))

    m.X = sb("residual", [P, NT, D])
    m.XN = sb("normed", [P, NT, D])
    m.XT = sb("normed_T", [P, KD, NP])
    m.AGG = sb("sums", [P, NT, AW])
    m.BB = sb("wide", [P, 2 * NT * D])
    m.WS = sb("work", [P, 7168])
    m.PS = ctx.enter_context(nc.psum_tensor("ps", [P, 8, 512], F32))
    m.ident = sb("ident", [P, P])
    m.identb = sb("identb", [P, P], BF16)
    m.iota = sb("iota", [P, P])
    m.before = sb("before", [P, P])
    m.after = sb("after", [P, P])
    m.ones = sb("ones", [P, P])
    m.zerob = sb("zerob", [P, 160], BF16)
    m.real = sb("real", [P, NT])
    m.wiota = sb("wiota", [1, WP])
    m.coef = sb("coef", [P, KD, 2])
    m.gate = sb("gate", [P, NT, 8])
    m.lo1 = sb("lo1", [P, WP])
    m.src1 = sb("src1", [P, WP], I32)
    m.rel1 = sb("rel1", [P, WP], I32)
    m.tn1 = sb("tn1", [1, WP], I32)
    m.tn2 = sb("tn2", [1, WP], I32)
    m.B2 = m.BB[:, 0:NT * D]
    m.B3 = m.BB[:, NT * D:2 * NT * D]
    m.AF = m.AGG[:].rearrange("p t d -> p (t d)")
    m.rec1 = nc.dram_tensor("rec1", (P * WP, 4), F32).ap()
    m.rec2 = nc.dram_tensor("rec2", (P * WP, EA + 4), F32).ap()
    m.table = nc.dram_tensor("table", (NP, D), F32).ap()
    m.table_gat = nc.dram_tensor("table_gat", (NP, D + 4), F32).ap()
    m.table_max = nc.dram_tensor("table_max", (NP, 4), F32).ap()
    m.table_rel = nc.dram_tensor("table_rel", (8 * NP, D), F32).ap()
    return m


def constants(nc, m, x):
    with Stage(nc) as st:
        pool_step, filled, loaded = st.sem("pool_step"), st.sem("filled"), st.sem("loaded")
        block = st.block()

        @block.sync
        def _(sp):
            sp.dma_start(m.X[:], x.rearrange("(t p) d -> p t d", p=P)).then_inc(loaded, 16)
            sp.wait_ge(loaded, 16)

        @block.gpsimd
        def _(pool):
            c = Chain(pool, pool_step)
            g = nc.gpsimd
            c.step(g.memset(m.ones[:], 1.0))
            c.step(g.iota(m.iota[:], [[1, P]], base=0, channel_multiplier=0,
                          allow_small_or_imprecise_dtypes=True))
            c.step(g.iota(m.wiota[:], [[1, WP]], base=0, channel_multiplier=0,
                          allow_small_or_imprecise_dtypes=True))
            for out, op, sign in ((m.ident, ALU.is_equal, 1), (m.before, ALU.is_gt, 1), (m.after, ALU.is_gt, -1)):
                c.step(g.affine_select(out=out[:], in_=m.ones[:], compare_op=op, fill=0.0, base=0,
                                       pattern=[[-sign, P]], channel_multiplier=sign))
            c.step(g.affine_select(out=m.real[:], in_=m.ones[:, 0:NT], compare_op=ALU.is_ge, fill=0.0,
                                   base=N - 1, pattern=[[-P, NT]], channel_multiplier=-1))

        @block.vector
        def _(dve):
            dve.wait_ge(pool_step, 4)
            nc.vector.tensor_copy(m.identb[:], m.ident[:]).then_inc(filled, 1)
            nc.vector.memset(m.zerob[:], 0.0).then_inc(filled, 1)


def sort_edges(nc, m, keys, keys_row, etype, attr, other, by_source):
    W = EA + 4 if by_source else 4
    rec = m.rec2 if by_source else m.rec1
    tn = m.tn2 if by_source else m.tn1
    GROUPS = ET // SG
    ROUNDS = GROUPS // 2
    assert GROUPS % 2 == 0
    o = 0

    def take(n, *shape):
        nonlocal o
        v = view(m.BB, o, *(shape or (n,)))
        o += n
        return v

    keyi = take(ET).bitcast(I32)
    lo_i = take(ET).bitcast(I32)
    hi_i = take(ET).bitcast(I32)
    key = take(ET)
    lo = take(ET)
    hi = take(ET)
    trash = take(ET)
    othf = take(ET)
    ty_i = take(ET).bitcast(I32)
    pay = take(ET * 4, ET, 4)
    back = take(WP * 4, WP, 4)
    counts = take(32)
    base = take(32)
    first = take(NT)
    tiles_i = take(NT).bitcast(I32)
    tiles = take(NT)
    tnf = take(WP)
    blank = view(m.AF, 0, BLANK * W) if by_source else view(m.AF, 0, WP * 4)
    blank3 = blank.rearrange("p (a b) -> p a b", b=W)
    rank = take(2 * SG, 2, SG)
    slot, slot_f, hi_f = take(SG), take(SG), take(SG)
    slot_i, hi_s = take(SG).bitcast(I32), take(SG).bitcast(I32)
    idxr = take(2 * SG, 2, SG).bitcast(I32)
    prod = take(SG * NT, SG, NT)
    snap = take(2 * SG * NT, 2, SG, NT)
    rowk = view(m.WS, 0, 2, SG * P).bitcast(I32)
    eqs = view(m.WS, 2 * SG * P, SG, P)
    payr = view(m.WS, 3 * SG * P, 2 * SG, EA + 4)
    fl = m.XN[:].rearrange("p t d -> p (t d)")
    ol = fl[:, 0:SG * P].bitcast(BF16).rearrange("p (u s e) -> p u s e", u=2, s=SG)
    oh = fl[:, 1024:1024 + SG * NT].bitcast(BF16).rearrange("p (u s e) -> p u s e", u=2, s=SG)
    olt = view(fl, 2048, 2, SG, P)

    def one_hots(v, g, u):
        v.tensor_tensor(ol[:, u], m.iota[:].unsqueeze(1).to_broadcast([P, SG, P]),
                        bcast(lo[:, bass.ds(g * SG, SG)], [P, SG, P]), ALU.is_equal)
        return v.tensor_tensor(oh[:, u], m.iota[:, 0:NT].unsqueeze(1).to_broadcast([P, SG, NT]),
                               bcast(hi[:, bass.ds(g * SG, SG)], [P, SG, NT]), ALU.is_equal)

    with Stage(nc) as st:
        loaded, blanked, stored = st.sem("loaded"), st.sem("blanked"), st.sem("stored")
        dstep, hot, used, counted = st.sem("dstep"), st.sem("hot"), st.sem("used"), st.sem("counted")
        tstep, sums, prefix = st.sem("tstep"), st.sem("sums"), st.sem("prefix")
        block = st.block()

        @block.sync
        def _(sp):
            sp.dma_start(keyi, keys).then_inc(loaded, 16)
            sp.dma_start(othf.bitcast(I32), other).then_inc(loaded, 16)
            if not by_source:
                sp.dma_start(ty_i, etype).then_inc(loaded, 16)
            sp.wait_ge(blanked, 2)
            r = rec.rearrange("(p w) c -> p (w c)", p=P)
            n = blank3.shape[1] * W
            for k in range(WP * W // n):
                sp.dma_start(r[:, k * n:(k + 1) * n], blank).then_inc(stored, 16)
            sp.wait_ge(stored, 16 * (WP * W // n))

        @block.gpsimd
        def _(pool):
            nc.gpsimd.memset(payr[:, :, EA:EA + 4], 0.0)
            nc.gpsimd.memset(blank, 0.0).then_inc(blanked, 1)
            pool.wait_ge(blanked, 1)
            col = EA + 1 if by_source else 1
            nc.gpsimd.memset(blank3[:, :, col:col + 1], -1.0).then_inc(blanked, 1)

        @block.vector
        def _(dve):
            v = nc.vector
            c = Chain(dve, dstep)
            dve.wait_ge(loaded, 32 if by_source else 48)
            c.step(v.tensor_scalar(hi_i, keyi, 7, None, ALU.arith_shift_right))
            c.step(v.tensor_scalar(lo_i, keyi, 127, None, ALU.bitwise_and))
            c.step(v.tensor_copy(key, keyi))
            c.step(v.tensor_copy(lo, lo_i))
            c.step(v.tensor_copy(hi, hi_i))
            c.step(v.tensor_scalar(trash, key, 0.0, float(WT * P), ALU.is_lt, ALU.mult))
            c.step(v.tensor_copy(othf, othf.bitcast(I32)))
            if not by_source:
                c.step(v.tensor_copy(pay[:, :, 0], othf))
                c.step(v.tensor_copy(pay[:, :, 1], lo))
                c.step(v.tensor_copy(pay[:, :, 3], ty_i))
                c.step(v.scalar_tensor_tensor(pay[:, :, 2], pay[:, :, 3], float(NP), othf, ALU.mult, ALU.add))
            with dve.Fori(0, ROUNDS) as i:
                for u in range(2):
                    dve.wait_ge(used, i * 2 + u + 1)
                    one_hots(v, i * 2 + u, u).then_inc(hot, 1)
            dve.wait_ge(counted, 1)
            v.tensor_copy(counts[:, 0:NT], m.PS[:, 0, 0:NT]).then_inc(sums, 1)
            dve.wait_ge(prefix, 1)
            c2 = Chain(dve, tstep)
            c2.step(v.tensor_scalar(tiles, m.PS[:, 1, 0:NT], float(P - 1), None, ALU.add))
            c2.step(v.tensor_copy(tiles_i, tiles))
            c2.step(v.tensor_scalar(tiles_i, tiles_i, 7, None, ALU.arith_shift_right))
            c2.step(v.tensor_copy(tiles, tiles_i))
            c2.step(v.tensor_tensor_scan(first, m.ones[:, 0:NT], tiles, 0.0, ALU.mult, ALU.add))
            c2.step(v.tensor_tensor(first, first, tiles, ALU.subtract))
            c2.step(v.scalar_tensor_tensor(base[:, 0:NT], first, float(P), m.PS[:, 2, 0:NT],
                                           ALU.mult, ALU.add))
            c2.step(v.tensor_scalar(tnf[0:1, :], m.wiota[:], first[0:1, 1:2], None, ALU.is_ge))
            for j in range(2, NT):
                c2.step(v.scalar_tensor_tensor(tnf[0:1, :], m.wiota[:], first[0:1, j:j + 1], tnf[0:1, :],
                                               ALU.is_ge, ALU.add))
            c2.step(v.tensor_copy(tn[:], tnf[0:1, :]))

        @block.tensor
        def _(pe):
            pe.sem_inc(used, 2)
            nc.tensor.matmul(m.PS[:, 0, 0:NT], m.zerob[:, 0:P], m.zerob[:, 0:NT], start=True, stop=False,
                             skip_group_check=True)
            with pe.Fori(0, ROUNDS) as i:
                for u in range(2):
                    pe.wait_ge(hot, i * 2 + u + 1)
                    for s in range(SG):
                        mm = nc.tensor.matmul(m.PS[:, 0, 0:NT], ol[:, u, s], oh[:, u, s], start=False, stop=False,
                                              skip_group_check=True)
                    mm.then_inc(used, 1)
            nc.tensor.matmul(m.PS[:, 0, 0:NT], m.zerob[:, 0:P], m.zerob[:, 0:NT], start=False, stop=True,
                             skip_group_check=True).then_inc(counted, 1)
            pe.wait_ge(sums, 1)
            nc.tensor.matmul(m.PS[:, 1, 0:NT], m.ones[:], counts[:, 0:NT], start=True, stop=True)
            nc.tensor.matmul(m.PS[:, 2, 0:NT], m.after[:], counts[:, 0:NT], start=True,
                             stop=True).then_inc(prefix, 1)

    with Stage(nc) as st:
        names = ("rows_used", "hot", "turned", "olt_ready", "prefixed", "snapped", "picked", "taken", "dstep",
                 "ready", "drained", "issue", "carried")
        (rows_used, hot, turned, olt_ready, prefixed, snapped, picked, taken, dstep, ready, drained, issue,
         carried) = (st.sem(s) for s in names)
        rows, arrived, sent = st.sems("rows", 2), st.sems("arrived", 2), st.sems("sent", 2 * SG)
        block = st.block()

        @block.sync
        def _(sp):
            kr = keys_row.rearrange("(i e) -> i e", e=SG * P)
            at = attr.rearrange("(t p) c -> p t c", p=P) if by_source else None

            def keys_in(g, u):
                sp.wait_ge(rows_used, g + 1)
                sp.dma_start(rowk[:, u, :], kr[bass.ds(g, 1), :].to_broadcast([P, SG * P])).then_inc(rows[u], 16)

            def attributes_in(g, u):
                if by_source:
                    sp.dma_start(payr[:, u * SG:(u + 1) * SG, 0:EA], at[:, bass.ds(g * SG, SG), :]
                                 ).then_inc(arrived[u], 16)

            sp.sem_inc(drained, 2)
            for g in range(2):
                keys_in(g, g)
                attributes_in(g, g)
            with sp.Fori(1, ROUNDS) as i:
                for u in range(2):
                    keys_in(i * 2 + u, u)
                    for s in range(SG):
                        sp.wait_ge(sent[u * SG + s], i * 16)
                    sp.sem_inc(drained, 1)
                    attributes_in(i * 2 + u, u)
            for s in range(2 * SG):
                sp.wait_ge(sent[s], ROUNDS * 16)

        @block.vector
        def _(dve):
            v = nc.vector
            c = Chain(dve, dstep)
            STEPS = 11
            dve.sem_inc(rows_used, 2)

            def front(g, u):
                one_hots(v, g, u).then_inc(hot, 1)

            def counts_so_far(g, u):
                dve.wait_ge(prefixed, g + 1)
                dve.wait_ge(carried, g + 2)
                v.tensor_tensor(snap[:, u], m.PS[:, u, 0:SG * NT].rearrange("p (s e) -> p s e", s=SG),
                                base[:, 0:NT].unsqueeze(1).to_broadcast([P, SG, NT]), ALU.add).then_inc(snapped, 1)
                dve.wait_ge(snapped, g + 1)
                v.tensor_tensor(base[:, 0:NT], base[:, 0:NT], m.PS[:, u, SG * NT:(SG + 1) * NT], ALU.add
                                ).then_inc(carried, 1)

            def ranks(i, g, u):
                dve.wait_ge(rows[u], i * 16 + 16)
                for s in range(SG):
                    ins = v.scalar_tensor_tensor(eqs[:, s], rowk[:, u, s * P:(s + 1) * P], key[:, bass.ds(g * SG + s, 1)],
                                                 m.before[:], ALU.is_equal, ALU.mult, accum_out=rank[:, u, s:s + 1])
                c.at(g * STEPS)
                c.step(ins)
                dve.sem_inc(rows_used, 1)

            def place(g, u):
                group = bass.ds(g * SG, SG)
                dve.wait_ge(picked, g + 3)
                c.step(v.tensor_tensor(prod, m.PS[:, 4 + u, 0:SG * NT].rearrange("p (s e) -> p s e", s=SG), oh[:, u],
                                       ALU.mult))
                dve.sem_inc(taken, 1)
                c.step(v.reduce_sum(slot, prod, AX))
                c.step(v.tensor_tensor(slot, slot, rank[:, u], ALU.add))
                c.step(v.tensor_tensor(slot, slot, trash[:, group], ALU.add))
                c.step(v.tensor_copy(slot_i, slot))
                c.step(v.tensor_scalar(hi_s, slot_i, 7, None, ALU.arith_shift_right))
                c.step(v.tensor_copy(hi_f, hi_s))
                c.step(v.scalar_tensor_tensor(slot_f, hi_f, -float(P), slot, ALU.mult, ALU.add))
                c.step(v.scalar_tensor_tensor(slot_f, slot_f, float(WP), hi_f, ALU.mult, ALU.add))
                dve.wait_ge(drained, g + 1)
                if by_source:
                    v.tensor_copy(payr[:, u * SG:(u + 1) * SG, EA], othf[:, group])
                    v.tensor_copy(payr[:, u * SG:(u + 1) * SG, EA + 1], lo[:, group])
                else:
                    v.tensor_copy(payr[:, u * SG:(u + 1) * SG, 0:4], pay[:, group, :])
                c.step(v.tensor_copy(idxr[:, u, :], slot_f))
                assert c.k == STEPS
                dve.sem_inc(ready, 1)

            def two_groups(i, last=False):
                for u in range(2):
                    g = i * 2 + u
                    more = not (last and u == 1)
                    if more:
                        front(g + 1, 1 - u)
                    ranks(i, g, u)
                    if more:
                        counts_so_far(g + 1, 1 - u)
                    place(g, u)

            dve.sem_inc(carried, 2)
            dve.sem_inc(taken, 2)
            front(0, 0)
            counts_so_far(0, 0)
            with dve.Fori(0, ROUNDS - 1) as i:
                two_groups(i)
            two_groups(ROUNDS - 1, last=True)

        @block.scalar
        def _(act):
            with act.Fori(0, ROUNDS) as i:
                for u in range(2):
                    g = i * 2 + u
                    act.wait_ge(turned, g + 1)
                    act.wait_ge(picked, g + 1)
                    nc.scalar.copy(olt[:, u].rearrange("p s e -> p (s e)"), m.PS[:, 2 + u, :].bitcast(BF16)
                                   ).then_inc(olt_ready, 1)

        @block.tensor
        def _(pe):
            te = nc.tensor
            pe.sem_inc(picked, 2)

            def counts_before(g, u):
                pe.wait_ge(hot, g + 1)
                pe.wait_ge(carried, g + 1)
                te.matmul(m.PS[:, u, 0:(SG + 1) * NT], m.zerob[:, 0:P],
                          m.zerob[:, 0:NT].unsqueeze(1).to_broadcast([P, SG + 1, NT]), start=True, stop=False,
                          skip_group_check=True)
                for s in range(SG):
                    mm = te.matmul(m.PS[:, u, (s + 1) * NT:(SG + 1) * NT], ol[:, u, s],
                                   oh[:, u, s].unsqueeze(1).to_broadcast([P, SG - s, NT]), start=False,
                                   stop=(s == SG - 1), skip_group_check=True)
                mm.then_inc(prefixed, 1)
                for s in range(SG):
                    mm = te.transpose(m.PS[:, 2 + u, s * P // 2:(s + 1) * P // 2].bitcast(BF16), ol[:, u, s],
                                      m.identb[:])
                mm.then_inc(turned, 1)

            def read_counts(g, u):
                pe.wait_ge(olt_ready, g + 1)
                pe.wait_ge(snapped, g + 1)
                pe.wait_ge(taken, g + 1)
                for s in range(SG):
                    mm = te.matmul(m.PS[:, 4 + u, s * NT:(s + 1) * NT], olt[:, u, s], snap[:, u, s], start=True,
                                   stop=True)
                mm.then_inc(picked, 1)

            counts_before(0, 0)
            with pe.Fori(0, ROUNDS - 1) as i:
                for u in range(2):
                    counts_before(i * 2 + u + 1, 1 - u)
                    read_counts(i * 2 + u, u)
            counts_before(GROUPS - 1, 1)
            read_counts(GROUPS - 2, 0)
            read_counts(GROUPS - 1, 1)

        @block.gpsimd
        def _(pool):
            with pool.Fori(0, ROUNDS) as i:
                for u in range(2):
                    pool.wait_ge(ready, i * 2 + u + 1)
                    if by_source:
                        pool.wait_ge(arrived[u], i * 16 + 16)
                    pool.sem_inc(issue, 1)
                    for s in range(SG):
                        nc.gpsimd.indirect_dma_start(rec, bass.IndirectOffsetOnAxis(ap=idxr[:, u, s:s + 1], axis=0),
                                                     payr[:, u * SG + s, 0:W], None).then_inc(sent[u * SG + s], 16)

    if by_source:
        return
    with Stage(nc) as st:
        loaded, split = st.sem("loaded"), st.sem("split")
        block = st.block()

        @block.sync
        def _(sp):
            sp.dma_start(back, rec.rearrange("(p w) c -> p w c", p=P)).then_inc(loaded, 16)

        @block.vector
        def _(dve):
            dve.wait_ge(loaded, 16)
            nc.vector.tensor_copy(m.src1[:], back[:, :, 0])
            nc.vector.tensor_copy(m.lo1[:], back[:, :, 1])
            nc.vector.tensor_copy(m.rel1[:], back[:, :, 2])


def layernorm(nc, m, src, dst):
    with Stage(nc) as st:
        dstep, centred, squared, vared, rooted = (st.sem(s) for s in ("dstep", "centred", "squared", "vared", "rooted"))
        mean, var, rstd = (view(m.WS, k * 32, 32)[:, 0:NT] for k in range(3))
        sq = view(m.BB, 0, NT, D)
        block = st.block()

        @block.vector
        def _(dve):
            v, c = nc.vector, Chain(dve, dstep)
            c.step(v.reduce_sum(mean, src[:], AX))
            c.step(v.tensor_scalar(mean, mean, 1.0 / D, None, ALU.mult))
            v.tensor_tensor(dst[:], src[:], bcast(mean, [P, NT, D]), ALU.subtract).then_inc(centred, 1)
            dve.wait_ge(squared, 1)
            c.step(v.reduce_sum(var, sq, AX))
            v.tensor_scalar(var, var, 1.0 / D, EPS, ALU.mult, ALU.add).then_inc(vared, 1)
            dve.wait_ge(rooted, 1)
            c.step(v.reciprocal(rstd, rstd))
            dve.wait_ge(centred, 1)
            c.step(v.tensor_tensor(dst[:], dst[:], bcast(rstd, [P, NT, D]), ALU.mult))

        @block.scalar
        def _(act):
            act.wait_ge(centred, 1)
            nc.scalar.activation(sq, dst[:], ACT.Square).then_inc(squared, 1)
            act.wait_ge(vared, 1)
            nc.scalar.activation(rstd, var, ACT.Sqrt).then_inc(rooted, 1)


def turn(nc, m, src, dst, affine=None):
    with Stage(nc) as st:
        staged, turned, ps_used = (st.sem(s) for s in ("staged", "turned", "ps_used"))
        ring = view(m.WS, 0, U, D)
        block = st.block()

        @block.scalar
        def _(act):
            with act.Fori(0, NT // U) as i:
                for s in range(U):
                    t = i * U + s
                    act.wait_ge(turned, t + 1)
                    nc.scalar.copy(ring[:, s, :], tile_at(src, t)).then_inc(staged, 1)

        @block.tensor
        def _(pe):
            pe.sem_inc(turned, U)
            with pe.Fori(0, NT // U) as i:
                for s in range(U):
                    t = i * U + s
                    pe.wait_ge(staged, t + 1)
                    pe.wait_ge(ps_used, t + 1)
                    for k in range(KD):
                        mm = nc.tensor.transpose(m.PS[:, s, k * P:(k + 1) * P], ring[:, s, k * P:(k + 1) * P],
                                                 m.ident[:])
                    mm.then_inc(turned, 1)

        @block.vector
        def _(dve):
            dve.sem_inc(ps_used, U)
            with dve.Fori(0, NT // U) as i:
                for s in range(U):
                    t = i * U + s
                    dve.wait_ge(turned, t + 1 + U)
                    nc.vector.tensor_copy(dst[:, :, bass.ds(t * P, P)],
                                          m.PS[:, s, 0:D].rearrange("p (k n) -> p k n", k=KD)).then_inc(ps_used, 1)


def aggregate(nc, m, table, index):
    with Stage(nc) as st:
        indexed, hot, summed, added, issue = (st.sem(s) for s in ("indexed", "hot", "summed", "added", "issue"))
        gathered = st.sems("gathered", 2 * G)
        rows = view(m.WS, 0, 2 * G, D)
        S = view(m.WS, 2 * G * D, 2 * G, P)
        idx = view(m.WS, 2 * G * D + 2 * G * P, 2 * G).bitcast(I32)
        PAIRS = G // 2
        block = st.block()

        def bank(u, s):
            return m.PS[:, u * PAIRS + s // 2, s % 2 * D:(s % 2 + 1) * D]

        @block.scalar
        def _(act):
            with act.Fori(0, ROUNDS) as i:
                for u in range(2):
                    g = i * 2 + u
                    act.wait_ge(summed, (g + 1) * PAIRS)
                    nc.scalar.copy(idx[:, u * G:(u + 1) * G], index[:, bass.ds(g * G, G)]).then_inc(indexed, 1)

        @block.gpsimd
        def _(pool):
            with pool.Fori(0, ROUNDS) as i:
                for u in range(2):
                    pool.wait_ge(indexed, i * 2 + u + 1)
                    pool.sem_inc(issue, 1)
                    for q in range(u * G, (u + 1) * G):
                        nc.gpsimd.indirect_dma_start(rows[:, q, :], None, table,
                                                     bass.IndirectOffsetOnAxis(ap=idx[:, q:q + 1], axis=0)
                                                     ).then_inc(gathered[q], 16)

        @block.tensor
        def _(pe):
            pe.sem_inc(summed, 2 * PAIRS)
            with pe.Fori(0, ROUNDS) as i:
                for u in range(2):
                    g = i * 2 + u
                    pe.wait_ge(hot, g + 1)
                    for s in range(G):
                        q = u * G + s
                        if s % 2 == 0:
                            pe.wait_ge(added, g * G + s + 2)
                        pe.wait_ge(gathered[q], i * 16 + 16)
                        mm = nc.tensor.matmul(bank(u, s), S[:, q, :], rows[:, q, :], start=True, stop=True)
                        if s % 2 == 1:
                            mm.then_inc(summed, 1)

        @block.vector
        def _(dve):
            v = nc.vector
            dve.sem_inc(added, 2 * G)

            def hots(g, u):
                dve.wait_ge(summed, (g + 1) * PAIRS)
                one_hot_rows(v, m, S[:, u * G:(u + 1) * G, :], m.lo1[:, bass.ds(g * G, G)]).then_inc(hot, 1)

            def add(g, u):
                tiles = node_tiles(nc, dve, m.tn1, g)
                for s in range(G):
                    if s % 2 == 0:
                        dve.wait_ge(summed, 2 * PAIRS + g * PAIRS + s // 2 + 1)
                    dve.wait_ge(added, 2 * G + g * G + s)
                    at = tile_at(m.AGG, tiles[s])
                    v.tensor_tensor(at, at, bank(u, s), ALU.add).then_inc(added, 1)

            hots(0, 0)
            with dve.Fori(0, ROUNDS - 1) as i:
                for u in range(2):
                    hots(i * 2 + u + 1, 1 - u)
                    add(i * 2 + u, u)
            hots(GROUPS - 1, 1)
            add(GROUPS - 2, 0)
            add(GROUPS - 1, 1)


def store_table(nc, m, src, table, sums=None):
    with Stage(nc) as st:
        stored = st.sem("stored")
        block = st.block()

        @block.sync
        def _(sp):
            sp.dma_start(table.rearrange("(t p) d -> p t d", p=P), src[:]).then_inc(stored, 16)
            sp.wait_ge(stored, 16)

        @block.vector
        def _(dve):
            if sums is None:
                nc.vector.tensor_copy(m.AGG[:, :, 0:D], src[:])
            else:
                nc.vector.memset(m.AGG[:], sums)


def free2(eng, sem, s, t):
    eng.wait_ge(sem, t + 2 if s == 0 else t + 1)


def linear_nodes(nc, m, srcT, weight, bias, width, finish):
    with Stage(nc) as st:
        loaded, staged, made, taken, fstep = (st.sem(s) for s in ("loaded", "staged", "made", "taken", "fstep"))
        ring = view(m.WS, 0, U, KD, P)
        w = view(m.WS, U * D, KD, width)
        b = m.WS[0:1, U * D + KD * width:U * D + KD * width + width]
        block = st.block()

        @block.sync
        def _(sp):
            sp.dma_start(w, weight.rearrange("(k p) n -> p k n", p=P)).then_inc(loaded, 16)
            if bias is not None:
                sp.dma_start(b, bias.unsqueeze(0)).then_inc(loaded, 16)

        @block.scalar
        def _(act):
            with act.Fori(0, NT // U) as i:
                for s in range(U):
                    t = i * U + s
                    act.wait_ge(made, t + 1)
                    nc.scalar.copy(ring[:, s, :, :], srcT[:, :, bass.ds(t * P, P)]).then_inc(staged, 1)

        @block.tensor
        def _(pe):
            pe.sem_inc(made, U)
            pe.wait_ge(loaded, 32 if bias is not None else 16)
            with pe.Fori(0, NT // U) as i:
                for s in range(U):
                    t = i * U + s
                    pe.wait_ge(staged, t + 1)
                    pe.wait_ge(taken, t + 1)
                    for k in range(KD):
                        mm = nc.tensor.matmul(m.PS[:, s, 0:width], ring[:, s, k, :], w[:, k, :], start=(k == 0),
                                              stop=(bias is None and k == KD - 1))
                    if bias is not None:
                        mm = nc.tensor.matmul(m.PS[:, s, 0:width], m.ones[0:1, :], b, start=False, stop=True)
                    mm.then_inc(made, 1)

        @block.vector
        def _(dve):
            dve.sem_inc(taken, U)
            c = Chain(dve, fstep)
            with dve.Fori(0, NT // U) as i:
                for s in range(U):
                    t = i * U + s
                    dve.wait_ge(made, t + 1 + U)
                    c.at(t * finish.steps)
                    finish(dve, c, t, m.PS[:, s, 0:width]).then_inc(taken, 1)


class Finish:

    def __init__(self, fn, steps=0):
        self.fn, self.steps = fn, steps

    def __call__(self, *a):
        return self.fn(*a)



def batch_stats(nc, m, zT, gamma, beta):
    with Stage(nc) as st:
        loaded, dstep, vared, rooted = (st.sem(s) for s in ("loaded", "dstep", "vared", "rooted"))
        cuts = [(a, min(a + 512, N)) for a in range(0, N, 512)]
        stats = view(m.WS, 0, KD, 6 * len(cuts))
        mv = view(m.WS, 200, KD, 2)
        gb = view(m.WS, 210, 2, KD)
        std = view(m.WS, 220, KD)
        block = st.block()

        @block.sync
        def _(sp):
            sp.dma_start(gb[:, 0, :], gamma).then_inc(loaded, 16)
            sp.dma_start(gb[:, 1, :], beta).then_inc(loaded, 16)

        @block.vector
        def _(dve):
            v, c = nc.vector, Chain(dve, dstep)
            for k in range(KD):
                for j, (a, b) in enumerate(cuts):
                    ins = v.bn_stats(stats[:, k, 6 * j:6 * j + 6], zT[:, k, a:b])
            c.step(ins)
            for k in range(KD):
                ins = v.bn_aggr(mv[:, k, :], stats[:, k, :])
            c.step(ins)
            v.tensor_scalar(std, mv[:, :, 1], EPS, None, ALU.add).then_inc(vared, 1)
            dve.wait_ge(rooted, 1)
            c.step(v.reciprocal(std, std))
            dve.wait_ge(loaded, 32)
            c.step(v.tensor_tensor(m.coef[:, :, 0], std, gb[:, 0, :], ALU.mult))
            c.step(v.tensor_tensor(std, mv[:, :, 0], m.coef[:, :, 0], ALU.mult))
            c.step(v.tensor_tensor(m.coef[:, :, 1], gb[:, 1, :], std, ALU.subtract))

        @block.scalar
        def _(act):
            act.wait_ge(vared, 1)
            nc.scalar.activation(std, std, ACT.Sqrt).then_inc(rooted, 1)


def normalise_nodes(nc, m, zT, dst):
    with Stage(nc) as st:
        scaled, turned, taken = (st.sem(s) for s in ("scaled", "turned", "taken"))
        ring = view(m.WS, 0, U, KD, P)
        block = st.block()

        @block.scalar
        def _(act):
            with act.Fori(0, NT // U) as i:
                for s in range(U):
                    t = i * U + s
                    act.wait_ge(turned, t + 1)
                    for k in range(KD):
                        ins = nc.scalar.activation(ring[:, s, k, :], zT[:, k, bass.ds(t * P, P)], ACT.Identity,
                                                   bias=m.coef[:, k, 1:2], scale=m.coef[:, k, 0:1])
                    ins.then_inc(scaled, 1)

        @block.tensor
        def _(pe):
            pe.sem_inc(turned, U)
            with pe.Fori(0, NT // U) as i:
                for s in range(U):
                    t = i * U + s
                    pe.wait_ge(scaled, t + 1)
                    pe.wait_ge(taken, t + 1)
                    for k in range(KD):
                        mm = nc.tensor.transpose(m.PS[:, s, k * P:(k + 1) * P], ring[:, s, k, :], m.ident[:])
                    mm.then_inc(turned, 1)

        @block.vector
        def _(dve):
            dve.sem_inc(taken, U)
            with dve.Fori(0, NT // U) as i:
                for s in range(U):
                    t = i * U + s
                    dve.wait_ge(turned, t + 1 + U)
                    nc.vector.tensor_copy(tile_at(dst, t), m.PS[:, s, 0:D]).then_inc(taken, 1)


def linear_features(nc, m, srcT, weight, bias, dstT):
    with Stage(nc) as st:
        loaded, made, taken = (st.sem(s) for s in ("loaded", "made", "taken"))
        w = view(m.WS, 0, KD, D)
        b = view(m.WS, KD * D, KD)
        block = st.block()

        @block.sync
        def _(sp):
            sp.dma_start(w, weight.rearrange("(k p) n -> p k n", p=P)).then_inc(loaded, 16)
            sp.dma_start(b, bias).then_inc(loaded, 16)

        @block.tensor
        def _(pe):
            pe.wait_ge(loaded, 32)
            with pe.Fori(0, NP // CH // 2) as i:
                for u in range(2):
                    for j in range(KD):
                        n = (i * 2 + u) * KD + j
                        pe.wait_ge(taken, n + 1)
                        for k in range(KD):
                            mm = nc.tensor.matmul(m.PS[:, u * KD + j, 0:CH], w[:, k, j * P:(j + 1) * P],
                                                  srcT[:, k, bass.ds((i * 2 + u) * CH, CH)], start=(k == 0),
                                                  stop=(k == KD - 1))
                        mm.then_inc(made, 1)

        @block.scalar
        def _(act):
            act.sem_inc(taken, 2 * KD)
            act.wait_ge(loaded, 32)
            with act.Fori(0, NP // CH // 2) as i:
                for u in range(2):
                    for j in range(KD):
                        n = (i * 2 + u) * KD + j
                        act.wait_ge(made, n + 1)
                        nc.scalar.activation(dstT[:, j, bass.ds((i * 2 + u) * CH, CH)], m.PS[:, u * KD + j, 0:CH],
                                             ACT.Identity, bias=b[:, j:j + 1]).then_inc(taken, 1)


def gin_output(nc, m, zT, weight, bias, into_residual):
    with Stage(nc) as st:
        loaded, scaled, made, taken = (st.sem(s) for s in ("loaded", "scaled", "made", "taken"))
        ring = view(m.WS, 0, U, KD, P)
        w = view(m.WS, U * D, KD, D)
        b = m.WS[0:1, U * D + KD * D:U * D + KD * D + D]
        block = st.block()

        @block.sync
        def _(sp):
            sp.dma_start(w, weight.rearrange("(k p) n -> p k n", p=P)).then_inc(loaded, 16)
            sp.dma_start(b, bias.unsqueeze(0)).then_inc(loaded, 16)

        @block.scalar
        def _(act):
            with act.Fori(0, NT // U) as i:
                for s in range(U):
                    t = i * U + s
                    act.wait_ge(made, t + 1)
                    for k in range(KD):
                        ins = nc.scalar.activation(ring[:, s, k, :], zT[:, k, bass.ds(t * P, P)], ACT.Relu,
                                                   bias=m.coef[:, k, 1:2], scale=m.coef[:, k, 0:1])
                    ins.then_inc(scaled, 1)

        @block.tensor
        def _(pe):
            pe.sem_inc(made, U)
            pe.wait_ge(loaded, 32)
            with pe.Fori(0, NT // U) as i:
                for s in range(U):
                    t = i * U + s
                    pe.wait_ge(scaled, t + 1)
                    pe.wait_ge(taken, t + 1)
                    for k in range(KD):
                        nc.tensor.matmul(m.PS[:, s, 0:D], ring[:, s, k, :], w[:, k, :], start=(k == 0), stop=False)
                    nc.tensor.matmul(m.PS[:, s, 0:D], m.ones[0:1, :], b, start=False, stop=True).then_inc(made, 1)

        @block.vector
        def _(dve):
            dve.sem_inc(taken, U)
            with dve.Fori(0, NT // U) as i:
                for s in range(U):
                    t = i * U + s
                    dve.wait_ge(made, t + 1 + U)
                    if into_residual:
                        at = tile_at(m.X, t)
                        ins = nc.vector.scalar_tensor_tensor(at, m.PS[:, s, 0:D], 0.0, at, ALU.max, ALU.add)
                    else:
                        ins = nc.vector.tensor_scalar(tile_at(m.XN, t), m.PS[:, s, 0:D], 0.0, None, ALU.max)
                    ins.then_inc(taken, 1)


def gin(nc, m, a):
    zT = view(m.BB, 0, KD, NP)
    layernorm(nc, m, m.X, m.XN)
    turn(nc, m, m.XN, m.XT)
    batch_stats(nc, m, m.XT, a["L0_gnn_g0"], a["L0_gnn_b0"])
    normalise_nodes(nc, m, m.XT, m.XN)
    for conv, last in (("1", False), ("2", True)):
        store_table(nc, m, m.XN, m.table)
        aggregate(nc, m, m.table, m.src1)
        turn(nc, m, m.AGG, m.XT)
        linear_features(nc, m, m.XT, a[f"L0_gnn_W{conv}a"], a[f"L0_gnn_b{conv}a"], zT)
        batch_stats(nc, m, zT, a[f"L0_gnn_g{conv}"], a[f"L0_gnn_bt{conv}"])
        gin_output(nc, m, zT, a[f"L0_gnn_W{conv}b"], a[f"L0_gnn_b{conv}b"], last)


def slice_attention(nc, m, a):
    H, C, QG = 8, 64, 64
    PR = H // 2
    HW = H * QG
    layernorm(nc, m, m.X, m.XN)
    turn(nc, m, m.XN, m.XT)
    weights = view(m.BB, 0, NT, HW)
    o = 0

    def take(*shape):
        nonlocal o
        v = view(m.AF, o, *shape)
        n = 1
        for k in shape:
            n *= k
        o += n
        return v

    w_fx, w_xs = take(KD, HW), take(KD, HW)
    w_xT, w_out, w_mix = take(PR, D), take(PR, D), take(PR, D)
    w_sl = take(P)
    b_fx, b_xs = take(HW), take(HW)
    xn = m.XN[:].rearrange("p t d -> p (t d)")
    w_q, w_k, w_v = (xn[:, k * P:(k + 1) * P] for k in range(3))
    b_x = xn[:, 384:384 + PR]
    temp = xn[:, 400:408]
    b_sl = xn[:, 416:480]
    b_out = xn[:, 512:768]
    tok, tokT, qT, kT, vv, att, attT, oT = (view(xn, 1024 + 512 * k, PR, P) for k in range(8))
    small = view(xn, 5200, 8, 8)

    with Stage(nc) as st:
        zeroed, loaded, dstep, folded = (st.sem(s) for s in ("zeroed", "loaded", "dstep", "folded"))
        block = st.block()
        LOADS = 8 + 5

        @block.gpsimd
        def _(pool):
            for w in (w_sl, w_q, w_k, w_v):
                nc.gpsimd.memset(w, 0.0).then_inc(zeroed, 1)

        @block.sync
        def _(sp):
            sp.wait_ge(zeroed, 4)
            for w, name in ((w_sl, "W_slice"), (w_q, "W_q"), (w_k, "W_k"), (w_v, "W_v")):
                for h in range(2):
                    sp.dma_start(w[h * C:(h + 1) * C, h * C:(h + 1) * C], a["L0_ffn_" + name]).then_inc(loaded, 16)
            sp.dma_start(w_xT, a["L0_ffn_W_x"].rearrange("(r p) d -> p r d", p=P)).then_inc(loaded, 16)
            sp.dma_start(b_x, a["L0_ffn_b_x"]).then_inc(loaded, 16)
            sp.dma_start(temp, a["L0_ffn_temperature"].rearrange("a h b c -> a (h b c)").to_broadcast([P, H])
                         ).then_inc(loaded, 16)
            sp.dma_start(b_sl[0:1, :], a["L0_ffn_b_slice"].unsqueeze(0)).then_inc(loaded, 16)
            sp.dma_start(w_fx, a["L0_ffn_W_fx"].rearrange("(k p) n -> p k n", p=P)).then_inc(loaded, 16)

        @block.tensor
        def _(pe):
            pe.wait_ge(loaded, 16 * LOADS)
            for r in range(PR):
                for k in range(KD):
                    nc.tensor.matmul(m.PS[:, k, r * P:(r + 1) * P], w_xT[:, r, k * P:(k + 1) * P], w_sl,
                                     start=True, stop=True)
                mm = nc.tensor.matmul(m.PS[0:1, KD, r * P:(r + 1) * P], b_x[:, r:r + 1], w_sl,
                                      start=True, stop=True)
            mm.then_inc(folded, 1)

        @block.vector
        def _(dve):
            v, c = nc.vector, Chain(dve, dstep)
            dve.wait_ge(loaded, 16 * LOADS)
            c.step(v.tensor_scalar(temp, temp, 0.1, 5.0, ALU.max, ALU.min))
            c.step(v.reciprocal(temp, temp))
            dve.wait_ge(folded, 1)
            for k in range(KD):
                v.tensor_tensor(w_xs[:, k, :].rearrange("p (h g) -> p h g", h=H),
                                m.PS[:, k, :].rearrange("p (h g) -> p h g", h=H), bcast(temp, [P, H, QG]), ALU.mult)
            row = b_xs[0:1, :].rearrange("p (h g) -> p h g", h=H)
            c.step(v.tensor_tensor(row, m.PS[0:1, KD, :].rearrange("p (h g) -> p h g", h=H),
                                   b_sl[0:1, :].unsqueeze(1).to_broadcast([1, H, QG]), ALU.add))
            c.step(v.tensor_tensor(row, row, bcast(temp[0:1, :], [1, H, QG]), ALU.mult))

    FW = C * 2 + 1
    with Stage(nc) as st:
        names = ("loaded", "staged", "scored", "read", "centred", "expd", "weighted", "fxed", "fxcopied", "summed",
                 "kept", "dstep", "oned", "outed")
        (loaded, staged, scored, read, centred, expd, weighted, fxed, fxcopied, summed, kept, dstep, oned,
         outed) = (st.sem(s) for s in names)
        ring = view(m.WS, 0, U, KD, P)
        sw = view(m.WS, U * D, U, HW)
        fx = m.WS[:, U * D + U * HW:U * D + U * HW + U * PR * FW].rearrange("p (u r f) -> p u r f", u=U, r=PR)
        mx = view(xn, 5200, 8)
        den = view(xn, 5216, 8)
        block = st.block()

        @block.sync
        def _(sp):
            sp.dma_start(b_fx[0:1, :], a["L0_ffn_b_fx"].unsqueeze(0)).then_inc(loaded, 16)
            sp.dma_start(w_out, a["L0_ffn_W_out"].rearrange("(r p) d -> p r d", p=P)).then_inc(loaded, 16)
            sp.dma_start(b_out[0:1, :], a["L0_ffn_b_out"].unsqueeze(0)).then_inc(loaded, 16)
            sp.wait_ge(loaded, 48)

        @block.gpsimd
        def _(pool):
            for s in range(U):
                ins = nc.gpsimd.memset(fx[:, s, :, FW - 1], 1.0)
            ins.then_inc(oned, 1)

        @block.scalar
        def _(act):
            act.sem_inc(fxcopied, 2)
            with act.Fori(0, NT // U) as i:
                for s in range(U):
                    t = i * U + s
                    act.wait_ge(summed, t + 1)
                    nc.scalar.copy(ring[:, s, :, :], m.XT[:, :, bass.ds(t * P, P)]).then_inc(staged, 1)
                    act.wait_ge(centred, t + 1)
                    nc.scalar.activation(sw[:, s, :], sw[:, s, :], ACT.Exp).then_inc(expd, 1)
                    act.wait_ge(fxed, t + 1)
                    nc.scalar.copy(fx[:, s, :, 0:FW - 1], m.PS[:, 2 + s % 2, :].rearrange("p (r f) -> p r f", r=PR)
                                   ).then_inc(fxcopied, 1)
                    act.wait_ge(weighted, t + 1)
                    nc.scalar.copy(weights[:, bass.ds(t, 1), :].rearrange("p o d -> p (o d)"), sw[:, s, :]
                                   ).then_inc(kept, 1)

        @block.tensor
        def _(pe):
            pe.sem_inc(summed, U)
            pe.wait_ge(loaded, 48)
            pe.wait_ge(oned, 1)
            for r in range(PR):
                nc.tensor.matmul(m.PS[:, 4 + r, 0:FW], m.zerob[:, 0:P], m.zerob[:, 0:FW], start=True, stop=False,
                                 skip_group_check=True)

            def tokens(i, s):
                t = i * U + s
                pe.wait_ge(weighted, t + 1)
                pe.wait_ge(fxcopied, t + 3)
                for r in range(PR):
                    mm = nc.tensor.matmul(m.PS[:, 4 + r, 0:FW], sw[:, s, r * P:(r + 1) * P], fx[:, s, r, :],
                                          start=False, stop=False, skip_group_check=True)
                mm.then_inc(summed, 1)

            with pe.Fori(0, NT // U) as i:
                for s in range(U):
                    t = i * U + s
                    pe.wait_ge(staged, t + 1)
                    free2(pe, read, s, t)
                    for k in range(KD):
                        nc.tensor.matmul(m.PS[:, s % 2, :], ring[:, s, k, :], w_xs[:, k, :], start=(k == 0),
                                         stop=False)
                    nc.tensor.matmul(m.PS[:, s % 2, :], m.ones[0:1, :], b_xs[0:1, :], start=False,
                                     stop=True).then_inc(scored, 1)
                    free2(pe, fxcopied, s, t)
                    for k in range(KD):
                        nc.tensor.matmul(m.PS[:, 2 + s % 2, :], ring[:, s, k, :], w_fx[:, k, :], start=(k == 0),
                                         stop=False)
                    nc.tensor.matmul(m.PS[:, 2 + s % 2, :], m.ones[0:1, :], b_fx[0:1, :], start=False,
                                     stop=True).then_inc(fxed, 1)
                    tokens(i, s)

            for r in range(PR):
                mm = nc.tensor.matmul(m.PS[:, 4 + r, 0:FW], m.zerob[:, 0:P], m.zerob[:, 0:FW], start=False,
                                      stop=True, skip_group_check=True)
            mm.then_inc(outed, 1)

        @block.vector
        def _(dve):
            v, c = nc.vector, Chain(dve, dstep)
            dve.sem_inc(read, 2)
            dve.sem_inc(kept, U)
            with dve.Fori(0, NT // U) as i:
                for s in range(U):
                    t = i * U + s
                    c.at(t * 5)
                    dve.wait_ge(scored, t + 1)
                    ps = m.PS[:, s % 2, :].rearrange("p (h g) -> p h g", h=H)
                    at = sw[:, s, :].rearrange("p (h g) -> p h g", h=H)
                    c.step(v.reduce_max(mx, ps, AX))
                    dve.wait_ge(summed, t + 1)
                    dve.wait_ge(kept, t + 1)
                    c.step(v.tensor_tensor(at, ps, bcast(mx, [P, H, QG]), ALU.subtract))
                    dve.sem_inc(read, 1)
                    dve.sem_inc(centred, 1)
                    dve.wait_ge(expd, t + 1)
                    c.step(v.reduce_sum(den, at, AX))
                    c.step(v.reciprocal(den, den))
                    c.step(v.tensor_scalar(den, den, m.real[:, bass.ds(t, 1)], None, ALU.mult))
                    v.tensor_tensor(at, at, bcast(den, [P, H, QG]), ALU.mult).then_inc(weighted, 1)
            dve.wait_ge(outed, 1)

    with Stage(nc) as st:
        dstep, zeroed, made, expd, copied = (st.sem(s) for s in ("dstep", "zeroed", "made", "expd", "copied"))
        rn = small[:, 0, 0:PR]
        mx = small[:, 1, 0:PR]
        den = small[:, 2, 0:PR]
        SCALE = C ** -0.5
        halves = [slice(h * C, (h + 1) * C) for h in range(2)]
        bank = [m.PS[:, b, :].rearrange("p (r f) -> p r f", r=PR) for b in range(8)]
        block = st.block()

        @block.gpsimd
        def _(pool):
            nc.gpsimd.memset(tok, 0.0).then_inc(zeroed, 1)
            nc.gpsimd.memset(att, 0.0).then_inc(zeroed, 1)

        @block.vector
        def _(dve):
            v, c = nc.vector, Chain(dve, dstep)
            dve.wait_ge(zeroed, 2)
            c.step(v.tensor_scalar(rn, m.PS[:, 4:8, FW - 1], 1e-5, None, ALU.add))
            c.step(v.reciprocal(rn, rn))
            for h in halves:
                ins = v.tensor_tensor(tok[h, :, h], m.PS[h, 4:8, h], bcast(rn[h, :], [C, PR, C]), ALU.mult)
            ins.then_inc(copied, 1)
            n = 0

            def copy(outs):
                nonlocal n
                n += 1
                dve.wait_ge(made, n)
                for dst, b in outs:
                    ins = v.tensor_copy(dst, bank[b])
                ins.then_inc(copied, 1)

            copy([(tokT, 0)])
            copy([(qT, 1), (kT, 2), (vv, 3)])
            n += 1
            dve.wait_ge(made, n)
            for h in halves:
                c.step(v.reduce_max(mx[h, :], bank[0][h, :, h], AX))
                c.step(v.tensor_tensor(att[h, :, h], bank[0][h, :, h], bcast(mx[h, :], [C, PR, C]), ALU.subtract))
            dve.sem_inc(copied, 1)
            dve.wait_ge(expd, 2)
            for h in halves:
                c.step(v.reduce_sum(den[h, :], att[h, :, h], AX))
                c.step(v.reciprocal(den[h, :], den[h, :]))
                c.step(v.tensor_tensor(att[h, :, h], att[h, :, h], bcast(den[h, :], [C, PR, C]), ALU.mult))
            dve.sem_inc(copied, 1)
            copy([(attT, 4)])
            copy([(oT, 5)])
            n += 1
            dve.wait_ge(made, n)
            for r in range(PR):
                ins = v.tensor_copy(w_mix[:, r, :], m.PS[:, 6 + r // 2, (r % 2) * D:(r % 2 + 1) * D])

        @block.scalar
        def _(act):
            act.wait_ge(copied, 4)
            for h in halves:
                nc.scalar.activation(att[h, :, h], att[h, :, h], ACT.Exp, scale=SCALE).then_inc(expd, 1)

        @block.tensor
        def _(pe):
            te = nc.tensor
            pe.wait_ge(copied, 1)
            for r in range(PR):
                mm = te.transpose(bank[0][:, r, :], tok[:, r, :], m.ident[:])
            mm.then_inc(made, 1)
            pe.wait_ge(copied, 2)
            te.matmul(bank[1], w_q, tokT, start=True, stop=True)
            te.matmul(bank[2], w_k, tokT, start=True, stop=True)
            for r in range(PR):
                mm = te.matmul(bank[3][:, r, :], tokT[:, r, :], w_v, start=True, stop=True)
            mm.then_inc(made, 1)
            pe.wait_ge(copied, 3)
            for r in range(PR):
                mm = te.matmul(bank[0][:, r, :], qT[:, r, :], kT[:, r, :], start=True, stop=True)
            mm.then_inc(made, 1)
            pe.wait_ge(copied, 5)
            for r in range(PR):
                mm = te.transpose(bank[4][:, r, :], att[:, r, :], m.ident[:])
            mm.then_inc(made, 1)
            pe.wait_ge(copied, 6)
            for r in range(PR):
                mm = te.matmul(bank[5][:, r, :], vv[:, r, :], attT[:, r, :], start=True, stop=True)
            mm.then_inc(made, 1)
            pe.wait_ge(copied, 7)
            for r in range(PR):
                mm = te.matmul(m.PS[:, 6 + r // 2, (r % 2) * D:(r % 2 + 1) * D], oT[:, r, :], w_out[:, r, :],
                               start=True, stop=True)
            mm.then_inc(made, 1)

    with Stage(nc) as st:
        staged, turned, copied, made, taken = (st.sem(s) for s in ("staged", "turned", "copied", "made", "taken"))
        ring = view(m.WS, 0, U, HW)
        ringT = view(m.WS, U * HW, U, HW)
        block = st.block()

        @block.scalar
        def _(act):
            with act.Fori(0, NT // U) as i:
                for s in range(U):
                    t = i * U + s
                    act.wait_ge(turned, t + 1)
                    nc.scalar.copy(ring[:, s, :], weights[:, bass.ds(t, 1), :].rearrange("p o d -> p (o d)")
                                   ).then_inc(staged, 1)

        @block.tensor
        def _(pe):
            pe.sem_inc(turned, U)
            with pe.Fori(0, NT // U) as i:
                for s in range(U + 1):
                    t = i * U + s
                    if s < U:
                        pe.wait_ge(staged, t + 1)
                        free2(pe, copied, s, t)
                        for r in range(PR):
                            mm = nc.tensor.transpose(m.PS[:, s % 2, r * P:(r + 1) * P], ring[:, s, r * P:(r + 1) * P],
                                                     m.ident[:])
                        mm.then_inc(turned, 1)
                    if s > 0:
                        q = s - 1
                        pe.wait_ge(copied, t + 2)
                        free2(pe, taken, q, t - 1)
                        for r in range(PR):
                            nc.tensor.matmul(m.PS[:, 2 + q % 2, 0:D], ringT[:, q, r * P:(r + 1) * P], w_mix[:, r, :],
                                             start=(r == 0), stop=False)
                        nc.tensor.matmul(m.PS[:, 2 + q % 2, 0:D], m.ones[0:1, :], b_out[0:1, :], start=False,
                                         stop=True).then_inc(made, 1)

        @block.vector
        def _(dve):
            dve.sem_inc(copied, 2)
            dve.sem_inc(taken, 2)
            dve.sem_inc(made, U)
            with dve.Fori(0, NT // U) as i:
                for s in range(U + 1):
                    t = i * U + s
                    if s < U:
                        dve.wait_ge(turned, t + 1 + U)
                        dve.wait_ge(made, t + 1)
                        nc.vector.tensor_copy(ringT[:, s, :], m.PS[:, s % 2, :]).then_inc(copied, 1)
                    if s > 0:
                        q = s - 1
                        dve.wait_ge(made, t + U)
                        at = tile_at(m.X, t - 1)
                        nc.vector.tensor_tensor(at, at, m.PS[:, 2 + q % 2, 0:D], ALU.add).then_inc(taken, 1)



def graph_attention(nc, m, a):
    H, C = 4, 64
    RW = D + H
    layernorm(nc, m, m.X, m.XN)
    turn(nc, m, m.XN, m.XT)
    node = m.BB[:, 0:NT * 8].rearrange("p (t c) -> p t c", c=8)
    src_score = m.BB[:, 256:256 + NT * H].rearrange("p (t c) -> p t c", c=H)
    best = m.BB[:, 384:384 + NT * H].rearrange("p (t c) -> p t c", c=H)
    high = m.BB[:, 512:]

    with Stage(nc) as st:
        (loaded, staged, made, copied, rowed, dstep, tabled) = (
            st.sem(s) for s in ("loaded", "staged", "made", "copied", "rowed", "dstep", "tabled"))
        stored = st.sems("stored", U)
        ring = view(m.WS, 0, U, KD, P)
        row = view(m.WS, U * D, U, RW)
        w = view(m.WS, U * D + U * RW, KD, D)
        o = U * D + U * RW + KD * D
        att = [m.WS[:, o + k * D:o + (k + 1) * D] for k in range(2)]
        tmp = m.WS[:, o + 2 * D:o + 3 * D]
        block = st.block()

        @block.sync
        def _(sp):
            sp.dma_start(w, a["L1_gnn_W"].rearrange("(k p) n -> p k n", p=P)).then_inc(loaded, 16)
            for k, name in enumerate(("L1_gnn_att_src", "L1_gnn_att_dst")):
                sp.dma_start(att[k], a[name].rearrange("h c -> (h c)").unsqueeze(0).to_broadcast([P, D])
                             ).then_inc(loaded, 16)
            to = m.table_gat.rearrange("(t p) c -> p t c", p=P)
            with sp.Fori(0, NT // U) as i:
                for s in range(U):
                    t = i * U + s
                    sp.wait_ge(rowed, t + 1)
                    sp.dma_start(to[:, bass.ds(t, 1), :].rearrange("p o c -> p (o c)"), row[:, s, :]
                                 ).then_inc(stored[s], 16)
            for s in range(U):
                sp.wait_ge(stored[s], 16 * (NT // U + 1))
            sp.dma_start(m.table_max.rearrange("(t p) c -> p t c", p=P), src_score).then_inc(tabled, 16)
            sp.wait_ge(tabled, 16)

        @block.scalar
        def _(act):
            act.sem_inc(copied, U)
            for s in range(U):
                act.sem_inc(stored[s], 16)
            with act.Fori(0, NT // U) as i:
                for s in range(U):
                    t = i * U + s
                    act.wait_ge(made, t + 1)
                    nc.scalar.copy(ring[:, s, :, :], m.XT[:, :, bass.ds(t * P, P)]).then_inc(staged, 1)
                    act.wait_ge(made, t + 1 + U)
                    act.wait_ge(stored[s], i * 16 + 16)
                    nc.scalar.copy(row[:, s, 0:D], m.PS[:, s, 0:D]).then_inc(copied, 1)

        @block.tensor
        def _(pe):
            pe.sem_inc(made, U)
            pe.wait_ge(loaded, 48)

            with pe.Fori(0, NT // U) as i:
                for s in range(U):
                    t = i * U + s
                    pe.wait_ge(staged, t + 1)
                    pe.wait_ge(copied, t + 1)
                    for k in range(KD):
                        mm = nc.tensor.matmul(m.PS[:, s, 0:D], ring[:, s, k, :], w[:, k, :], start=(k == 0),
                                              stop=(k == KD - 1))
                    mm.then_inc(made, 1)

        @block.vector
        def _(dve):
            v, c = nc.vector, Chain(dve, dstep)
            dve.wait_ge(loaded, 48)
            with dve.Fori(0, NT // U) as i:
                for s in range(U):
                    t = i * U + s
                    c.at(t * 4)
                    dve.wait_ge(copied, t + 1 + U)
                    ps = row[:, s, 0:D]
                    heads = tmp.rearrange("p (h c) -> p h c", h=H)
                    c.step(v.tensor_tensor(tmp, ps, att[0], ALU.mult))
                    c.step(v.reduce_sum(row[:, s, D:RW], heads, AX))
                    c.step(v.tensor_tensor(tmp, ps, att[1], ALU.mult))
                    c.step(v.reduce_sum(tile_at(node, t, 0, H), heads, AX))
                    v.tensor_copy(tile_at(src_score, t, 0, H), row[:, s, D:RW]).then_inc(rowed, 1)

    with Stage(nc) as st:
        names = ("indexed", "hot", "masked", "made", "topped", "bested", "issue", "initial")
        indexed, hot, masked, made, topped, bested, issue, initial = (st.sem(s) for s in names)
        R, RS = 8, 4
        gathered = st.sems("gathered", R * Q)
        S = view(m.WS, 0, RS * Q, P)
        off = view(m.WS, RS * Q * P, RS * Q * P // 2).bitcast(BF16).rearrange("p (u e) -> p u e", e=P)
        o = RS * Q * P * 3 // 2
        rows = view(m.WS, o, R * Q, H)
        idx = view(m.WS, o + R * Q * H, R * Q).bitcast(I32)
        top = view(m.WS, o + R * Q * (H + 1), 2 * Q, H)
        minus = m.WS[:, o + R * Q * (2 * H + 1):o + R * Q * (2 * H + 1) + 1]
        diag = high[:, 0:RS * Q * H * P].rearrange("p (u h e) -> p u h e", u=RS * Q, h=H)
        MASK = float(2.0 ** 100)
        block = st.block()

        @block.scalar
        def _(act):
            def indices(j, u, r):
                act.wait_ge(made, j + 1)
                nc.scalar.copy(idx[:, u * Q:(u + 1) * Q], m.src1[:, bass.ds(j * Q, Q)]).then_inc(indexed, 1)

            def masks(j, u, r):
                k = u % RS
                act.wait_ge(hot, j + 1)
                nc.scalar.activation(off[:, k * Q:(k + 1) * Q, :], S[:, k * Q:(k + 1) * Q, :], ACT.Identity,
                                     bias=minus, scale=MASK)
                for s in range(Q):
                    act.wait_ge(gathered[u * Q + s], r * 16 + 16)
                    for h in range(1, H):
                        ins = nc.scalar.mul(diag[:, k * Q + s, h, :], m.ident[:], rows[:, u * Q + s, h:h + 1])
                ins.then_inc(masked, 1)

            act.wait_ge(initial, 2)
            pipeline(act, R, (6, indices), (2, masks))

        @block.gpsimd
        def _(pool):
            nc.gpsimd.memset(minus, -MASK).then_inc(initial, 1)
            nc.gpsimd.tensor_copy(best, src_score).then_inc(initial, 1)
            with pool.Fori(0, QUADS // R) as i:
                for u in range(R):
                    pool.wait_ge(indexed, i * R + u + 1)
                    pool.sem_inc(issue, 1)
                    for q in range(u * Q, (u + 1) * Q):
                        nc.gpsimd.indirect_dma_start(rows[:, q, :], None, m.table_max,
                                                     bass.IndirectOffsetOnAxis(ap=idx[:, q:q + 1], axis=0)
                                                     ).then_inc(gathered[q], 16)

        @block.tensor
        def _(pe):
            pe.sem_inc(made, R)
            with pe.Fori(0, QUADS // R) as i:
                for u in range(R):
                    j, k = i * R + u, u % RS
                    pe.wait_ge(masked, j + 1)
                    pe.wait_ge(topped, j + 1)
                    for s in range(Q):
                        at = m.PS[:, u % 2 * Q + s, :]
                        nc.tensor.matmul(at, off[:, k * Q + s, :], m.identb[:].unsqueeze(1).to_broadcast([P, H, P]),
                                         start=True, stop=False)
                        mm = nc.tensor.matmul(at, S[:, k * Q + s, :], diag[:, k * Q + s].rearrange("p h e -> p (h e)"),
                                              start=False, stop=True)
                    mm.then_inc(made, 1)

        @block.vector
        def _(dve):
            v = nc.vector
            dve.sem_inc(topped, 2)
            dve.sem_inc(bested, 1)
            dve.wait_ge(initial, 2)

            def hots(j, u, r):
                k = slice(u % RS * Q, (u % RS + 1) * Q)
                dve.wait_ge(made, j + 1 + R - RS)
                for s in range(Q):
                    dve.wait_ge(gathered[u * Q + s], r * 16 + 16)
                v.tensor_tensor(diag[:, k, 0, :], m.ident[:].unsqueeze(1).to_broadcast([P, Q, P]),
                                rows[:, u * Q:(u + 1) * Q, 0:1].to_broadcast([P, Q, P]), ALU.mult)
                one_hot_rows(v, m, S[:, k, :], m.lo1[:, bass.ds(j * Q, Q)]).then_inc(hot, 1)

            def greatest(j, u, r):
                half = u % 2
                tiles = node_tiles(nc, dve, m.tn1, j, Q)
                dve.wait_ge(made, j + 1 + R)
                t = top[:, half * Q:(half + 1) * Q, :]
                v.reduce_max(t, m.PS[:, half * Q:(half + 1) * Q, :].rearrange("p s (h e) -> p s h e", h=H), AX
                             ).then_inc(topped, 1)
                dve.wait_ge(topped, j + 3)
                for s in range(Q):
                    at = tile_at(best, tiles[s], 0, H)
                    dve.wait_ge(bested, j * Q + s + 1)
                    v.tensor_tensor(at, at, t[:, s, :], ALU.max).then_inc(bested, 1)

            pipeline(dve, R, (2, hots), (0, greatest))

    with Stage(nc) as st:
        names = ("dstep", "ready", "own_diffed", "own_expd", "selfed", "indexed", "hot", "turned", "tcopied",
                 "scored", "taken", "estep", "diffed", "expd", "weighted", "summed", "added", "issue")
        (dstep, ready, own_diffed, own_expd, selfed, indexed, hot, turned, tcopied, scored, taken, estep, diffed,
         expd, weighted, summed, added, issue) = (st.sem(s) for s in names)
        R, RS = 8, 4
        gathered = st.sems("gathered", R * Q)
        S = view(m.WS, 0, RS * Q, P)
        ST = view(m.WS, RS * Q * P, RS * Q, P)
        o = 2 * RS * Q * P
        idx = view(m.WS, o, R * Q).bitcast(I32)
        e, lk, p = (view(m.WS, o + (1 + k * H) * R * Q, R * Q, H) for k in range(3))
        own = view(m.WS, o + (1 + 3 * H) * R * Q, NT, H)
        rows = view(high, 0, R * Q, RW)
        block = st.block()

        @block.sync
        def _(sp):
            sp.dma_start(m.AGG[:, :, 0:RW], m.table_gat.rearrange("(t p) c -> p t c", p=P)).then_inc(selfed, 16)

        @block.scalar
        def _(act):
            def indices(j, u, r):
                act.wait_ge(summed, (j + 1) * Q)
                nc.scalar.copy(idx[:, u * Q:(u + 1) * Q], m.src1[:, bass.ds(j * Q, Q)]).then_inc(indexed, 1)

            def turned_hots(j, u, r):
                k = u % RS
                act.wait_ge(turned, j + 1)
                nc.scalar.copy(ST[:, k * Q:(k + 1) * Q, :], m.PS[:, u % 2, :].rearrange("p (s e) -> p s e", s=Q)
                               ).then_inc(tcopied, 1)

            def numerators(j, u, r):
                act.wait_ge(diffed, j + 1)
                nc.scalar.activation(p[:, u * Q:(u + 1) * Q, :], e[:, u * Q:(u + 1) * Q, :], ACT.Exp
                                     ).then_inc(expd, 1)

            act.sem_inc(tcopied, 2)
            act.wait_ge(own_diffed, 1)
            nc.scalar.activation(own, own, ACT.Exp).then_inc(own_expd, 1)
            pipeline(act, R, (6, indices), (3, turned_hots), (2, numerators))

        @block.gpsimd
        def _(pool):
            with pool.Fori(0, QUADS // R) as i:
                for u in range(R):
                    pool.wait_ge(indexed, i * R + u + 1)
                    pool.sem_inc(issue, 1)
                    for q in range(u * Q, (u + 1) * Q):
                        nc.gpsimd.indirect_dma_start(rows[:, q, :], None, m.table_gat,
                                                     bass.IndirectOffsetOnAxis(ap=idx[:, q:q + 1], axis=0)
                                                     ).then_inc(gathered[q], 16)

        @block.tensor
        def _(pe):
            te = nc.tensor

            def turn_hots(j, u, r):
                pe.wait_ge(hot, j + 1)
                pe.wait_ge(tcopied, j + 1)
                for s in range(Q):
                    mm = te.transpose(m.PS[:, u % 2, s * P:(s + 1) * P], S[:, u % RS * Q + s, :], m.ident[:])
                mm.then_inc(turned, 1)

            def scores(j, u, r):
                tiles = node_tiles(nc, pe, m.tn1, j, Q)
                pe.wait_ge(tcopied, j + 3)
                pe.wait_ge(taken, j + 1)
                for s in range(Q):
                    mm = te.matmul(m.PS[:, 2 + u % 2, s * 8:(s + 1) * 8], ST[:, u % RS * Q + s, :],
                                   tile_at(node, tiles[s], 0, 8), start=True, stop=True)
                mm.then_inc(scored, 1)

            def sums(j, u, r):
                pe.wait_ge(weighted, j + 1)
                for s in range(Q):
                    pe.wait_ge(added, j * Q + s + 1)
                    te.matmul(m.PS[:, 4 + s, 0:RW], S[:, u % RS * Q + s, :], rows[:, u * Q + s, :], start=True,
                              stop=True).then_inc(summed, 1)

            pe.sem_inc(summed, R * Q)
            pe.wait_ge(ready, 1)
            pipeline(pe, R, (3, turn_hots), (2, scores), (0, sums))

        @block.vector
        def _(dve):
            v, c = nc.vector, Chain(dve, dstep)
            dve.sem_inc(added, Q)
            dve.sem_inc(taken, 2)
            c.step(v.tensor_tensor(best, best, node[:, :, 0:H], ALU.add))
            c.step(v.scalar_tensor_tensor(node[:, :, H:2 * H], best, 0.2, best, ALU.mult, ALU.max))
            dve.wait_ge(selfed, 16)
            c.step(v.tensor_tensor(best, m.AGG[:, :, D:RW], node[:, :, 0:H], ALU.add))
            c.step(v.scalar_tensor_tensor(own, best, 0.2, best, ALU.mult, ALU.max))
            c.step(v.tensor_tensor(own, own, node[:, :, H:2 * H], ALU.subtract))
            v.tensor_scalar(own, own, 0.0, None, ALU.min).then_inc(own_diffed, 1)
            dve.wait_ge(own_expd, 1)
            at = m.AGG[:, :, 0:D].rearrange("p t (h c) -> p t h c", h=H)
            c.step(v.tensor_tensor(at, at, own.unsqueeze(3).to_broadcast([P, NT, H, C]), ALU.mult))
            c.step(v.tensor_copy(m.AGG[:, :, D:RW], own))
            dve.sem_inc(ready, 1)
            ce = Chain(dve, estep)

            def hots(j, u, r):
                k = u % RS
                dve.wait_ge(summed, (j + 1 + R - RS) * Q)
                one_hot_rows(v, m, S[:, k * Q:(k + 1) * Q, :], m.lo1[:, bass.ds(j * Q, Q)]).then_inc(hot, 1)

            def exponents(j, u, r):
                k = slice(u * Q, (u + 1) * Q)
                ce.at(j * 3)
                for s in range(Q):
                    dve.wait_ge(gathered[u * Q + s], r * 16 + 16)
                dve.wait_ge(scored, j + 1)
                sc = m.PS[:, 2 + u % 2, 0:Q * 8].rearrange("p (s c) -> p s c", s=Q)
                ce.step(v.tensor_tensor(e[:, k], rows[:, k, D:RW], sc[:, :, 0:H], ALU.add))
                ce.step(v.scalar_tensor_tensor(lk[:, k], e[:, k], 0.2, e[:, k], ALU.mult, ALU.max))
                ce.step(v.tensor_tensor(e[:, k], lk[:, k], sc[:, :, H:2 * H], ALU.subtract))
                dve.sem_inc(taken, 1)
                v.tensor_scalar(e[:, k], e[:, k], 0.0, None, ALU.min).then_inc(diffed, 1)

            def weigh(j, u, r):
                k = slice(u * Q, (u + 1) * Q)
                dve.wait_ge(expd, j + 1)
                f = rows[:, k, 0:D].rearrange("p s (h c) -> p s h c", h=H)
                v.tensor_tensor(f, f, p[:, k].unsqueeze(3).to_broadcast([P, Q, H, C]), ALU.mult)
                v.tensor_copy(rows[:, k, D:RW], p[:, k]).then_inc(weighted, 1)

            def add(j, u, r):
                tiles = node_tiles(nc, dve, m.tn1, j, Q)
                for s in range(Q):
                    dve.wait_ge(summed, (j + R) * Q + s + 1)
                    dve.wait_ge(added, (j + 1) * Q + s)
                    at = tile_at(m.AGG, tiles[s], 0, RW)
                    v.tensor_tensor(at, at, m.PS[:, 4 + s, 0:RW], ALU.add).then_inc(added, 1)

            pipeline(dve, R, (3, hots), (2, exponents), (1, weigh), (0, add))

    with Stage(nc) as st:
        loaded, dstep = st.sem("loaded"), st.sem("dstep")
        bias = m.WS[:, 0:D]
        rd = view(m.WS, D, NT, H)
        block = st.block()

        @block.sync
        def _(sp):
            sp.dma_start(bias, a["L1_gnn_bias"].unsqueeze(0).to_broadcast([P, D])).then_inc(loaded, 16)

        @block.vector
        def _(dve):
            v, c = nc.vector, Chain(dve, dstep)
            c.step(v.tensor_scalar(rd, m.AGG[:, :, D:RW], 1e-16, None, ALU.add))
            c.step(v.reciprocal(rd, rd))
            heads = [x.rearrange("p t (h c) -> p t h c", h=H) for x in (m.XN[:], m.AGG[:, :, 0:D])]
            c.step(v.tensor_tensor(heads[0], heads[1], rd.unsqueeze(3).to_broadcast([P, NT, H, C]), ALU.mult))
            dve.wait_ge(loaded, 16)
            c.step(v.tensor_tensor(m.XN[:], m.XN[:], bias.unsqueeze(1).to_broadcast([P, NT, D]), ALU.add))

    turn(nc, m, m.XN, m.XT)

    def finish(dve, c, t, ps):
        at = tile_at(m.X, t)
        return nc.vector.scalar_tensor_tensor(at, ps, 0.0, at, ALU.max, ALU.add)

    linear_nodes(nc, m, m.XT, a["L1_gnn_lin_w"], a["L1_gnn_lin_b"], D, Finish(finish))


def expert_pair(nc, m, a):
    NE, HD = 8, 1024
    KH = HD // P
    layernorm(nc, m, m.X, m.XN)
    gates(nc, m, a["L1_ffn_Wr"], a["L1_ffn_br"], NE, False)
    layernorm(nc, m, m.XN, m.XN)
    turn(nc, m, m.XN, m.XT)
    with Stage(nc) as st:
        names = ("shifted", "made_b", "w1_used", "w2_used", "scaled", "made", "active", "done", "taken", "smalls", "passed")
        shifted, made_b, w1_used, w2_used, scaled, made, active, done, taken, smalls, passed = (st.sem(s) for s in names)
        came1, came2 = st.sems("came1", 2), st.sems("came2", 2)
        hid = view(m.BB, 0, KH, CB)
        o = KH * CB
        w1 = [view(m.BB, o + q * KD * HD, KD, HD) for q in range(2)]
        o += 2 * KD * HD
        w2 = [view(m.BB, o, KH, D), view(m.AF, 0, KH, D)]
        ln_g = view(m.WS, 0, NE, KD)
        ln_b = view(m.WS, 16, NE, KD)
        b1 = view(m.WS, 32, NE, KH)
        b1s = view(m.WS, 96, 2, KH)
        b2 = m.WS[0:1, 128:128 + NE * D]
        block = st.block()

        @block.sync
        def _(sp):
            sp.dma_start(ln_g, a["L1_ffn_ln_g"].rearrange("p (e k) -> p e k", k=KD)).then_inc(smalls, 16)
            sp.dma_start(ln_b, a["L1_ffn_ln_b"].rearrange("p (e k) -> p e k", k=KD)).then_inc(smalls, 16)
            sp.dma_start(b1, a["L1_ffn_b1"].rearrange("p (e k) -> p e k", k=KH)).then_inc(smalls, 16)
            sp.dma_start(b2, a["L1_ffn_b2"].rearrange("e d -> (e d)").unsqueeze(0)).then_inc(smalls, 16)
            w1d = a["L1_ffn_W1"].rearrange("e (k p) h -> e p k h", p=P)
            w2d = a["L1_ffn_W2"].rearrange("e (k p) d -> e p k d", p=P)
            with sp.Fori(0, NE // 2) as i:
                for q in range(2):
                    ex = i * 2 + q
                    sp.wait_ge(w1_used, ex + 1)
                    sp.dma_start(w1[q], w1d[bass.ds(ex, 1), :, :, :].rearrange("o p k h -> (o p) k h")
                                 ).then_inc(came1[q], 16)
                    sp.dma_start(w2[q], w2d[bass.ds(ex, 1), :, :, :].rearrange("o p k d -> (o p) k d")
                                 ).then_inc(came2[q], 16)

        @block.tensor
        def _(pe):
            pe.sem_inc(w1_used, 2)
            pe.wait_ge(smalls, 64)
            te = nc.tensor
            with pe.Fori(0, NE // 2) as i:
                for q in range(2):
                    ex = i * 2 + q
                    pe.wait_ge(came1[q], i * 16 + 16)
                    pe.wait_ge(taken, ex * NT + U)
                    for j in range(KH):
                        for k in range(KD):
                            mm = te.matmul(m.PS[:, 3, j:j + 1], w1[q][:, k, j * P:(j + 1) * P],
                                           ln_b[:, bass.ds(ex, 1), k:k + 1].rearrange("p o k -> p (o k)"),
                                           start=(k == 0), stop=(k == KD - 1))
                    mm.then_inc(made_b, 1)
                    pe.wait_ge(scaled, ex + 1)
                    pe.wait_ge(came2[q], i * 16 + 16)
                    pe.sem_inc(passed, 1)
                    with pe.Fori(0, NT // TB) as b:
                        base = (ex * (NT // TB) + b) * KH * 2
                        for j in range(KH):
                            for h in range(2):
                                n = base + j * 2 + h
                                pe.wait_ge(active, n + 1)
                                for k in range(KD):
                                    mm = te.matmul(m.PS[:, h, 0:CH2], w1[q][:, k, j * P:(j + 1) * P],
                                                   m.XT[:, k, bass.ds(b * CB + h * CH2, CH2)], start=(k == 0),
                                                   stop=(k == KD - 1))
                                mm.then_inc(made, 1)
                        pe.wait_ge(active, base + KH * 2 + 2)
                        for s in range(TB):
                            t = ex * NT + b * TB + s
                            pe.wait_ge(taken, t + 1)
                            for j in range(KH):
                                te.matmul(m.PS[:, 3 + s, 0:D], hid[:, j, s * P:(s + 1) * P], w2[q][:, j, :],
                                          start=(j == 0), stop=False)
                            te.matmul(m.PS[:, 3 + s, 0:D], m.ones[0:1, :],
                                      b2[:, bass.ds(ex * D, D)], start=False, stop=True).then_inc(done, 1)
                    pe.wait_ge(done, (ex + 1) * NT)
                    pe.sem_inc(w1_used, 1)

        @block.scalar
        def _(act):
            act.sem_inc(active, 2)
            with act.Fori(0, NE // 2) as i:
                for q in range(2):
                    ex = i * 2 + q
                    act.wait_ge(shifted, ex + 1)
                    act.sem_inc(passed, 1)
                    with act.Fori(0, NT // TB) as b:
                        base = (ex * (NT // TB) + b) * KH * 2
                        for j in range(KH):
                            for h in range(2):
                                n = base + j * 2 + h
                                act.wait_ge(made, n + 1)
                                nc.scalar.activation(hid[:, j, h * CH2:(h + 1) * CH2], m.PS[:, h, 0:CH2], ACT.Gelu,
                                                     bias=b1s[:, q, j:j + 1]).then_inc(active, 1)

        @block.vector
        def _(dve):
            v = nc.vector
            dve.sem_inc(taken, U)
            dve.wait_ge(smalls, 64)
            with dve.Fori(0, NE // 2) as i:
                for q in range(2):
                    ex = i * 2 + q
                    dve.wait_ge(made_b, ex + 1)
                    v.tensor_tensor(b1s[:, q, :], m.PS[:, 3, 0:KH],
                                    b1[:, bass.ds(ex, 1), :].rearrange("p o k -> p (o k)"), ALU.add
                                    ).then_inc(shifted, 1)
                    for k in range(KD):
                        ins = v.tensor_scalar(w1[q][:, k, :], w1[q][:, k, :],
                                              ln_g[:, bass.ds(ex, 1), k:k + 1].rearrange("p o k -> p (o k)"), None,
                                              ALU.mult)
                    ins.then_inc(scaled, 1)
                    with dve.Fori(0, NT // TB) as b:
                        for s in range(TB):
                            t = b * TB + s
                            n = ex * NT + t
                            dve.wait_ge(done, n + 1)
                            dve.wait_ge(taken, n + U)
                            at = tile_at(m.X, t)
                            g = m.gate[:, bass.ds(t, 1), bass.ds(ex, 1)].rearrange("p o k -> p (o k)")
                            v.scalar_tensor_tensor(at, m.PS[:, 3 + s, 0:D], g, at, ALU.mult,
                                                   ALU.add).then_inc(taken, 1)


def gates(nc, m, weight, bias, ne, softmax_first, hidden=None):
    if hidden is None:
        turn(nc, m, m.XN, m.XT)
    srcT = m.XT if hidden is None else hidden
    KX = 1 if hidden is not None else KD
    with Stage(nc) as st:
        names = ("loaded", "staged", "made", "taken", "dstep", "differed", "expd", "passed")
        loaded, staged, made, taken, dstep, differed, expd, passed = (st.sem(s) for s in names)
        ring = view(m.WS, 0, U, KX, P)
        w = view(m.WS, U * D, KX, ne)
        b = m.WS[0:1, U * D + 64:U * D + 64 + ne]
        lg = m.WS[:, 2000:2008]
        top = m.WS[:, 2008:2016]
        which = m.WS[:, 2016:2024].bitcast(U32)
        whichf = m.WS[:, 2024:2032]
        ex = m.WS[:, 2032:2040]
        sh = m.WS[:, 2040:2048]
        eq = m.WS[:, 2048:2056]
        eq2 = m.WS[:, 2064:2072]
        prob = m.WS[:, 2072:2080]
        total = m.WS[:, 2056:2057]
        block = st.block()

        @block.sync
        def _(sp):
            sp.dma_start(w, weight.rearrange("(k p) n -> p k n", p=P)).then_inc(loaded, 16)
            sp.dma_start(b, bias.unsqueeze(0)).then_inc(loaded, 16)

        @block.scalar
        def _(act):
            with act.Fori(0, NT // U) as i:
                for s in range(U):
                    t = i * U + s
                    act.wait_ge(made, t + 1)
                    nc.scalar.copy(ring[:, s, :, :], srcT[:, 0:KX, bass.ds(t * P, P)]).then_inc(staged, 1)
                for s in range(U):
                    t = i * U + s
                    if softmax_first:
                        act.wait_ge(differed, t * 2 + 1)
                        nc.scalar.activation(ex, sh, ACT.Exp).then_inc(expd, 1)
                        act.wait_ge(differed, t * 2 + 2)
                        nc.scalar.activation(ex[:, 0:2], sh[:, 0:2], ACT.Exp).then_inc(expd, 1)
                    else:
                        act.wait_ge(differed, t + 1)
                        nc.scalar.activation(ex[:, 0:2], sh[:, 0:2], ACT.Exp).then_inc(expd, 1)

        @block.tensor
        def _(pe):
            pe.sem_inc(made, U)
            pe.wait_ge(loaded, 32)
            with pe.Fori(0, NT // U) as i:
                for s in range(U):
                    t = i * U + s
                    pe.wait_ge(staged, t + 1)
                    pe.wait_ge(taken, t + 1)
                    for k in range(KX):
                        nc.tensor.matmul(m.PS[:, s, 0:ne], ring[:, s, k, :], w[:, k, :], start=(k == 0), stop=False)
                    nc.tensor.matmul(m.PS[:, s, 0:ne], m.ones[0:1, :], b, start=False, stop=True).then_inc(made, 1)

        @block.vector
        def _(dve):
            v, c = nc.vector, Chain(dve, dstep)
            dve.sem_inc(taken, U)
            c.step(v.memset(lg, -BIG))

            def tile(t, s):
                dve.wait_ge(made, t + 1 + U)
                c.step(v.tensor_copy(lg[:, 0:ne], m.PS[:, s, 0:ne]))
                dve.sem_inc(taken, 1)
                c.step(v.max(top, lg))
                if softmax_first:
                    v.tensor_scalar(sh, lg, top[:, 0:1], None, ALU.subtract).then_inc(differed, 1)
                    dve.wait_ge(expd, t * 2 + 1)
                    c.step(v.reduce_sum(total, ex, AX))
                    c.step(v.reciprocal(total, total))
                    c.step(v.tensor_scalar(prob[:, 0:ne], ex[:, 0:ne], total, None, ALU.mult))
                    dve.sem_inc(passed, 1)
                    c.step(v.max(top, prob))
                dve.sem_inc(passed, 1)
                c.step(v.max_index(which, top, prob if softmax_first else lg))
                c.step(v.tensor_copy(whichf, which))
                v.tensor_scalar(sh[:, 0:2], top[:, 0:2], top[:, 0:1], None, ALU.subtract).then_inc(differed, 1)
                dve.wait_ge(expd, t * 2 + 2 if softmax_first else t + 1)
                c.step(v.reduce_sum(total, ex[:, 0:2], AX))
                c.step(v.reciprocal(total, total))
                c.step(v.tensor_scalar(eq, m.iota[:, 0:8], whichf[:, 0:1], ex[:, 0:1], ALU.is_equal, ALU.mult))
                c.step(v.tensor_scalar(eq2, m.iota[:, 0:8], whichf[:, 1:2], ex[:, 1:2], ALU.is_equal, ALU.mult))
                c.step(v.tensor_tensor(eq, eq, eq2, ALU.add))
                v.tensor_scalar(tile_at(m.gate, t, 0, 8), eq, total, None, ALU.mult)

            c.step(v.memset(prob, -1.0))
            steps = 13 if softmax_first else 9
            with dve.Fori(0, NT // U) as i:
                for s in range(U):
                    c.at((i * U + s) * steps + 2)
                    tile(i * U + s, s)
                    assert c.k == steps



def edge_update(nc, m, a):
    layernorm(nc, m, m.X, m.XN)
    turn(nc, m, m.XN, m.XT)
    w1 = a["L2_gnn_W1"]
    by_dst = view(m.BB, 0, NT, D)
    by_src = view(m.BB, NT * D, NT, D)

    def keep(dst):
        return Finish(lambda dve, c, t, ps: nc.vector.tensor_copy(tile_at(dst, t), ps))

    linear_nodes(nc, m, m.XT, w1[D:2 * D, :], None, D, keep(by_dst))
    store_table(nc, m, by_dst, m.table, sums=0.0)
    linear_nodes(nc, m, m.XT, w1[0:D, :], a["L2_gnn_b1"], D, keep(by_src))

    CW = D + 1
    with Stage(nc) as st:
        names = ("loaded", "oned", "indexed", "hot", "turned", "tcopied", "made", "mixed", "active", "summed",
                 "added", "issue")
        loaded, oned, indexed, hot, turned, tcopied, made, mixed, active, summed, added, issue = (
            st.sem(s) for s in names)
        R, RS = 8, 4
        gathered, came = st.sems("gathered", RS * Q), st.sems("came", R)
        rows = view(m.WS, 0, RS * Q, CW)
        rec = view(m.WS, RS * Q * CW, R * Q, EA + 4)
        o = RS * Q * CW + R * Q * (EA + 4)
        idx = view(m.WS, o, R * Q).bitcast(I32)
        wa = m.WS[0:EA, o + R * Q:o + R * Q + D]
        S = view(m.BB, 0, RS * Q, P)
        ST = view(m.BB, RS * Q * P, RS * Q, P)
        attT = view(m.BB, 2 * RS * Q * P, RS * Q, P)
        block = st.block()

        @block.sync
        def _(sp):
            sp.dma_start(wa, w1[2 * D:2 * D + EA, :]).then_inc(loaded, 16)
            r = m.rec2.rearrange("(p w) c -> p w c", p=P)
            with sp.Fori(0, QUADS // R) as i:
                for u in range(R):
                    j = i * R + u
                    sp.wait_ge(summed, (j + 1) * Q)
                    sp.dma_start(rec[:, u * Q:(u + 1) * Q, :], r[:, bass.ds(j * Q, Q), :]).then_inc(came[u], 16)

        @block.scalar
        def _(act):
            def indices(j, u, r):
                act.wait_ge(came[u], r * 16 + 16)
                nc.scalar.copy(idx[:, u * Q:(u + 1) * Q], rec[:, u * Q:(u + 1) * Q, EA]).then_inc(indexed, 1)

            def turned_in(j, u, r):
                k = slice(u % RS * Q, (u % RS + 1) * Q)
                act.wait_ge(turned, j + 1)
                nc.scalar.copy(ST[:, k, :], m.PS[:, 0, :].rearrange("p (s e) -> p s e", s=Q))
                nc.scalar.copy(attT[0:EA, k, :], m.PS[0:EA, 1, :].rearrange("p (s e) -> p s e", s=Q)
                               ).then_inc(tcopied, 1)

            def relu(j, u, r):
                k = slice(u % RS * Q, (u % RS + 1) * Q)
                act.wait_ge(mixed, j + 2)
                nc.scalar.activation(rows[:, k, 0:D], rows[:, k, 0:D], ACT.Relu).then_inc(active, 1)

            act.sem_inc(tcopied, 1)
            pipeline(act, R, (6, indices), (2, turned_in), (1, relu))

        @block.gpsimd
        def _(pool):
            nc.gpsimd.memset(rows[:, :, D:CW], 1.0).then_inc(oned, 1)
            with pool.Fori(0, QUADS // R) as i:
                for u in range(R):
                    j = i * R + u
                    pool.wait_ge(indexed, j + 1)
                    pool.wait_ge(summed, (j + 1 + R - RS) * Q)
                    pool.sem_inc(issue, 1)
                    for s in range(Q):
                        k = u % RS * Q + s
                        nc.gpsimd.indirect_dma_start(
                            rows[:, k, 0:D], None, m.table,
                            bass.IndirectOffsetOnAxis(ap=idx[:, u * Q + s:u * Q + s + 1], axis=0)
                        ).then_inc(gathered[k], 16)

        @block.tensor
        def _(pe):
            te = nc.tensor

            def turn_in(j, u, r):
                pe.wait_ge(hot, j + 1)
                pe.wait_ge(tcopied, j + 1)
                for s in range(Q):
                    te.transpose(m.PS[:, 0, s * P:(s + 1) * P], S[:, u % RS * Q + s, :], m.ident[:])
                    mm = te.transpose(m.PS[0:EA, 1, s * P:(s + 1) * P], rec[:, u * Q + s, 0:EA], m.ident[:])
                mm.then_inc(turned, 1)

            def inner(j, u, r):
                tiles = node_tiles(nc, pe, m.tn2, j, Q)
                pe.wait_ge(tcopied, j + 2)
                pe.wait_ge(mixed, j + 1)
                for s in range(Q):
                    k = u % RS * Q + s
                    at = m.PS[:, 2 + s // 2, s % 2 * D:(s % 2 + 1) * D]
                    te.matmul(at, ST[:, k, :], tile_at(by_src, tiles[s]), start=True, stop=False)
                    mm = te.matmul(at, attT[0:EA, k, :], wa, start=False, stop=True)
                mm.then_inc(made, 1)

            def sums(j, u, r):
                pe.wait_ge(active, j + 1)
                for s in range(Q):
                    k = u % RS * Q + s
                    pe.wait_ge(added, j * Q + s + 1)
                    te.matmul(m.PS[:, 4 + s, 0:CW], S[:, k, :], rows[:, k, :], start=True, stop=True
                              ).then_inc(summed, 1)

            pe.sem_inc(summed, R * Q)
            pe.wait_ge(loaded, 16)
            pe.wait_ge(oned, 1)
            pipeline(pe, R, (2, turn_in), (1, inner), (0, sums))

        @block.vector
        def _(dve):
            v = nc.vector

            def hots(j, u, r):
                k = u % RS
                dve.wait_ge(summed, (j + 1 + R - RS) * Q)
                dve.wait_ge(came[u], r * 16 + 16)
                one_hot_rows(v, m, S[:, k * Q:(k + 1) * Q, :], rec[:, u * Q:(u + 1) * Q, EA + 1]).then_inc(hot, 1)

            def mix(j, u, r):
                k = u % RS
                for s in range(Q):
                    dve.wait_ge(gathered[k * Q + s], r * (16 * R // RS) + (u // RS + 1) * 16)
                dve.wait_ge(made, j + 1)
                at = rows[:, k * Q:(k + 1) * Q, 0:D]
                v.tensor_tensor(at, at, m.PS[:, 2:4, :].rearrange("p b (s d) -> p (b s) d", s=2), ALU.add
                                ).then_inc(mixed, 1)

            def add(j, u, r):
                tiles = node_tiles(nc, dve, m.tn2, j, Q)
                for s in range(Q):
                    dve.wait_ge(summed, (j + R) * Q + s + 1)
                    dve.wait_ge(added, (j + 1) * Q + s)
                    at = tile_at(m.AGG, tiles[s], 0, CW)
                    v.tensor_tensor(at, at, m.PS[:, 4 + s, 0:CW], ALU.add).then_inc(added, 1)

            dve.sem_inc(added, Q)
            dve.sem_inc(mixed, 1)
            pipeline(dve, R, (3, hots), (1, mix), (0, add))

    sumsT = view(m.BB, 0, KD, NP)
    b2 = view(m.BB, 12800 - D, D)
    turn(nc, m, m.AGG, sumsT)
    with Stage(nc) as st:
        loaded = st.sem("loaded")
        block = st.block()

        @block.sync
        def _(sp):
            sp.dma_start(b2, a["L2_gnn_b2"].unsqueeze(0).to_broadcast([P, D])).then_inc(loaded, 16)
            sp.wait_ge(loaded, 16)

    def message(dve, c, t, ps):
        count = tile_at(m.AGG, t, D, D + 1)
        return nc.vector.scalar_tensor_tensor(tile_at(m.AGG, t), b2, count, ps, ALU.mult, ALU.add)

    linear_nodes(nc, m, sumsT, a["L2_gnn_W2"], None, D, Finish(message))
    turn(nc, m, m.AGG, sumsT)

    with Stage(nc) as st:
        names = ("loaded", "dstep", "rowed", "staged", "made", "gated", "sread", "tanhed", "inner", "used")
        loaded, dstep, rowed, staged, made, gated, sread, tanhed, inner, used = (st.sem(s) for s in names)
        D3 = 3 * D
        wi = view(m.BB, KD * NP, KD, D3)
        wh = view(m.BB, KD * NP + KD * D3, KD, D3)
        o = KD * NP + 2 * KD * D3
        bi, bh = (m.BB[0:1, o + k * D3:o + (k + 1) * D3] for k in range(2))
        ring = view(m.WS, 0, U, 2 * KD, P)
        rz = view(m.WS, U * 512, U, 512)
        cand = view(m.AF, 0, U, D)
        gap = view(m.AF, U * D, U, D)
        block = st.block()

        @block.sync
        def _(sp):
            sp.dma_start(wi, a["L2_gnn_W_ih"].rearrange("(k p) n -> p k n", p=P)).then_inc(loaded, 16)
            sp.dma_start(wh, a["L2_gnn_W_hh"].rearrange("(k p) n -> p k n", p=P)).then_inc(loaded, 16)
            sp.dma_start(bi, a["L2_gnn_b_ih"].unsqueeze(0)).then_inc(loaded, 16)
            sp.dma_start(bh, a["L2_gnn_b_hh"].unsqueeze(0)).then_inc(loaded, 16)

        @block.scalar
        def _(act):
            with act.Fori(0, NT // U) as i:
                for s in range(U):
                    t = i * U + s
                    act.wait_ge(made, t + 1)
                    nc.scalar.copy(ring[:, s, 0:KD, :], sumsT[:, :, bass.ds(t * P, P)])
                    nc.scalar.copy(ring[:, s, KD:2 * KD, :], m.XT[:, :, bass.ds(t * P, P)]).then_inc(staged, 1)
                    act.wait_ge(made, t + 1 + U)
                    nc.scalar.activation(rz[:, s, :], m.PS[:, s % 2, :], ACT.Sigmoid).then_inc(gated, 1)
                    act.wait_ge(inner, t + 1)
                    nc.scalar.activation(cand[:, s, :], cand[:, s, :], ACT.Tanh).then_inc(tanhed, 1)

        @block.tensor
        def _(pe):
            te = nc.tensor
            pe.sem_inc(made, U)
            pe.wait_ge(loaded, 64)
            one = m.ones[0:1, :]
            with pe.Fori(0, NT // U) as i:
                for s in range(U):
                    t = i * U + s
                    pe.wait_ge(staged, t + 1)
                    free2(pe, used, s, t)
                    b0, b1 = m.PS[:, s % 2, :], m.PS[:, 2 + s % 2, :]
                    for k in range(KD):
                        te.matmul(b0, ring[:, s, k, :], wi[:, k, 0:2 * D], start=(k == 0), stop=False)
                        te.matmul(b0, ring[:, s, KD + k, :], wh[:, k, 0:2 * D], start=False, stop=False)
                    te.matmul(b0, one, bi[:, 0:2 * D], start=False, stop=False)
                    te.matmul(b0, one, bh[:, 0:2 * D], start=False, stop=True)
                    for half, (w, b, q) in enumerate(((wi, bi, 0), (wh, bh, KD))):
                        at = b1[:, half * D:(half + 1) * D]
                        for k in range(KD):
                            te.matmul(at, ring[:, s, q + k, :], w[:, k, 2 * D:D3], start=(k == 0), stop=False)
                        mm = te.matmul(at, one, b[:, 2 * D:D3], start=False, stop=True)
                    mm.then_inc(made, 1)

        @block.vector
        def _(dve):
            v, c = nc.vector, Chain(dve, dstep)
            dve.sem_inc(used, 2)
            with dve.Fori(0, NT // U) as i:
                for s in range(U):
                    t = i * U + s
                    c.at(t * 5)
                    dve.wait_ge(gated, t + 1)
                    b1 = m.PS[:, 2 + s % 2, :]
                    c.step(v.tensor_tensor(cand[:, s, :], rz[:, s, 0:D], b1[:, D:2 * D], ALU.mult))
                    c.step(v.tensor_tensor(cand[:, s, :], cand[:, s, :], b1[:, 0:D], ALU.add))
                    dve.sem_inc(used, 1)
                    dve.sem_inc(inner, 1)
                    dve.wait_ge(tanhed, t + 1)
                    c.step(v.tensor_tensor(gap[:, s, :], tile_at(m.XN, t), cand[:, s, :], ALU.subtract))
                    c.step(v.tensor_tensor(gap[:, s, :], gap[:, s, :], rz[:, s, D:2 * D], ALU.mult))
                    c.step(v.tensor_tensor(gap[:, s, :], gap[:, s, :], cand[:, s, :], ALU.add))
                    at = tile_at(m.X, t)
                    v.tensor_tensor(at, at, gap[:, s, :], ALU.add)


def one_expert(nc, m, a):
    NE, HD = 32, 64
    KH = NE * HD // P
    layernorm(nc, m, m.X, m.XN)
    turn(nc, m, m.XN, m.XT)
    w1 = view(m.AF, 0, KD, NE * HD)
    pick = m.AF[0:NE, KD * NE * HD:KD * NE * HD + KH * P]
    w2 = m.XN[:].rearrange("p t d -> p (t d)")[:, 0:KH * D].rearrange("p (k d) -> p k d", d=D)
    chosen = m.WS[0:NE, 0:NP]
    others = m.WS[0:NE, NP:2 * NP]
    b2 = m.WS[0:NE, 2 * NP:2 * NP + D]
    b1 = view(m.WS, 2 * NP + D, KH)
    high = view(m.BB, 0, 3000)

    with Stage(nc) as st:
        names = ("loaded", "staged", "made", "dstep", "passed", "turned", "taken", "read", "hot", "picked")
        loaded, staged, made, dstep, passed, turned, taken, read, hot, picked = (st.sem(s) for s in names)
        ring = view(high, 0, U, KD, P)
        wr = view(high, U * D, KD, NE)
        br = high[0:1, U * D + 64:U * D + 96]
        lg = high[:, 1400:1400 + NE]
        top = high[:, 1440:1448]
        which = high[:, 1448:1456].bitcast(U32)
        whichf = high[:, 1456:1464]
        hots = view(high, 1500, U, NE)
        block = st.block()

        @block.sync
        def _(sp):
            sp.dma_start(wr, a["L2_ffn_router_w"].rearrange("(k p) n -> p k n", p=P)).then_inc(loaded, 16)
            sp.dma_start(br, a["L2_ffn_router_b"].unsqueeze(0)).then_inc(loaded, 16)

        @block.gpsimd
        def _(pool):
            g = nc.gpsimd
            pv = pick.rearrange("p (k j) -> p k j", k=KH)
            g.memset(pick, BIG).then_inc(picked, 1)
            pool.wait_ge(picked, 1)
            g.affine_select(out=pv, in_=pv, compare_op=ALU.is_ge, fill=0.0, base=0, pattern=[[P, KH], [1, P]],
                            channel_multiplier=-HD).then_inc(picked, 1)
            pool.wait_ge(picked, 2)
            g.affine_select(out=pv, in_=pv, compare_op=ALU.is_ge, fill=0.0, base=HD - 1,
                            pattern=[[-P, KH], [-1, P]], channel_multiplier=HD).then_inc(picked, 1)

        @block.scalar
        def _(act):
            with act.Fori(0, NT // U) as i:
                for s in range(U):
                    t = i * U + s
                    act.wait_ge(made, t + 1)
                    nc.scalar.copy(ring[:, s, :, :], m.XT[:, :, bass.ds(t * P, P)]).then_inc(staged, 1)

        @block.tensor
        def _(pe):
            pe.sem_inc(made, U)
            pe.sem_inc(turned, U)
            pe.wait_ge(loaded, 32)
            with pe.Fori(0, NT // U) as i:
                for s in range(U):
                    t = i * U + s
                    pe.wait_ge(staged, t + 1)
                    pe.wait_ge(read, t + 1)
                    for k in range(KD):
                        nc.tensor.matmul(m.PS[:, s, 0:NE], ring[:, s, k, :], wr[:, k, :], start=(k == 0), stop=False)
                    nc.tensor.matmul(m.PS[:, s, 0:NE], m.ones[0:1, :], br, start=False, stop=True).then_inc(made, 1)
                for s in range(U):
                    t = i * U + s
                    pe.wait_ge(hot, t + 1)
                    free2(pe, taken, s, t)
                    nc.tensor.transpose(m.PS[0:NE, 5 + s % 2, 0:P], hots[:, s, :], m.ident[:]).then_inc(turned, 1)

        @block.vector
        def _(dve):
            v, c = nc.vector, Chain(dve, dstep)
            dve.sem_inc(read, U)
            dve.sem_inc(taken, 2)
            with dve.Fori(0, NT // U) as i:
                for s in range(U):
                    t = i * U + s
                    c.at(t * 4)
                    dve.wait_ge(made, t + 1 + U)
                    c.step(v.tensor_copy(lg, m.PS[:, s, 0:NE]))
                    dve.sem_inc(read, 1)
                    c.step(v.max(top, lg))
                    dve.sem_inc(passed, 1)
                    c.step(v.max_index(which, top, lg))
                    c.step(v.tensor_copy(whichf, which))
                    dve.wait_ge(turned, t + 1)
                    v.tensor_scalar(hots[:, s, :], m.iota[:, 0:NE], whichf[:, 0:1], None,
                                    ALU.is_equal).then_inc(hot, 1)
                for s in range(U):
                    t = i * U + s
                    dve.wait_ge(turned, t + 1 + U)
                    v.tensor_copy(chosen[:, bass.ds(t * P, P)], m.PS[0:NE, 5 + s % 2, 0:P])
                    v.tensor_scalar(others[:, bass.ds(t * P, P)], m.PS[0:NE, 5 + s % 2, 0:P], 1.0, None,
                                    ALU.subtract).then_inc(taken, 1)

    with Stage(nc) as st:
        loaded, made, active, done, taken, cstaged = (
            st.sem(s) for s in ("loaded", "made", "active", "done", "taken", "cstaged"))
        hid = view(m.BB, 0, KH, CB)
        cring = m.BB[0:NE, KH * CB:KH * CB + U * P].rearrange("p (u n) -> p u n", u=U)
        block = st.block()

        @block.sync
        def _(sp):
            for k in range(KD):
                sp.dma_start(w1[:, k, :].rearrange("p (e h) -> p e h", e=NE),
                             a["L2_ffn_W1"].rearrange("e (k p) h -> k p e h", p=P)[k]).then_inc(loaded, 16)
            sp.dma_start(w2, a["L2_ffn_W2"].rearrange("e h d -> (e h) d").rearrange("(k p) d -> p k d", p=P)
                         ).then_inc(loaded, 16)
            sp.dma_start(b1, a["L2_ffn_b1"]).then_inc(loaded, 16)
            sp.dma_start(b2, a["L2_ffn_b2"]).then_inc(loaded, 16)

        @block.tensor
        def _(pe):
            te = nc.tensor
            pe.wait_ge(loaded, 80)
            with pe.Fori(0, NT // TB) as b:
                for j in range(KH):
                    for h in range(2):
                        pe.wait_ge(active, (b * KH + j) * 2 + h + 1)
                        cols = bass.ds(b * CB + h * CH2, CH2)
                        for k in range(KD):
                            te.matmul(m.PS[:, h, 0:CH2], w1[:, k, j * P:(j + 1) * P], m.XT[:, k, cols],
                                      start=(k == 0), stop=False)
                        te.matmul(m.PS[:, h, 0:CH2], pick[:, j * P:(j + 1) * P], others[:, cols], start=False,
                                  stop=True).then_inc(made, 1)
                pe.wait_ge(active, (b + 1) * KH * 2 + 2)
                pe.wait_ge(cstaged, b + 1)
                for s in range(TB):
                    pe.wait_ge(taken, b * TB + s + 1)
                    for j in range(KH):
                        te.matmul(m.PS[:, 3 + s, 0:D], hid[:, j, s * P:(s + 1) * P], w2[:, j, :], start=(j == 0),
                                  stop=False)
                    te.matmul(m.PS[:, 3 + s, 0:D], cring[:, s, :], b2, start=False, stop=True).then_inc(done, 1)

        @block.scalar
        def _(act):
            act.sem_inc(active, 2)
            act.wait_ge(loaded, 80)
            with act.Fori(0, NT // TB) as b:
                for j in range(KH):
                    for h in range(2):
                        act.wait_ge(made, (b * KH + j) * 2 + h + 1)
                        nc.scalar.activation(hid[:, j, h * CH2:(h + 1) * CH2], m.PS[:, h, 0:CH2], ACT.Relu,
                                             bias=b1[:, j:j + 1]).then_inc(active, 1)

        @block.vector
        def _(dve):
            v = nc.vector
            dve.sem_inc(taken, U)
            with dve.Fori(0, NT // TB) as b:
                v.tensor_copy(cring.rearrange("p u n -> p (u n)"), chosen[:, bass.ds(b * CB, CB)]).then_inc(cstaged, 1)
                for s in range(TB):
                    t = b * TB + s
                    dve.wait_ge(done, t + 1)
                    at = tile_at(m.X, t)
                    v.scalar_tensor_tensor(at, m.PS[:, 3 + s, 0:D], 0.0, at, ALU.max, ALU.add).then_inc(taken, 1)



def relations(nc, m, a):
    NR, NB = 8, 4
    layernorm(nc, m, m.X, m.XN)
    turn(nc, m, m.XN, m.XT)
    IL = 16
    w = m.BB[:, 0:KD * NR * D].rearrange("p (k r d) -> p k r d", k=KD, r=NR)
    mixer = m.AF[0:IL * NB, 0:P]
    comp = m.AF[0:IL * NB, P:P + NR]
    basis = m.AF[0:IL * NB, 256:256 + NR * KD * D].rearrange("p (q d) -> p q d", d=D)

    with Stage(nc) as st:
        loaded, masked, mixed, made, taken = (st.sem(s) for s in ("loaded", "masked", "mixed", "made", "taken"))
        block = st.block()

        @block.sync
        def _(sp):
            for i in range(IL):
                sp.dma_start(comp[i * NB:(i + 1) * NB, :], a["L3_gnn_w_comp"]).then_inc(loaded, 16)
            sp.dma_start(basis, a["L3_gnn_basis"].rearrange("b i d -> (b i) d").rearrange("(q p) d -> p q d", p=IL * NB)
                         ).then_inc(loaded, 16)

        @block.gpsimd
        def _(pool):
            g = nc.gpsimd
            mv = mixer.rearrange("p (i r) -> p i r", r=NR)
            g.memset(mixer, 1.0).then_inc(masked, 1)
            pool.wait_ge(masked, 1)
            g.affine_select(out=mv, in_=mv, compare_op=ALU.is_ge, fill=0.0, base=0, pattern=[[-NB, IL], [0, NR]],
                            channel_multiplier=1).then_inc(masked, 1)
            pool.wait_ge(masked, 2)
            g.affine_select(out=mv, in_=mv, compare_op=ALU.is_ge, fill=0.0, base=NB - 1,
                            pattern=[[NB, IL], [0, NR]], channel_multiplier=-1).then_inc(masked, 1)

        @block.vector
        def _(dve):
            dve.wait_ge(masked, 3)
            dve.wait_ge(loaded, 16 * (IL + 1))
            mv = mixer.rearrange("p (i r) -> p i r", r=NR)
            nc.vector.tensor_tensor(mv, mv, comp.unsqueeze(1).to_broadcast([IL * NB, IL, NR]), ALU.mult
                                    ).then_inc(mixed, 1)
            for q in range(NR * KD):
                dve.wait_ge(made, q + 1)
                nc.vector.tensor_copy(w[:, q % KD, q // KD, :], m.PS[:, q % 4, 0:D]).then_inc(taken, 1)

        @block.tensor
        def _(pe):
            pe.wait_ge(mixed, 1)
            for q in range(NR * KD):
                if q >= 4:
                    pe.wait_ge(taken, q - 3)
                nc.tensor.matmul(m.PS[:, q % 4, 0:D], mixer, basis[:, q, :], start=True, stop=True).then_inc(made, 1)

    with Stage(nc) as st:
        staged, made, taken_a, taken_v = (st.sem(s) for s in ("staged", "made", "taken_a", "taken_v"))
        stored = st.sems("stored", U)
        ring = view(m.WS, 0, U, KD, P)
        RO = NR * D
        outs = [view(m.BB, KD * RO + s * RO, RO) if s < 4 else view(m.AF, 0, RO) for s in range(U)]
        block = st.block()
        QB = RO // 512

        @block.sync
        def _(sp):
            to = m.table_rel.rearrange("(r t p) d -> p t r d", p=P, t=NT)
            with sp.Fori(0, NT // U) as i:
                for s in range(U):
                    t = i * U + s
                    sp.wait_ge(taken_a, 2 * t + 4)
                    sp.wait_ge(taken_v, 2 * t + 4)
                    sp.dma_start(to[:, bass.ds(t, 1), :, :].rearrange("p o r d -> p (o r) d"),
                                 outs[s].rearrange("p (r d) -> p r d", r=NR)).then_inc(stored[s], 16)
            for s in range(U):
                sp.wait_ge(stored[s], 16 * (NT // U + 1))

        @block.tensor
        def _(pe):
            pe.sem_inc(made, 2 * U)
            with pe.Fori(0, NT // U) as i:
                for s in range(U):
                    t = i * U + s
                    pe.wait_ge(staged, t + 1)
                    for half, sem in ((0, taken_a), (1, taken_v)):
                        pe.wait_ge(sem, 2 * t + 2)
                        for q in range(QB // 2 * half, QB // 2 * (half + 1)):
                            for k in range(KD):
                                mm = nc.tensor.matmul(m.PS[:, q, :], ring[:, s, k, :],
                                                      w[:, k, 2 * q:2 * q + 2, :].rearrange("p r d -> p (r d)"),
                                                      start=(k == 0), stop=(k == KD - 1))
                        mm.then_inc(made, 1)

        @block.scalar
        def _(act):
            act.sem_inc(taken_a, 2)
            for s in range(U):
                act.sem_inc(stored[s], 16)
            with act.Fori(0, NT // U) as i:
                for s in range(U):
                    t = i * U + s
                    act.wait_ge(made, 2 * t + 2)
                    nc.scalar.copy(ring[:, s, :, :], m.XT[:, :, bass.ds(t * P, P)]).then_inc(staged, 1)
                    act.wait_ge(made, 2 * t + 1 + 2 * U)
                    act.wait_ge(stored[s], i * 16 + 16)
                    for q in range(2):
                        nc.scalar.copy(outs[s][:, q * 512:(q + 1) * 512], m.PS[:, q, :]).then_inc(taken_a, 1)

        @block.vector
        def _(dve):
            dve.sem_inc(taken_v, 2)
            with dve.Fori(0, NT // U) as i:
                for s in range(U):
                    t = i * U + s
                    dve.wait_ge(made, 2 * t + 2 + 2 * U)
                    dve.wait_ge(stored[s], i * 16 + 16)
                    for q in range(2, 4):
                        nc.vector.tensor_copy(outs[s][:, q * 512:(q + 1) * 512], m.PS[:, q, :]).then_inc(taken_v, 1)

    with Stage(nc) as st:
        block = st.block()

        @block.vector
        def _(dve):
            nc.vector.memset(m.AGG[:], 0.0)

    aggregate(nc, m, m.table_rel, m.rel1)
    with Stage(nc) as st:
        loaded, dstep = st.sem("loaded"), st.sem("dstep")
        bias = m.WS[:, 0:D]
        block = st.block()

        @block.sync
        def _(sp):
            sp.dma_start(bias, a["L3_gnn_bias"].unsqueeze(0).to_broadcast([P, D])).then_inc(loaded, 16)

        @block.vector
        def _(dve):
            c = Chain(dve, dstep)
            dve.wait_ge(loaded, 16)
            c.step(nc.vector.tensor_tensor(m.XN[:], m.AGG[:, :, 0:D], bias.unsqueeze(1).to_broadcast([P, NT, D]),
                                           ALU.add))
            c.step(nc.vector.scalar_tensor_tensor(m.X[:], m.XN[:], 0.0, m.X[:], ALU.max, ALU.add))


def deep_experts(nc, m, a):
    NE, HR = 6, 128
    layernorm(nc, m, m.X, m.XN)
    turn(nc, m, m.XN, m.XT)
    routed = view(m.BB, 0, 1, NP)
    with Stage(nc) as st:
        loaded, made, taken = (st.sem(s) for s in ("loaded", "made", "taken"))
        w = view(m.WS, 0, KD, HR)
        b = view(m.WS, KD * HR, 1)
        block = st.block()

        @block.sync
        def _(sp):
            sp.dma_start(w, a["L3_ffn_router_w1"].rearrange("(k p) n -> p k n", p=P)).then_inc(loaded, 16)
            sp.dma_start(b, a["L3_ffn_router_b1"]).then_inc(loaded, 16)

        @block.tensor
        def _(pe):
            pe.wait_ge(loaded, 32)
            with pe.Fori(0, NP // CH // 2) as i:
                for u in range(2):
                    n = i * 2 + u
                    pe.wait_ge(taken, n + 1)
                    for k in range(KD):
                        mm = nc.tensor.matmul(m.PS[:, u, 0:CH], w[:, k, :], m.XT[:, k, bass.ds(n * CH, CH)],
                                              start=(k == 0), stop=(k == KD - 1))
                    mm.then_inc(made, 1)

        @block.scalar
        def _(act):
            act.sem_inc(taken, 2)
            act.wait_ge(loaded, 32)
            with act.Fori(0, NP // CH // 2) as i:
                for u in range(2):
                    n = i * 2 + u
                    act.wait_ge(made, n + 1)
                    nc.scalar.activation(routed[:, 0, bass.ds(n * CH, CH)], m.PS[:, u, 0:CH], ACT.Relu, bias=b
                                         ).then_inc(taken, 1)

    gates(nc, m, a["L3_ffn_router_w2"], a["L3_ffn_router_b2"], NE, True, hidden=routed)

    with Stage(nc) as st:
        loaded, made, active, done, taken = (st.sem(s) for s in ("loaded", "made", "active", "done", "taken"))
        w = [view(m.BB, q * NE * KD * D, NE * KD, D) for q in range(3)]
        h1 = view(m.AF, 0, KD, CB)
        h2 = view(m.AF, KD * CB, KD, CB)
        b1, b2 = view(m.AF, 3000, NE, KD), view(m.AF, 3020, NE, KD)
        b3 = m.AF[0:1, 3100:3100 + NE * D]
        block = st.block()
        LAYER = KD * 2

        @block.sync
        def _(sp):
            for q in range(3):
                sp.dma_start(w[q], a[f"L3_ffn_expert_w{q + 1}"].rearrange("e (k p) n -> p (e k) n", p=P)
                             ).then_inc(loaded, 16)
            sp.dma_start(b1, a["L3_ffn_expert_b1"].rearrange("p (e k) -> p e k", k=KD)).then_inc(loaded, 16)
            sp.dma_start(b2, a["L3_ffn_expert_b2"].rearrange("p (e k) -> p e k", k=KD)).then_inc(loaded, 16)
            sp.dma_start(b3, a["L3_ffn_expert_b3"].rearrange("e d -> (e d)").unsqueeze(0)).then_inc(loaded, 16)

        @block.tensor
        def _(pe):
            te = nc.tensor
            pe.wait_ge(loaded, 96)
            with pe.Fori(0, NT // TB) as b:
                for e in range(NE):
                    for layer in range(2):
                        base = ((b * NE + e) * 2 + layer) * LAYER
                        for j in range(KD):
                            for h in range(2):
                                pe.wait_ge(active, base + j * 2 + h + 1)
                                if layer == 1 and j == 0 and h == 0:
                                    pe.wait_ge(active, base + 2)
                                for k in range(KD):
                                    src = (m.XT[:, k, bass.ds(b * CB + h * CH2, CH2)] if layer == 0
                                           else h1[:, k, h * CH2:(h + 1) * CH2])
                                    mm = te.matmul(m.PS[:, h, 0:CH2], w[layer][:, e * KD + k, j * P:(j + 1) * P], src,
                                                   start=(k == 0), stop=(k == KD - 1))
                                mm.then_inc(made, 1)
                    pe.wait_ge(active, ((b * NE + e) * 2 + 2) * LAYER + 2)
                    for s in range(TB):
                        pe.wait_ge(taken, (b * NE + e) * TB + s + 1)
                        for k in range(KD):
                            te.matmul(m.PS[:, 3 + s, 0:D], h2[:, k, s * P:(s + 1) * P], w[2][:, e * KD + k, :],
                                      start=(k == 0), stop=False)
                        te.matmul(m.PS[:, 3 + s, 0:D], m.ones[0:1, :], b3[:, e * D:(e + 1) * D], start=False,
                                  stop=True).then_inc(done, 1)

        @block.scalar
        def _(act):
            act.sem_inc(active, 2)
            act.wait_ge(loaded, 96)
            with act.Fori(0, NT // TB) as b:
                for e in range(NE):
                    for layer, (dst, bias) in enumerate(((h1, b1), (h2, b2))):
                        base = ((b * NE + e) * 2 + layer) * LAYER
                        for j in range(KD):
                            for h in range(2):
                                act.wait_ge(made, base + j * 2 + h + 1)
                                nc.scalar.activation(dst[:, j, h * CH2:(h + 1) * CH2], m.PS[:, h, 0:CH2], ACT.Relu,
                                                     bias=bias[:, e, j:j + 1]).then_inc(active, 1)

        @block.vector
        def _(dve):
            dve.sem_inc(taken, U)
            with dve.Fori(0, NT // TB) as b:
                for e in range(NE):
                    for s in range(TB):
                        t = b * TB + s
                        n = (b * NE + e) * TB + s
                        dve.wait_ge(done, n + 1)
                        dve.wait_ge(taken, n + U)
                        at = tile_at(m.X, t)
                        g = tile_at(m.gate, t, e, e + 1)
                        nc.vector.scalar_tensor_tensor(at, m.PS[:, 3 + s, 0:D], g, at, ALU.mult, ALU.add
                                                       ).then_inc(taken, 1)


def build(nc, a, out):
    with ExitStack() as ctx:
        m = setup_memory(nc, ctx)
        constants(nc, m, a["x"])
        sort_edges(nc, m, a["dst_cols"], a["dst"], a["edge_type_8_cols"], None, a["src_cols"], False)
        gin(nc, m, a)
        slice_attention(nc, m, a)
        graph_attention(nc, m, a)
        expert_pair(nc, m, a)
        sort_edges(nc, m, a["src_cols"], a["src"], None, a["edge_attr_64"], a["dst_cols"], True)
        edge_update(nc, m, a)
        one_expert(nc, m, a)
        relations(nc, m, a)
        deep_experts(nc, m, a)
        with Stage(nc) as st:
            stored = st.sem("stored")
            block = st.block()

            @block.sync
            def _(sp):
                sp.dma_start(out.rearrange("(t p) d -> p t d", p=P), m.X[:]).then_inc(stored, 16)
                sp.wait_ge(stored, 16)


EDGE_ROWS = ET * P
TURNED = ("L0_ffn_W_x", "L2_gnn_W1", "L2_gnn_W2", "L2_gnn_W_ih", "L2_gnn_W_hh", "L2_ffn_router_w", "L3_gnn_w_comp")
COLUMNS = ("L0_gnn_g0", "L0_gnn_b0", "L0_gnn_b1a", "L0_gnn_g1", "L0_gnn_bt1", "L0_gnn_b2a", "L0_gnn_g2",
           "L0_gnn_bt2", "L0_ffn_b_x", "L1_ffn_ln_g", "L1_ffn_ln_b", "L1_ffn_b1", "L2_ffn_b1", "L3_ffn_router_b1",
           "L3_ffn_expert_b1", "L3_ffn_expert_b2")


def kernel(**inputs):
    import concourse.bacc as bacc
    from concourse.bass_utils import run_bass_kernel_spmd

    def pad(a, rows, fill=0):
        return np.concatenate([a, np.full((rows - a.shape[0],) + a.shape[1:], fill, a.dtype)])

    arrays = {}
    for name, a in inputs.items():
        a = np.asarray(a)
        if name == "x":
            a = pad(a, NP)
        elif name in ("src", "dst", "edge_type_8"):
            a = pad(a, EDGE_ROWS, 0 if name == "edge_type_8" else -1)
            arrays[name + "_cols"] = np.ascontiguousarray(a.reshape(ET, P).T)
        elif name == "edge_attr_64":
            a = pad(a, EDGE_ROWS)
        elif name in TURNED:
            a = a.T
        elif name in COLUMNS:
            a = a.reshape(-1, P).T
        arrays[name] = np.ascontiguousarray(a)
    nc = bacc.Bacc("TRN2", target_bir_lowering=False, num_devices=1)
    arrays = {f"in_{k}": a for k, a in arrays.items()}
    ins = {k[3:]: nc.dram_tensor(k, a.shape, mybir.dt.from_np(a.dtype), kind="ExternalInput").ap()
           for k, a in arrays.items()}
    out = nc.dram_tensor("out", (NP, D), F32, kind="ExternalOutput").ap()
    build(nc, ins, out)
    r = run_bass_kernel_spmd(nc, [arrays], core_ids=[0])
    return r.results[0]["out"][:N]
```

```python
from contextlib import ExitStack

import numpy as np
import concourse.bass as bass
from concourse import mybir

ALU = mybir.AluOpType
ACT = mybir.ActivationFunctionType
F32 = mybir.dt.float32
BF16 = mybir.dt.bfloat16
I32 = mybir.dt.int32
U32 = mybir.dt.uint32
AX = mybir.AxisListType.X

P = 128
D = 256
KD = D // P
N = 3125
NT = -(-N // P)
NP = NT * P
E = 53125
ET = -(-E // P)
EA = 64
G = 8
Q = 4
WT = -(-(ET + NT) // (8 * Q)) * 8 * Q
WP = WT + 1
U = 5
SG = 8
AW = 264
CH = 400
CB, CH2 = 640, 320
TB = CB // P
assert TB == U
GROUPS = WT // G
ROUNDS = GROUPS // 2
QUADS = WT // Q
BLANK = 64
EPS = 1e-5
BIG = 1e30
assert NT % U == 0 and GROUPS % 2 == 0 and G % 2 == 0 and ET % SG == 0 and NP % (2 * CH) == 0


class Chain:

    def __init__(self, eng, sem):
        self.eng, self.sem, self.base, self.k = eng, sem, 0, 0

    def at(self, base):
        self.base, self.k = base, 0

    def step(self, ins):
        ins.then_inc(self.sem, 1)
        self.k += 1
        self.eng.wait_ge(self.sem, self.base + self.k)


class Stage:

    number = 0

    def __init__(self, nc):
        self.nc, self.ctx, self.handles = nc, ExitStack(), []
        Stage.number += 1

    def __enter__(self):
        return self

    def sem(self, name):
        self.handles.append(self.nc.alloc_semaphore(f"{name}_{Stage.number}"))
        return self.handles[-1]

    def sems(self, name, n):
        return [self.sem(f"{name}{i}") for i in range(n)]

    def block(self):
        return self.ctx.enter_context(self.nc.Block())

    def __exit__(self, *a):
        self.ctx.close()
        self.nc.clear_and_free_semaphores(self.handles)
        self.nc.all_engine_barrier()
        return False


def view(buf, off, *shape):
    n = 1
    for s in shape:
        n *= s
    v = buf[:, off:off + n]
    if len(shape) == 2:
        v = v.rearrange("p (a b) -> p a b", b=shape[1])
    if len(shape) == 3:
        v = v.rearrange("p (a b c) -> p a b c", b=shape[1], c=shape[2])
    return v


def tile_at(buf, t, a=0, b=D):
    return buf[:, bass.ds(t, 1), a:b].rearrange("p o d -> p (o d)")


def bcast(col, shape):
    return col.unsqueeze(len(col.shape)).to_broadcast(shape)


def one_hot_rows(v, m, S, rows):
    n = S.shape[1]
    return v.tensor_tensor(S, m.iota[:].unsqueeze(1).to_broadcast([P, n, P]), bcast(rows, [P, n, P]), ALU.is_equal)


class NodeTiles:

    def __init__(self, nc, eng, tn):
        self.nc, self.eng, self.tn, self.tiles = nc, eng, tn, None

    def of(self, j, u):
        if u % 2 == 0:
            self.tiles = node_tiles(self.nc, self.eng, self.tn[0:1, bass.ds(j * Q, 2 * Q)])
        return self.tiles[u % 2 * Q:(u % 2 + 1) * Q]


def pipeline(eng, ring, *steps):
    def turn_of(q):
        for ahead, step in steps:
            if 0 <= q + ahead < QUADS:
                step(q + ahead, (q + ahead) % ring, (q + ahead) // ring)

    for q in range(-max(ahead for ahead, _ in steps), 0):
        turn_of(q)
    with eng.Fori(0, QUADS // ring - 1) as i:
        for u in range(ring):
            for ahead, step in steps:
                step(i * ring + (u + ahead), (u + ahead) % ring, i + (u + ahead) // ring)
    for q in range(QUADS - ring, QUADS):
        turn_of(q)


def node_tiles(nc, eng, tn):
    return nc.values_load_multi_w_load_instructions(tn, engines=[eng.engine], min_val=0, max_val=NT - 1)[1]


def setup_memory(nc, ctx):
    class M:
        pass

    m = M()

    def sb(name, shape, dt=F32):
        return ctx.enter_context(nc.sbuf_tensor(name, shape, dt))

    m.X = sb("residual", [P, NT, D])
    m.XN = sb("normed", [P, NT, D])
    m.XT = sb("normed_T", [P, KD, NP])
    m.AGG = sb("sums", [P, NT, AW])
    m.BB = sb("wide", [P, 2 * NT * D])
    m.WS = sb("work", [P, 7168])
    m.PS = ctx.enter_context(nc.psum_tensor("ps", [P, 8, 512], F32))
    m.ident = sb("ident", [P, P])
    m.identb = sb("identb", [P, P], BF16)
    m.iota = sb("iota", [P, P])
    m.before = sb("before", [P, P])
    m.after = sb("after", [P, P])
    m.ones = sb("ones", [P, P])
    m.zerob = sb("zerob", [P, 160], BF16)
    m.real = sb("real", [P, NT])
    m.wiota = sb("wiota", [NT, WP])
    m.coef = sb("coef", [P, KD, 2])
    m.gate = sb("gate", [P, NT, 8])
    m.lo1 = sb("lo1", [P, WP])
    m.src1 = sb("src1", [P, WP], I32)
    m.rel1 = sb("rel1", [P, WP], I32)
    m.tn1 = sb("tn1", [1, WP], I32)
    m.tn2 = sb("tn2", [1, WP], I32)
    m.AF = m.AGG[:].rearrange("p t d -> p (t d)")
    m.rec1 = nc.dram_tensor("rec1", (P * WP, 4), F32).ap()
    m.rec2 = nc.dram_tensor("rec2", (P * WP, EA + 4), F32).ap()
    m.table = nc.dram_tensor("table", (NP, D), F32).ap()
    m.table_gat = nc.dram_tensor("table_gat", (NP, D + 4), F32).ap()
    m.table_max = nc.dram_tensor("table_max", (NP, 4), F32).ap()
    m.table_rel = nc.dram_tensor("table_rel", (8 * NP, D), F32).ap()
    return m


def constants(nc, m, x):
    with Stage(nc) as st:
        pool_step, loaded = st.sem("pool_step"), st.sem("loaded")
        block = st.block()

        @block.sync
        def _(sp):
            sp.dma_start(m.X[:], x.rearrange("(t p) d -> p t d", p=P)).then_inc(loaded, 16)
            sp.wait_ge(loaded, 16)

        @block.gpsimd
        def _(pool):
            c = Chain(pool, pool_step)
            g = nc.gpsimd
            c.step(g.memset(m.ones[:], 1.0))
            c.step(g.iota(m.iota[:], [[1, P]], base=0, channel_multiplier=0,
                          allow_small_or_imprecise_dtypes=True))
            c.step(g.iota(m.wiota[:], [[1, WP]], base=0, channel_multiplier=0,
                          allow_small_or_imprecise_dtypes=True))
            for out, op, sign in ((m.ident, ALU.is_equal, 1), (m.before, ALU.is_gt, 1), (m.after, ALU.is_gt, -1)):
                c.step(g.affine_select(out=out[:], in_=m.ones[:], compare_op=op, fill=0.0, base=0,
                                       pattern=[[-sign, P]], channel_multiplier=sign))
            c.step(g.affine_select(out=m.real[:], in_=m.ones[:, 0:NT], compare_op=ALU.is_ge, fill=0.0,
                                   base=N - 1, pattern=[[-P, NT]], channel_multiplier=-1))

        @block.vector
        def _(dve):
            dve.wait_ge(pool_step, 4)
            nc.vector.tensor_copy(m.identb[:], m.ident[:])
            nc.vector.memset(m.zerob[:], 0.0)


def sort_edges(nc, m, keys, keys_row, etype, attr, other, by_source):
    W = EA + 4 if by_source else 4
    rec = m.rec2 if by_source else m.rec1
    tn = m.tn2 if by_source else m.tn1
    GROUPS = ET // SG
    ROUNDS = GROUPS // 2
    assert GROUPS % 2 == 0
    o = 0

    def take(n, *shape):
        nonlocal o
        v = view(m.BB, o, *(shape or (n,)))
        o += n
        return v

    keyi = take(ET).bitcast(I32)
    lo_i = take(ET).bitcast(I32)
    hi_i = take(ET).bitcast(I32)
    key = take(ET)
    lo = take(ET)
    hi = take(ET)
    trash = take(ET)
    othf = take(ET)
    ty_i = take(ET).bitcast(I32)
    pay = take(ET * 4, ET, 4)
    back = take(WP * 4, WP, 4)
    counts = take(32)
    base = take(32)
    first = take(NT)
    tiles_i = take(NT).bitcast(I32)
    tiles = take(NT)
    started = take(WP)
    diagonal, start = take(NT), take(1)
    blank = view(m.AF, 0, WP, 4)
    rank = take(2 * SG, 2, SG)
    slot, slot_f, hi_f = take(SG), take(SG), take(SG)
    slot_i, hi_s = take(SG).bitcast(I32), take(SG).bitcast(I32)
    idxr = take(2 * SG, 2, SG).bitcast(I32)
    prod = take(SG * NT, SG, NT)
    snap = take(2 * SG * NT, 2, SG, NT)
    rowk = view(m.WS, 0, 2, SG * P).bitcast(I32)
    eqs = view(m.WS, 2 * SG * P, SG, P)
    payr = view(m.WS, 3 * SG * P, 2 * SG, EA + 4)
    fl = m.XN[:].rearrange("p t d -> p (t d)")
    ol = fl[:, 0:SG * P].bitcast(BF16).rearrange("p (u s e) -> p u s e", u=2, s=SG)
    oh = fl[:, 1024:1024 + SG * NT].bitcast(BF16).rearrange("p (u s e) -> p u s e", u=2, s=SG)
    olt = view(fl, 2048, 2, SG, P)

    def one_hots(v, g, u):
        v.tensor_tensor(ol[:, u], m.iota[:].unsqueeze(1).to_broadcast([P, SG, P]),
                        bcast(lo[:, bass.ds(g * SG, SG)], [P, SG, P]), ALU.is_equal)
        return v.tensor_tensor(oh[:, u], m.iota[:, 0:NT].unsqueeze(1).to_broadcast([P, SG, NT]),
                               bcast(hi[:, bass.ds(g * SG, SG)], [P, SG, NT]), ALU.is_equal)

    with Stage(nc) as st:
        loaded, blanked, stored = st.sem("loaded"), st.sem("blanked"), st.sem("stored")
        dstep, hot, used, counted = st.sem("dstep"), st.sem("hot"), st.sem("used"), st.sem("counted")
        tstep, sums, prefix = st.sem("tstep"), st.sem("sums"), st.sem("prefix")
        compared, totalled = st.sem("compared"), st.sem("totalled")
        block = st.block()

        @block.sync
        def _(sp):
            sp.dma_start(keyi, keys).then_inc(loaded, 16)
            sp.dma_start(othf.bitcast(I32), other).then_inc(loaded, 16)
            if not by_source:
                sp.dma_start(ty_i, etype).then_inc(loaded, 16)
            if not by_source:
                sp.wait_ge(blanked, 2)
                sp.dma_start(rec.rearrange("(p w) c -> p w c", p=P), blank).then_inc(stored, 16)
                sp.wait_ge(stored, 16)

        @block.gpsimd
        def _(pool):
            nc.gpsimd.memset(payr[:, :, EA:EA + 4], 0.0)
            if not by_source:
                nc.gpsimd.memset(blank, 0.0).then_inc(blanked, 1)
                pool.wait_ge(blanked, 1)
                nc.gpsimd.memset(blank[:, :, 1:2], -1.0).then_inc(blanked, 1)

        @block.vector
        def _(dve):
            v = nc.vector
            c = Chain(dve, dstep)
            dve.wait_ge(loaded, 32 if by_source else 48)
            c.step(v.tensor_scalar(hi_i, keyi, 7, None, ALU.arith_shift_right))
            c.step(v.tensor_scalar(lo_i, keyi, 127, None, ALU.bitwise_and))
            c.step(v.tensor_copy(key, keyi))
            c.step(v.tensor_copy(lo, lo_i))
            c.step(v.tensor_copy(hi, hi_i))
            c.step(v.tensor_scalar(trash, key, 0.0, float(WT * P), ALU.is_lt, ALU.mult))
            c.step(v.tensor_copy(othf, othf.bitcast(I32)))
            if not by_source:
                c.step(v.tensor_copy(pay[:, :, 0], othf))
                c.step(v.tensor_copy(pay[:, :, 1], lo))
                c.step(v.tensor_copy(pay[:, :, 3], ty_i))
                c.step(v.scalar_tensor_tensor(pay[:, :, 2], pay[:, :, 3], float(NP), othf, ALU.mult, ALU.add))
            with dve.Fori(0, ROUNDS) as i:
                for u in range(2):
                    dve.wait_ge(used, i * 2 + u + 1)
                    one_hots(v, i * 2 + u, u).then_inc(hot, 1)
            dve.wait_ge(counted, 1)
            v.tensor_copy(counts[:, 0:NT], m.PS[:, 0, 0:NT]).then_inc(sums, 1)
            dve.wait_ge(prefix, 1)
            c2 = Chain(dve, tstep)
            c2.step(v.tensor_scalar(tiles, m.PS[:, 1, 0:NT], float(P - 1), None, ALU.add))
            c2.step(v.tensor_copy(tiles_i, tiles))
            c2.step(v.tensor_scalar(tiles_i, tiles_i, 7, None, ALU.arith_shift_right))
            c2.step(v.tensor_copy(tiles, tiles_i))
            c2.step(v.tensor_tensor_scan(first, m.ones[:, 0:NT], tiles, 0.0, ALU.mult, ALU.add))
            c2.step(v.tensor_tensor(first, first, tiles, ALU.subtract))
            c2.step(v.scalar_tensor_tensor(base[:, 0:NT], first, float(P), m.PS[:, 2, 0:NT],
                                           ALU.mult, ALU.add))
            c2.step(v.tensor_tensor(diagonal, first, m.ident[:, 0:NT], ALU.mult))
            c2.step(v.reduce_sum(start, diagonal, AX))
            c2.step(v.tensor_scalar(started[0:NT, :], m.wiota[:], start[0:NT, :], None, ALU.is_ge))
            dve.sem_inc(compared, 1)
            dve.wait_ge(totalled, 1)
            c2.step(v.tensor_scalar(tn[:], m.PS[0:1, 3, 0:WP], 1.0, None, ALU.subtract))

        @block.tensor
        def _(pe):
            pe.sem_inc(used, 2)
            nc.tensor.matmul(m.PS[:, 0, 0:NT], m.zerob[:, 0:P], m.zerob[:, 0:NT], start=True, stop=False,
                             skip_group_check=True)
            with pe.Fori(0, ROUNDS) as i:
                for u in range(2):
                    pe.wait_ge(hot, i * 2 + u + 1)
                    for s in range(SG):
                        mm = nc.tensor.matmul(m.PS[:, 0, 0:NT], ol[:, u, s], oh[:, u, s], start=False, stop=False,
                                              skip_group_check=True)
                    mm.then_inc(used, 1)
            nc.tensor.matmul(m.PS[:, 0, 0:NT], m.zerob[:, 0:P], m.zerob[:, 0:NT], start=False, stop=True,
                             skip_group_check=True).then_inc(counted, 1)
            pe.wait_ge(sums, 1)
            nc.tensor.matmul(m.PS[:, 1, 0:NT], m.ones[:], counts[:, 0:NT], start=True, stop=True)
            nc.tensor.matmul(m.PS[:, 2, 0:NT], m.after[:], counts[:, 0:NT], start=True,
                             stop=True).then_inc(prefix, 1)
            pe.wait_ge(compared, 1)
            nc.tensor.matmul(m.PS[0:1, 3, 0:WP], m.ones[0:NT, 0:1], started[0:NT, :], start=True,
                             stop=True).then_inc(totalled, 1)

    with Stage(nc) as st:
        names = ("rows_used", "hot", "turned", "olt_ready", "prefixed", "snapped", "picked", "taken", "dstep",
                 "ready", "drained", "issue", "carried")
        (rows_used, hot, turned, olt_ready, prefixed, snapped, picked, taken, dstep, ready, drained, issue,
         carried) = (st.sem(s) for s in names)
        rows, arrived, sent = st.sems("rows", 2), st.sems("arrived", 2), st.sems("sent", 2 * SG)
        block = st.block()

        @block.sync
        def _(sp):
            kr = keys_row.rearrange("(i e) -> i e", e=SG * P)
            at = attr.rearrange("(t p) c -> p t c", p=P) if by_source else None

            def keys_in(g, u):
                sp.wait_ge(rows_used, g + 1)
                sp.dma_start(rowk[:, u, :], kr[bass.ds(g, 1), :].to_broadcast([P, SG * P])).then_inc(rows[u], 16)

            def attributes_in(g, u):
                if by_source:
                    sp.dma_start(payr[:, u * SG:(u + 1) * SG, 0:EA], at[:, bass.ds(g * SG, SG), :]
                                 ).then_inc(arrived[u], 16)

            sp.sem_inc(drained, 2)
            for g in range(2):
                keys_in(g, g)
                attributes_in(g, g)
            with sp.Fori(1, ROUNDS) as i:
                for u in range(2):
                    keys_in(i * 2 + u, u)
                    for s in range(SG):
                        sp.wait_ge(sent[u * SG + s], i * 16)
                    sp.sem_inc(drained, 1)
                    attributes_in(i * 2 + u, u)
            for s in range(2 * SG):
                sp.wait_ge(sent[s], ROUNDS * 16)

        @block.vector
        def _(dve):
            v = nc.vector
            c = Chain(dve, dstep)
            STEPS = 11
            dve.sem_inc(rows_used, 2)

            def front(g, u):
                one_hots(v, g, u).then_inc(hot, 1)

            def counts_so_far(g, u):
                dve.wait_ge(prefixed, g + 1)
                dve.wait_ge(carried, g + 2)
                v.tensor_tensor(snap[:, u], m.PS[:, u, 0:SG * NT].rearrange("p (s e) -> p s e", s=SG),
                                base[:, 0:NT].unsqueeze(1).to_broadcast([P, SG, NT]), ALU.add).then_inc(snapped, 1)
                dve.wait_ge(snapped, g + 1)
                v.tensor_tensor(base[:, 0:NT], base[:, 0:NT], m.PS[:, u, SG * NT:(SG + 1) * NT], ALU.add
                                ).then_inc(carried, 1)

            def ranks(i, g, u):
                dve.wait_ge(rows[u], i * 16 + 16)
                for s in range(SG):
                    ins = v.scalar_tensor_tensor(eqs[:, s], rowk[:, u, s * P:(s + 1) * P],
                                                 key[:, bass.ds(g * SG + s, 1)], m.before[:], ALU.is_equal, ALU.mult,
                                                 accum_out=rank[:, u, s:s + 1])
                c.at(g * STEPS)
                c.step(ins)
                dve.sem_inc(rows_used, 1)

            def place(g, u):
                group = bass.ds(g * SG, SG)
                dve.wait_ge(picked, g + 3)
                c.step(v.tensor_tensor(prod, m.PS[:, 4 + u, 0:SG * NT].rearrange("p (s e) -> p s e", s=SG), oh[:, u],
                                       ALU.mult))
                dve.sem_inc(taken, 1)
                c.step(v.reduce_sum(slot, prod, AX))
                c.step(v.tensor_tensor(slot, slot, rank[:, u], ALU.add))
                c.step(v.tensor_tensor(slot, slot, trash[:, group], ALU.add))
                c.step(v.tensor_copy(slot_i, slot))
                c.step(v.tensor_scalar(hi_s, slot_i, 7, None, ALU.arith_shift_right))
                c.step(v.tensor_copy(hi_f, hi_s))
                c.step(v.scalar_tensor_tensor(slot_f, hi_f, -float(P), slot, ALU.mult, ALU.add))
                c.step(v.scalar_tensor_tensor(slot_f, slot_f, float(WP), hi_f, ALU.mult, ALU.add))
                dve.wait_ge(drained, g + 1)
                if by_source:
                    v.tensor_copy(payr[:, u * SG:(u + 1) * SG, EA], othf[:, group])
                    v.tensor_copy(payr[:, u * SG:(u + 1) * SG, EA + 1], lo[:, group])
                else:
                    v.tensor_copy(payr[:, u * SG:(u + 1) * SG, 0:4], pay[:, group, :])
                c.step(v.tensor_copy(idxr[:, u, :], slot_f))
                assert c.k == STEPS
                dve.sem_inc(ready, 1)

            def two_groups(i, last=False):
                for u in range(2):
                    g = i * 2 + u
                    more = not (last and u == 1)
                    if more:
                        front(g + 1, 1 - u)
                    ranks(i, g, u)
                    place(g, u)
                    if more:
                        counts_so_far(g + 1, 1 - u)

            dve.sem_inc(carried, 2)
            dve.sem_inc(taken, 2)
            front(0, 0)
            counts_so_far(0, 0)
            with dve.Fori(0, ROUNDS - 1) as i:
                two_groups(i)
            two_groups(ROUNDS - 1, last=True)

        @block.scalar
        def _(act):
            with act.Fori(0, ROUNDS) as i:
                for u in range(2):
                    g = i * 2 + u
                    act.wait_ge(turned, g + 1)
                    act.wait_ge(picked, g + 1)
                    nc.scalar.copy(olt[:, u].rearrange("p s e -> p (s e)"), m.PS[:, 2 + u, :].bitcast(BF16)
                                   ).then_inc(olt_ready, 1)

        @block.tensor
        def _(pe):
            te = nc.tensor
            pe.sem_inc(picked, 2)

            def counts_before(g, u):
                pe.wait_ge(hot, g + 1)
                pe.wait_ge(carried, g + 1)
                te.matmul(m.PS[:, u, 0:(SG + 1) * NT], m.zerob[:, 0:P],
                          m.zerob[:, 0:NT].unsqueeze(1).to_broadcast([P, SG + 1, NT]), start=True, stop=False,
                          skip_group_check=True)
                for s in range(SG):
                    mm = te.matmul(m.PS[:, u, (s + 1) * NT:(SG + 1) * NT], ol[:, u, s],
                                   oh[:, u, s].unsqueeze(1).to_broadcast([P, SG - s, NT]), start=False,
                                   stop=(s == SG - 1), skip_group_check=True)
                mm.then_inc(prefixed, 1)
                for s in range(SG):
                    mm = te.transpose(m.PS[:, 2 + u, s * P // 2:(s + 1) * P // 2].bitcast(BF16), ol[:, u, s],
                                      m.identb[:])
                mm.then_inc(turned, 1)

            def read_counts(g, u):
                pe.wait_ge(olt_ready, g + 1)
                pe.wait_ge(snapped, g + 1)
                pe.wait_ge(taken, g + 1)
                for s in range(SG):
                    mm = te.matmul(m.PS[:, 4 + u, s * NT:(s + 1) * NT], olt[:, u, s], snap[:, u, s], start=True,
                                   stop=True)
                mm.then_inc(picked, 1)

            counts_before(0, 0)
            with pe.Fori(0, ROUNDS - 1) as i:
                for u in range(2):
                    read_counts(i * 2 + u, u)
                    counts_before(i * 2 + u + 1, 1 - u)
            read_counts(GROUPS - 2, 0)
            counts_before(GROUPS - 1, 1)
            read_counts(GROUPS - 1, 1)

        @block.gpsimd
        def _(pool):
            with pool.Fori(0, ROUNDS) as i:
                for u in range(2):
                    pool.wait_ge(ready, i * 2 + u + 1)
                    if by_source:
                        pool.wait_ge(arrived[u], i * 16 + 16)
                    pool.sem_inc(issue, 1)
                    for s in range(SG):
                        nc.gpsimd.indirect_dma_start(rec, bass.IndirectOffsetOnAxis(ap=idxr[:, u, s:s + 1], axis=0),
                                                     payr[:, u * SG + s, 0:W], None).then_inc(sent[u * SG + s], 16)

    if by_source:
        return
    with Stage(nc) as st:
        loaded = st.sem("loaded")
        block = st.block()

        @block.sync
        def _(sp):
            sp.dma_start(back, rec.rearrange("(p w) c -> p w c", p=P)).then_inc(loaded, 16)

        @block.vector
        def _(dve):
            dve.wait_ge(loaded, 16)
            nc.vector.tensor_copy(m.src1[:], back[:, :, 0])
            nc.vector.tensor_copy(m.lo1[:], back[:, :, 1])
            nc.vector.tensor_copy(m.rel1[:], back[:, :, 2])


def blank_records(nc, pool, m, buf, blanked, stored):
    W = EA + 4
    blank = view(buf, 0, BLANK, W)
    nc.gpsimd.memset(blank, 0.0).then_inc(blanked, 1)
    pool.wait_ge(blanked, 1)
    nc.gpsimd.memset(blank[:, :, EA + 1:EA + 2], -1.0).then_inc(blanked, 1)
    pool.wait_ge(blanked, 2)
    r = m.rec2.rearrange("(p w) c -> p w c", p=P)
    for n, w in enumerate(range(0, WP, BLANK)):
        if n:
            pool.wait_ge(stored, 16 * n)
        width = min(BLANK, WP - w)
        pool.dma_start(r[:, w:w + width, :], blank[:, 0:width, :]).then_inc(stored, 16)
    pool.wait_ge(stored, 16 * len(range(0, WP, BLANK)))


def layernorm(nc, m, src, dst):
    BY_ACT = 2
    with Stage(nc) as st:
        dstep, vared, rooted, shifted = (st.sem(s) for s in ("dstep", "vared", "rooted", "shifted"))
        stats, mv = view(m.WS, 0, NT, 6), view(m.WS, NT * 6, NT, 2)
        rstd, shift = (view(m.WS, NT * 8 + k * 32, 32)[:, 0:NT] for k in range(2))
        block = st.block()

        def column(a, t):
            return a[:, bass.ds(t, 1)]

        @block.vector
        def _(dve):
            v, c = nc.vector, Chain(dve, dstep)
            with dve.Fori(0, NT // U) as i:
                for s in range(U):
                    ins = v.bn_stats(tile_at(stats, i * U + s, 0, 6), tile_at(src, i * U + s))
                c.at(i)
                c.step(ins)
            c.at(NT // U)
            for t in range(NT):
                ins = v.bn_aggr(mv[:, t, :], stats[:, t, :])
            c.step(ins)
            v.tensor_scalar(rstd, mv[:, :, 1], EPS, None, ALU.add).then_inc(vared, 1)
            dve.wait_ge(rooted, 1)
            c.step(v.reciprocal(rstd, rstd))
            v.scalar_tensor_tensor(shift, mv[:, :, 0], -1.0, rstd, ALU.mult, ALU.mult).then_inc(shifted, 1)
            dve.wait_ge(shifted, 1)
            with dve.Fori(0, NT // U) as i:
                for s in range(BY_ACT, U):
                    t = i * U + s
                    v.tensor_scalar(tile_at(dst, t), tile_at(src, t), column(rstd, t), column(shift, t),
                                    ALU.mult, ALU.add)

        @block.scalar
        def _(act):
            act.wait_ge(vared, 1)
            nc.scalar.activation(rstd, rstd, ACT.Sqrt).then_inc(rooted, 1)
            act.wait_ge(shifted, 1)
            with act.Fori(0, NT // U) as i:
                for s in range(BY_ACT):
                    t = i * U + s
                    nc.scalar.activation(tile_at(dst, t), tile_at(src, t), ACT.Identity, bias=column(shift, t),
                                         scale=column(rstd, t))


def turn(nc, m, src, dst):
    with Stage(nc) as st:
        staged, turned, ps_used = (st.sem(s) for s in ("staged", "turned", "ps_used"))
        ring = view(m.WS, 0, U, D)
        block = st.block()

        @block.scalar
        def _(act):
            with act.Fori(0, NT // U) as i:
                for s in range(U):
                    t = i * U + s
                    act.wait_ge(turned, t + 1)
                    nc.scalar.copy(ring[:, s, :], tile_at(src, t)).then_inc(staged, 1)

        @block.tensor
        def _(pe):
            pe.sem_inc(turned, U)
            with pe.Fori(0, NT // U) as i:
                for s in range(U):
                    t = i * U + s
                    pe.wait_ge(staged, t + 1)
                    pe.wait_ge(ps_used, t + 1)
                    for k in range(KD):
                        mm = nc.tensor.transpose(m.PS[:, s, k * P:(k + 1) * P], ring[:, s, k * P:(k + 1) * P],
                                                 m.ident[:])
                    mm.then_inc(turned, 1)

        @block.vector
        def _(dve):
            dve.sem_inc(ps_used, U)
            with dve.Fori(0, NT // U) as i:
                for s in range(U):
                    t = i * U + s
                    dve.wait_ge(turned, t + 1 + U)
                    nc.vector.tensor_copy(dst[:, :, bass.ds(t * P, P)],
                                          m.PS[:, s, 0:D].rearrange("p (k n) -> p k n", k=KD)).then_inc(ps_used, 1)


def aggregate(nc, m, table, index):
    with Stage(nc) as st:
        indexed, hot, summed, added, issue = (st.sem(s) for s in ("indexed", "hot", "summed", "added", "issue"))
        gathered = st.sems("gathered", 2 * G)
        rows = view(m.WS, 0, 2 * G, D)
        S = view(m.WS, 2 * G * D, 2 * G, P)
        idx = view(m.WS, 2 * G * D + 2 * G * P, 2 * G).bitcast(I32)
        PAIRS = G // 2
        block = st.block()

        def bank(u, s):
            return m.PS[:, u * PAIRS + s // 2, s % 2 * D:(s % 2 + 1) * D]

        @block.scalar
        def _(act):
            with act.Fori(0, ROUNDS) as i:
                for u in range(2):
                    g = i * 2 + u
                    act.wait_ge(summed, (g + 1) * PAIRS)
                    nc.scalar.copy(idx[:, u * G:(u + 1) * G], index[:, bass.ds(g * G, G)]).then_inc(indexed, 1)

        @block.gpsimd
        def _(pool):
            with pool.Fori(0, ROUNDS) as i:
                for u in range(2):
                    pool.wait_ge(indexed, i * 2 + u + 1)
                    pool.sem_inc(issue, 1)
                    for q in range(u * G, (u + 1) * G):
                        nc.gpsimd.indirect_dma_start(rows[:, q, :], None, table,
                                                     bass.IndirectOffsetOnAxis(ap=idx[:, q:q + 1], axis=0)
                                                     ).then_inc(gathered[q], 16)

        @block.tensor
        def _(pe):
            pe.sem_inc(summed, 2 * PAIRS)
            with pe.Fori(0, ROUNDS) as i:
                for u in range(2):
                    g = i * 2 + u
                    pe.wait_ge(hot, g + 1)
                    for s in range(G):
                        q = u * G + s
                        if s % 2 == 0:
                            pe.wait_ge(added, g * G + s + 2)
                        pe.wait_ge(gathered[q], i * 16 + 16)
                        mm = nc.tensor.matmul(bank(u, s), S[:, q, :], rows[:, q, :], start=True, stop=True)
                        if s % 2 == 1:
                            mm.then_inc(summed, 1)

        @block.vector
        def _(dve):
            v = nc.vector
            dve.sem_inc(added, 2 * G)

            def hots(g, u):
                dve.wait_ge(summed, (g + 1) * PAIRS)
                one_hot_rows(v, m, S[:, u * G:(u + 1) * G, :], m.lo1[:, bass.ds(g * G, G)]).then_inc(hot, 1)

            def add(g, u):
                tiles = node_tiles(nc, dve, m.tn1[0:1, bass.ds(g * G, G)])
                for s in range(G):
                    if s % 2 == 0:
                        dve.wait_ge(summed, 2 * PAIRS + g * PAIRS + s // 2 + 1)
                    dve.wait_ge(added, 2 * G + g * G + s)
                    at = tile_at(m.AGG, tiles[s])
                    v.tensor_tensor(at, at, bank(u, s), ALU.add).then_inc(added, 1)

            hots(0, 0)
            with dve.Fori(0, ROUNDS - 1) as i:
                for u in range(2):
                    hots(i * 2 + u + 1, 1 - u)
                    add(i * 2 + u, u)
            hots(GROUPS - 1, 1)
            add(GROUPS - 2, 0)
            add(GROUPS - 1, 1)


def store_table(nc, m, src, table, sums=None):
    with Stage(nc) as st:
        stored = st.sem("stored")
        block = st.block()

        @block.sync
        def _(sp):
            sp.dma_start(table.rearrange("(t p) d -> p t d", p=P), src[:]).then_inc(stored, 16)
            sp.wait_ge(stored, 16)

        @block.vector
        def _(dve):
            if sums is None:
                nc.vector.tensor_copy(m.AGG[:, :, 0:D], src[:])
            else:
                nc.vector.memset(m.AGG[:], sums)


def free2(eng, sem, s, t):
    eng.wait_ge(sem, t + 2 if s == 0 else t + 1)


def linear_nodes(nc, m, srcT, weight, bias, width, finish):
    with Stage(nc) as st:
        loaded, staged, made, biased, taken = (st.sem(s) for s in ("loaded", "staged", "made", "biased", "taken"))
        ring = view(m.WS, 0, U, KD, P)
        w = view(m.WS, U * D, KD, width)
        b = m.WS[:, U * D + KD * width:U * D + (KD + 1) * width]
        total = view(m.WS, U * D + (KD + 1) * width, U, width)
        block = st.block()

        @block.sync
        def _(sp):
            sp.dma_start(w, weight.rearrange("(k p) n -> p k n", p=P)).then_inc(loaded, 16)
            if bias is not None:
                sp.dma_start(b, bias.unsqueeze(0).to_broadcast([P, width])).then_inc(loaded, 16)

        @block.scalar
        def _(act):
            with act.Fori(0, NT // U) as i:
                for s in range(U):
                    t = i * U + s
                    act.wait_ge(made, t + 1)
                    nc.scalar.copy(ring[:, s, :, :], srcT[:, :, bass.ds(t * P, P)]).then_inc(staged, 1)

        @block.tensor
        def _(pe):
            pe.sem_inc(made, U)
            pe.wait_ge(loaded, 32 if bias is not None else 16)
            with pe.Fori(0, NT // U) as i:
                for s in range(U):
                    t = i * U + s
                    pe.wait_ge(staged, t + 1)
                    pe.wait_ge(taken, t + 1)
                    for k in range(KD):
                        mm = nc.tensor.matmul(m.PS[:, s, 0:width], ring[:, s, k, :], w[:, k, :], start=(k == 0),
                                              stop=(k == KD - 1))
                    mm.then_inc(made, 1)

        @block.vector
        def _(dve):
            dve.sem_inc(taken, U)
            dve.wait_ge(loaded, 32 if bias is not None else 16)
            with dve.Fori(0, NT // U) as i:
                for s in range(U):
                    t = i * U + s
                    dve.wait_ge(made, t + 1 + U)
                    ps = m.PS[:, s, 0:width]
                    if bias is not None:
                        nc.vector.tensor_tensor(total[:, s, :], ps, b, ALU.add).then_inc(biased, 1)
                        dve.wait_ge(biased, t + 1)
                        ps = total[:, s, :]
                    finish(t, ps).then_inc(taken, 1)



def batch_stats(nc, m, zT, gamma, beta):
    with Stage(nc) as st:
        loaded, dstep, vared, rooted = (st.sem(s) for s in ("loaded", "dstep", "vared", "rooted"))
        cuts = [(a, min(a + 512, N)) for a in range(0, N, 512)]
        stats = view(m.WS, 0, KD, 6 * len(cuts))
        mv = view(m.WS, 200, KD, 2)
        gb = view(m.WS, 210, 2, KD)
        std = view(m.WS, 220, KD)
        block = st.block()

        @block.sync
        def _(sp):
            sp.dma_start(gb[:, 0, :], gamma).then_inc(loaded, 16)
            sp.dma_start(gb[:, 1, :], beta).then_inc(loaded, 16)

        @block.vector
        def _(dve):
            v, c = nc.vector, Chain(dve, dstep)
            for k in range(KD):
                for j, (a, b) in enumerate(cuts):
                    ins = v.bn_stats(stats[:, k, 6 * j:6 * j + 6], zT[:, k, a:b])
            c.step(ins)
            for k in range(KD):
                ins = v.bn_aggr(mv[:, k, :], stats[:, k, :])
            c.step(ins)
            v.tensor_scalar(std, mv[:, :, 1], EPS, None, ALU.add).then_inc(vared, 1)
            dve.wait_ge(rooted, 1)
            c.step(v.reciprocal(std, std))
            dve.wait_ge(loaded, 32)
            c.step(v.tensor_tensor(m.coef[:, :, 0], std, gb[:, 0, :], ALU.mult))
            c.step(v.tensor_tensor(std, mv[:, :, 0], m.coef[:, :, 0], ALU.mult))
            c.step(v.tensor_tensor(m.coef[:, :, 1], gb[:, 1, :], std, ALU.subtract))

        @block.scalar
        def _(act):
            act.wait_ge(vared, 1)
            nc.scalar.activation(std, std, ACT.Sqrt).then_inc(rooted, 1)


def normalise_nodes(nc, m, zT, dst):
    with Stage(nc) as st:
        scaled, turned, taken = (st.sem(s) for s in ("scaled", "turned", "taken"))
        ring = view(m.WS, 0, U, KD, P)
        block = st.block()

        @block.scalar
        def _(act):
            with act.Fori(0, NT // U) as i:
                for s in range(U):
                    t = i * U + s
                    act.wait_ge(turned, t + 1)
                    for k in range(KD):
                        ins = nc.scalar.activation(ring[:, s, k, :], zT[:, k, bass.ds(t * P, P)], ACT.Identity,
                                                   bias=m.coef[:, k, 1:2], scale=m.coef[:, k, 0:1])
                    ins.then_inc(scaled, 1)

        @block.tensor
        def _(pe):
            pe.sem_inc(turned, U)
            with pe.Fori(0, NT // U) as i:
                for s in range(U):
                    t = i * U + s
                    pe.wait_ge(scaled, t + 1)
                    pe.wait_ge(taken, t + 1)
                    for k in range(KD):
                        mm = nc.tensor.transpose(m.PS[:, s, k * P:(k + 1) * P], ring[:, s, k, :], m.ident[:])
                    mm.then_inc(turned, 1)

        @block.vector
        def _(dve):
            dve.sem_inc(taken, U)
            with dve.Fori(0, NT // U) as i:
                for s in range(U):
                    t = i * U + s
                    dve.wait_ge(turned, t + 1 + U)
                    nc.vector.tensor_copy(tile_at(dst, t), m.PS[:, s, 0:D]).then_inc(taken, 1)


def linear_features(nc, m, srcT, weight, bias, dstT):
    with Stage(nc) as st:
        loaded, made, taken = (st.sem(s) for s in ("loaded", "made", "taken"))
        w = view(m.WS, 0, KD, D)
        b = view(m.WS, KD * D, KD)
        block = st.block()

        @block.sync
        def _(sp):
            sp.dma_start(w, weight.rearrange("(k p) n -> p k n", p=P)).then_inc(loaded, 16)
            sp.dma_start(b, bias).then_inc(loaded, 16)

        @block.tensor
        def _(pe):
            pe.wait_ge(loaded, 32)
            with pe.Fori(0, NP // CH // 2) as i:
                for u in range(2):
                    for j in range(KD):
                        n = (i * 2 + u) * KD + j
                        pe.wait_ge(taken, n + 1)
                        for k in range(KD):
                            mm = nc.tensor.matmul(m.PS[:, u * KD + j, 0:CH], w[:, k, j * P:(j + 1) * P],
                                                  srcT[:, k, bass.ds((i * 2 + u) * CH, CH)], start=(k == 0),
                                                  stop=(k == KD - 1))
                        mm.then_inc(made, 1)

        @block.scalar
        def _(act):
            act.sem_inc(taken, 2 * KD)
            act.wait_ge(loaded, 32)
            with act.Fori(0, NP // CH // 2) as i:
                for u in range(2):
                    for j in range(KD):
                        n = (i * 2 + u) * KD + j
                        act.wait_ge(made, n + 1)
                        nc.scalar.activation(dstT[:, j, bass.ds((i * 2 + u) * CH, CH)], m.PS[:, u * KD + j, 0:CH],
                                             ACT.Identity, bias=b[:, j:j + 1]).then_inc(taken, 1)


def gin_output(nc, m, zT, weight, bias, into_residual):
    with Stage(nc) as st:
        loaded, scaled, made, biased, taken = (st.sem(s) for s in ("loaded", "scaled", "made", "biased", "taken"))
        ring = view(m.WS, 0, U, KD, P)
        w = view(m.WS, U * D, KD, D)
        b = m.WS[:, U * D + KD * D:U * D + (KD + 1) * D]
        total = view(m.WS, U * D + (KD + 1) * D, U, D)
        block = st.block()

        @block.sync
        def _(sp):
            sp.dma_start(w, weight.rearrange("(k p) n -> p k n", p=P)).then_inc(loaded, 16)
            sp.dma_start(b, bias.unsqueeze(0).to_broadcast([P, D])).then_inc(loaded, 16)

        @block.scalar
        def _(act):
            with act.Fori(0, NT // U) as i:
                for s in range(U):
                    t = i * U + s
                    act.wait_ge(made, t + 1)
                    for k in range(KD):
                        ins = nc.scalar.activation(ring[:, s, k, :], zT[:, k, bass.ds(t * P, P)], ACT.Relu,
                                                   bias=m.coef[:, k, 1:2], scale=m.coef[:, k, 0:1])
                    ins.then_inc(scaled, 1)

        @block.tensor
        def _(pe):
            pe.sem_inc(made, U)
            pe.wait_ge(loaded, 32)
            with pe.Fori(0, NT // U) as i:
                for s in range(U):
                    t = i * U + s
                    pe.wait_ge(scaled, t + 1)
                    pe.wait_ge(taken, t + 1)
                    for k in range(KD):
                        mm = nc.tensor.matmul(m.PS[:, s, 0:D], ring[:, s, k, :], w[:, k, :], start=(k == 0),
                                              stop=(k == KD - 1))
                    mm.then_inc(made, 1)

        @block.vector
        def _(dve):
            dve.sem_inc(taken, U)
            dve.wait_ge(loaded, 32)
            with dve.Fori(0, NT // U) as i:
                for s in range(U):
                    t = i * U + s
                    dve.wait_ge(made, t + 1 + U)
                    nc.vector.tensor_tensor(total[:, s, :], m.PS[:, s, 0:D], b, ALU.add).then_inc(biased, 1)
                    dve.wait_ge(biased, t + 1)
                    if into_residual:
                        at = tile_at(m.X, t)
                        ins = nc.vector.scalar_tensor_tensor(at, total[:, s, :], 0.0, at, ALU.max, ALU.add)
                    else:
                        ins = nc.vector.tensor_scalar(tile_at(m.XN, t), total[:, s, :], 0.0, None, ALU.max)
                    ins.then_inc(taken, 1)


def gin(nc, m, a):
    zT = view(m.BB, 0, KD, NP)
    layernorm(nc, m, m.X, m.XN)
    turn(nc, m, m.XN, m.XT)
    batch_stats(nc, m, m.XT, a["L0_gnn_g0"], a["L0_gnn_b0"])
    normalise_nodes(nc, m, m.XT, m.XN)
    for conv, last in (("1", False), ("2", True)):
        store_table(nc, m, m.XN, m.table)
        aggregate(nc, m, m.table, m.src1)
        turn(nc, m, m.AGG, m.XT)
        linear_features(nc, m, m.XT, a[f"L0_gnn_W{conv}a"], a[f"L0_gnn_b{conv}a"], zT)
        batch_stats(nc, m, zT, a[f"L0_gnn_g{conv}"], a[f"L0_gnn_bt{conv}"])
        gin_output(nc, m, zT, a[f"L0_gnn_W{conv}b"], a[f"L0_gnn_b{conv}b"], last)


def slice_attention(nc, m, a):
    H, C, QG = 8, 64, 64
    PR = H // 2
    HW = H * QG
    layernorm(nc, m, m.X, m.XN)
    turn(nc, m, m.XN, m.XT)
    weights = view(m.BB, 0, NT, HW)
    o = 0

    def take(*shape):
        nonlocal o
        v = view(m.AF, o, *shape)
        n = 1
        for k in shape:
            n *= k
        o += n
        return v

    w_fx, w_xs = take(KD, HW), take(KD, HW)
    w_xT, w_out, w_mix = take(PR, D), take(PR, D), take(PR, D)
    w_sl = take(P)
    b_fx, b_xs = take(HW), take(HW)
    xn = m.XN[:].rearrange("p t d -> p (t d)")
    w_q, w_k, w_v = (xn[:, k * P:(k + 1) * P] for k in range(3))
    b_x = xn[:, 384:384 + PR]
    temp = xn[:, 400:408]
    b_sl = xn[:, 416:480]
    b_out = xn[:, 512:768]
    tok, tokT, qT, kT, vv, att, attT, oT = (view(xn, 1024 + 512 * k, PR, P) for k in range(8))
    small = view(xn, 5200, 8, 8)

    with Stage(nc) as st:
        zeroed, loaded, dstep, folded = (st.sem(s) for s in ("zeroed", "loaded", "dstep", "folded"))
        block = st.block()
        LOADS = 8 + 5

        @block.gpsimd
        def _(pool):
            for w in (w_sl, w_q, w_k, w_v):
                nc.gpsimd.memset(w, 0.0).then_inc(zeroed, 1)

        @block.sync
        def _(sp):
            sp.wait_ge(zeroed, 4)
            for w, name in ((w_sl, "W_slice"), (w_q, "W_q"), (w_k, "W_k"), (w_v, "W_v")):
                for h in range(2):
                    sp.dma_start(w[h * C:(h + 1) * C, h * C:(h + 1) * C], a["L0_ffn_" + name]).then_inc(loaded, 16)
            sp.dma_start(w_xT, a["L0_ffn_W_x"].rearrange("(r p) d -> p r d", p=P)).then_inc(loaded, 16)
            sp.dma_start(b_x, a["L0_ffn_b_x"]).then_inc(loaded, 16)
            sp.dma_start(temp, a["L0_ffn_temperature"].rearrange("a h b c -> a (h b c)").to_broadcast([P, H])
                         ).then_inc(loaded, 16)
            sp.dma_start(b_sl[0:1, :], a["L0_ffn_b_slice"].unsqueeze(0)).then_inc(loaded, 16)
            sp.dma_start(w_fx, a["L0_ffn_W_fx"].rearrange("(k p) n -> p k n", p=P)).then_inc(loaded, 16)

        @block.tensor
        def _(pe):
            pe.wait_ge(loaded, 16 * LOADS)
            for r in range(PR):
                for k in range(KD):
                    nc.tensor.matmul(m.PS[:, k, r * P:(r + 1) * P], w_xT[:, r, k * P:(k + 1) * P], w_sl,
                                     start=True, stop=True)
                mm = nc.tensor.matmul(m.PS[0:1, KD, r * P:(r + 1) * P], b_x[:, r:r + 1], w_sl,
                                      start=True, stop=True)
            mm.then_inc(folded, 1)

        @block.vector
        def _(dve):
            v, c = nc.vector, Chain(dve, dstep)
            dve.wait_ge(loaded, 16 * LOADS)
            c.step(v.tensor_scalar(temp, temp, 0.1, 5.0, ALU.max, ALU.min))
            c.step(v.reciprocal(temp, temp))
            dve.wait_ge(folded, 1)
            for k in range(KD):
                v.tensor_tensor(w_xs[:, k, :].rearrange("p (h g) -> p h g", h=H),
                                m.PS[:, k, :].rearrange("p (h g) -> p h g", h=H), bcast(temp, [P, H, QG]), ALU.mult)
            row = b_xs[0:1, :].rearrange("p (h g) -> p h g", h=H)
            c.step(v.tensor_tensor(row, m.PS[0:1, KD, :].rearrange("p (h g) -> p h g", h=H),
                                   b_sl[0:1, :].unsqueeze(1).to_broadcast([1, H, QG]), ALU.add))
            c.step(v.tensor_tensor(row, row, bcast(temp[0:1, :], [1, H, QG]), ALU.mult))

    FW = C * 2 + 1
    with Stage(nc) as st:
        names = ("loaded", "staged", "scored", "read", "centred", "expd", "weighted", "fxed", "fxcopied", "summed",
                 "kept", "dstep", "oned", "outed")
        (loaded, staged, scored, read, centred, expd, weighted, fxed, fxcopied, summed, kept, dstep, oned,
         outed) = (st.sem(s) for s in names)
        ring = view(m.WS, 0, U, KD, P)
        sw = view(m.WS, U * D, U, HW)
        fx = m.WS[:, U * D + U * HW:U * D + U * HW + U * PR * FW].rearrange("p (u r f) -> p u r f", u=U, r=PR)
        mx = view(xn, 5200, 8)
        den = view(xn, 5216, 8)
        block = st.block()

        @block.sync
        def _(sp):
            sp.dma_start(b_fx, a["L0_ffn_b_fx"].unsqueeze(0).to_broadcast([P, HW])).then_inc(loaded, 16)
            sp.dma_start(w_out, a["L0_ffn_W_out"].rearrange("(r p) d -> p r d", p=P)).then_inc(loaded, 16)
            sp.dma_start(b_out, a["L0_ffn_b_out"].unsqueeze(0).to_broadcast([P, D])).then_inc(loaded, 16)
            sp.wait_ge(loaded, 48)

        @block.gpsimd
        def _(pool):
            for s in range(U):
                ins = nc.gpsimd.memset(fx[:, s, :, FW - 1], 1.0)
            ins.then_inc(oned, 1)

        @block.scalar
        def _(act):
            act.sem_inc(fxcopied, 2)

            def stage(i, s):
                act.wait_ge(summed, i * U + s + 1)
                nc.scalar.copy(ring[:, s, :, :], m.XT[:, :, bass.ds((i * U + s) * P, P)]).then_inc(staged, 1)

            def keep(i, s):
                act.wait_ge(weighted, i * U + s + 1)
                nc.scalar.copy(weights[:, bass.ds(i * U + s, 1), :].rearrange("p o d -> p (o d)"), sw[:, s, :]
                               ).then_inc(kept, 1)

            with act.Fori(0, NT // U) as i:
                stage(i, 0)
                for s in range(U):
                    t = i * U + s
                    if s < U - 1:
                        stage(i, s + 1)
                    act.wait_ge(centred, t + 1)
                    nc.scalar.activation(sw[:, s, :], sw[:, s, :], ACT.Exp).then_inc(expd, 1)
                    act.wait_ge(fxed, t + 1)
                    nc.scalar.copy(fx[:, s, :, 0:FW - 1], m.PS[:, 2 + s % 2, :].rearrange("p (r f) -> p r f", r=PR)
                                   ).then_inc(fxcopied, 1)
                    if s:
                        keep(i, s - 1)
                keep(i, U - 1)

        @block.tensor
        def _(pe):
            pe.sem_inc(summed, U)
            pe.wait_ge(loaded, 48)
            pe.wait_ge(oned, 1)
            for r in range(PR):
                nc.tensor.matmul(m.PS[:, 4 + r, 0:FW], m.zerob[:, 0:P], m.zerob[:, 0:FW], start=True, stop=False,
                                 skip_group_check=True)

            def tokens(i, s):
                t = i * U + s
                pe.wait_ge(weighted, t + 1)
                pe.wait_ge(fxcopied, t + 3)
                for r in range(PR):
                    mm = nc.tensor.matmul(m.PS[:, 4 + r, 0:FW], sw[:, s, r * P:(r + 1) * P], fx[:, s, r, :],
                                          start=False, stop=False, skip_group_check=True)
                mm.then_inc(summed, 1)

            with pe.Fori(0, NT // U) as i:
                for s in range(U):
                    t = i * U + s
                    pe.wait_ge(staged, t + 1)
                    free2(pe, read, s, t)
                    for k in range(KD):
                        nc.tensor.matmul(m.PS[:, s % 2, :], ring[:, s, k, :], w_xs[:, k, :], start=(k == 0),
                                         stop=False)
                    nc.tensor.matmul(m.PS[:, s % 2, :], m.ones[0:1, :], b_xs[0:1, :], start=False,
                                     stop=True).then_inc(scored, 1)
                    free2(pe, fxcopied, s, t)
                    for k in range(KD):
                        mm = nc.tensor.matmul(m.PS[:, 2 + s % 2, :], ring[:, s, k, :], w_fx[:, k, :],
                                              start=(k == 0), stop=(k == KD - 1))
                    mm.then_inc(fxed, 1)
                    if s:
                        tokens(i, s - 1)
                tokens(i, U - 1)

            for r in range(PR):
                mm = nc.tensor.matmul(m.PS[:, 4 + r, 0:FW], m.zerob[:, 0:P], m.zerob[:, 0:FW], start=False,
                                      stop=True, skip_group_check=True)
            mm.then_inc(outed, 1)

        @block.vector
        def _(dve):
            v, c = nc.vector, Chain(dve, dstep)
            dve.sem_inc(read, 2)
            dve.sem_inc(kept, U)
            with dve.Fori(0, NT // U) as i:
                for s in range(U):
                    t = i * U + s
                    c.at(t * 5)
                    dve.wait_ge(scored, t + 1)
                    ps = m.PS[:, s % 2, :].rearrange("p (h g) -> p h g", h=H)
                    at = sw[:, s, :].rearrange("p (h g) -> p h g", h=H)
                    c.step(v.reduce_max(mx, ps, AX))
                    dve.wait_ge(summed, t + 1)
                    dve.wait_ge(kept, t + 1)
                    c.step(v.tensor_tensor(at, ps, bcast(mx, [P, H, QG]), ALU.subtract))
                    dve.sem_inc(read, 1)
                    dve.sem_inc(centred, 1)
                    dve.wait_ge(expd, t + 1)
                    c.step(v.reduce_sum(den, at, AX))
                    c.step(v.reciprocal(den, den))
                    c.step(v.tensor_scalar(den, den, m.real[:, bass.ds(t, 1)], None, ALU.mult))
                    v.tensor_tensor(at, at, bcast(den, [P, H, QG]), ALU.mult).then_inc(weighted, 1)
            dve.wait_ge(outed, 1)

    with Stage(nc) as st:
        dstep, zeroed, made, expd, copied = (st.sem(s) for s in ("dstep", "zeroed", "made", "expd", "copied"))
        rn = small[:, 0, 0:PR]
        mx = small[:, 1, 0:PR]
        den = small[:, 2, 0:PR]
        SCALE = C ** -0.5
        halves = [slice(h * C, (h + 1) * C) for h in range(2)]
        bank = [m.PS[:, b, :].rearrange("p (r f) -> p r f", r=PR) for b in range(8)]
        block = st.block()

        @block.gpsimd
        def _(pool):
            nc.gpsimd.memset(tok, 0.0).then_inc(zeroed, 1)
            nc.gpsimd.memset(att, 0.0).then_inc(zeroed, 1)

        @block.vector
        def _(dve):
            v, c = nc.vector, Chain(dve, dstep)
            dve.wait_ge(zeroed, 2)
            c.step(v.tensor_scalar(rn, m.PS[:, 4:8, FW - 1], 1e-5, None, ALU.add))
            c.step(v.reciprocal(rn, rn))
            bias = b_fx.rearrange("p (r f) -> p r f", r=PR)
            for h in halves:
                norm = m.PS[h, 4:8, FW - 1:FW].to_broadcast([C, PR, C])
                c.step(v.tensor_tensor(tok[h, :, h], bias[h, :, h], norm, ALU.mult))
                c.step(v.tensor_tensor(tok[h, :, h], tok[h, :, h], m.PS[h, 4:8, h], ALU.add))
                c.step(v.tensor_tensor(tok[h, :, h], tok[h, :, h], bcast(rn[h, :], [C, PR, C]), ALU.mult))
            dve.sem_inc(copied, 1)
            n = 0

            def copy(outs):
                nonlocal n
                n += 1
                dve.wait_ge(made, n)
                for dst, b in outs:
                    ins = v.tensor_copy(dst, bank[b])
                ins.then_inc(copied, 1)

            copy([(tokT, 0)])
            copy([(qT, 1), (kT, 2), (vv, 3)])
            n += 1
            dve.wait_ge(made, n)
            for h in halves:
                c.step(v.reduce_max(mx[h, :], bank[0][h, :, h], AX))
                c.step(v.tensor_tensor(att[h, :, h], bank[0][h, :, h], bcast(mx[h, :], [C, PR, C]), ALU.subtract))
            dve.sem_inc(copied, 1)
            dve.wait_ge(expd, 2)
            for h in halves:
                c.step(v.reduce_sum(den[h, :], att[h, :, h], AX))
                c.step(v.reciprocal(den[h, :], den[h, :]))
                c.step(v.tensor_tensor(att[h, :, h], att[h, :, h], bcast(den[h, :], [C, PR, C]), ALU.mult))
            dve.sem_inc(copied, 1)
            copy([(attT, 4)])
            copy([(oT, 5)])
            n += 1
            dve.wait_ge(made, n)
            for r in range(PR):
                ins = v.tensor_copy(w_mix[:, r, :], m.PS[:, 6 + r // 2, (r % 2) * D:(r % 2 + 1) * D])

        @block.scalar
        def _(act):
            act.wait_ge(copied, 4)
            for h in halves:
                nc.scalar.activation(att[h, :, h], att[h, :, h], ACT.Exp, scale=SCALE).then_inc(expd, 1)

        @block.tensor
        def _(pe):
            te = nc.tensor
            pe.wait_ge(copied, 1)
            for r in range(PR):
                mm = te.transpose(bank[0][:, r, :], tok[:, r, :], m.ident[:])
            mm.then_inc(made, 1)
            pe.wait_ge(copied, 2)
            te.matmul(bank[1], w_q, tokT, start=True, stop=True)
            te.matmul(bank[2], w_k, tokT, start=True, stop=True)
            for r in range(PR):
                mm = te.matmul(bank[3][:, r, :], tokT[:, r, :], w_v, start=True, stop=True)
            mm.then_inc(made, 1)
            pe.wait_ge(copied, 3)
            for r in range(PR):
                mm = te.matmul(bank[0][:, r, :], qT[:, r, :], kT[:, r, :], start=True, stop=True)
            mm.then_inc(made, 1)
            pe.wait_ge(copied, 5)
            for r in range(PR):
                mm = te.transpose(bank[4][:, r, :], att[:, r, :], m.ident[:])
            mm.then_inc(made, 1)
            pe.wait_ge(copied, 6)
            for r in range(PR):
                mm = te.matmul(bank[5][:, r, :], vv[:, r, :], attT[:, r, :], start=True, stop=True)
            mm.then_inc(made, 1)
            pe.wait_ge(copied, 7)
            for r in range(PR):
                mm = te.matmul(m.PS[:, 6 + r // 2, (r % 2) * D:(r % 2 + 1) * D], oT[:, r, :], w_out[:, r, :],
                               start=True, stop=True)
            mm.then_inc(made, 1)

    with Stage(nc) as st:
        names = ("staged", "turned", "copied", "made", "biased", "taken")
        staged, turned, copied, made, biased, taken = (st.sem(s) for s in names)
        ring = view(m.WS, 0, U, HW)
        ringT = view(m.WS, U * HW, U, HW)
        total = view(m.WS, 2 * U * HW, U, D)
        block = st.block()

        @block.scalar
        def _(act):
            with act.Fori(0, NT // U) as i:
                for s in range(U):
                    t = i * U + s
                    act.wait_ge(turned, t + 1)
                    nc.scalar.copy(ring[:, s, :], weights[:, bass.ds(t, 1), :].rearrange("p o d -> p (o d)")
                                   ).then_inc(staged, 1)

        @block.tensor
        def _(pe):
            pe.sem_inc(turned, U)
            with pe.Fori(0, NT // U) as i:
                for s in range(U + 1):
                    t = i * U + s
                    if s < U:
                        pe.wait_ge(staged, t + 1)
                        free2(pe, copied, s, t)
                        for r in range(PR):
                            mm = nc.tensor.transpose(m.PS[:, s % 2, r * P:(r + 1) * P], ring[:, s, r * P:(r + 1) * P],
                                                     m.ident[:])
                        mm.then_inc(turned, 1)
                    if s > 0:
                        q = s - 1
                        pe.wait_ge(copied, t + 2)
                        free2(pe, taken, q, t - 1)
                        for r in range(PR):
                            mm = nc.tensor.matmul(m.PS[:, 2 + q % 2, 0:D], ringT[:, q, r * P:(r + 1) * P],
                                                  w_mix[:, r, :], start=(r == 0), stop=(r == PR - 1))
                        mm.then_inc(made, 1)

        @block.vector
        def _(dve):
            dve.sem_inc(copied, 2)
            dve.sem_inc(taken, 2)
            dve.sem_inc(made, U)
            with dve.Fori(0, NT // U) as i:
                for s in range(U + 1):
                    t = i * U + s
                    if s < U:
                        dve.wait_ge(turned, t + 1 + U)
                        dve.wait_ge(made, t + 1)
                        nc.vector.tensor_copy(ringT[:, s, :], m.PS[:, s % 2, :]).then_inc(copied, 1)
                    if s > 0:
                        q = s - 1
                        dve.wait_ge(made, t + U)
                        at = tile_at(m.X, t - 1)
                        nc.vector.tensor_tensor(total[:, q, :], m.PS[:, 2 + q % 2, 0:D], b_out, ALU.add
                                                ).then_inc(biased, 1)
                        dve.wait_ge(biased, t)
                        nc.vector.tensor_tensor(at, at, total[:, q, :], ALU.add).then_inc(taken, 1)



def graph_attention(nc, m, a):
    H, C = 4, 64
    RW = D + H
    layernorm(nc, m, m.X, m.XN)
    turn(nc, m, m.XN, m.XT)
    node = m.BB[:, 0:NT * 8].rearrange("p (t c) -> p t c", c=8)
    src_score = m.BB[:, 256:256 + NT * H].rearrange("p (t c) -> p t c", c=H)
    best = m.BB[:, 384:384 + NT * H].rearrange("p (t c) -> p t c", c=H)
    high = m.BB[:, 512:]

    with Stage(nc) as st:
        (loaded, staged, made, copied, rowed, dstep, tabled) = (
            st.sem(s) for s in ("loaded", "staged", "made", "copied", "rowed", "dstep", "tabled"))
        stored = st.sems("stored", U)
        ring = view(m.WS, 0, U, KD, P)
        row = view(m.WS, U * D, U, RW)
        w = view(m.WS, U * D + U * RW, KD, D)
        o = U * D + U * RW + KD * D
        att = [m.WS[:, o + k * D:o + (k + 1) * D] for k in range(2)]
        tmp = m.WS[:, o + 2 * D:o + 3 * D]
        block = st.block()

        @block.sync
        def _(sp):
            sp.dma_start(w, a["L1_gnn_W"].rearrange("(k p) n -> p k n", p=P)).then_inc(loaded, 16)
            for k, name in enumerate(("L1_gnn_att_src", "L1_gnn_att_dst")):
                sp.dma_start(att[k], a[name].rearrange("h c -> (h c)").unsqueeze(0).to_broadcast([P, D])
                             ).then_inc(loaded, 16)
            to = m.table_gat.rearrange("(t p) c -> p t c", p=P)
            with sp.Fori(0, NT // U) as i:
                for s in range(U):
                    t = i * U + s
                    sp.wait_ge(rowed, t + 1)
                    sp.dma_start(to[:, bass.ds(t, 1), :].rearrange("p o c -> p (o c)"), row[:, s, :]
                                 ).then_inc(stored[s], 16)
            for s in range(U):
                sp.wait_ge(stored[s], 16 * (NT // U + 1))
            sp.dma_start(m.table_max.rearrange("(t p) c -> p t c", p=P), src_score).then_inc(tabled, 16)
            sp.wait_ge(tabled, 16)

        @block.scalar
        def _(act):
            act.sem_inc(copied, U)
            for s in range(U):
                act.sem_inc(stored[s], 16)
            with act.Fori(0, NT // U) as i:
                for s in range(U):
                    t = i * U + s
                    act.wait_ge(made, t + 1)
                    nc.scalar.copy(ring[:, s, :, :], m.XT[:, :, bass.ds(t * P, P)]).then_inc(staged, 1)
                    act.wait_ge(made, t + 1 + U)
                    act.wait_ge(stored[s], i * 16 + 16)
                    nc.scalar.copy(row[:, s, 0:D], m.PS[:, s, 0:D]).then_inc(copied, 1)

        @block.tensor
        def _(pe):
            pe.sem_inc(made, U)
            pe.wait_ge(loaded, 48)

            with pe.Fori(0, NT // U) as i:
                for s in range(U):
                    t = i * U + s
                    pe.wait_ge(staged, t + 1)
                    pe.wait_ge(copied, t + 1)
                    for k in range(KD):
                        mm = nc.tensor.matmul(m.PS[:, s, 0:D], ring[:, s, k, :], w[:, k, :], start=(k == 0),
                                              stop=(k == KD - 1))
                    mm.then_inc(made, 1)

        @block.vector
        def _(dve):
            v, c = nc.vector, Chain(dve, dstep)
            dve.wait_ge(loaded, 48)
            with dve.Fori(0, NT // U) as i:
                for s in range(U):
                    t = i * U + s
                    c.at(t * 4)
                    dve.wait_ge(copied, t + 1 + U)
                    ps = row[:, s, 0:D]
                    heads = tmp.rearrange("p (h c) -> p h c", h=H)
                    c.step(v.tensor_tensor(tmp, ps, att[0], ALU.mult))
                    c.step(v.reduce_sum(row[:, s, D:RW], heads, AX))
                    c.step(v.tensor_tensor(tmp, ps, att[1], ALU.mult))
                    c.step(v.reduce_sum(tile_at(node, t, 0, H), heads, AX))
                    v.tensor_copy(tile_at(src_score, t, 0, H), row[:, s, D:RW]).then_inc(rowed, 1)

    with Stage(nc) as st:
        names = ("indexed", "hot", "masked", "made", "topped", "bested", "issue", "initial")
        indexed, hot, masked, made, topped, bested, issue, initial = (st.sem(s) for s in names)
        R, RS = 8, 4
        gathered = st.sems("gathered", R * Q)
        S = view(m.WS, 0, RS * Q, P)
        off = view(m.WS, RS * Q * P, RS * Q * P // 2).bitcast(BF16).rearrange("p (u e) -> p u e", e=P)
        o = RS * Q * P * 3 // 2
        rows = view(m.WS, o, R * Q, H)
        idx = view(m.WS, o + R * Q * H, R * Q).bitcast(I32)
        top = view(m.WS, o + R * Q * (H + 1), 2 * Q, H)
        minus = m.WS[:, o + R * Q * (2 * H + 1):o + R * Q * (2 * H + 1) + 1]
        diag = high[:, 0:RS * Q * H * P].rearrange("p (u h e) -> p u h e", u=RS * Q, h=H)
        MASK = float(2.0 ** 100)
        block = st.block()

        @block.scalar
        def _(act):
            def indices(j, u, r):
                act.wait_ge(made, j + 1)
                nc.scalar.copy(idx[:, u * Q:(u + 1) * Q], m.src1[:, bass.ds(j * Q, Q)]).then_inc(indexed, 1)

            def masks(j, u, r):
                k = u % RS
                act.wait_ge(made, j + 1 + R - RS)
                for s in range(Q):
                    act.wait_ge(gathered[u * Q + s], r * 16 + 16)
                    for h in range(1, H):
                        nc.scalar.mul(diag[:, k * Q + s, h, :], m.ident[:], rows[:, u * Q + s, h:h + 1])
                act.wait_ge(hot, j + 1)
                nc.scalar.activation(off[:, k * Q:(k + 1) * Q, :], S[:, k * Q:(k + 1) * Q, :], ACT.Identity,
                                     bias=minus, scale=MASK).then_inc(masked, 1)

            act.wait_ge(initial, 2)
            pipeline(act, R, (6, indices), (2, masks))

        @block.gpsimd
        def _(pool):
            nc.gpsimd.memset(minus, -MASK).then_inc(initial, 1)
            nc.gpsimd.tensor_copy(best, src_score).then_inc(initial, 1)
            with pool.Fori(0, QUADS // R) as i:
                for u in range(R):
                    pool.wait_ge(indexed, i * R + u + 1)
                    pool.sem_inc(issue, 1)
                    for q in range(u * Q, (u + 1) * Q):
                        nc.gpsimd.indirect_dma_start(rows[:, q, :], None, m.table_max,
                                                     bass.IndirectOffsetOnAxis(ap=idx[:, q:q + 1], axis=0)
                                                     ).then_inc(gathered[q], 16)

        @block.tensor
        def _(pe):
            pe.sem_inc(made, R)
            with pe.Fori(0, QUADS // R) as i:
                for u in range(R):
                    j, k = i * R + u, u % RS
                    pe.wait_ge(masked, j + 1)
                    pe.wait_ge(topped, j + 1)
                    for s in range(Q):
                        at = m.PS[:, u % 2 * Q + s, :]
                        nc.tensor.matmul(at, off[:, k * Q + s, :], m.identb[:].unsqueeze(1).to_broadcast([P, H, P]),
                                         start=True, stop=False)
                        mm = nc.tensor.matmul(at, S[:, k * Q + s, :], diag[:, k * Q + s].rearrange("p h e -> p (h e)"),
                                              start=False, stop=True)
                    mm.then_inc(made, 1)

        @block.vector
        def _(dve):
            v = nc.vector
            dve.sem_inc(topped, 2)
            dve.sem_inc(bested, 1)
            dve.wait_ge(initial, 2)

            def first_heads(j, u, r):
                k = slice(u % RS * Q, (u % RS + 1) * Q)
                dve.wait_ge(made, j + 1 + R - RS)
                for s in range(Q):
                    dve.wait_ge(gathered[u * Q + s], r * 16 + 16)
                v.tensor_tensor(diag[:, k, 0, :], m.ident[:].unsqueeze(1).to_broadcast([P, Q, P]),
                                rows[:, u * Q:(u + 1) * Q, 0:1].to_broadcast([P, Q, P]), ALU.mult)

            def hots(j, u, r):
                k = slice(u % RS * Q, (u % RS + 1) * Q)
                one_hot_rows(v, m, S[:, k, :], m.lo1[:, bass.ds(j * Q, Q)]).then_inc(hot, 1)

            def greatest(j, u, r):
                half = u % 2
                tiles[:] = node_tile.of(j, u)
                dve.wait_ge(made, j + 1 + R)
                v.reduce_max(top[:, half * Q:(half + 1) * Q, :],
                             m.PS[:, half * Q:(half + 1) * Q, :].rearrange("p s (h e) -> p s h e", h=H), AX
                             ).then_inc(topped, 1)

            def keep(s):
                def step(j, u, r):
                    if s == 0:
                        dve.wait_ge(topped, j + 3)
                    dve.wait_ge(bested, j * Q + s + 1)
                    at = tile_at(best, tiles[s], 0, H)
                    v.tensor_tensor(at, at, top[:, u % 2 * Q + s, :], ALU.max).then_inc(bested, 1)
                return step

            node_tile, tiles = NodeTiles(nc, dve, m.tn1), [None] * Q
            pipeline(dve, R, (0, greatest), (2, first_heads), (0, keep(0)), (2, hots), (0, keep(1)), (0, keep(2)),
                     (0, keep(3)))

    with Stage(nc) as st:
        names = ("dstep", "ready", "own_diffed", "own_expd", "selfed", "indexed", "hot", "turned", "tcopied",
                 "scored", "taken", "estep", "diffed", "expd", "weighted", "summed", "added", "issue")
        (dstep, ready, own_diffed, own_expd, selfed, indexed, hot, turned, tcopied, scored, taken, estep, diffed,
         expd, weighted, summed, added, issue) = (st.sem(s) for s in names)
        R, RT = 8, 4
        gathered = st.sems("gathered", R * Q)
        S = view(m.WS, 0, R * Q, P)
        ST = view(m.WS, R * Q * P, RT * Q, P)
        o = (R + RT) * Q * P
        idx = view(m.WS, o, R * Q).bitcast(I32)
        e, lk, p = (view(m.WS, o + (1 + k * H) * R * Q, R * Q, H) for k in range(3))
        own = view(m.WS, o + (1 + 3 * H) * R * Q, NT, H)
        rows = view(high, 0, R * Q, RW)
        block = st.block()

        @block.sync
        def _(sp):
            sp.dma_start(m.AGG[:, :, 0:RW], m.table_gat.rearrange("(t p) c -> p t c", p=P)).then_inc(selfed, 16)

        @block.scalar
        def _(act):
            def indices(j, u, r):
                act.wait_ge(summed, (j + 1) * Q)
                nc.scalar.copy(idx[:, u * Q:(u + 1) * Q], m.src1[:, bass.ds(j * Q, Q)]).then_inc(indexed, 1)

            def turned_hots(j, u, r):
                k = u % RT
                act.wait_ge(turned, j + 1)
                nc.scalar.copy(ST[:, k * Q:(k + 1) * Q, :], m.PS[:, u % 2, :].rearrange("p (s e) -> p s e", s=Q)
                               ).then_inc(tcopied, 1)

            def numerators(j, u, r):
                act.wait_ge(diffed, j + 1)
                nc.scalar.activation(p[:, u * Q:(u + 1) * Q, :], e[:, u * Q:(u + 1) * Q, :], ACT.Exp
                                     ).then_inc(expd, 1)

            act.sem_inc(tcopied, 2)
            act.wait_ge(own_diffed, 1)
            nc.scalar.activation(own, own, ACT.Exp).then_inc(own_expd, 1)
            pipeline(act, R, (6, indices), (4, turned_hots), (2, numerators))

        @block.gpsimd
        def _(pool):
            with pool.Fori(0, QUADS // R) as i:
                for u in range(R):
                    pool.wait_ge(indexed, i * R + u + 1)
                    pool.sem_inc(issue, 1)
                    for q in range(u * Q, (u + 1) * Q):
                        nc.gpsimd.indirect_dma_start(rows[:, q, :], None, m.table_gat,
                                                     bass.IndirectOffsetOnAxis(ap=idx[:, q:q + 1], axis=0)
                                                     ).then_inc(gathered[q], 16)

        @block.tensor
        def _(pe):
            te = nc.tensor

            def turn_hots(j, u, r):
                pe.wait_ge(hot, j + 1)
                pe.wait_ge(tcopied, j + 1)
                for s in range(Q):
                    mm = te.transpose(m.PS[:, u % 2, s * P:(s + 1) * P], S[:, u * Q + s, :], m.ident[:])
                mm.then_inc(turned, 1)

            def scores(j, u, r):
                tiles = node_tile.of(j, u)
                pe.wait_ge(tcopied, j + 3)
                pe.wait_ge(taken, j + 1)
                for s in range(Q):
                    mm = te.matmul(m.PS[:, 2 + u % 2, s * 8:(s + 1) * 8], ST[:, u % RT * Q + s, :],
                                   tile_at(node, tiles[s], 0, 8), start=True, stop=True)
                mm.then_inc(scored, 1)

            def sums(j, u, r):
                pe.wait_ge(weighted, j + 1)
                for s in range(Q):
                    pe.wait_ge(added, j * Q + s + 1)
                    te.matmul(m.PS[:, 4 + s, 0:RW], S[:, u * Q + s, :], rows[:, u * Q + s, :], start=True,
                              stop=True).then_inc(summed, 1)

            pe.sem_inc(summed, R * Q)
            pe.wait_ge(ready, 1)
            node_tile = NodeTiles(nc, pe, m.tn1)
            pipeline(pe, R, (2, scores), (0, sums), (4, turn_hots))

        @block.vector
        def _(dve):
            v, c = nc.vector, Chain(dve, dstep)
            dve.sem_inc(added, Q)
            dve.sem_inc(taken, 2)
            c.step(v.tensor_tensor(best, best, node[:, :, 0:H], ALU.add))
            c.step(v.scalar_tensor_tensor(node[:, :, H:2 * H], best, 0.2, best, ALU.mult, ALU.max))
            dve.wait_ge(selfed, 16)
            c.step(v.tensor_tensor(best, m.AGG[:, :, D:RW], node[:, :, 0:H], ALU.add))
            c.step(v.scalar_tensor_tensor(own, best, 0.2, best, ALU.mult, ALU.max))
            c.step(v.tensor_tensor(own, own, node[:, :, H:2 * H], ALU.subtract))
            v.tensor_scalar(own, own, 0.0, None, ALU.min).then_inc(own_diffed, 1)
            dve.wait_ge(own_expd, 1)
            at = m.AGG[:, :, 0:D].rearrange("p t (h c) -> p t h c", h=H)
            c.step(v.tensor_tensor(at, at, own.unsqueeze(3).to_broadcast([P, NT, H, C]), ALU.mult))
            c.step(v.tensor_copy(m.AGG[:, :, D:RW], own))
            dve.sem_inc(ready, 1)

            def hots(j, u, r):
                dve.wait_ge(summed, (j + 1) * Q)
                one_hot_rows(v, m, S[:, u * Q:(u + 1) * Q, :], m.lo1[:, bass.ds(j * Q, Q)]).then_inc(hot, 1)

            def exponents(n):
                def step(j, u, r):
                    k = slice(u * Q, (u + 1) * Q)
                    sc = m.PS[:, 2 + u % 2, 0:Q * 8].rearrange("p (s c) -> p s c", s=Q)
                    if n == 0:
                        for s in range(Q):
                            dve.wait_ge(gathered[u * Q + s], r * 16 + 16)
                        dve.wait_ge(scored, j + 1)
                        v.tensor_tensor(e[:, k], rows[:, k, D:RW], sc[:, :, 0:H], ALU.add).then_inc(estep, 1)
                    if n == 1:
                        dve.wait_ge(estep, j * 3 + 1)
                        v.scalar_tensor_tensor(lk[:, k], e[:, k], 0.2, e[:, k], ALU.mult, ALU.max
                                               ).then_inc(estep, 1)
                    if n == 2:
                        dve.wait_ge(estep, j * 3 + 2)
                        v.tensor_tensor(e[:, k], lk[:, k], sc[:, :, H:2 * H], ALU.subtract).then_inc(estep, 1)
                    if n == 3:
                        dve.wait_ge(estep, j * 3 + 3)
                        dve.sem_inc(taken, 1)
                        v.tensor_scalar(e[:, k], e[:, k], 0.0, None, ALU.min).then_inc(diffed, 1)
                return step

            def weigh(j, u, r):
                k = slice(u * Q, (u + 1) * Q)
                dve.wait_ge(expd, j + 1)
                f = rows[:, k, 0:D].rearrange("p s (h c) -> p s h c", h=H)
                v.tensor_tensor(f, f, p[:, k].unsqueeze(3).to_broadcast([P, Q, H, C]), ALU.mult)
                v.tensor_copy(rows[:, k, D:RW], p[:, k]).then_inc(weighted, 1)

            def add(s):
                def step(j, u, r):
                    if s == 0:
                        tiles[:] = node_tile.of(j, u)
                    dve.wait_ge(summed, (j + R) * Q + s + 1)
                    dve.wait_ge(added, (j + 1) * Q + s)
                    at = tile_at(m.AGG, tiles[s], 0, RW)
                    v.tensor_tensor(at, at, m.PS[:, 4 + s, 0:RW], ALU.add).then_inc(added, 1)
                return step

            node_tile, tiles = NodeTiles(nc, dve, m.tn1), [None] * Q
            mixed = [f for n in range(4) for f in ((0, add(n)), (2, exponents(n)))]
            pipeline(dve, R, (4, hots), (1, weigh), *mixed)

    with Stage(nc) as st:
        loaded, dstep = st.sem("loaded"), st.sem("dstep")
        bias = m.WS[:, 0:D]
        rd = view(m.WS, D, NT, H)
        block = st.block()

        @block.sync
        def _(sp):
            sp.dma_start(bias, a["L1_gnn_bias"].unsqueeze(0).to_broadcast([P, D])).then_inc(loaded, 16)

        @block.vector
        def _(dve):
            v, c = nc.vector, Chain(dve, dstep)
            c.step(v.tensor_scalar(rd, m.AGG[:, :, D:RW], 1e-16, None, ALU.add))
            c.step(v.reciprocal(rd, rd))
            heads = [x.rearrange("p t (h c) -> p t h c", h=H) for x in (m.XN[:], m.AGG[:, :, 0:D])]
            c.step(v.tensor_tensor(heads[0], heads[1], rd.unsqueeze(3).to_broadcast([P, NT, H, C]), ALU.mult))
            dve.wait_ge(loaded, 16)
            c.step(v.tensor_tensor(m.XN[:], m.XN[:], bias.unsqueeze(1).to_broadcast([P, NT, D]), ALU.add))

    turn(nc, m, m.XN, m.XT)

    def finish(t, ps):
        at = tile_at(m.X, t)
        return nc.vector.scalar_tensor_tensor(at, ps, 0.0, at, ALU.max, ALU.add)

    linear_nodes(nc, m, m.XT, a["L1_gnn_lin_w"], a["L1_gnn_lin_b"], D, finish)


def expert_pair(nc, m, a):
    NE, HD = 8, 1024
    KH = HD // P
    layernorm(nc, m, m.X, m.XN)
    gates(nc, m, a["L1_ffn_Wr"], a["L1_ffn_br"], NE, False)
    layernorm(nc, m, m.XN, m.XN)
    turn(nc, m, m.XN, m.XT)
    with Stage(nc) as st:
        names = ("shifted", "made_b", "w1_used", "scaled", "made", "active", "done", "biased", "taken", "smalls",
                 "passed", "blanked", "stored")
        (shifted, made_b, w1_used, scaled, made, active, done, biased, taken, smalls, passed, blanked,
         stored) = (st.sem(s) for s in names)
        came1, came2 = st.sems("came1", 2), st.sems("came2", 2)
        hid = view(m.BB, 0, KH, CB)
        o = KH * CB
        w1 = [view(m.BB, o + q * KD * HD, KD, HD) for q in range(2)]
        o += 2 * KD * HD
        w2 = [view(m.BB, o, KH, D), view(m.AF, 0, KH, D)]
        ln_g = view(m.WS, 0, NE, KD)
        ln_b = view(m.WS, 16, NE, KD)
        b1 = view(m.WS, 32, NE, KH)
        b1s = view(m.WS, 96, 2, KH)
        b2 = m.WS[:, 128:128 + NE * D]
        block = st.block()

        @block.gpsimd
        def _(pool):
            blank_records(nc, pool, m, m.XN[:].rearrange("p t d -> p (t d)"), blanked, stored)

        @block.sync
        def _(sp):
            sp.dma_start(ln_g, a["L1_ffn_ln_g"].rearrange("p (e k) -> p e k", k=KD)).then_inc(smalls, 16)
            sp.dma_start(ln_b, a["L1_ffn_ln_b"].rearrange("p (e k) -> p e k", k=KD)).then_inc(smalls, 16)
            sp.dma_start(b1, a["L1_ffn_b1"].rearrange("p (e k) -> p e k", k=KH)).then_inc(smalls, 16)
            sp.dma_start(b2, a["L1_ffn_b2"].rearrange("e d -> (e d)").unsqueeze(0).to_broadcast([P, NE * D])
                         ).then_inc(smalls, 16)
            w1d = a["L1_ffn_W1"].rearrange("e (k p) h -> e p k h", p=P)
            w2d = a["L1_ffn_W2"].rearrange("e (k p) d -> e p k d", p=P)
            with sp.Fori(0, NE // 2) as i:
                for q in range(2):
                    ex = i * 2 + q
                    sp.wait_ge(w1_used, ex + 1)
                    sp.dma_start(w1[q], w1d[bass.ds(ex, 1), :, :, :].rearrange("o p k h -> (o p) k h")
                                 ).then_inc(came1[q], 16)
                    sp.dma_start(w2[q], w2d[bass.ds(ex, 1), :, :, :].rearrange("o p k d -> (o p) k d")
                                 ).then_inc(came2[q], 16)

        @block.tensor
        def _(pe):
            pe.sem_inc(w1_used, 2)
            pe.wait_ge(smalls, 64)
            te = nc.tensor
            with pe.Fori(0, NE // 2) as i:
                for q in range(2):
                    ex = i * 2 + q
                    pe.wait_ge(came1[q], i * 16 + 16)
                    pe.wait_ge(taken, ex * NT + U)
                    for j in range(KH):
                        for k in range(KD):
                            mm = te.matmul(m.PS[:, 3, j:j + 1], w1[q][:, k, j * P:(j + 1) * P],
                                           ln_b[:, bass.ds(ex, 1), k:k + 1].rearrange("p o k -> p (o k)"),
                                           start=(k == 0), stop=(k == KD - 1))
                    mm.then_inc(made_b, 1)
                    pe.wait_ge(scaled, ex + 1)
                    pe.wait_ge(came2[q], i * 16 + 16)
                    pe.sem_inc(passed, 1)
                    with pe.Fori(0, NT // TB) as b:
                        base = (ex * (NT // TB) + b) * KH * 2
                        for h in range(2):
                            for j in range(KH):
                                pe.wait_ge(active, base + h * KH + j + 1)
                                for k in range(KD):
                                    mm = te.matmul(m.PS[:, j % 2, 0:CH2], w1[q][:, k, j * P:(j + 1) * P],
                                                   m.XT[:, k, bass.ds(b * CB + h * CH2, CH2)], start=(k == 0),
                                                   stop=(k == KD - 1))
                                mm.then_inc(made, 1)
                        for s in range(TB):
                            t = ex * NT + b * TB + s
                            pe.wait_ge(active, base + (1 if (s + 1) * P <= CH2 else 2) * KH + 2)
                            pe.wait_ge(taken, t + 1)
                            for j in range(KH):
                                mm = te.matmul(m.PS[:, 3 + s, 0:D], hid[:, j, s * P:(s + 1) * P], w2[q][:, j, :],
                                               start=(j == 0), stop=(j == KH - 1))
                            mm.then_inc(done, 1)
                    pe.wait_ge(done, (ex + 1) * NT)
                    pe.sem_inc(w1_used, 1)

        @block.scalar
        def _(act):
            act.sem_inc(active, 2)
            with act.Fori(0, NE // 2) as i:
                for q in range(2):
                    ex = i * 2 + q
                    act.wait_ge(shifted, ex + 1)
                    act.sem_inc(passed, 1)
                    with act.Fori(0, NT // TB) as b:
                        base = (ex * (NT // TB) + b) * KH * 2
                        for h in range(2):
                            for j in range(KH):
                                act.wait_ge(made, base + h * KH + j + 1)
                                nc.scalar.activation(hid[:, j, h * CH2:(h + 1) * CH2], m.PS[:, j % 2, 0:CH2], ACT.Gelu,
                                                     bias=b1s[:, q, j:j + 1]).then_inc(active, 1)

        @block.vector
        def _(dve):
            v = nc.vector
            dve.sem_inc(taken, U)
            dve.wait_ge(smalls, 64)
            with dve.Fori(0, NE // 2) as i:
                for q in range(2):
                    ex = i * 2 + q
                    dve.wait_ge(made_b, ex + 1)
                    v.tensor_tensor(b1s[:, q, :], m.PS[:, 3, 0:KH],
                                    b1[:, bass.ds(ex, 1), :].rearrange("p o k -> p (o k)"), ALU.add
                                    ).then_inc(shifted, 1)
                    for k in range(KD):
                        ins = v.tensor_scalar(w1[q][:, k, :], w1[q][:, k, :],
                                              ln_g[:, bass.ds(ex, 1), k:k + 1].rearrange("p o k -> p (o k)"), None,
                                              ALU.mult)
                    ins.then_inc(scaled, 1)
                    with dve.Fori(0, NT // TB) as b:
                        for s in range(TB):
                            t = b * TB + s
                            n = ex * NT + t
                            dve.wait_ge(taken, n + U)
                            at = tile_at(m.X, t)
                            g = m.gate[:, bass.ds(t, 1), bass.ds(ex, 1)].rearrange("p o k -> p (o k)")
                            v.scalar_tensor_tensor(at, b2[:, bass.ds(ex * D, D)], g, at, ALU.mult,
                                                   ALU.add).then_inc(biased, 1)
                            dve.wait_ge(biased, n + 1)
                            dve.wait_ge(done, n + 1)
                            v.scalar_tensor_tensor(at, m.PS[:, 3 + s, 0:D], g, at, ALU.mult,
                                                   ALU.add).then_inc(taken, 1)


def gates(nc, m, weight, bias, ne, softmax_first, hidden=None):
    if hidden is None:
        turn(nc, m, m.XN, m.XT)
    srcT = m.XT if hidden is None else hidden
    KX = 1 if hidden is not None else KD
    with Stage(nc) as st:
        names = ("loaded", "staged", "made", "dstep", "differed", "expd", "passed")
        loaded, staged, made, dstep, differed, expd, passed = (st.sem(s) for s in names)
        W = 8
        ring = view(m.WS, 0, U, KX, P)
        w = view(m.WS, U * D, KX, ne)
        b = m.WS[0:1, U * D + 64:U * D + 64 + ne]
        lg, prob, top, whichf, hit, hit2 = (view(m.WS, 1500 + k * NT * W, NT, W) for k in range(6))
        which = view(m.WS, 1500 + 6 * NT * W, NT, W).bitcast(U32)
        two = view(m.WS, 1500 + 7 * NT * W, NT, 2)
        total = view(m.WS, 1500 + 7 * NT * W + 64, 32)[:, 0:NT]
        block = st.block()

        @block.sync
        def _(sp):
            sp.dma_start(w, weight.rearrange("(k p) n -> p k n", p=P)).then_inc(loaded, 16)
            sp.dma_start(b, bias.unsqueeze(0)).then_inc(loaded, 16)

        @block.scalar
        def _(act):
            with act.Fori(0, NT // U) as i:
                for s in range(U):
                    t = i * U + s
                    act.wait_ge(made, t + 1)
                    nc.scalar.copy(ring[:, s, :, :], srcT[:, 0:KX, bass.ds(t * P, P)]).then_inc(staged, 1)
            if softmax_first:
                act.wait_ge(differed, 1)
                nc.scalar.activation(prob[:, :, 0:ne], prob[:, :, 0:ne], ACT.Exp).then_inc(expd, 1)
            act.wait_ge(differed, 2 if softmax_first else 1)
            nc.scalar.activation(two, two, ACT.Exp).then_inc(expd, 1)

        @block.tensor
        def _(pe):
            pe.sem_inc(made, U)
            pe.wait_ge(loaded, 32)
            with pe.Fori(0, NT // U) as i:
                for s in range(U):
                    t = i * U + s
                    pe.wait_ge(staged, t + 1)
                    at = m.PS[:, 0, bass.ds(t * W, ne)]
                    for k in range(KX):
                        nc.tensor.matmul(at, ring[:, s, k, :], w[:, k, :], start=(k == 0), stop=False)
                    nc.tensor.matmul(at, m.ones[0:1, :], b, start=False, stop=True).then_inc(made, 1)

        @block.vector
        def _(dve):
            v, c = nc.vector, Chain(dve, dstep)
            c.step(v.memset(lg, -BIG))
            c.step(v.memset(prob, -1.0))
            dve.wait_ge(made, U + NT)
            c.step(v.tensor_copy(lg[:, :, 0:ne], m.PS[:, 0, 0:NT * W].rearrange("p (t c) -> p t c", c=W)[:, :, 0:ne]))
            if softmax_first:
                c.step(v.reduce_max(total, lg, AX))
                v.tensor_tensor(prob[:, :, 0:ne], lg[:, :, 0:ne], bcast(total, [P, NT, ne]), ALU.subtract
                                ).then_inc(differed, 1)
                dve.wait_ge(expd, 1)
                c.step(v.reduce_sum(total, prob[:, :, 0:ne], AX))
                c.step(v.reciprocal(total, total))
                c.step(v.tensor_tensor(prob[:, :, 0:ne], prob[:, :, 0:ne], bcast(total, [P, NT, ne]), ALU.mult))
            of = prob if softmax_first else lg
            dve.sem_inc(passed, 1)
            for t in range(NT):
                ins = v.max(top[:, t, :], of[:, t, :])
            c.step(ins)
            dve.sem_inc(passed, 1)
            for t in range(NT):
                ins = v.max_index(which[:, t, :], top[:, t, :], of[:, t, :])
            c.step(ins)
            c.step(v.tensor_copy(whichf, which))
            v.tensor_tensor(two, top[:, :, 0:2], top[:, :, 0:1].to_broadcast([P, NT, 2]), ALU.subtract
                            ).then_inc(differed, 1)
            dve.wait_ge(expd, 2 if softmax_first else 1)
            c.step(v.reduce_sum(total, two, AX))
            c.step(v.reciprocal(total, total))
            c.step(v.tensor_tensor(two, two, bcast(total, [P, NT, 2]), ALU.mult))
            experts = m.iota[:, 0:W].unsqueeze(1).to_broadcast([P, NT, W])
            for k, at in ((0, hit), (1, hit2)):
                c.step(v.tensor_tensor(at, experts, whichf[:, :, k:k + 1].to_broadcast([P, NT, W]), ALU.is_equal))
                c.step(v.tensor_tensor(at, at, two[:, :, k:k + 1].to_broadcast([P, NT, W]), ALU.mult))
            v.tensor_tensor(m.gate[:], hit, hit2, ALU.add)



def edge_update(nc, m, a):
    layernorm(nc, m, m.X, m.XN)
    turn(nc, m, m.XN, m.XT)
    w1 = a["L2_gnn_W1"]
    by_dst = view(m.BB, 0, NT, D)
    by_src = view(m.BB, NT * D, NT, D)

    def keep(dst):
        return lambda t, ps: nc.vector.tensor_copy(tile_at(dst, t), ps)

    linear_nodes(nc, m, m.XT, w1[D:2 * D, :], None, D, keep(by_dst))
    store_table(nc, m, by_dst, m.table, sums=0.0)
    linear_nodes(nc, m, m.XT, w1[0:D, :], a["L2_gnn_b1"], D, keep(by_src))

    CW = D + 1
    with Stage(nc) as st:
        names = ("loaded", "oned", "indexed", "hot", "turned", "tcopied", "made", "mixed", "active", "summed",
                 "added", "issue")
        loaded, oned, indexed, hot, turned, tcopied, made, mixed, active, summed, added, issue = (
            st.sem(s) for s in names)
        R, RS = 8, 4
        gathered, came = st.sems("gathered", RS * Q), st.sems("came", R)
        rows = view(m.WS, 0, RS * Q, CW)
        rec = view(m.WS, RS * Q * CW, R * Q, EA + 4)
        o = RS * Q * CW + R * Q * (EA + 4)
        idx = view(m.WS, o, R * Q).bitcast(I32)
        wa = m.WS[0:EA, o + R * Q:o + R * Q + D]
        S = view(m.BB, 0, RS * Q, P)
        ST = view(m.BB, RS * Q * P, RS * Q, P)
        attT = view(m.BB, 2 * RS * Q * P, RS * Q, P)
        o += R * Q + D
        Sb = m.WS[:, o:o + 2 * Q * P // 2].bitcast(BF16).rearrange("p (s e) -> p s e", e=P)
        block = st.block()

        @block.sync
        def _(sp):
            sp.dma_start(wa, w1[2 * D:2 * D + EA, :]).then_inc(loaded, 16)
            r = m.rec2.rearrange("(p w) c -> p w c", p=P)
            with sp.Fori(0, QUADS // R) as i:
                for u in range(R):
                    j = i * R + u
                    sp.wait_ge(summed, (j + 1) * Q)
                    sp.dma_start(rec[:, u * Q:(u + 1) * Q, :], r[:, bass.ds(j * Q, Q), :]).then_inc(came[u], 16)

        @block.scalar
        def _(act):
            def indices(j, u, r):
                act.wait_ge(came[u], r * 16 + 16)
                nc.scalar.copy(idx[:, u * Q:(u + 1) * Q], rec[:, u * Q:(u + 1) * Q, EA]).then_inc(indexed, 1)

            def turned_in(j, u, r):
                k = slice(u % RS * Q, (u % RS + 1) * Q)
                act.wait_ge(turned, j + 3)
                nc.scalar.copy(ST[:, k, :], m.PS[:, 0, 0:Q * P // 2].bitcast(BF16).rearrange("p (s e) -> p s e", s=Q))
                nc.scalar.copy(attT[0:EA, k, :], m.PS[0:EA, 1, :].rearrange("p (s e) -> p s e", s=Q)
                               ).then_inc(tcopied, 1)

            def relu(j, u, r):
                k = slice(u % RS * Q, (u % RS + 1) * Q)
                act.wait_ge(mixed, j + 2)
                nc.scalar.activation(rows[:, k, 0:D], rows[:, k, 0:D], ACT.Relu).then_inc(active, 1)

            act.sem_inc(tcopied, 1)
            pipeline(act, R, (6, indices), (2, turned_in), (1, relu))

        @block.gpsimd
        def _(pool):
            nc.gpsimd.memset(rows[:, :, D:CW], 1.0).then_inc(oned, 1)
            with pool.Fori(0, QUADS // R) as i:
                for u in range(R):
                    j = i * R + u
                    pool.wait_ge(indexed, j + 1)
                    pool.wait_ge(summed, (j + 1 + R - RS) * Q)
                    pool.sem_inc(issue, 1)
                    for s in range(Q):
                        k = u % RS * Q + s
                        nc.gpsimd.indirect_dma_start(
                            rows[:, k, 0:D], None, m.table,
                            bass.IndirectOffsetOnAxis(ap=idx[:, u * Q + s:u * Q + s + 1], axis=0)
                        ).then_inc(gathered[k], 16)

        @block.tensor
        def _(pe):
            te = nc.tensor

            def turn_in(j, u, r):
                pe.wait_ge(hot, j + 1)
                pe.wait_ge(tcopied, j + 1)
                for s in range(Q):
                    te.transpose(m.PS[:, 0, s * P // 2:(s + 1) * P // 2].bitcast(BF16), Sb[:, u % 2 * Q + s, :],
                                 m.identb[:])
                    mm = te.transpose(m.PS[0:EA, 1, s * P:(s + 1) * P], rec[:, u * Q + s, 0:EA], m.ident[:])
                mm.then_inc(turned, 1)

            def inner(j, u, r):
                tiles = node_tiles(nc, pe, m.tn2[0:1, bass.ds(j * Q, Q)])
                pe.wait_ge(tcopied, j + 2)
                pe.wait_ge(mixed, j + 1)
                for s in range(Q):
                    k = u % RS * Q + s
                    at = m.PS[:, 2 + s // 2, s % 2 * D:(s % 2 + 1) * D]
                    te.matmul(at, ST[:, k, :], tile_at(by_src, tiles[s]), start=True, stop=False)
                    mm = te.matmul(at, attT[0:EA, k, :], wa, start=False, stop=True)
                mm.then_inc(made, 1)

            def sums(j, u, r):
                pe.wait_ge(active, j + 1)
                for s in range(Q):
                    k = u % RS * Q + s
                    pe.wait_ge(added, j * Q + s + 1)
                    te.matmul(m.PS[:, 4 + s, 0:CW], S[:, k, :], rows[:, k, :], start=True, stop=True
                              ).then_inc(summed, 1)

            pe.sem_inc(summed, R * Q)
            pe.sem_inc(turned, 2)
            pe.wait_ge(loaded, 16)
            pe.wait_ge(oned, 1)
            pipeline(pe, R, (2, turn_in), (1, inner), (0, sums))

        @block.vector
        def _(dve):
            v = nc.vector

            def hots(j, u, r):
                k = u % RS
                dve.wait_ge(summed, (j + 1 + R - RS) * Q)
                dve.wait_ge(came[u], r * 16 + 16)
                dve.wait_ge(turned, j + 1)
                one_hot_rows(v, m, Sb[:, u % 2 * Q:(u % 2 + 1) * Q, :], rec[:, u * Q:(u + 1) * Q, EA + 1])
                one_hot_rows(v, m, S[:, k * Q:(k + 1) * Q, :], rec[:, u * Q:(u + 1) * Q, EA + 1]).then_inc(hot, 1)

            def mix(j, u, r):
                k = u % RS
                for s in range(Q):
                    dve.wait_ge(gathered[k * Q + s], r * (16 * R // RS) + (u // RS + 1) * 16)
                dve.wait_ge(made, j + 1)
                at = rows[:, k * Q:(k + 1) * Q, 0:D]
                v.tensor_tensor(at, at, m.PS[:, 2:4, :].rearrange("p b (s d) -> p (b s) d", s=2), ALU.add
                                ).then_inc(mixed, 1)

            def add(j, u, r):
                tiles = node_tile.of(j, u)
                for s in range(Q):
                    dve.wait_ge(summed, (j + R) * Q + s + 1)
                    dve.wait_ge(added, (j + 1) * Q + s)
                    at = tile_at(m.AGG, tiles[s], 0, CW)
                    v.tensor_tensor(at, at, m.PS[:, 4 + s, 0:CW], ALU.add).then_inc(added, 1)

            dve.sem_inc(added, Q)
            dve.sem_inc(mixed, 1)
            node_tile = NodeTiles(nc, dve, m.tn2)
            pipeline(dve, R, (3, hots), (1, mix), (0, add))

    sumsT = view(m.BB, 0, KD, NP)
    b2 = view(m.BB, 12800 - D, D)
    turn(nc, m, m.AGG, sumsT)
    with Stage(nc) as st:
        loaded = st.sem("loaded")
        block = st.block()

        @block.sync
        def _(sp):
            sp.dma_start(b2, a["L2_gnn_b2"].unsqueeze(0).to_broadcast([P, D])).then_inc(loaded, 16)
            sp.wait_ge(loaded, 16)

    def message(t, ps):
        count = tile_at(m.AGG, t, D, D + 1)
        return nc.vector.scalar_tensor_tensor(tile_at(m.AGG, t), b2, count, ps, ALU.mult, ALU.add)

    linear_nodes(nc, m, sumsT, a["L2_gnn_W2"], None, D, message)
    turn(nc, m, m.AGG, sumsT)

    with Stage(nc) as st:
        names = ("loaded", "dstep", "staged", "made", "biased", "gated", "tanhed", "reset", "inner", "used")
        loaded, dstep, staged, made, biased, gated, tanhed, reset, inner, used = (st.sem(s) for s in names)
        D3 = 3 * D
        wi = view(m.BB, KD * NP, KD, D3)
        wh = view(m.BB, KD * NP + KD * D3, KD, D3)
        o = KD * NP + 2 * KD * D3
        bi, bh = (m.BB[:, o + k * D3:o + (k + 1) * D3] for k in range(2))
        ring = view(m.WS, 0, U, 2 * KD, P)
        rz = view(m.WS, U * 512, U, 512)
        cand = view(m.AF, 0, U, D)
        gap = view(m.AF, U * D, U, D)
        block = st.block()

        @block.sync
        def _(sp):
            sp.dma_start(wi, a["L2_gnn_W_ih"].rearrange("(k p) n -> p k n", p=P)).then_inc(loaded, 16)
            sp.dma_start(wh, a["L2_gnn_W_hh"].rearrange("(k p) n -> p k n", p=P)).then_inc(loaded, 16)
            sp.dma_start(bi, a["L2_gnn_b_ih"].unsqueeze(0).to_broadcast([P, D3])).then_inc(loaded, 16)
            sp.dma_start(bh, a["L2_gnn_b_hh"].unsqueeze(0).to_broadcast([P, D3])).then_inc(loaded, 16)

        @block.scalar
        def _(act):
            def stage(t, s):
                act.wait_ge(made, t + 1)
                nc.scalar.copy(ring[:, s, 0:KD, :], sumsT[:, :, bass.ds(t * P, P)])
                nc.scalar.copy(ring[:, s, KD:2 * KD, :], m.XT[:, :, bass.ds(t * P, P)]).then_inc(staged, 1)

            def body(i, last):
                for s in range(U):
                    act.wait_ge(biased, i * U + s + 1)
                    nc.scalar.activation(rz[:, s, :], rz[:, s, :], ACT.Sigmoid).then_inc(gated, 1)
                    if not last:
                        stage((i + 1) * U + s, s)
                for s in range(U):
                    act.wait_ge(inner, i * U + s + 1)
                    nc.scalar.activation(cand[:, s, :], cand[:, s, :], ACT.Tanh).then_inc(tanhed, 1)

            for s in range(U):
                stage(s, s)
            with act.Fori(0, NT // U - 1) as i:
                body(i, False)
            body(NT // U - 1, True)

        @block.tensor
        def _(pe):
            te = nc.tensor
            pe.sem_inc(made, U)
            pe.wait_ge(loaded, 64)
            with pe.Fori(0, NT // U) as i:
                for s in range(U):
                    t = i * U + s
                    pe.wait_ge(staged, t + 1)
                    free2(pe, used, s, t)
                    b0, b1 = m.PS[:, s % 2, :], m.PS[:, 2 + s % 2, :]
                    for k in range(KD):
                        te.matmul(b0, ring[:, s, k, :], wi[:, k, 0:2 * D], start=(k == 0), stop=False)
                        te.matmul(b0, ring[:, s, KD + k, :], wh[:, k, 0:2 * D], start=False, stop=(k == KD - 1))
                    for half, (w, q) in enumerate(((wi, 0), (wh, KD))):
                        at = b1[:, half * D:(half + 1) * D]
                        for k in range(KD):
                            mm = te.matmul(at, ring[:, s, q + k, :], w[:, k, 2 * D:D3], start=(k == 0),
                                           stop=(k == KD - 1))
                    mm.then_inc(made, 1)

        @block.vector
        def _(dve):
            v, c = nc.vector, Chain(dve, dstep)
            dve.sem_inc(used, 2)
            dve.wait_ge(loaded, 64)
            c.step(v.tensor_tensor(bi[:, 0:2 * D], bi[:, 0:2 * D], bh[:, 0:2 * D], ALU.add))

            def biases(i, s):
                t = i * U + s
                dve.wait_ge(made, t + 1 + U)
                b1 = m.PS[:, 2 + s % 2, :]
                v.tensor_tensor(rz[:, s, :], m.PS[:, s % 2, :], bi[:, 0:2 * D], ALU.add).then_inc(biased, 1)
                v.tensor_tensor(gap[:, s, :], b1[:, D:2 * D], bh[:, 2 * D:D3], ALU.add)
                c.at(i * 4 * U + s + 1)
                c.step(v.tensor_tensor(cand[:, s, :], b1[:, 0:D], bi[:, 2 * D:D3], ALU.add))
                dve.sem_inc(used, 1)

            def candidate(i, s):
                t = i * U + s
                dve.wait_ge(gated, t + 1)
                v.tensor_tensor(gap[:, s, :], gap[:, s, :], rz[:, s, 0:D], ALU.mult).then_inc(reset, 1)
                dve.wait_ge(reset, t + 1)
                v.tensor_tensor(cand[:, s, :], cand[:, s, :], gap[:, s, :], ALU.add).then_inc(inner, 1)

            def update(i, s):
                t = i * U + s
                dve.wait_ge(tanhed, t + 1)
                c.at(i * 4 * U + U + 3 * s + 1)
                c.step(v.tensor_tensor(gap[:, s, :], tile_at(m.XN, t), cand[:, s, :], ALU.subtract))
                c.step(v.tensor_tensor(gap[:, s, :], gap[:, s, :], rz[:, s, D:2 * D], ALU.mult))
                c.step(v.tensor_tensor(gap[:, s, :], gap[:, s, :], cand[:, s, :], ALU.add))
                at = tile_at(m.X, t)
                v.tensor_tensor(at, at, gap[:, s, :], ALU.add)

            with dve.Fori(0, NT // U) as i:
                for s in range(U):
                    biases(i, s)
                    if s:
                        candidate(i, s - 1)
                candidate(i, U - 1)
                for s in range(U):
                    update(i, s)


def one_expert(nc, m, a):
    NE, HD = 32, 64
    KH = NE * HD // P
    MASK = float(2.0 ** 100)
    layernorm(nc, m, m.X, m.XN)
    turn(nc, m, m.XN, m.XT)
    w1 = view(m.AF, 0, KD, NE * HD)
    pick = m.AF[0:NE, KD * NE * HD:KD * NE * HD + KH * P]
    w2 = m.XN[:].rearrange("p t d -> p (t d)")[:, 0:KH * D].rearrange("p (k d) -> p k d", d=D)
    chosen = m.WS[0:NE, 0:NP]
    others = m.WS[0:NE, NP:NP + NP // 2].bitcast(BF16)
    pickb = m.WS[0:NE, NP + NP // 2:NP + NP // 2 + KH * P // 2].bitcast(BF16)
    b2 = m.WS[0:NE, 2 * NP:2 * NP + D]
    b1 = view(m.WS, 2 * NP + D, KH)
    high = view(m.BB, 0, 4000)

    with Stage(nc) as st:
        names = ("loaded", "staged", "made", "dstep", "passed", "turned", "taken", "hot", "picked")
        loaded, staged, made, dstep, passed, turned, taken, hot, picked = (st.sem(s) for s in names)
        logits = m.PS[:, 0:2, :].rearrange("p b e -> p (b e)")
        quads = [range(t, min(t + Q, NT)) for t in range(0, NT, Q)]
        ring = view(high, 0, U, KD, P)
        wr = view(high, U * D, KD, NE)
        br = high[0:1, U * D + 64:U * D + 96]
        lg, hots = view(high, 1400, NT, NE), view(high, 1400 + NT * NE, NT, NE)
        o = 1400 + 2 * NT * NE
        top, whichf = view(high, o, NT, 8), view(high, o + NT * 8, NT, 8)
        which = view(high, o + 2 * NT * 8, NT, 8).bitcast(U32)
        block = st.block()

        @block.sync
        def _(sp):
            sp.dma_start(wr, a["L2_ffn_router_w"].rearrange("(k p) n -> p k n", p=P)).then_inc(loaded, 16)
            sp.dma_start(br, a["L2_ffn_router_b"].unsqueeze(0)).then_inc(loaded, 16)

        @block.gpsimd
        def _(pool):
            g = nc.gpsimd
            pv = pick.rearrange("p (k j) -> p k j", k=KH)
            g.memset(pick, MASK).then_inc(picked, 1)
            pool.wait_ge(picked, 1)
            g.affine_select(out=pv, in_=pv, compare_op=ALU.is_ge, fill=0.0, base=0, pattern=[[P, KH], [1, P]],
                            channel_multiplier=-HD).then_inc(picked, 1)
            pool.wait_ge(picked, 2)
            g.affine_select(out=pv, in_=pv, compare_op=ALU.is_ge, fill=0.0, base=HD - 1,
                            pattern=[[-P, KH], [-1, P]], channel_multiplier=HD).then_inc(picked, 1)

        @block.scalar
        def _(act):
            with act.Fori(0, NT // U) as i:
                for s in range(U):
                    t = i * U + s
                    act.wait_ge(made, t + 1)
                    nc.scalar.copy(ring[:, s, :, :], m.XT[:, :, bass.ds(t * P, P)]).then_inc(staged, 1)

        @block.tensor
        def _(pe):
            pe.sem_inc(made, U)
            pe.wait_ge(loaded, 32)
            with pe.Fori(0, NT // U) as i:
                for s in range(U):
                    t = i * U + s
                    pe.wait_ge(staged, t + 1)
                    at = logits[:, bass.ds(t * NE, NE)]
                    for k in range(KD):
                        nc.tensor.matmul(at, ring[:, s, k, :], wr[:, k, :], start=(k == 0), stop=False)
                    nc.tensor.matmul(at, m.ones[0:1, :], br, start=False, stop=True).then_inc(made, 1)
            pe.wait_ge(hot, 1)
            for n, tiles in enumerate(quads):
                if n >= 2:
                    pe.wait_ge(taken, n - 1)
                for q, t in enumerate(tiles):
                    mm = nc.tensor.transpose(m.PS[0:NE, 2 + n % 2, q * P:(q + 1) * P], hots[:, t, :], m.ident[:])
                mm.then_inc(turned, 1)

        @block.vector
        def _(dve):
            v, c = nc.vector, Chain(dve, dstep)
            dve.wait_ge(picked, 3)
            v.tensor_copy(pickb, pick)
            dve.wait_ge(made, U + NT)
            c.step(v.tensor_copy(lg.rearrange("p t e -> p (t e)"), logits[:, 0:NT * NE]))
            dve.sem_inc(passed, 1)
            for t in range(NT):
                ins = v.max(top[:, t, :], lg[:, t, :])
            c.step(ins)
            dve.sem_inc(passed, 1)
            for t in range(NT):
                ins = v.max_index(which[:, t, :], top[:, t, :], lg[:, t, :])
            c.step(ins)
            c.step(v.tensor_copy(whichf, which))
            v.tensor_tensor(hots, m.iota[:, 0:NE].unsqueeze(1).to_broadcast([P, NT, NE]),
                            whichf[:, :, 0:1].to_broadcast([P, NT, NE]), ALU.is_equal).then_inc(hot, 1)
            for n, tiles in enumerate(quads):
                dve.wait_ge(turned, n + 1)
                nodes = slice(tiles[0] * P, (tiles[-1] + 1) * P)
                at = m.PS[0:NE, 2 + n % 2, 0:len(tiles) * P]
                v.tensor_copy(chosen[:, nodes], at)
                v.tensor_scalar(others[:, nodes], at, 1.0, None, ALU.subtract).then_inc(taken, 1)

    with Stage(nc) as st:
        loaded, made, active, done, taken, cstaged = (
            st.sem(s) for s in ("loaded", "made", "active", "done", "taken", "cstaged"))
        hid = view(m.BB, 0, KH, CB)
        cring = m.BB[0:NE, KH * CB:KH * CB + U * P].rearrange("p (u n) -> p u n", u=U)
        block = st.block()

        @block.sync
        def _(sp):
            for k in range(KD):
                sp.dma_start(w1[:, k, :].rearrange("p (e h) -> p e h", e=NE),
                             a["L2_ffn_W1"].rearrange("e (k p) h -> k p e h", p=P)[k]).then_inc(loaded, 16)
            sp.dma_start(w2, a["L2_ffn_W2"].rearrange("e h d -> (e h) d").rearrange("(k p) d -> p k d", p=P)
                         ).then_inc(loaded, 16)
            sp.dma_start(b1, a["L2_ffn_b1"]).then_inc(loaded, 16)
            sp.dma_start(b2, a["L2_ffn_b2"]).then_inc(loaded, 16)

        @block.tensor
        def _(pe):
            te = nc.tensor
            pe.wait_ge(loaded, 80)
            with pe.Fori(0, NT // TB) as b:
                for h in range(2):
                    for j in range(KH):
                        pe.wait_ge(active, b * KH * 2 + h * KH + j + 1)
                        cols = bass.ds(b * CB + h * CH2, CH2)
                        for k in range(KD):
                            te.matmul(m.PS[:, j % 2, 0:CH2], w1[:, k, j * P:(j + 1) * P], m.XT[:, k, cols],
                                      start=(k == 0), stop=False)
                        te.matmul(m.PS[:, j % 2, 0:CH2], pickb[:, j * P:(j + 1) * P], others[:, cols], start=False,
                                  stop=True).then_inc(made, 1)
                pe.wait_ge(cstaged, b + 1)
                for s in range(TB):
                    pe.wait_ge(active, b * KH * 2 + (1 if (s + 1) * P <= CH2 else 2) * KH + 2)
                    pe.wait_ge(taken, b * TB + s + 1)
                    for j in range(KH):
                        te.matmul(m.PS[:, 3 + s, 0:D], hid[:, j, s * P:(s + 1) * P], w2[:, j, :], start=(j == 0),
                                  stop=False)
                    te.matmul(m.PS[:, 3 + s, 0:D], cring[:, s, :], b2, start=False, stop=True).then_inc(done, 1)

        @block.scalar
        def _(act):
            act.sem_inc(active, 2)
            act.wait_ge(loaded, 80)
            with act.Fori(0, NT // TB) as b:
                for h in range(2):
                    for j in range(KH):
                        act.wait_ge(made, b * KH * 2 + h * KH + j + 1)
                        nc.scalar.activation(hid[:, j, h * CH2:(h + 1) * CH2], m.PS[:, j % 2, 0:CH2], ACT.Relu,
                                             bias=b1[:, j:j + 1]).then_inc(active, 1)

        @block.vector
        def _(dve):
            v = nc.vector
            dve.sem_inc(taken, U)
            with dve.Fori(0, NT // TB) as b:
                v.tensor_copy(cring.rearrange("p u n -> p (u n)"), chosen[:, bass.ds(b * CB, CB)]).then_inc(cstaged, 1)
                for s in range(TB):
                    t = b * TB + s
                    dve.wait_ge(done, t + 1)
                    at = tile_at(m.X, t)
                    v.scalar_tensor_tensor(at, m.PS[:, 3 + s, 0:D], 0.0, at, ALU.max, ALU.add).then_inc(taken, 1)



def relations(nc, m, a):
    NR, NB = 8, 4
    layernorm(nc, m, m.X, m.XN)
    turn(nc, m, m.XN, m.XT)
    IL = 16
    w = m.BB[:, 0:KD * NR * D].rearrange("p (k r d) -> p k r d", k=KD, r=NR)
    mixer = m.AF[0:IL * NB, 0:P]
    comp = m.AF[0:IL * NB, P:P + NR]
    basis = m.AF[0:IL * NB, 256:256 + NR * KD * D].rearrange("p (q d) -> p q d", d=D)

    with Stage(nc) as st:
        loaded, masked, mixed, made, taken = (st.sem(s) for s in ("loaded", "masked", "mixed", "made", "taken"))
        block = st.block()

        @block.sync
        def _(sp):
            for i in range(IL):
                sp.dma_start(comp[i * NB:(i + 1) * NB, :], a["L3_gnn_w_comp"]).then_inc(loaded, 16)
            sp.dma_start(basis, a["L3_gnn_basis"].rearrange("b i d -> (b i) d").rearrange("(q p) d -> p q d", p=IL * NB)
                         ).then_inc(loaded, 16)

        @block.gpsimd
        def _(pool):
            g = nc.gpsimd
            mv = mixer.rearrange("p (i r) -> p i r", r=NR)
            g.memset(mixer, 1.0).then_inc(masked, 1)
            pool.wait_ge(masked, 1)
            g.affine_select(out=mv, in_=mv, compare_op=ALU.is_ge, fill=0.0, base=0, pattern=[[-NB, IL], [0, NR]],
                            channel_multiplier=1).then_inc(masked, 1)
            pool.wait_ge(masked, 2)
            g.affine_select(out=mv, in_=mv, compare_op=ALU.is_ge, fill=0.0, base=NB - 1,
                            pattern=[[NB, IL], [0, NR]], channel_multiplier=-1).then_inc(masked, 1)

        @block.vector
        def _(dve):
            dve.wait_ge(masked, 3)
            dve.wait_ge(loaded, 16 * (IL + 1))
            mv = mixer.rearrange("p (i r) -> p i r", r=NR)
            nc.vector.tensor_tensor(mv, mv, comp.unsqueeze(1).to_broadcast([IL * NB, IL, NR]), ALU.mult
                                    ).then_inc(mixed, 1)
            for q in range(NR * KD):
                dve.wait_ge(made, q + 1)
                nc.vector.tensor_copy(w[:, q % KD, q // KD, :], m.PS[:, q % 4, 0:D]).then_inc(taken, 1)

        @block.tensor
        def _(pe):
            pe.wait_ge(mixed, 1)
            for q in range(NR * KD):
                if q >= 4:
                    pe.wait_ge(taken, q - 3)
                nc.tensor.matmul(m.PS[:, q % 4, 0:D], mixer, basis[:, q, :], start=True, stop=True).then_inc(made, 1)

    with Stage(nc) as st:
        staged, made, taken_a, taken_v = (st.sem(s) for s in ("staged", "made", "taken_a", "taken_v"))
        stored = st.sems("stored", U)
        ring = view(m.WS, 0, U, KD, P)
        RO = NR * D
        outs = [view(m.BB, KD * RO + s * RO, RO) if s < 4 else view(m.AF, 0, RO) for s in range(U)]
        block = st.block()
        QB = RO // 512

        @block.sync
        def _(sp):
            to = m.table_rel.rearrange("(r t p) d -> p t r d", p=P, t=NT)
            with sp.Fori(0, NT // U) as i:
                for s in range(U):
                    t = i * U + s
                    sp.wait_ge(taken_a, 2 * t + 4)
                    sp.wait_ge(taken_v, 2 * t + 4)
                    sp.dma_start(to[:, bass.ds(t, 1), :, :].rearrange("p o r d -> p (o r) d"),
                                 outs[s].rearrange("p (r d) -> p r d", r=NR)).then_inc(stored[s], 16)
            for s in range(U):
                sp.wait_ge(stored[s], 16 * (NT // U + 1))

        @block.tensor
        def _(pe):
            pe.sem_inc(made, 2 * U)
            with pe.Fori(0, NT // U) as i:
                for s in range(U):
                    t = i * U + s
                    pe.wait_ge(staged, t + 1)
                    for half, sem in ((0, taken_a), (1, taken_v)):
                        pe.wait_ge(sem, 2 * t + 2)
                        for q in range(QB // 2 * half, QB // 2 * (half + 1)):
                            for k in range(KD):
                                mm = nc.tensor.matmul(m.PS[:, q, :], ring[:, s, k, :],
                                                      w[:, k, 2 * q:2 * q + 2, :].rearrange("p r d -> p (r d)"),
                                                      start=(k == 0), stop=(k == KD - 1))
                        mm.then_inc(made, 1)

        @block.scalar
        def _(act):
            act.sem_inc(taken_a, 2)
            for s in range(U):
                act.sem_inc(stored[s], 16)
            with act.Fori(0, NT // U) as i:
                for s in range(U):
                    t = i * U + s
                    act.wait_ge(made, 2 * t + 2)
                    nc.scalar.copy(ring[:, s, :, :], m.XT[:, :, bass.ds(t * P, P)]).then_inc(staged, 1)
                    act.wait_ge(made, 2 * t + 1 + 2 * U)
                    act.wait_ge(stored[s], i * 16 + 16)
                    for q in range(2):
                        nc.scalar.copy(outs[s][:, q * 512:(q + 1) * 512], m.PS[:, q, :]).then_inc(taken_a, 1)

        @block.vector
        def _(dve):
            dve.sem_inc(taken_v, 2)
            with dve.Fori(0, NT // U) as i:
                for s in range(U):
                    t = i * U + s
                    dve.wait_ge(made, 2 * t + 2 + 2 * U)
                    dve.wait_ge(stored[s], i * 16 + 16)
                    for q in range(2, 4):
                        nc.vector.tensor_copy(outs[s][:, q * 512:(q + 1) * 512], m.PS[:, q, :]).then_inc(taken_v, 1)

    with Stage(nc) as st:
        block = st.block()

        @block.vector
        def _(dve):
            nc.vector.memset(m.AGG[:], 0.0)

    aggregate(nc, m, m.table_rel, m.rel1)
    with Stage(nc) as st:
        loaded, dstep = st.sem("loaded"), st.sem("dstep")
        bias = m.WS[:, 0:D]
        block = st.block()

        @block.sync
        def _(sp):
            sp.dma_start(bias, a["L3_gnn_bias"].unsqueeze(0).to_broadcast([P, D])).then_inc(loaded, 16)

        @block.vector
        def _(dve):
            c = Chain(dve, dstep)
            dve.wait_ge(loaded, 16)
            c.step(nc.vector.tensor_tensor(m.XN[:], m.AGG[:, :, 0:D], bias.unsqueeze(1).to_broadcast([P, NT, D]),
                                           ALU.add))
            c.step(nc.vector.scalar_tensor_tensor(m.X[:], m.XN[:], 0.0, m.X[:], ALU.max, ALU.add))


def deep_experts(nc, m, a):
    NE, HR = 6, 128
    layernorm(nc, m, m.X, m.XN)
    turn(nc, m, m.XN, m.XT)
    routed = view(m.BB, 0, 1, NP)
    with Stage(nc) as st:
        loaded, made, taken = (st.sem(s) for s in ("loaded", "made", "taken"))
        w = view(m.WS, 0, KD, HR)
        b = view(m.WS, KD * HR, 1)
        block = st.block()

        @block.sync
        def _(sp):
            sp.dma_start(w, a["L3_ffn_router_w1"].rearrange("(k p) n -> p k n", p=P)).then_inc(loaded, 16)
            sp.dma_start(b, a["L3_ffn_router_b1"]).then_inc(loaded, 16)

        @block.tensor
        def _(pe):
            pe.wait_ge(loaded, 32)
            with pe.Fori(0, NP // CH // 2) as i:
                for u in range(2):
                    n = i * 2 + u
                    pe.wait_ge(taken, n + 1)
                    for k in range(KD):
                        mm = nc.tensor.matmul(m.PS[:, u, 0:CH], w[:, k, :], m.XT[:, k, bass.ds(n * CH, CH)],
                                              start=(k == 0), stop=(k == KD - 1))
                    mm.then_inc(made, 1)

        @block.scalar
        def _(act):
            act.sem_inc(taken, 2)
            act.wait_ge(loaded, 32)
            with act.Fori(0, NP // CH // 2) as i:
                for u in range(2):
                    n = i * 2 + u
                    act.wait_ge(made, n + 1)
                    nc.scalar.activation(routed[:, 0, bass.ds(n * CH, CH)], m.PS[:, u, 0:CH], ACT.Relu, bias=b
                                         ).then_inc(taken, 1)

    gates(nc, m, a["L3_ffn_router_w2"], a["L3_ffn_router_b2"], NE, True, hidden=routed)

    with Stage(nc) as st:
        loaded, made, active, done, biased, taken = (
            st.sem(s) for s in ("loaded", "made", "active", "done", "biased", "taken"))
        w = [view(m.BB, q * NE * KD * D, NE * KD, D) for q in range(3)]
        h1 = view(m.AF, 0, KD, CB)
        h2 = view(m.AF, KD * CB, KD, CB)
        b1, b2 = view(m.AF, 3000, NE, KD), view(m.AF, 3020, NE, KD)
        b3 = m.AF[:, 3100:3100 + NE * D]
        block = st.block()
        LAYER = KD * 2

        @block.sync
        def _(sp):
            for q in range(3):
                sp.dma_start(w[q], a[f"L3_ffn_expert_w{q + 1}"].rearrange("e (k p) n -> p (e k) n", p=P)
                             ).then_inc(loaded, 16)
            sp.dma_start(b1, a["L3_ffn_expert_b1"].rearrange("p (e k) -> p e k", k=KD)).then_inc(loaded, 16)
            sp.dma_start(b2, a["L3_ffn_expert_b2"].rearrange("p (e k) -> p e k", k=KD)).then_inc(loaded, 16)
            sp.dma_start(b3, a["L3_ffn_expert_b3"].rearrange("e d -> (e d)").unsqueeze(0).to_broadcast([P, NE * D])
                         ).then_inc(loaded, 16)

        @block.tensor
        def _(pe):
            te = nc.tensor
            pe.wait_ge(loaded, 96)
            with pe.Fori(0, NT // TB) as b:
                for e in range(NE):
                    for layer in range(2):
                        base = ((b * NE + e) * 2 + layer) * LAYER
                        for h in range(2):
                            for j in range(KD):
                                pe.wait_ge(active, base + h * KD + j + 1)
                                for k in range(KD):
                                    src = (m.XT[:, k, bass.ds(b * CB + h * CH2, CH2)] if layer == 0
                                           else h1[:, k, h * CH2:(h + 1) * CH2])
                                    mm = te.matmul(m.PS[:, j, 0:CH2], w[layer][:, e * KD + k, j * P:(j + 1) * P], src,
                                                   start=(k == 0), stop=(k == KD - 1))
                                mm.then_inc(made, 1)
                    for s in range(TB):
                        pe.wait_ge(active, ((b * NE + e) * 2 + 2) * LAYER + (0 if (s + 1) * P <= CH2 else 2))
                        pe.wait_ge(taken, (b * NE + e) * TB + s + 1)
                        for k in range(KD):
                            mm = te.matmul(m.PS[:, 3 + s, 0:D], h2[:, k, s * P:(s + 1) * P], w[2][:, e * KD + k, :],
                                           start=(k == 0), stop=(k == KD - 1))
                        mm.then_inc(done, 1)

        @block.scalar
        def _(act):
            act.sem_inc(active, 2)
            act.wait_ge(loaded, 96)
            with act.Fori(0, NT // TB) as b:
                for e in range(NE):
                    for layer, (dst, bias) in enumerate(((h1, b1), (h2, b2))):
                        base = ((b * NE + e) * 2 + layer) * LAYER
                        for h in range(2):
                            for j in range(KD):
                                act.wait_ge(made, base + h * KD + j + 1)
                                nc.scalar.activation(dst[:, j, h * CH2:(h + 1) * CH2], m.PS[:, j, 0:CH2], ACT.Relu,
                                                     bias=bias[:, e, j:j + 1]).then_inc(active, 1)

        @block.vector
        def _(dve):
            dve.sem_inc(taken, U)
            dve.wait_ge(loaded, 96)
            with dve.Fori(0, NT // TB) as b:
                for e in range(NE):
                    for s in range(TB):
                        t = b * TB + s
                        n = (b * NE + e) * TB + s
                        dve.wait_ge(taken, n + U)
                        at = tile_at(m.X, t)
                        g = tile_at(m.gate, t, e, e + 1)
                        nc.vector.scalar_tensor_tensor(at, b3[:, e * D:(e + 1) * D], g, at, ALU.mult, ALU.add
                                                       ).then_inc(biased, 1)
                        dve.wait_ge(biased, n + 1)
                        dve.wait_ge(done, n + 1)
                        nc.vector.scalar_tensor_tensor(at, m.PS[:, 3 + s, 0:D], g, at, ALU.mult, ALU.add
                                                       ).then_inc(taken, 1)


def build(nc, a, out):
    with ExitStack() as ctx:
        m = setup_memory(nc, ctx)
        constants(nc, m, a["x"])
        sort_edges(nc, m, a["dst_cols"], a["dst"], a["edge_type_8_cols"], None, a["src_cols"], False)
        gin(nc, m, a)
        slice_attention(nc, m, a)
        graph_attention(nc, m, a)
        expert_pair(nc, m, a)
        sort_edges(nc, m, a["src_cols"], a["src"], None, a["edge_attr_64"], a["dst_cols"], True)
        edge_update(nc, m, a)
        one_expert(nc, m, a)
        relations(nc, m, a)
        deep_experts(nc, m, a)
        with Stage(nc) as st:
            stored = st.sem("stored")
            block = st.block()

            @block.sync
            def _(sp):
                sp.dma_start(out.rearrange("(t p) d -> p t d", p=P), m.X[:]).then_inc(stored, 16)
                sp.wait_ge(stored, 16)


EDGE_ROWS = ET * P
TURNED = ("L0_ffn_W_x", "L2_gnn_W1", "L2_gnn_W2", "L2_gnn_W_ih", "L2_gnn_W_hh", "L2_ffn_router_w", "L3_gnn_w_comp")
COLUMNS = ("L0_gnn_g0", "L0_gnn_b0", "L0_gnn_b1a", "L0_gnn_g1", "L0_gnn_bt1", "L0_gnn_b2a", "L0_gnn_g2",
           "L0_gnn_bt2", "L0_ffn_b_x", "L1_ffn_ln_g", "L1_ffn_ln_b", "L1_ffn_b1", "L2_ffn_b1", "L3_ffn_router_b1",
           "L3_ffn_expert_b1", "L3_ffn_expert_b2")


def kernel(**inputs):
    import concourse.bacc as bacc
    from concourse.bass_utils import run_bass_kernel_spmd

    def pad(a, rows, fill=0):
        return np.concatenate([a, np.full((rows - a.shape[0],) + a.shape[1:], fill, a.dtype)])

    arrays = {}
    for name, a in inputs.items():
        a = np.asarray(a)
        if name == "x":
            a = pad(a, NP)
        elif name in ("src", "dst", "edge_type_8"):
            a = pad(a, EDGE_ROWS, 0 if name == "edge_type_8" else -1)
            arrays[name + "_cols"] = np.ascontiguousarray(a.reshape(ET, P).T)
        elif name == "edge_attr_64":
            a = pad(a, EDGE_ROWS)
        elif name in TURNED:
            a = a.T
        elif name in COLUMNS:
            a = a.reshape(-1, P).T
        arrays[name] = np.ascontiguousarray(a)
    nc = bacc.Bacc("TRN2", target_bir_lowering=False, num_devices=1)
    arrays = {f"in_{k}": a for k, a in arrays.items()}
    ins = {k[3:]: nc.dram_tensor(k, a.shape, mybir.dt.from_np(a.dtype), kind="ExternalInput").ap()
           for k, a in arrays.items()}
    out = nc.dram_tensor("out", (NP, D), F32, kind="ExternalOutput").ap()
    build(nc, ins, out)
    r = run_bass_kernel_spmd(nc, [arrays], core_ids=[0])
    return r.results[0]["out"][:N]
```
